# Optimizing a Trainium2 kernel written in Bass

```python
import numpy as np
import jax
import jax.numpy as jnp

def _softmax(x, axis=-1):
    return jax.nn.softmax(x, axis=axis)

def _gelu(x):
    return jax.nn.gelu(x, approximate=True)

def _silu(x):
    return jax.nn.silu(x)

def _sigmoid(x):
    return jax.nn.sigmoid(x)

def _layernorm(x, axis=-1, eps=1e-05):
    m = jnp.mean(x, axis=axis, keepdims=True)
    v = jnp.var(x, axis=axis, keepdims=True)
    return (x - m) / jnp.sqrt(v + eps)

def _scatter_add(tgt, idx, src, axis=0):
    return tgt.at[idx].add(src)

def _segment_sum(src, seg, n):
    return jax.ops.segment_sum(src, seg, n)
kernel_name = 'mk_decoder_postln_d4_seqx_r8_9a095b'

def setup_inputs(seed: int=0):
    np.random.seed(seed)
    _w = jnp.asarray

    def _rec_inputs():
        import jax
        import jax.numpy as jnp
        _rk = jax.random.key(seed)
        x = -0.0002928 + 1 * jax.random.normal(jax.random.fold_in(_rk, 1), (16, 128, 128), jnp.float32)
        _lenS = 128 - jax.random.randint(jax.random.fold_in(_rk, 7), (16,), 0, max(1, 128 // 4) + 1, jnp.int32)
        _lenS2 = 128 - jax.random.randint(jax.random.fold_in(_rk, 8), (16,), 0, max(1, 128 // 4) + 1, jnp.int32)
        _ctx_1024P = jax.random.normal(jax.random.fold_in(_rk, 11), (16, 16, 128), jnp.float32)
        _ctx_1024c = jax.random.dirichlet(jax.random.fold_in(_rk, 511), 0.3 * jnp.ones((16,), jnp.float32), (16, 128))
        _ctx_1024t = jnp.einsum('bsk,bkd->bsd', _ctx_1024c, _ctx_1024P)
        _ctx_1024t = _ctx_1024t * jax.lax.rsqrt(jnp.mean(jnp.square(_ctx_1024t)) + 1e-12) * 0.953939
        ctx_1024 = -1.39393e-06 + 0.999914 * (_ctx_1024t + 0.3 * jax.random.normal(jax.random.fold_in(_rk, 611), (16, 128, 128), jnp.float32))
        _validS = jnp.arange(128)[None, :] < _lenS[:, None]
        _validS2 = jnp.arange(128)[None, :] < _lenS2[:, None]
        _causal = jnp.tril(jnp.ones((128, 128), dtype=bool))
        mask_BxSxS2_ik1 = jnp.where(jnp.broadcast_to(_validS2[:, None, :], (16, 128, 128)), 1, 0).astype(jnp.int32)
        mask_BxS2_if1 = jnp.where(jnp.ones((16, 128), dtype=bool), 1, 0).astype(jnp.int32)
        return (x, ctx_1024, mask_BxSxS2_ik1, mask_BxS2_if1)
    x, ctx_1024, mask_BxSxS2_ik1, mask_BxS2_if1 = _rec_inputs()

    def _L0_attn_setup():
        import jax, jax.numpy as jnp
        import numpy as np
        from jax import lax
        B, S, D = (16, 128, 128)
        PE = 20
        NB = 3
        EPS = 1e-12

        def _lstm(x, W_ih, W_hh, b_ih, b_hh):
            b, _, _ = x.shape
            H = W_hh.shape[1]
            xg = jnp.einsum('bsd,gd->bsg', x, W_ih) + b_ih + b_hh

            def step(carry, xg_t):
                h, c = carry
                g = xg_t + h @ W_hh.T
                i, f, gg, o = jnp.split(g, 4, axis=-1)
                c = jax.nn.sigmoid(f) * c + jax.nn.sigmoid(i) * jnp.tanh(gg)
                h = jax.nn.sigmoid(o) * jnp.tanh(c)
                return ((h, c), h)
            init = (jnp.zeros((b, H), x.dtype), jnp.zeros((b, H), x.dtype))
            _, hs = lax.scan(step, init, xg.transpose(1, 0, 2))
            return hs.transpose(1, 0, 2)

        def _forward(x, W_ih, W_hh, b_ih, b_hh, W_mu, b_mu, W_sig, b_sig):
            b, s, d = x.shape
            pw = _lstm(x, W_ih, W_hh, b_ih, b_hh)
            mu_w = jax.nn.relu(jnp.einsum('bsp,np->bsn', pw, W_mu) + b_mu)
            sigma = jax.nn.sigmoid(jnp.einsum('bsp,op->bso', pw, W_sig) + b_sig)[..., 0]
            j_idx = jnp.arange(s, dtype=x.dtype)

            def mu_step(prev_mu, inputs):
                w_t, j = inputs
                mu = w_t[:, 0] * prev_mu + w_t[:, 1] / s + w_t[:, 2] * (j + 1.0) / s
                return (mu, mu)
            _, mus = lax.scan(mu_step, jnp.zeros((b,), x.dtype), (mu_w.transpose(1, 0, 2), j_idx))
            mu = mus.T
            i_idx = jnp.arange(s, dtype=x.dtype)
            rel = i_idx[None, :] / (j_idx[:, None] + 1.0)
            mask = i_idx[None, :] <= j_idx[:, None]
            w = jnp.exp(-(rel[None] - mu[:, :, None]) ** 2 / (2.0 * sigma[:, :, None] ** 2))
            w = jnp.where(mask[None], w, 0.0)
            norm = jnp.sqrt(jnp.sum(w * w, axis=-1, keepdims=True))
            w = w / jnp.maximum(norm, EPS)
            context = jnp.einsum('bji,bid->bjd', w, x)
            return context
        key = jax.random.key(seed)
        ks = jax.random.split(key, 10)
        s = lambda *sh: 0.05
        inp = {'x': jax.random.normal(ks[0], (B, S, D), dtype=jnp.float32), 'W_ih': jax.random.normal(ks[1], (4 * PE, D), dtype=jnp.float32) * 0.02, 'W_hh': jax.random.normal(ks[2], (4 * PE, PE), dtype=jnp.float32) * 0.02, 'b_ih': jax.random.normal(ks[3], (4 * PE,), dtype=jnp.float32) * 0.02, 'b_hh': jax.random.normal(ks[4], (4 * PE,), dtype=jnp.float32) * 0.02, 'W_mu': jax.random.normal(ks[5], (NB, PE), dtype=jnp.float32) * 0.1, 'b_mu': jax.random.normal(ks[6], (NB,), dtype=jnp.float32) * 0.1, 'W_sig': jax.random.normal(ks[7], (1, PE), dtype=jnp.float32) * 0.1, 'b_sig': jax.random.normal(ks[8], (1,), dtype=jnp.float32) * 0.1}
        return inp
    _L0_attn_all = _L0_attn_setup()
    _L0_attn_in = {k: v for k, v in _L0_attn_all.items() if k in ('W_ih', 'W_hh', 'b_ih', 'b_hh', 'W_mu', 'b_mu', 'W_sig', 'b_sig')}
    del _L0_attn_all

    def _L0_xattn_setup():
        import jax, jax.numpy as jnp
        import numpy as np
        H = 16
        NEG = -10000000000.0
        key = jax.random.key(seed)
        ks = jax.random.split(key, 12)
        B, S, D = (2, 256, 128)
        sc = 1.0 / np.sqrt(D)
        inp = {'q': jax.random.normal(ks[0], (B, S, D), jnp.float32), 'k': jax.random.normal(ks[1], (B, S, D), jnp.float32), 'v': jax.random.normal(ks[2], (B, S, D), jnp.float32), 'Wq': jax.random.normal(ks[3], (D, D), jnp.float32) * sc, 'bq': jax.random.normal(ks[4], (D,), jnp.float32) * 0.02, 'Wk': jax.random.normal(ks[5], (D, D), jnp.float32) * sc, 'bk': jax.random.normal(ks[6], (D,), jnp.float32) * 0.02, 'Wv': jax.random.normal(ks[7], (D, D), jnp.float32) * sc, 'bv': jax.random.normal(ks[8], (D,), jnp.float32) * 0.02, 'Wo': jax.random.normal(ks[9], (D, D), jnp.float32) * sc, 'bo': jax.random.normal(ks[10], (D,), jnp.float32) * 0.02, 'mask': jax.random.randint(ks[11], (B, S, S), 0, 2, jnp.int32)}
        return inp
    _L0_xattn_all = _L0_xattn_setup()
    _L0_xattn_in = {k: v for k, v in _L0_xattn_all.items() if k in ('Wq', 'bq', 'Wk', 'bk', 'Wv', 'bv', 'Wo', 'bo')}
    del _L0_xattn_all

    def _L0_ffn_setup():
        import jax, jax.numpy as jnp
        import numpy as np
        B, N, C, H, REG = (1, 2309, 128, 16, 5)
        D = C // H
        key = jax.random.key(seed)
        k0, k1, k2, k3 = jax.random.split(key, 4)
        x = jax.random.normal(k0, (B, N, C), dtype=jnp.float32)
        g_info = jax.random.normal(k1, (12, 2, C), dtype=jnp.float32)
        W_qkv = jax.random.normal(k2, (C, 3 * C), dtype=jnp.float32) * 0.02
        W_proj = jax.random.normal(k3, (C, C), dtype=jnp.float32) * 0.02
        b_proj = jnp.zeros((C,), dtype=jnp.float32)
        return {'x': x, 'g_info': g_info, 'W_qkv': W_qkv, 'W_proj': W_proj, 'b_proj': b_proj}
    _L0_ffn_all = _L0_ffn_setup()
    _L0_ffn_in = {k: v for k, v in _L0_ffn_all.items() if k in ('g_info', 'W_qkv', 'W_proj', 'b_proj')}
    del _L0_ffn_all

    def _L1_attn_setup():
        import jax, jax.numpy as jnp
        import numpy as np
        NUM_HEADS = 16
        LN_EPS = 1e-05
        FEAT_EPS = 0.0001
        key = jax.random.key(seed)
        ks = jax.random.split(key, 4)
        B, L, D = (2, 256, 128)
        scale = 0.02
        return {'x': jax.random.normal(ks[0], (B, L, D), dtype=jnp.float32), 'Wqkv': jax.random.normal(ks[1], (3 * D, D), dtype=jnp.float32) * scale, 'bqkv': jnp.zeros((3 * D,), dtype=jnp.float32), 'Wout': jax.random.normal(ks[2], (D, D), dtype=jnp.float32) * scale, 'bout': jnp.zeros((D,), dtype=jnp.float32), 'gamma': jnp.ones((D,), dtype=jnp.float32), 'beta': jnp.zeros((D,), dtype=jnp.float32)}
    _L1_attn_all = _L1_attn_setup()
    _L1_attn_in = {k: v for k, v in _L1_attn_all.items() if k in ('Wqkv', 'bqkv', 'Wout', 'bout', 'gamma', 'beta')}
    del _L1_attn_all

    def _L1_xattn_setup():
        import jax, jax.numpy as jnp
        import numpy as np
        key = jax.random.key(seed)
        ks = jax.random.split(key, 9)
        B, T, D = (4, 512, 128)
        scale = 1.0 / np.sqrt(D)
        inp = {'q': jax.random.normal(ks[0], (B, T, D), dtype=jnp.float32), 'k': jax.random.normal(ks[1], (B, T, D), dtype=jnp.float32), 'v': jax.random.normal(ks[2], (B, T, D), dtype=jnp.float32), 'Wq': jax.random.normal(ks[3], (D, D), dtype=jnp.float32) * scale, 'bq': jnp.zeros((D,), dtype=jnp.float32), 'Wk': jax.random.normal(ks[4], (D, D), dtype=jnp.float32) * scale, 'bk': jnp.zeros((D,), dtype=jnp.float32), 'Wv': jax.random.normal(ks[5], (D, D), dtype=jnp.float32) * scale, 'bv': jnp.zeros((D,), dtype=jnp.float32), 'mask': jnp.ones((B, T), dtype=jnp.int32)}
        return inp
    _L1_xattn_all = _L1_xattn_setup()
    _L1_xattn_in = {k: v for k, v in _L1_xattn_all.items() if k in ('Wq', 'bq', 'Wk', 'bk', 'Wv', 'bv')}
    del _L1_xattn_all

    def _L1_ffn_setup():
        import jax, jax.numpy as jnp
        import numpy as np
        LN_EPS = 1e-05

        def layer_norm(x, g, b):
            mu = jnp.mean(x, axis=-1, keepdims=True)
            var = jnp.mean(jnp.square(x - mu), axis=-1, keepdims=True)
            return (x - mu) * jax.lax.rsqrt(var + LN_EPS) * g + b

        def ternary_quant(w):
            scale = 1.0 / jnp.clip(jnp.mean(jnp.abs(w)), 1e-05)
            wq = jnp.clip(jnp.round(w * scale), -1.0, 1.0) / scale
            return w + jax.lax.stop_gradient(wq - w)
        key = jax.random.key(seed)
        ks = jax.random.split(key, 3)
        dim, hidden = (128, 512)
        B, S = (8, 128)
        x = jax.random.normal(ks[0], (B, S, dim), dtype=jnp.float32)
        w1 = jax.random.normal(ks[1], (hidden, dim), dtype=jnp.float32) * 0.02
        w2 = jax.random.normal(ks[2], (dim, hidden), dtype=jnp.float32) * 0.02
        return {'x': x, 'ln1_g': jnp.ones((dim,), jnp.float32), 'ln1_b': jnp.zeros((dim,), jnp.float32), 'w1': w1, 'b1': jnp.zeros((hidden,), jnp.float32), 'ln2_g': jnp.ones((hidden,), jnp.float32), 'ln2_b': jnp.zeros((hidden,), jnp.float32), 'w2': w2, 'b2': jnp.zeros((dim,), jnp.float32)}
    _L1_ffn_all = _L1_ffn_setup()
    _L1_ffn_in = {k: v for k, v in _L1_ffn_all.items() if k in ('ln1_g', 'ln1_b', 'w1', 'b1', 'ln2_g', 'ln2_b', 'w2', 'b2')}
    del _L1_ffn_all

    def _L2_attn_setup():
        import jax, jax.numpy as jnp
        import numpy as np
        DIM = 128
        HEADS = 16
        HIDDEN = 512
        B, N = (4, 256)

        def _mlp(x, w1, b1, w2, b2):
            h = jax.nn.gelu(x @ w1 + b1, approximate=False)
            return h @ w2 + b2
        key = jax.random.key(seed)
        ks = jax.random.split(key, 15)
        s_in = 1.0 / np.sqrt(DIM)
        s_hid = 1.0 / np.sqrt(HIDDEN)
        inp = {'x': jax.random.normal(ks[0], (B, N, DIM), dtype=jnp.float32)}
        i = 1
        for name in ('q', 'k', 'v'):
            inp[f'{name}_w1'] = jax.random.normal(ks[i], (DIM, HIDDEN), jnp.float32) * s_in
            i += 1
            inp[f'{name}_b1'] = jax.random.normal(ks[i], (HIDDEN,), jnp.float32) * s_in
            i += 1
            inp[f'{name}_w2'] = jax.random.normal(ks[i], (HIDDEN, DIM), jnp.float32) * s_hid
            i += 1
            inp[f'{name}_b2'] = jax.random.normal(ks[i], (DIM,), jnp.float32) * s_hid
            i += 1
        inp['proj_w'] = jax.random.normal(ks[13], (DIM, DIM), jnp.float32) * s_in
        inp['proj_b'] = jax.random.normal(ks[14], (DIM,), jnp.float32) * s_in
        return inp
    _L2_attn_all = _L2_attn_setup()
    _L2_attn_in = {k: v for k, v in _L2_attn_all.items() if k in ('q_w1', 'q_b1', 'q_w2', 'q_b2', 'k_w1', 'k_b1', 'k_w2', 'k_b2', 'v_w1', 'v_b1', 'v_w2', 'v_b2', 'proj_w', 'proj_b')}
    del _L2_attn_all

    def _L2_xattn_setup():
        import jax, jax.numpy as jnp
        import numpy as np
        DIM = 128
        NUM_HEADS = 16
        HEAD_DIM = DIM // NUM_HEADS
        key = jax.random.key(seed)
        ks = jax.random.split(key, 11)
        B, N, C = (2, 256, DIM)
        s = 1.0 / np.sqrt(C)
        inp = {'q': jax.random.normal(ks[0], (B, N, C), jnp.float32), 'k': jax.random.normal(ks[1], (B, N, C), jnp.float32), 'v': jax.random.normal(ks[2], (B, N, C), jnp.float32), 'Wq': jax.random.normal(ks[3], (C, C), jnp.float32) * s, 'bq': jnp.zeros((C,), jnp.float32), 'Wk': jax.random.normal(ks[4], (C, C), jnp.float32) * s, 'bk': jnp.zeros((C,), jnp.float32), 'Wv': jax.random.normal(ks[5], (C, C), jnp.float32) * s, 'bv': jnp.zeros((C,), jnp.float32), 'Wo': jax.random.normal(ks[6], (C, C), jnp.float32) * s, 'bo': jnp.zeros((C,), jnp.float32)}
        return inp
    _L2_xattn_all = _L2_xattn_setup()
    _L2_xattn_in = {k: v for k, v in _L2_xattn_all.items() if k in ('Wq', 'bq', 'Wk', 'bk', 'Wv', 'bv', 'Wo', 'bo')}
    del _L2_xattn_all

    def _L2_ffn_setup():
        import jax, jax.numpy as jnp
        import numpy as np
        LN_EPS = 1e-05

        def layernorm(x, g, b):
            mu = jnp.mean(x, axis=-1, keepdims=True)
            var = jnp.mean((x - mu) ** 2, axis=-1, keepdims=True)
            return (x - mu) * jax.lax.rsqrt(var + LN_EPS) * g + b

        def act_quant_fake(x):
            scale = 127.0 / jnp.clip(jnp.max(jnp.abs(x), axis=-1, keepdims=True), 1e-05)
            return jnp.clip(jnp.round(x * scale), -128.0, 127.0) / scale

        def weight_quant_fake(w):
            scale = 1.0 / jnp.clip(jnp.mean(jnp.abs(w)), 1e-05)
            return jnp.clip(jnp.round(w * scale), -1.0, 1.0) / scale

        def bitlinear(x, w, b):
            dqx = act_quant_fake(x)
            dqw = weight_quant_fake(w)
            return jnp.einsum('btd,hd->bth', dqx, dqw) + b
        key = jax.random.key(seed)
        ks = jax.random.split(key, 5)
        B, T, D, H = (8, 512, 128, 512)
        return {'x': jax.random.normal(ks[0], (B, T, D), dtype=jnp.float32), 'ln1_g': jnp.ones((D,), jnp.float32), 'ln1_b': jnp.zeros((D,), jnp.float32), 'w1': jax.random.normal(ks[1], (H, D), dtype=jnp.float32) * (1.0 / np.sqrt(D)), 'b1': jax.random.normal(ks[2], (H,), dtype=jnp.float32) * 0.02, 'ln2_g': jnp.ones((H,), jnp.float32), 'ln2_b': jnp.zeros((H,), jnp.float32), 'w2': jax.random.normal(ks[3], (D, H), dtype=jnp.float32) * (1.0 / np.sqrt(H)), 'b2': jax.random.normal(ks[4], (D,), jnp.float32) * 0.02}
    _L2_ffn_all = _L2_ffn_setup()
    _L2_ffn_in = {k: v for k, v in _L2_ffn_all.items() if k in ('ln1_g', 'ln1_b', 'w1', 'b1', 'ln2_g', 'ln2_b', 'w2', 'b2')}
    del _L2_ffn_all

    def _L3_attn_setup():
        import jax, jax.numpy as jnp
        import numpy as np
        DIM = 128
        N_HEADS = 16
        HEAD_DIM = DIM // N_HEADS

        def apply_rope(x):
            T, D = (x.shape[-2], x.shape[-1])
            half = D // 2
            theta = 10000.0 ** (-jnp.arange(half, dtype=jnp.float32) / half)
            pos = jnp.arange(T, dtype=jnp.float32)
            freqs = pos[:, None] * theta[None, :]
            cos, sin = (jnp.cos(freqs), jnp.sin(freqs))
            x1 = x[..., :half]
            q = half // 2
            rot = jnp.concatenate([-x1[..., q:], x1[..., :q]], axis=-1)
            x_rot = x1 * cos + rot * sin
            return jnp.concatenate([x_rot, x[..., half:]], axis=-1)
        key = jax.random.key(seed)
        ks = jax.random.split(key, 9)
        B, T = (2, 256)
        s = 0.02
        return {'x': jax.random.normal(ks[0], (B, T, DIM), dtype=jnp.float32), 'Wq': jax.random.normal(ks[1], (DIM, DIM), dtype=jnp.float32) * s, 'bq': jnp.zeros((DIM,), dtype=jnp.float32), 'Wk': jax.random.normal(ks[2], (DIM, HEAD_DIM), dtype=jnp.float32) * s, 'bk': jnp.zeros((HEAD_DIM,), dtype=jnp.float32), 'Wv': jax.random.normal(ks[3], (DIM, HEAD_DIM), dtype=jnp.float32) * s, 'bv': jnp.zeros((HEAD_DIM,), dtype=jnp.float32), 'Wo': jax.random.normal(ks[4], (DIM, DIM), dtype=jnp.float32) * s, 'bo': jnp.zeros((DIM,), dtype=jnp.float32)}
    _L3_attn_all = _L3_attn_setup()
    _L3_attn_in = {k: v for k, v in _L3_attn_all.items() if k in ('Wq', 'bq', 'Wk', 'bk', 'Wv', 'bv', 'Wo', 'bo')}
    del _L3_attn_all

    def _L3_xattn_setup():
        import jax, jax.numpy as jnp
        import numpy as np
        EPS = 1e-05

        def layer_norm(x, g, b):
            mu = jnp.mean(x, axis=-1, keepdims=True)
            var = jnp.var(x, axis=-1, keepdims=True)
            return (x - mu) * jax.lax.rsqrt(var + EPS) * g + b
        key = jax.random.key(seed)
        ks = jax.random.split(key, 8)
        dim, heads, dim_head = (128, 16, 64)
        inner = heads * dim_head
        b, n, m = (8, 512, 64)
        s = dim ** (-0.5)
        return {'x': jax.random.normal(ks[0], (b, n, dim), jnp.float32), 'latents': jax.random.normal(ks[1], (b, m, dim), jnp.float32), 'ln_m_g': jnp.ones((dim,), jnp.float32), 'ln_m_b': jnp.zeros((dim,), jnp.float32), 'ln_l_g': jnp.ones((dim,), jnp.float32), 'ln_l_b': jnp.zeros((dim,), jnp.float32), 'Wq': jax.random.normal(ks[2], (dim, inner), jnp.float32) * s, 'Wkv': jax.random.normal(ks[3], (dim, 2 * inner), jnp.float32) * s, 'Wout': jax.random.normal(ks[4], (inner, dim), jnp.float32) * s}
    _L3_xattn_all = _L3_xattn_setup()
    _L3_xattn_in = {k: v for k, v in _L3_xattn_all.items() if k in ('ln_m_g', 'ln_m_b', 'ln_l_g', 'ln_l_b', 'Wq', 'Wkv', 'Wout')}
    del _L3_xattn_all

    def _L3_ffn_setup():
        import jax, jax.numpy as jnp
        import numpy as np
        TOP_K = 2
        EPS = 1e-09
        key = jax.random.key(seed)
        ks = jax.random.split(key, 6)
        B, T, D, H, E = (4, 256, 128, 256, 8)
        x = jax.random.normal(ks[0], (B, T, D), dtype=jnp.float32)
        Wg = jax.random.normal(ks[1], (E, D), dtype=jnp.float32) * 0.02
        W1 = jax.random.normal(ks[2], (E, 2 * H, D), dtype=jnp.float32) * 0.02
        b1 = jax.random.normal(ks[3], (E, 2 * H), dtype=jnp.float32) * 0.02
        Wo = jax.random.normal(ks[4], (D, H), dtype=jnp.float32) * 0.02
        bo = jax.random.normal(ks[5], (D,), dtype=jnp.float32) * 0.02
        return {'x': x, 'Wg': Wg, 'W1': W1, 'b1': b1, 'Wo': Wo, 'bo': bo}
    _L3_ffn_all = _L3_ffn_setup()
    _L3_ffn_in = {k: v for k, v in _L3_ffn_all.items() if k in ('Wg', 'W1', 'b1', 'Wo', 'bo')}
    del _L3_ffn_all
    return {'x': x, 'ctx_1024': ctx_1024, 'mask_BxSxS2_ik1': mask_BxSxS2_ik1, 'mask_BxS2_if1': mask_BxS2_if1, 'L0_attn_W_ih': _L0_attn_in['W_ih'], 'L0_attn_W_hh': _L0_attn_in['W_hh'], 'L0_attn_b_ih': _L0_attn_in['b_ih'], 'L0_attn_b_hh': _L0_attn_in['b_hh'], 'L0_attn_W_mu': _L0_attn_in['W_mu'], 'L0_attn_b_mu': _L0_attn_in['b_mu'], 'L0_attn_W_sig': _L0_attn_in['W_sig'], 'L0_attn_b_sig': _L0_attn_in['b_sig'], 'L0_xattn_Wq': _L0_xattn_in['Wq'], 'L0_xattn_bq': _L0_xattn_in['bq'], 'L0_xattn_Wk': _L0_xattn_in['Wk'], 'L0_xattn_bk': _L0_xattn_in['bk'], 'L0_xattn_Wv': _L0_xattn_in['Wv'], 'L0_xattn_bv': _L0_xattn_in['bv'], 'L0_xattn_Wo': _L0_xattn_in['Wo'], 'L0_xattn_bo': _L0_xattn_in['bo'], 'L0_ffn_g_info': _L0_ffn_in['g_info'], 'L0_ffn_W_qkv': _L0_ffn_in['W_qkv'], 'L0_ffn_W_proj': _L0_ffn_in['W_proj'], 'L0_ffn_b_proj': _L0_ffn_in['b_proj'], 'L1_attn_Wqkv': _L1_attn_in['Wqkv'], 'L1_attn_bqkv': _L1_attn_in['bqkv'], 'L1_attn_Wout': _L1_attn_in['Wout'], 'L1_attn_bout': _L1_attn_in['bout'], 'L1_attn_gamma': _L1_attn_in['gamma'], 'L1_attn_beta': _L1_attn_in['beta'], 'L1_xattn_Wq': _L1_xattn_in['Wq'], 'L1_xattn_bq': _L1_xattn_in['bq'], 'L1_xattn_Wk': _L1_xattn_in['Wk'], 'L1_xattn_bk': _L1_xattn_in['bk'], 'L1_xattn_Wv': _L1_xattn_in['Wv'], 'L1_xattn_bv': _L1_xattn_in['bv'], 'L1_ffn_ln1_g': _L1_ffn_in['ln1_g'], 'L1_ffn_ln1_b': _L1_ffn_in['ln1_b'], 'L1_ffn_w1': _L1_ffn_in['w1'], 'L1_ffn_b1': _L1_ffn_in['b1'], 'L1_ffn_ln2_g': _L1_ffn_in['ln2_g'], 'L1_ffn_ln2_b': _L1_ffn_in['ln2_b'], 'L1_ffn_w2': _L1_ffn_in['w2'], 'L1_ffn_b2': _L1_ffn_in['b2'], 'L2_attn_q_w1': _L2_attn_in['q_w1'], 'L2_attn_q_b1': _L2_attn_in['q_b1'], 'L2_attn_q_w2': _L2_attn_in['q_w2'], 'L2_attn_q_b2': _L2_attn_in['q_b2'], 'L2_attn_k_w1': _L2_attn_in['k_w1'], 'L2_attn_k_b1': _L2_attn_in['k_b1'], 'L2_attn_k_w2': _L2_attn_in['k_w2'], 'L2_attn_k_b2': _L2_attn_in['k_b2'], 'L2_attn_v_w1': _L2_attn_in['v_w1'], 'L2_attn_v_b1': _L2_attn_in['v_b1'], 'L2_attn_v_w2': _L2_attn_in['v_w2'], 'L2_attn_v_b2': _L2_attn_in['v_b2'], 'L2_attn_proj_w': _L2_attn_in['proj_w'], 'L2_attn_proj_b': _L2_attn_in['proj_b'], 'L2_xattn_Wq': _L2_xattn_in['Wq'], 'L2_xattn_bq': _L2_xattn_in['bq'], 'L2_xattn_Wk': _L2_xattn_in['Wk'], 'L2_xattn_bk': _L2_xattn_in['bk'], 'L2_xattn_Wv': _L2_xattn_in['Wv'], 'L2_xattn_bv': _L2_xattn_in['bv'], 'L2_xattn_Wo': _L2_xattn_in['Wo'], 'L2_xattn_bo': _L2_xattn_in['bo'], 'L2_ffn_ln1_g': _L2_ffn_in['ln1_g'], 'L2_ffn_ln1_b': _L2_ffn_in['ln1_b'], 'L2_ffn_w1': _L2_ffn_in['w1'], 'L2_ffn_b1': _L2_ffn_in['b1'], 'L2_ffn_ln2_g': _L2_ffn_in['ln2_g'], 'L2_ffn_ln2_b': _L2_ffn_in['ln2_b'], 'L2_ffn_w2': _L2_ffn_in['w2'], 'L2_ffn_b2': _L2_ffn_in['b2'], 'L3_attn_Wq': _L3_attn_in['Wq'], 'L3_attn_bq': _L3_attn_in['bq'], 'L3_attn_Wk': _L3_attn_in['Wk'], 'L3_attn_bk': _L3_attn_in['bk'], 'L3_attn_Wv': _L3_attn_in['Wv'], 'L3_attn_bv': _L3_attn_in['bv'], 'L3_attn_Wo': _L3_attn_in['Wo'], 'L3_attn_bo': _L3_attn_in['bo'], 'L3_xattn_ln_m_g': _L3_xattn_in['ln_m_g'], 'L3_xattn_ln_m_b': _L3_xattn_in['ln_m_b'], 'L3_xattn_ln_l_g': _L3_xattn_in['ln_l_g'], 'L3_xattn_ln_l_b': _L3_xattn_in['ln_l_b'], 'L3_xattn_Wq': _L3_xattn_in['Wq'], 'L3_xattn_Wkv': _L3_xattn_in['Wkv'], 'L3_xattn_Wout': _L3_xattn_in['Wout'], 'L3_ffn_Wg': _L3_ffn_in['Wg'], 'L3_ffn_W1': _L3_ffn_in['W1'], 'L3_ffn_b1': _L3_ffn_in['b1'], 'L3_ffn_Wo': _L3_ffn_in['Wo'], 'L3_ffn_bo': _L3_ffn_in['bo']}

def reference(x, ctx_1024, mask_BxSxS2_ik1, mask_BxS2_if1, L0_attn_W_ih, L0_attn_W_hh, L0_attn_b_ih, L0_attn_b_hh, L0_attn_W_mu, L0_attn_b_mu, L0_attn_W_sig, L0_attn_b_sig, L0_xattn_Wq, L0_xattn_bq, L0_xattn_Wk, L0_xattn_bk, L0_xattn_Wv, L0_xattn_bv, L0_xattn_Wo, L0_xattn_bo, L0_ffn_g_info, L0_ffn_W_qkv, L0_ffn_W_proj, L0_ffn_b_proj, L1_attn_Wqkv, L1_attn_bqkv, L1_attn_Wout, L1_attn_bout, L1_attn_gamma, L1_attn_beta, L1_xattn_Wq, L1_xattn_bq, L1_xattn_Wk, L1_xattn_bk, L1_xattn_Wv, L1_xattn_bv, L1_ffn_ln1_g, L1_ffn_ln1_b, L1_ffn_w1, L1_ffn_b1, L1_ffn_ln2_g, L1_ffn_ln2_b, L1_ffn_w2, L1_ffn_b2, L2_attn_q_w1, L2_attn_q_b1, L2_attn_q_w2, L2_attn_q_b2, L2_attn_k_w1, L2_attn_k_b1, L2_attn_k_w2, L2_attn_k_b2, L2_attn_v_w1, L2_attn_v_b1, L2_attn_v_w2, L2_attn_v_b2, L2_attn_proj_w, L2_attn_proj_b, L2_xattn_Wq, L2_xattn_bq, L2_xattn_Wk, L2_xattn_bk, L2_xattn_Wv, L2_xattn_bv, L2_xattn_Wo, L2_xattn_bo, L2_ffn_ln1_g, L2_ffn_ln1_b, L2_ffn_w1, L2_ffn_b1, L2_ffn_ln2_g, L2_ffn_ln2_b, L2_ffn_w2, L2_ffn_b2, L3_attn_Wq, L3_attn_bq, L3_attn_Wk, L3_attn_bk, L3_attn_Wv, L3_attn_bv, L3_attn_Wo, L3_attn_bo, L3_xattn_ln_m_g, L3_xattn_ln_m_b, L3_xattn_ln_l_g, L3_xattn_ln_l_b, L3_xattn_Wq, L3_xattn_Wkv, L3_xattn_Wout, L3_ffn_Wg, L3_ffn_W1, L3_ffn_b1, L3_ffn_Wo, L3_ffn_bo):
    import jax
    import jax.numpy as jnp

    def _L0_attn_ref(x, W_ih, W_hh, b_ih, b_hh, W_mu, b_mu, W_sig, b_sig):
        import jax, jax.numpy as jnp
        import numpy as np
        from jax import lax
        B, S, D = (16, 128, 128)
        PE = 20
        NB = 3
        EPS = 1e-12

        def _lstm(x, W_ih, W_hh, b_ih, b_hh):
            b, _, _ = x.shape
            H = W_hh.shape[1]
            xg = jnp.einsum('bsd,gd->bsg', x, W_ih) + b_ih + b_hh

            def step(carry, xg_t):
                h, c = carry
                g = xg_t + h @ W_hh.T
                i, f, gg, o = jnp.split(g, 4, axis=-1)
                c = jax.nn.sigmoid(f) * c + jax.nn.sigmoid(i) * jnp.tanh(gg)
                h = jax.nn.sigmoid(o) * jnp.tanh(c)
                return ((h, c), h)
            init = (jnp.zeros((b, H), x.dtype), jnp.zeros((b, H), x.dtype))
            _, hs = lax.scan(step, init, xg.transpose(1, 0, 2))
            return hs.transpose(1, 0, 2)

        def _forward(x, W_ih, W_hh, b_ih, b_hh, W_mu, b_mu, W_sig, b_sig):
            b, s, d = x.shape
            pw = _lstm(x, W_ih, W_hh, b_ih, b_hh)
            mu_w = jax.nn.relu(jnp.einsum('bsp,np->bsn', pw, W_mu) + b_mu)
            sigma = jax.nn.sigmoid(jnp.einsum('bsp,op->bso', pw, W_sig) + b_sig)[..., 0]
            j_idx = jnp.arange(s, dtype=x.dtype)

            def mu_step(prev_mu, inputs):
                w_t, j = inputs
                mu = w_t[:, 0] * prev_mu + w_t[:, 1] / s + w_t[:, 2] * (j + 1.0) / s
                return (mu, mu)
            _, mus = lax.scan(mu_step, jnp.zeros((b,), x.dtype), (mu_w.transpose(1, 0, 2), j_idx))
            mu = mus.T
            i_idx = jnp.arange(s, dtype=x.dtype)
            rel = i_idx[None, :] / (j_idx[:, None] + 1.0)
            mask = i_idx[None, :] <= j_idx[:, None]
            w = jnp.exp(-(rel[None] - mu[:, :, None]) ** 2 / (2.0 * sigma[:, :, None] ** 2))
            w = jnp.where(mask[None], w, 0.0)
            norm = jnp.sqrt(jnp.sum(w * w, axis=-1, keepdims=True))
            w = w / jnp.maximum(norm, EPS)
            context = jnp.einsum('bji,bid->bjd', w, x)
            return context
        return _forward(x, W_ih, W_hh, b_ih, b_hh, W_mu, b_mu, W_sig, b_sig)

    def _L0_xattn_ref(q, k, v, Wq, bq, Wk, bk, Wv, bv, Wo, bo, mask):
        import jax, jax.numpy as jnp
        import numpy as np
        H = 16
        NEG = -10000000000.0
        B, S, D = q.shape
        dk = D // H
        qh = (q @ Wq.T + bq).reshape(B, S, H, dk).transpose(0, 2, 1, 3)
        kh = (k @ Wk.T + bk).reshape(B, S, H, dk).transpose(0, 2, 1, 3)
        vh = (v @ Wv.T + bv).reshape(B, S, H, dk).transpose(0, 2, 1, 3)
        scores = jnp.einsum('bhqd,bhkd->bhqk', qh, kh) / jnp.sqrt(jnp.float32(dk))
        scores = jnp.where(mask[:, None, :, :] == 0, jnp.float32(NEG), scores)
        attn = jax.nn.softmax(scores, axis=-1)
        ctx = jnp.einsum('bhqk,bhkd->bhqd', attn, vh)
        concat = ctx.transpose(0, 2, 1, 3).reshape(B, S, D)
        return concat @ Wo.T + bo

    def _L0_ffn_ref(x, g_info, W_qkv, W_proj, b_proj):
        import jax, jax.numpy as jnp
        import numpy as np
        B, N, C, H, REG = (1, 2309, 128, 16, 5)
        D = C // H
        Bx, Nx, Cx = x.shape
        scale = D ** (-0.5)
        qkv = (x @ W_qkv).reshape(Bx, Nx, 3, H, D)
        q, k, v = (qkv[:, :, 0], qkv[:, :, 1], qkv[:, :, 2])
        g_layer = g_info[0].reshape(-1, H, D)
        q_g = g_layer[0]
        q_pure = q[:, REG:]
        q_n = q_pure / jnp.linalg.norm(q_pure, axis=-1, keepdims=True)
        qg_n = q_g / jnp.linalg.norm(q_g, axis=-1, keepdims=True)
        sim = (qg_n[None, None] * q_n).sum(-1).mean(-1)
        sim = (sim - sim.min()) / (sim.max() - sim.min())
        pos = sim > 0.9
        logits = jnp.einsum('bqhd,bkhd->bhqk', q * scale, k)

        def masked_attn(tok_mask):
            key_mask = jnp.concatenate([jnp.ones((Bx, REG), bool), tok_mask], axis=1)
            l = jnp.where(key_mask[:, None, None, :], logits, -jnp.inf)
            a = jax.nn.softmax(l, axis=-1)
            return jnp.einsum('bhqk,bkhd->bqhd', a, v)
        x_pos = masked_attn(pos)
        x_neg = masked_attn(~pos)
        reg_out = (x_pos[:, :REG] + x_neg[:, :REG]) * 0.5
        tok_out = jnp.where(pos[:, :, None, None], x_pos[:, REG:], x_neg[:, REG:])
        out = jnp.concatenate([reg_out, tok_out], axis=1).reshape(Bx, Nx, Cx)
        return out @ W_proj + b_proj

    def _L1_attn_ref(x, Wqkv, bqkv, Wout, bout, gamma, beta):
        import jax, jax.numpy as jnp
        import numpy as np
        NUM_HEADS = 16
        LN_EPS = 1e-05
        FEAT_EPS = 0.0001
        B, L, D = x.shape
        H = NUM_HEADS
        E = D // H
        qkv = x @ Wqkv.T + bqkv
        q, k, v = jnp.split(qkv, 3, axis=-1)
        q = q.reshape(B, L, H, E)
        k = k.reshape(B, L, H, E)
        v = v.reshape(B, L, H, E)
        q = (jax.nn.elu(q) + 1.0 + FEAT_EPS) / jnp.sqrt(jnp.asarray(E, q.dtype))
        k = jax.nn.elu(k) + 1.0 + FEAT_EPS
        kv = jnp.einsum('blhe,blhf->blhef', k, v)
        kv_cumsum = jnp.cumsum(kv, axis=1)
        k_cumsum = jnp.cumsum(k, axis=1)
        num = jnp.einsum('blhe,blhef->blhf', q, kv_cumsum)
        den = jnp.einsum('blhe,blhe->blh', q, k_cumsum)[..., None] + FEAT_EPS
        out = (num / den).reshape(B, L, D)
        out = out @ Wout.T + bout
        mu = jnp.mean(out, axis=-1, keepdims=True)
        var = jnp.var(out, axis=-1, keepdims=True)
        return (out - mu) / jnp.sqrt(var + LN_EPS) * gamma + beta

    def _L1_xattn_ref(q, k, v, Wq, bq, Wk, bk, Wv, bv, mask):
        import jax, jax.numpy as jnp
        import numpy as np
        query = jnp.einsum('btd,de->bte', q, Wq) + bq
        key_ = jnp.einsum('bsd,de->bse', k, Wk) + bk
        value = jnp.einsum('bsd,de->bse', v, Wv) + bv
        dim_k = key_.shape[-1]
        scores = jnp.einsum('bte,bse->bts', query, key_) / jnp.sqrt(jnp.asarray(dim_k, dtype=query.dtype))
        scores = jnp.where(mask[:, None, :] == 0, -jnp.inf, scores)
        weights = jax.nn.softmax(scores, axis=-1)
        outputs = jnp.einsum('bts,bse->bte', weights, value)
        return outputs

    def _L1_ffn_ref(x, ln1_g, ln1_b, w1, b1, ln2_g, ln2_b, w2, b2):
        import jax, jax.numpy as jnp
        import numpy as np
        LN_EPS = 1e-05

        def layer_norm(x, g, b):
            mu = jnp.mean(x, axis=-1, keepdims=True)
            var = jnp.mean(jnp.square(x - mu), axis=-1, keepdims=True)
            return (x - mu) * jax.lax.rsqrt(var + LN_EPS) * g + b

        def ternary_quant(w):
            scale = 1.0 / jnp.clip(jnp.mean(jnp.abs(w)), 1e-05)
            wq = jnp.clip(jnp.round(w * scale), -1.0, 1.0) / scale
            return w + jax.lax.stop_gradient(wq - w)
        h = layer_norm(x, ln1_g, ln1_b)
        h = jnp.einsum('bsd,hd->bsh', h, ternary_quant(w1)) + b1
        h = jax.nn.gelu(h, approximate=False)
        h = layer_norm(h, ln2_g, ln2_b)
        out = jnp.einsum('bsh,dh->bsd', h, ternary_quant(w2)) + b2
        return out

    def _L2_attn_ref(x, q_w1, q_b1, q_w2, q_b2, k_w1, k_b1, k_w2, k_b2, v_w1, v_b1, v_w2, v_b2, proj_w, proj_b):
        import jax, jax.numpy as jnp
        import numpy as np
        DIM = 128
        HEADS = 16
        HIDDEN = 512
        B, N = (4, 256)

        def _mlp(x, w1, b1, w2, b2):
            h = jax.nn.gelu(x @ w1 + b1, approximate=False)
            return h @ w2 + b2
        Bx, Nx, C = x.shape
        hd = C // HEADS
        scale = hd ** (-0.5)

        def split_heads(t):
            return t.reshape(Bx, Nx, HEADS, hd).transpose(0, 2, 1, 3)
        q = split_heads(_mlp(x, q_w1, q_b1, q_w2, q_b2))
        k = split_heads(_mlp(x, k_w1, k_b1, k_w2, k_b2))
        v = split_heads(_mlp(x, v_w1, v_b1, v_w2, v_b2))
        attn = jnp.einsum('bhqd,bhkd->bhqk', q, k) * scale
        attn = jax.nn.softmax(attn, axis=-1)
        out = jnp.einsum('bhqk,bhkd->bhqd', attn, v)
        out = out.transpose(0, 2, 1, 3).reshape(Bx, Nx, C)
        return out @ proj_w + proj_b

    def _L2_xattn_ref(q, k, v, Wq, bq, Wk, bk, Wv, bv, Wo, bo):
        import jax, jax.numpy as jnp
        import numpy as np
        DIM = 128
        NUM_HEADS = 16
        HEAD_DIM = DIM // NUM_HEADS
        B, Nq, C = q.shape
        Nkv = k.shape[1]
        H, D = (NUM_HEADS, HEAD_DIM)
        qh = (q @ Wq.T + bq).reshape(B, Nq, H, D).transpose(0, 2, 1, 3)
        kh = (k @ Wk.T + bk).reshape(B, Nkv, H, D).transpose(0, 2, 1, 3)
        vh = (v @ Wv.T + bv).reshape(B, Nkv, H, D).transpose(0, 2, 1, 3)
        scale = D ** (-0.5)
        attn = jax.nn.softmax(jnp.einsum('bhqd,bhkd->bhqk', qh, kh) * scale, axis=-1)
        out = jnp.einsum('bhqk,bhkd->bhqd', attn, vh)
        out = out.transpose(0, 2, 1, 3).reshape(B, Nq, C)
        return out @ Wo.T + bo

    def _L2_ffn_ref(x, ln1_g, ln1_b, w1, b1, ln2_g, ln2_b, w2, b2):
        import jax, jax.numpy as jnp
        import numpy as np
        LN_EPS = 1e-05

        def layernorm(x, g, b):
            mu = jnp.mean(x, axis=-1, keepdims=True)
            var = jnp.mean((x - mu) ** 2, axis=-1, keepdims=True)
            return (x - mu) * jax.lax.rsqrt(var + LN_EPS) * g + b

        def act_quant_fake(x):
            scale = 127.0 / jnp.clip(jnp.max(jnp.abs(x), axis=-1, keepdims=True), 1e-05)
            return jnp.clip(jnp.round(x * scale), -128.0, 127.0) / scale

        def weight_quant_fake(w):
            scale = 1.0 / jnp.clip(jnp.mean(jnp.abs(w)), 1e-05)
            return jnp.clip(jnp.round(w * scale), -1.0, 1.0) / scale

        def bitlinear(x, w, b):
            dqx = act_quant_fake(x)
            dqw = weight_quant_fake(w)
            return jnp.einsum('btd,hd->bth', dqx, dqw) + b
        h = layernorm(x, ln1_g, ln1_b)
        h = bitlinear(h, w1, b1)
        h = jax.nn.gelu(h, approximate=False)
        h = layernorm(h, ln2_g, ln2_b)
        h = bitlinear(h, w2, b2)
        return h

    def _L3_attn_ref(x, Wq, bq, Wk, bk, Wv, bv, Wo, bo):
        import jax, jax.numpy as jnp
        import numpy as np
        DIM = 128
        N_HEADS = 16
        HEAD_DIM = DIM // N_HEADS

        def apply_rope(x):
            T, D = (x.shape[-2], x.shape[-1])
            half = D // 2
            theta = 10000.0 ** (-jnp.arange(half, dtype=jnp.float32) / half)
            pos = jnp.arange(T, dtype=jnp.float32)
            freqs = pos[:, None] * theta[None, :]
            cos, sin = (jnp.cos(freqs), jnp.sin(freqs))
            x1 = x[..., :half]
            q = half // 2
            rot = jnp.concatenate([-x1[..., q:], x1[..., :q]], axis=-1)
            x_rot = x1 * cos + rot * sin
            return jnp.concatenate([x_rot, x[..., half:]], axis=-1)
        B, T, C = x.shape
        H, D = (N_HEADS, HEAD_DIM)
        q = (x @ Wq + bq).reshape(B, T, H, D).transpose(0, 2, 1, 3)
        k = x @ Wk + bk
        v = x @ Wv + bv
        q = apply_rope(q)
        k = apply_rope(k)
        att = jnp.einsum('bhqd,bkd->bhqk', q, k) / jnp.sqrt(jnp.float32(D))
        causal = jnp.tril(jnp.ones((T, T), dtype=bool))
        att = jnp.where(causal[None, None], att, jnp.float32(-jnp.inf))
        att = jax.nn.softmax(att, axis=-1)
        out = jnp.einsum('bhqk,bkd->bhqd', att, v)
        out = out.transpose(0, 2, 1, 3).reshape(B, T, C)
        return out @ Wo + bo

    def _L3_xattn_ref(x, latents, ln_m_g, ln_m_b, ln_l_g, ln_l_b, Wq, Wkv, Wout):
        import jax, jax.numpy as jnp
        import numpy as np
        EPS = 1e-05

        def layer_norm(x, g, b):
            mu = jnp.mean(x, axis=-1, keepdims=True)
            var = jnp.var(x, axis=-1, keepdims=True)
            return (x - mu) * jax.lax.rsqrt(var + EPS) * g + b
        heads, dim_head = (16, 64)
        scale = dim_head ** (-0.5)
        x = layer_norm(x, ln_m_g, ln_m_b)
        lat = layer_norm(latents, ln_l_g, ln_l_b)
        b, m, _ = lat.shape
        q = lat @ Wq
        kv_input = jnp.concatenate([x, lat], axis=1)
        kv = kv_input @ Wkv
        k, v = jnp.split(kv, 2, axis=-1)

        def split_heads(t):
            return t.reshape(t.shape[0], t.shape[1], heads, dim_head).transpose(0, 2, 1, 3)
        q, k, v = (split_heads(q), split_heads(k), split_heads(v))
        dots = jnp.einsum('bhid,bhjd->bhij', q, k) * scale
        attn = jax.nn.softmax(dots, axis=-1)
        out = jnp.einsum('bhij,bhjd->bhid', attn, v)
        out = out.transpose(0, 2, 1, 3).reshape(b, m, heads * dim_head)
        return out @ Wout

    def _L3_ffn_ref(x, Wg, W1, b1, Wo, bo):
        import jax, jax.numpy as jnp
        import numpy as np
        TOP_K = 2
        EPS = 1e-09
        E = Wg.shape[0]
        gate_logits = jnp.einsum('btd,ed->bte', x, Wg)
        gate_scores = jax.nn.softmax(gate_logits, axis=-1)
        topk_val, topk_idx = jax.lax.top_k(gate_scores, TOP_K)
        topk_val = topk_val / (topk_val.sum(axis=-1, keepdims=True) + EPS)
        comb = (jax.nn.one_hot(topk_idx, E, dtype=x.dtype) * topk_val[..., None]).sum(axis=-2)
        out = jnp.zeros_like(x)
        for e in range(E):
            h = jnp.einsum('btd,hd->bth', x, W1[e]) + b1[e]
            a, b = jnp.split(h, 2, axis=-1)
            g = a * jax.nn.sigmoid(b)
            eo = jnp.einsum('bth,dh->btd', g, Wo) + bo
            out = out + eo * comb[..., e:e + 1]
        return out
    x = _layernorm(x + _L0_attn_ref(x, L0_attn_W_ih, L0_attn_W_hh, L0_attn_b_ih, L0_attn_b_hh, L0_attn_W_mu, L0_attn_b_mu, L0_attn_W_sig, L0_attn_b_sig), axis=-1)
    x = _layernorm(x + _L0_xattn_ref(x, ctx_1024, ctx_1024, L0_xattn_Wq, L0_xattn_bq, L0_xattn_Wk, L0_xattn_bk, L0_xattn_Wv, L0_xattn_bv, L0_xattn_Wo, L0_xattn_bo, mask_BxSxS2_ik1), axis=-1)
    x = _layernorm(x + _L0_ffn_ref(x, L0_ffn_g_info, L0_ffn_W_qkv, L0_ffn_W_proj, L0_ffn_b_proj), axis=-1)
    x = _layernorm(x + _L1_attn_ref(x, L1_attn_Wqkv, L1_attn_bqkv, L1_attn_Wout, L1_attn_bout, L1_attn_gamma, L1_attn_beta), axis=-1)
    x = _layernorm(x + _L1_xattn_ref(x, ctx_1024, ctx_1024, L1_xattn_Wq, L1_xattn_bq, L1_xattn_Wk, L1_xattn_bk, L1_xattn_Wv, L1_xattn_bv, mask_BxS2_if1), axis=-1)
    x = _layernorm(x + _L1_ffn_ref(x, L1_ffn_ln1_g, L1_ffn_ln1_b, L1_ffn_w1, L1_ffn_b1, L1_ffn_ln2_g, L1_ffn_ln2_b, L1_ffn_w2, L1_ffn_b2), axis=-1)
    x = _layernorm(x + _L2_attn_ref(x, L2_attn_q_w1, L2_attn_q_b1, L2_attn_q_w2, L2_attn_q_b2, L2_attn_k_w1, L2_attn_k_b1, L2_attn_k_w2, L2_attn_k_b2, L2_attn_v_w1, L2_attn_v_b1, L2_attn_v_w2, L2_attn_v_b2, L2_attn_proj_w, L2_attn_proj_b), axis=-1)
    x = _layernorm(x + _L2_xattn_ref(x, ctx_1024, ctx_1024, L2_xattn_Wq, L2_xattn_bq, L2_xattn_Wk, L2_xattn_bk, L2_xattn_Wv, L2_xattn_bv, L2_xattn_Wo, L2_xattn_bo), axis=-1)
    x = _layernorm(x + _L2_ffn_ref(x, L2_ffn_ln1_g, L2_ffn_ln1_b, L2_ffn_w1, L2_ffn_b1, L2_ffn_ln2_g, L2_ffn_ln2_b, L2_ffn_w2, L2_ffn_b2), axis=-1)
    x = _layernorm(x + _L3_attn_ref(x, L3_attn_Wq, L3_attn_bq, L3_attn_Wk, L3_attn_bk, L3_attn_Wv, L3_attn_bv, L3_attn_Wo, L3_attn_bo), axis=-1)
    x = _layernorm(x + _L3_xattn_ref(ctx_1024, x, L3_xattn_ln_m_g, L3_xattn_ln_m_b, L3_xattn_ln_l_g, L3_xattn_ln_l_b, L3_xattn_Wq, L3_xattn_Wkv, L3_xattn_Wout), axis=-1)
    x = _layernorm(x + _L3_ffn_ref(x, L3_ffn_Wg, L3_ffn_W1, L3_ffn_b1, L3_ffn_Wo, L3_ffn_bo), axis=-1)
    return x

_drawn_inputs = setup_inputs


def setup_inputs(seed=0):
    import zlib

    import numpy as np

    out = dict(_drawn_inputs(seed))
    spreads = {'L0_ffn_b_proj': (0.0, 0.1),
     'L1_attn_bqkv': (0.0, 0.1),
     'L1_attn_bout': (0.0, 0.1),
     'L1_attn_gamma': (1.0, 0.2),
     'L1_attn_beta': (0.0, 0.1),
     'L1_xattn_bq': (0.0, 0.415),
     'L1_xattn_bk': (0.0, 2.0),
     'L1_xattn_bv': (0.0, 0.1),
     'L1_ffn_ln1_g': (1.0, 0.2),
     'L1_ffn_ln1_b': (0.0, 0.359),
     'L1_ffn_b1': (0.0, 0.1),
     'L1_ffn_ln2_g': (1.0, 0.2),
     'L1_ffn_ln2_b': (0.0, 0.1),
     'L1_ffn_b2': (0.0, 0.1),
     'L2_xattn_bq': (0.0, 0.323),
     'L2_xattn_bk': (0.0, 2.0),
     'L2_xattn_bv': (0.0, 0.1),
     'L2_xattn_bo': (0.0, 0.1),
     'L2_ffn_ln1_g': (1.0, 0.2),
     'L2_ffn_ln1_b': (0.0, 0.1),
     'L2_ffn_ln2_g': (1.0, 0.2),
     'L2_ffn_ln2_b': (0.0, 0.1),
     'L3_attn_bq': (0.0, 2.0),
     'L3_attn_bk': (0.0, 2.0),
     'L3_attn_bv': (0.0, 0.1),
     'L3_attn_bo': (0.0, 0.1),
     'L3_xattn_ln_m_g': (1.0, 0.2),
     'L3_xattn_ln_m_b': (0.0, 0.1),
     'L3_xattn_ln_l_g': (1.0, 0.2),
     'L3_xattn_ln_l_b': (0.0, 0.1)}
    factors = {'L0_attn_W_ih': 8.0,
     'L0_attn_W_hh': 8.0,
     'L0_attn_b_ih': 8.0,
     'L0_attn_b_hh': 8.0,
     'L0_attn_W_mu': 8.0,
     'L0_attn_b_mu': 4.937,
     'L0_attn_W_sig': 8.0,
     'L0_xattn_bq': 8.0,
     'L0_xattn_bk': 64.0,
     'L0_xattn_bv': 3.928,
     'L0_xattn_bo': 3.709,
     'L0_ffn_g_info': 64.0,
     'L2_attn_q_w1': 6.839,
     'L2_attn_q_b1': 8.0,
     'L2_attn_q_w2': 6.869,
     'L2_attn_q_b2': 21.458,
     'L2_attn_k_w1': 6.568,
     'L2_attn_k_b1': 8.0,
     'L2_attn_k_w2': 6.215,
     'L2_attn_k_b2': 64.0,
     'L2_ffn_b1': 3.023,
     'L2_ffn_b2': 3.281,
     'L3_attn_Wq': 64.0,
     'L3_attn_Wk': 62.743,
     'L3_ffn_b1': 24.567}
    for name, (base, spread) in spreads.items():
        noise = np.random.default_rng([zlib.crc32(name.encode()), seed]).standard_normal(out[name].shape)
        drawn = base * np.exp(spread * noise) if base else spread * noise
        out[name] = jnp.asarray(drawn.astype(out[name].dtype))
    for name, factor in factors.items():
        out[name] = (out[name] * factor).astype(out[name].dtype)
    return out
```

```python
import math
from contextlib import ExitStack

import numpy as np

import concourse.bass as bass
from concourse import mybir

F32 = mybir.dt.float32
BF16 = mybir.dt.bfloat16
I32 = mybir.dt.int32
ACT = mybir.ActivationFunctionType
ALU = mybir.AluOpType
AXX = mybir.AxisListType.X

BATCH, TOK, DIM, HEADS = 16, 128, 128, 16
HD = DIM // HEADS
PAD = 32
GROUPS = HEADS * PAD // 128
PAIRS = BATCH // 2
LSTM_H, REG = 20, 5
FF = 512
EXPERTS, XH, XD = 8, 16, 64
LN_EPS = 1e-5
NEG, BIG = -1.0e10, -2.0 ** 100
ROUND = 12582912.0
REG_ROWS = HEADS * REG
SCALE = 1.0 / math.sqrt(HD)

(S_LSTM, S_X0, S_SIM, S_REG, S_LIN, S_X1, S_FF1, S_MLP, S_SELF2, S_X2, S_FF2, S_MQA, S_LAT, S_GATE,
 S_MOE) = range(15)


def nth(run, i, s, each=1, part=None):
    part = each if part is None else part
    return i * (2 * each) + ((run * BATCH + s) * each + part)


class Columns:

    def __init__(self, *sizes):
        self.at, end = {}, 0
        for name, size in sizes:
            self.at[name] = (end, size)
            end += size
        self.size = end

    def __call__(self, name, of=0, width=None):
        a, n = self.at[name]
        return slice(a + of, a + (n if width is None else of + width))


W_EARLY = Columns(("ih", 4 * LSTM_H), ("hh", 4 * LSTM_H), ("musig", 4), ("x0", 512), ("reg", 512),
                  ("lin", 512), ("x1", 384), ("ff1_up", FF), ("ff1_down", FF),
                  ("mlp_up", 3 * FF), ("mlp_down", 3 * FF), ("self2_out", DIM))
W_LATE = Columns(("lat_q", 1024), ("lat_k", 1024), ("lat_v", 1024), ("lat_out", 1024),
                 ("gate", EXPERTS), ("experts", EXPERTS * FF), ("moe_out", 256))
W_REST = Columns(("x2", 512), ("mqa", 512), ("ff2_up", FF), ("ff2_down", FF))
BIAS = Columns(("ih", 80), ("hh", 80), ("x0", 512), ("reg_out", 128), ("lin", 512), ("x1", 384),
               ("ff1_up", FF), ("ff1_down", 128), ("mlp_up", 3 * FF), ("mlp_down", 384),
               ("self2_out", 128), ("x2", 512), ("mqa", 512), ("experts", EXPERTS * FF))
ROWS = Columns(("g_query", 128), ("lin_g", 128), ("lin_b", 128), ("ff1_g1", 128), ("ff1_b1", 128),
               ("ff1_g2", FF), ("ff1_b2", FF), ("ff2_g1", 128), ("ff2_b1", 128), ("ff2_g2", FF),
               ("ff2_b2", FF), ("ff2_up", FF), ("ff2_down", 128), ("lat_mg", 128), ("lat_mb", 128),
               ("lat_lg", 128), ("lat_lb", 128), ("moe_bo", 128), ("mu_b", 4))
CONST = Columns(("ident", 128), ("rel", 128), ("tri", 128), ("triT", 128), ("causal", 128),
                ("cos", 4), ("sin", 4), ("headmask", GROUPS * HEADS), ("blockmask", 128),
                ("regsel", 128), ("notreg", 1), ("regscale", 1), ("minushalf", 16), ("third", 3),
                ("step", 128), ("earlier", 64), ("negrow", REG_ROWS))

QKP, VAUG = slice(0, 1024), slice(1024, 1536)
ARENA = 11320
ATT = Columns(("kept", 1536), ("x", 128), ("c", 128), ("xcT", 128), ("qk", 256), ("qkT", 1024),
              ("P", 2048), ("PT", 2048), ("OT", 512), ("O", 128), ("OnT", 128), ("r", 128),
              ("m", 16), ("rec", 16), ("stats", 8), ("mv", 4), ("rstd", 1), ("m2", 4),
              ("regq", GROUPS * REG_ROWS))
QKV_KEPT = ATT.at["regq"][0]
assert QKV_KEPT + PAIRS * 384 <= ARENA
FFN = Columns(("kept", 1536), ("x", 128), ("h", 128), ("hT", 128), ("u", FF), ("n", FF), ("nT", FF),
              ("hq", 128), ("hqb", 64), ("nb", FF // 2), ("nbT", FF // 2), ("hbT", 64), ("r", 128), ("stats", 8),
              ("mv", 4), ("rstd", 1), ("a", 8))
MLP = Columns(("kept", 1536), ("x", 128), ("xT", 128), ("G", 3 * FF))
LAT = Columns(("x", 128), ("c", 128), ("n", 256), ("nT", 256), ("qT", 1024), ("kT", 2048),
              ("V", 2 * XH * XD), ("P", 2048), ("PT", 2048), ("O", 1024), ("r", 128),
              ("m", 16), ("rec", 16), ("stats", 16), ("mv", 4), ("rstd", 4))
MOE = Columns(("x", 128), ("xT", 128), ("sig", 512), ("t", 512), ("acc", 256), ("accT", 256),
              ("r", 128), ("stats", 8), ("mv", 4), ("rstd", 1), ("share", EXPERTS + 1))
for c in (ATT, FFN, MLP, LAT, MOE):
    assert c.size <= ARENA


def decoder(nc, x_tok, x_T, ctx_tok, ctx_T, mask, mask_row, w_early, w_late, w_rest, bias, rows,
            const, out, last=S_MOE):
    ctx = ExitStack()
    with ctx:
        def sb(name, shape, dt=F32):
            return ctx.enter_context(nc.sbuf_tensor(name, shape, dt))

        def sem(name):
            return ctx.enter_context(nc.semaphore(name))

        x_all = sb("x_all", [128, BATCH, DIM])
        xT_all = sb("xT_all", [128, BATCH, TOK])
        ctx_all = xT_all
        ctxT_all = sb("ctxT_all", [128, BATCH, TOK])
        maskadd = sb("maskadd", [128, BATCH, TOK], BF16)
        WA = sb("WA", [128, max(W_EARLY.size, W_LATE.size)])
        WB = sb("WB", [128, W_REST.size])
        bias3 = sb("bias3", [3, BIAS.size], BF16)
        R = sb("R", [128, ROWS.size])
        C = sb("C", [128, CONST.size])
        arena = [sb(f"arena{s}", [128, ARENA]) for s in range(2)]
        ident_b = sb("ident_b", [128, 128], BF16)
        causal_b = sb("causal_b", [128, 128], BF16)
        ones_b = sb("ones_b", [128, 128], BF16)
        negrow_b = sb("negrow_b", [2, REG_ROWS], BF16)
        tern_up = sb("tern_up", [128, FF], BF16)
        tern_down = sb("tern_down", [128, 4, DIM], BF16)
        small = sb("small", [128, 112])
        gates = sb("gates", [LSTM_H, 5, BATCH])
        prod = sb("prod", [LSTM_H, 2, BATCH])
        tanh_c = sb("tanh_c", [LSTM_H, BATCH])
        hid = [sb(f"hid{k}", [128, BATCH]) for k in range(2)]
        mu_cols = sb("mu_cols", [128, 4, BATCH])
        pos_rows = xT_all[:, :, :].rearrange("p b t -> p (b t)").bitcast(BF16).rearrange(
            "p (a b t) -> p a b t", a=2, b=BATCH)
        pos_q = [arena[s][:, QKV_KEPT + 1024:QKV_KEPT + 1088].bitcast(BF16) for s in range(2)]
        comb = sb("comb", [128, BATCH, EXPERTS])
        comb_sum = sb("comb_sum", [128, BATCH])
        mrow = sb("mrow", [1, BATCH, TOK], BF16)
        ps = [[ctx.enter_context(nc.psum_tensor(f"ps{s}_{k}", [128, 512], F32)) for k in range(4)]
              for s in range(2)]

        ident = C[:, CONST("ident")]

        def cst(name):
            return C[:, CONST(name)]

        def heads(ap, h=4):
            return ap.rearrange("p (h k) -> p h k", h=h)

        loaded = sem("loaded")
        bias_in = sem("bias_in")
        mask_in = sem("mask_in")
        late_in = sem("late_in")
        rows_in = sem("rows_in")
        rest_in = sem("rest_in")
        stored = sem("stored")
        seq_done = sem("seq_done")
        const_b = sem("const_b")
        bias_cut = sem("bias_cut")
        mask_cut = sem("mask_cut")
        scaled = sem("scaled")
        w_sum = sem("w_sum")
        w_mean = sem("w_mean")
        w_tern = sem("w_tern")
        gates_sum = sem("gates_sum")
        gates_tanh = sem("gates_tanh")
        cell_new = sem("cell_new")
        cell_tanh = sem("cell_tanh")
        hid_new = sem("hid_new")
        musig_sum = sem("musig_sum")
        musig_kept = sem("musig_kept")
        scan_exp = sem("scan_exp")
        scan_out = sem("scan_out")
        scan_ps = sem("scan_ps")
        scan_cols = sem("scan_cols")
        pos_sq = sem("pos_sq")
        pos_w = sem("pos_w")
        pos_masked = sem("pos_masked")
        pos_T = sem("pos_T")
        pos_T_sb = sem("pos_T_sb")
        staged = sem("staged")
        xT_ps = sem("xT_ps")
        xT_sb = sem("xT_sb")
        y_ps = sem("y_ps")
        var_ok = sem("var_ok")
        rstd_ok = sem("rstd_ok")
        qkv_ps = sem("qkv_ps")
        qk_sb = sem("qk_sb")
        v_sb = sem("v_sb")
        qkT_ps = sem("qkT_ps")
        qT_sb = sem("qT_sb")
        kT_sb = sem("kT_sb")
        s_ps = sem("s_ps")
        s_sub = sem("s_sub")
        p_exp = sem("p_exp")
        pT_ps = sem("pT_ps")
        pT_sb = sem("pT_sb")
        oT_ps = sem("oT_ps")
        oT_sb = sem("oT_sb")
        o_ps = sem("o_ps")
        o_sb = sem("o_sb")
        on_ps = sem("on_ps")
        on_sb = sem("on_sb")
        sim_q = sem("sim_q")
        sim_sb = sem("sim_sb")
        sim_mid = sem("sim_mid")
        sim_pool = sem("sim_pool")
        sim_rows = sem("sim_rows")
        reg_q = sem("reg_q")
        reg_ps = sem("reg_ps")
        reg_m = sem("reg_m")
        reg_e = sem("reg_e")
        reg_n = sem("reg_n")
        reg_T = sem("reg_T")
        reg_Tsb = sem("reg_Tsb")
        reg_o = sem("reg_o")
        reg_om = sem("reg_om")
        reg_add = sem("reg_add")
        lin_min = sem("lin_min")
        lin_exp = sem("lin_exp")
        h_sb = sem("h_sb")
        hT_ps = sem("hT_ps")
        hT_sb = sem("hT_sb")
        up_ps = sem("up_ps")
        up_in = sem("up_in")
        up_act = sem("up_act")
        n_sb = sem("n_sb")
        nT_ps = sem("nT_ps")
        nT_sb = sem("nT_sb")
        mid_var = sem("mid_var")
        mid_rstd = sem("mid_rstd")
        mlp_ps = sem("mlp_ps")
        mlp_act = sem("mlp_act")
        mlp_out = sem("mlp_out")
        w_qk = sem("w_qk")
        w_qk_sb = sem("w_qk_sb")
        w_s = sem("w_s")
        w_m = sem("w_m")
        w_e = sem("w_e")
        w_T = sem("w_T")
        w_Tsb = sem("w_Tsb")
        l_q = sem("l_q")
        l_qsb = sem("l_qsb")
        l_k = sem("l_k")
        l_ksb = sem("l_ksb")
        l_v = sem("l_v")
        l_vsb = sem("l_vsb")
        l_s = sem("l_s")
        l_sub = sem("l_sub")
        l_exp = sem("l_exp")
        l_T = sem("l_T")
        l_Tsb = sem("l_Tsb")
        l_o = sem("l_o")
        l_osb = sem("l_osb")
        l_osum = sem("l_osum")
        gate_ps = sem("gate_ps")
        gate_exp = sem("gate_exp")
        gate_sub = sem("gate_sub")
        e_ps = sem("e_ps")
        e_sig = sem("e_sig")
        e_acc = sem("e_acc")
        acc_T = sem("acc_T")
        acc_Tsb = sem("acc_Tsb")

        block = ctx.enter_context(nc.Block())

        def v_(s, cols, name, of=0, width=None):
            return arena[s][:, cols(name, of, width)]

        def add_bias(out_ap, name, of=0, width=None, stop=True):
            return nc.tensor.matmul(out_ap, ones_b[0:3, :], bias3[:, BIAS(name, of, width)],
                                    start=False, stop=stop, skip_group_check=True)

        def stage_x(pool, sub, cols, with_ctx=None, i=None):
            for s in range(2):
                pool.wait_ge(seq_done, nth(sub, i, s))
                b = i * 2 + s
                if with_ctx is not None:
                    nc.gpsimd.tensor_copy(v_(s, cols, "c"), with_ctx[:, bass.ds(b, 1), :].rearrange("p a d -> p (a d)"))
                nc.gpsimd.tensor_copy(v_(s, cols, "x"), x_all[:, bass.ds(b, 1), :].rearrange("p a d -> p (a d)"))
                pool.drain()
                pool.sem_inc(staged, 1)

        def rstd(pool, wait_sem, done_sem, run, i, s, cols, n=1):
            pool.wait_ge(wait_sem, nth(run, i, s))
            nc.gpsimd.tensor_tensor(v_(s, cols, "rstd", 0, n), v_(s, cols, "mv", 1, 2 * n - 1)[:, ::2] if n > 1
                                    else v_(s, cols, "mv", 1, 1),
                                    cst("minushalf")[:, 0:n], ALU.pow).then_inc(done_sem, 1)

        def stats(dve, s, cols, src, width=128, at=0):
            nc.vector.bn_stats(v_(s, cols, "stats", 0, 6), src)
            dve.drain()
            nc.vector.bn_aggr(v_(s, cols, "mv", at, 2), v_(s, cols, "stats", 0, 6))
            dve.drain()
            mv = v_(s, cols, "mv", at + 1, 1)
            return nc.vector.tensor_scalar(mv, mv, LN_EPS, None, ALU.add)

        def norm(dve, s, cols, dst, src, at=0):
            return nc.vector.tensor_scalar(dst, src, v_(s, cols, "mv", 2 * at, 1),
                                           v_(s, cols, "rstd", at, 1), ALU.subtract, ALU.mult)

        def x_of(i, s):
            return x_all[:, bass.ds(i * 2 + s, 1), :].rearrange("p a d -> p (a d)")

        def tail_stats(dve, run, i, s, cols, y):
            dve.wait_ge(y_ps, nth(run, i, s))
            nc.vector.tensor_tensor(v_(s, cols, "r"), y, v_(s, cols, "x"), ALU.add)
            dve.drain()
            stats(dve, s, cols, v_(s, cols, "r")).then_inc(var_ok, 1)

        def tail_norm(dve, run, i, s, cols):
            dve.wait_ge(rstd_ok, nth(run, i, s))
            norm(dve, s, cols, x_of(i, s), v_(s, cols, "r")).then_inc(seq_done, 1)

        def transpose_x(pe, sub, i, s, cols, src="x", bank=0):
            pe.wait_ge(staged, nth(sub, i, s))
            nc.tensor.transpose(ps[s][bank][:, 0:128], v_(s, cols, src), ident).then_inc(xT_ps, 1)

        def att_pool(pool, sub, kind):
            with pool.Fori(0, PAIRS) as i:
                if sub == S_REG:
                    for s in range(2):
                        pool.wait_ge(seq_done, nth(sub, i, s))
                        nc.gpsimd.tensor_copy(pos_q[s], pos_rows[:, 0, bass.ds(i * 2 + s, 1), :]
                                              .rearrange("p a d -> p (a d)"))
                stage_x(pool, sub, ATT, ctxT_all if kind == "cross" else None, i)
                if kind == "linear":
                    for s in range(2):
                        rstd(pool, mid_var, mid_rstd, mid_run[S_LIN], i, s, ATT)
                for s in range(2):
                    rstd(pool, var_ok, rstd_ok, tail_run[sub], i, s, ATT)

        def att_pe(pe, sub, kind, W, name, bias_name, mask_kind, out_w=384, out_name=None):
            out_name = out_name or name
            xt, a = xt_run.get(sub), att_run[sub]
            with pe.Fori(0, PAIRS) as i:
                for s in range(2):
                    if kind == "kept":
                        continue
                    transpose_x(pe, sub, i, s, ATT)
                for s in range(2):
                    if kind == "kept":
                        continue
                    pe.wait_ge(xT_sb, nth(xt, i, s))
                    xT, cT = v_(s, ATT, "xcT", 0, 128), v_(s, ATT, "c") if kind == "cross" else None
                    for bank, w, parts in ((1, 0, ((xT, 0, 128), (cT, 128, 128)) if kind == "cross" else ((xT, 0, 256),)),
                                           (0, 256, ((cT if kind == "cross" else xT, 0, 128),))):
                        for n, (src, of, width) in enumerate(parts):
                            mm = nc.tensor.matmul(ps[s][bank][:, of:of + width], src,
                                                  W[:, name_cols(name, w + of, width)], start=n == 0,
                                                  stop=bias_name is None, skip_group_check=True)
                        if bias_name is not None:
                            mm = add_bias(ps[s][bank][:, 0:of + width], bias_name, w, of + width)
                        mm.then_inc(qkv_ps, 1)
                for s in range(2):
                    pe.wait_ge(qk_sb, nth(a, i, s))
                    qkp = arena[s][:, QKP]
                    for t in range(2 * GROUPS):
                        mm = nc.tensor.transpose(ps[s][2 + t // GROUPS][:, (t % GROUPS) * 128:(t % GROUPS + 1) * 128],
                                                 qkp[:, t * 128:(t + 1) * 128], ident)
                        if t % GROUPS == GROUPS - 1:
                            mm.then_inc(qkT_ps, 1)
                for s in range(2):
                    pe.wait_ge(qT_sb, nth(a, i, s))
                    pe.wait_ge(kT_sb, nth(a, i, s))
                    pe.wait_ge(v_sb, nth(a, i, s))
                    qkT = v_(s, ATT, "qkT").rearrange("p (c t k) -> p c t k", c=2, t=GROUPS)
                    for j in range(4):
                        bank = ps[s][j]
                        if mask_kind == "full":
                            nc.tensor.matmul(heads(bank[:, :]), ident_b[:, :],
                                             maskadd[:, bass.ds(i * 2 + s, 1), :].broadcast_to([128, 4, 128]),
                                             start=True, stop=False, skip_group_check=True)
                        elif mask_kind == "causal":
                            nc.tensor.matmul(heads(bank[:, :]), ident_b[:, :],
                                             causal_b[:, :].unsqueeze(1).broadcast_to([128, 4, 128]),
                                             start=True, stop=False, skip_group_check=True)
                        elif mask_kind == "pos":
                            nc.tensor.matmul(heads(bank[:, :]), pos_q[s],
                                             pos_rows[:, 1, bass.ds(i * 2 + s, 1), :].broadcast_to([128, 4, 128]),
                                             start=True, stop=False, skip_group_check=True)
                        for t in range(GROUPS):
                            p0 = PAD * j
                            q, k = qkT[p0:p0 + HD, 0, t, :], qkT[p0:p0 + HD, 1, t, :]
                            l, r = (k, q) if kind == "linear" else (q, k)
                            mm = nc.tensor.matmul(bank[:, t * 128:(t + 1) * 128], l, r,
                                                  start=mask_kind is None, stop=True,
                                                  skip_group_check=True)
                        mm.then_inc(s_ps, 1)
                if kind != "linear":
                    for s in range(2):
                        P = v_(s, ATT, "P").rearrange("p (h k) -> p h k", h=HEADS)
                        for t in range(GROUPS):
                            pe.wait_ge(p_exp, nth(soft_run[sub], i, s, GROUPS, t + 1))
                            for j in range(4):
                                mm = nc.tensor.transpose(ps[s][t][:, j * 128:(j + 1) * 128],
                                                         P[:, 4 * t + j, :], ident)
                            mm.then_inc(pT_ps, 1)
                for s in range(2):
                    PT = v_(s, ATT, "PT").rearrange("p (h k) -> p h k", h=HEADS)
                    va = arena[s][:, VAUG].rearrange("p (h d) -> p h d", h=HEADS)
                    pe.wait_ge(pT_sb, nth(a, i, s, GROUPS))
                    for h in range(HEADS):
                        t, j = h // 4, h % 4
                        mm = nc.tensor.matmul(ps[s][0][PAD * j:PAD * (j + 1), t * 128:(t + 1) * 128],
                                              va[:, h, :], PT[:, 4 * j + t, :], start=True, stop=True,
                                              skip_group_check=True)
                    mm.then_inc(oT_ps, 1)
                if sub == S_REG:
                    reg_pe(pe, i)
                for s in range(2):
                    pe.wait_ge(oT_sb, nth(a, i, s))
                    OT = v_(s, ATT, "OT").rearrange("p (t q) -> p t q", t=GROUPS)
                    for t in range(GROUPS):
                        mm = nc.tensor.transpose(ps[s][1][:, t * 128:(t + 1) * 128], OT[:, t, :], ident)
                    mm.then_inc(o_ps, 1)
                for s in range(2):
                    pe.wait_ge(o_sb, nth(a, i, s))
                    nc.tensor.transpose(ps[s][2][:, 0:128], v_(s, ATT, "O"), ident).then_inc(on_ps, 1)
                for s in range(2):
                    pe.wait_ge(on_sb, nth(a, i, s))
                    yb = ps[s][3][:, 0:128]
                    nc.tensor.matmul(yb, v_(s, ATT, "OnT"), W[:, name_cols(out_name, out_w, 128)],
                                     start=True, stop=False, skip_group_check=True)
                    if bias_name in ("x0", "lin", "x2", "mqa"):
                        mm = add_bias(yb, bias_name, 384, 128)
                    else:
                        mm = add_bias(yb, "reg_out" if sub == S_REG else "self2_out")
                    mm.then_inc(y_ps, 1)

        def att_act(act, sub, kind):
            xt, a = xt_run.get(sub), att_run[sub]
            with act.Fori(0, PAIRS) as i:
                if kind != "kept":
                    for s in range(2):
                        act.wait_ge(xT_ps, nth(xt, i, s))
                        nc.scalar.copy(v_(s, ATT, "xcT", 0, 128), ps[s][0][:, 0:128]).then_inc(xT_sb, 1)
                for s in range(2):
                    va = arena[s][:, VAUG].rearrange("p (h d) -> p h d", h=HEADS)
                    if kind == "kept":
                        act.wait_ge(staged, nth(sub, i, s))
                        v = arena[s][:, bass.ds(i * 384 + QKV_KEPT + 256, 128)]
                    else:
                        act.wait_ge(qkv_ps, nth(qkv_run[sub], i, s, 2, 2))
                        v = ps[s][0][:, 0:128]
                    nc.scalar.copy(va[:, :, 0:HD], v.rearrange("p (h d) -> p h d", h=HEADS)).then_inc(v_sb, 1)
                if kind == "linear":
                    for s in range(2):
                        act.wait_ge(lin_min, nth(0, i, s))
                        e = v_(s, ATT, "P", 0, 256)
                        nc.scalar.activation(e, e, ACT.Exp).then_inc(lin_exp, 1)
                for s in range(2):
                    act.wait_ge(qkT_ps, nth(a, i, s, 2, 1))
                    nc.scalar.copy(v_(s, ATT, "qkT", 0, 512), ps[s][2][:, :]).then_inc(qT_sb, 1)
                if kind != "linear":
                    for s in range(2):
                        act.wait_ge(qkT_ps, nth(a, i, s, 2, 2))
                        nc.scalar.copy(v_(s, ATT, "qkT", 512, 512), ps[s][3][:, :]).then_inc(kT_sb, 1)
                    for s in range(2):
                        for t in range(GROUPS):
                            act.wait_ge(s_sub, nth(soft_run[sub], i, s, GROUPS, t + 1))
                            e = v_(s, ATT, "P", 512 * t, 512)
                            nc.scalar.activation(e, e, ACT.Exp, scale=SCALE).then_inc(p_exp, 1)
                    for s in range(2):
                        for t in range(GROUPS):
                            act.wait_ge(pT_ps, nth(soft_run[sub], i, s, GROUPS, t + 1))
                            nc.scalar.copy(v_(s, ATT, "PT", 512 * t, 512), ps[s][t][:, :]).then_inc(pT_sb, 1)
                if sub == S_REG:
                    reg_act(act, i)
                for s in range(2):
                    act.wait_ge(oT_ps, nth(a, i, s))
                    nc.scalar.copy(v_(s, ATT, "OT"), ps[s][0][:, :]).then_inc(oT_sb, 1)
                for s in range(2):
                    act.wait_ge(on_ps, nth(a, i, s))
                    nc.scalar.copy(v_(s, ATT, "OnT"), ps[s][2][:, 0:128]).then_inc(on_sb, 1)

        def att_dve(dve, sub, kind):
            a = att_run[sub]
            with dve.Fori(0, PAIRS) as i:
                for s in range(2):
                    qkp = arena[s][:, QKP].rearrange("p (h d) -> p h d", d=PAD)[:, :, 0:HD]
                    if kind == "kept":
                        dve.wait_ge(staged, nth(sub, i, s))
                        src = arena[s][:, bass.ds(i * 384 + QKV_KEPT, 256)]
                    else:
                        dve.wait_ge(qkv_ps, nth(qkv_run[sub], i, s, 2, 1))
                        src = ps[s][1][:, 0:256]
                    if kind == "linear":
                        nc.vector.tensor_scalar(v_(s, ATT, "P", 0, 256), src, 0.0, None, ALU.min).then_inc(lin_min, 1)
                        continue
                    if sub == S_MQA:
                        qk = v_(s, ATT, "qk").rearrange("p (h d) -> p h d", d=HD)
                        turn = v_(s, ATT, "P", 0, 128).rearrange("p (h d) -> p h d", d=4)
                        nc.vector.tensor_copy(v_(s, ATT, "qk"), src)
                        dve.drain()
                        cos = cst("cos").unsqueeze(1).broadcast_to([128, 2 * HEADS, 4])
                        for half in range(2):
                            nc.vector.tensor_tensor(turn[:, :, 2 * half:2 * half + 2],
                                                    qk[:, :, 2 - 2 * half:4 - 2 * half],
                                                    cst("sin")[:, 2 * half:2 * half + 2].unsqueeze(1)
                                                    .broadcast_to([128, 2 * HEADS, 2]), ALU.mult)
                        dve.drain()
                        nc.vector.tensor_tensor(qkp[:, :, 0:4], qk[:, :, 0:4], cos, ALU.mult)
                        nc.vector.tensor_copy(qkp[:, :, 4:8], qk[:, :, 4:8])
                        dve.drain()
                        nc.vector.tensor_tensor(qkp[:, :, 0:4], qkp[:, :, 0:4], turn, ALU.add).then_inc(qk_sb, 1)
                        continue
                    nc.vector.tensor_copy(qkp, src.rearrange("p (h d) -> p h d", d=HD)).then_inc(qk_sb, 1)
                if kind == "linear":
                    for s in range(2):
                        qkp = arena[s][:, QKP].rearrange("p (h d) -> p h d", d=PAD)[:, :, 0:HD]
                        dve.wait_ge(lin_exp, nth(0, i, s))
                        qk = v_(s, ATT, "qk")
                        nc.vector.scalar_tensor_tensor(qk, ps[s][1][:, 0:256], 0.0, v_(s, ATT, "P", 0, 256),
                                                       ALU.max, ALU.add)
                        dve.drain()
                        nc.vector.tensor_scalar(qkp[:, 0:HEADS], qk[:, 0:128].rearrange("p (h d) -> p h d", d=HD),
                                                1e-4, SCALE, ALU.add, ALU.mult)
                        nc.vector.tensor_scalar(qkp[:, HEADS:], qk[:, 128:256].rearrange("p (h d) -> p h d", d=HD),
                                                1e-4, None, ALU.add)
                        dve.drain()
                        dve.sem_inc(qk_sb, 1)
                    for s in range(2):
                        dve.wait_ge(qkT_ps, nth(a, i, s, 2, 2))
                        nc.vector.tensor_copy(v_(s, ATT, "qkT", 512, 512), ps[s][3][:, :]).then_inc(kT_sb, 1)
                    for s in range(2):
                        for t in range(GROUPS):
                            dve.wait_ge(s_ps, nth(a, i, s, GROUPS, t + 1))
                            nc.vector.tensor_tensor(heads(v_(s, ATT, "PT", 512 * t, 512)), heads(ps[s][t][:, :]),
                                                    cst("triT").unsqueeze(1).broadcast_to([128, 4, 128]),
                                                    ALU.mult).then_inc(pT_sb, 1)
                else:
                    if sub == S_REG:
                        reg_dve_q(dve, i, a)
                    for s in range(2):
                        m = v_(s, ATT, "m")
                        for t in range(GROUPS):
                            dve.wait_ge(s_ps, nth(a, i, s, GROUPS, t + 1))
                            nc.vector.tensor_reduce(m[:, 4 * t:4 * t + 4], heads(ps[s][t][:, :]), AXX, ALU.max)
                        dve.drain()
                        for t in range(GROUPS):
                            nc.vector.tensor_tensor(heads(v_(s, ATT, "P", 512 * t, 512)), heads(ps[s][t][:, :]),
                                                    m[:, 4 * t:4 * t + 4].unsqueeze(2).broadcast_to([128, 4, 128]),
                                                    ALU.subtract).then_inc(s_sub, 1)
                if sub == S_REG:
                    reg_dve(dve, i)
                for s in range(2):
                    dve.wait_ge(o_ps, nth(a, i, s))
                    o = ps[s][1][:, :].rearrange("p (h d) -> p h d", d=PAD)
                    rec = v_(s, ATT, "rec")
                    if kind == "linear":
                        nc.vector.tensor_scalar(rec, o[:, :, HD:HD + 1].rearrange("p h d -> p (h d)"), 1e-4, None, ALU.add)
                        dve.drain()
                        nc.vector.reciprocal(rec, rec)
                    else:
                        nc.vector.reciprocal(rec, o[:, :, HD:HD + 1].rearrange("p h d -> p (h d)"))
                    dve.drain()
                    if sub == S_REG:
                        nc.vector.tensor_scalar(rec, rec, cst("regscale"), None, ALU.mult)
                        dve.drain()
                    O = v_(s, ATT, "O").rearrange("p (h d) -> p h d", d=HD)
                    mul = nc.vector.tensor_tensor(O, o[:, :, 0:HD], rec.unsqueeze(2).broadcast_to([128, HEADS, HD]), ALU.mult)
                    if sub == S_REG:
                        dve.drain()
                        dve.wait_ge(reg_add, nth(0, i, s))
                        nc.vector.tensor_tensor(v_(s, ATT, "O"), v_(s, ATT, "O"), ps[s][3][:, 0:128],
                                                ALU.add).then_inc(o_sb, 1)
                    else:
                        mul.then_inc(o_sb, 1)
                for s in range(2):
                    yb = ps[s][3][:, 0:128]
                    if kind == "linear":
                        dve.wait_ge(y_ps, nth(tail_run[sub], i, s))
                        nc.vector.tensor_copy(v_(s, ATT, "r"), yb)
                        dve.drain()
                        stats(dve, s, ATT, v_(s, ATT, "r")).then_inc(mid_var, 1)
                    else:
                        tail_stats(dve, tail_run[sub], i, s, ATT, yb)
                if kind == "linear":
                    for s in range(2):
                        dve.wait_ge(mid_rstd, nth(mid_run[S_LIN], i, s))
                        r = v_(s, ATT, "r")
                        norm(dve, s, ATT, r, r)
                        dve.drain()
                        nc.vector.tensor_tensor(r, r, R[:, ROWS("lin_g")], ALU.mult)
                        dve.drain()
                        nc.vector.tensor_tensor(r, r, R[:, ROWS("lin_b")], ALU.add)
                        dve.drain()
                        nc.vector.tensor_tensor(r, r, v_(s, ATT, "x"), ALU.add)
                        dve.drain()
                        stats(dve, s, ATT, r).then_inc(var_ok, 1)
                for s in range(2):
                    tail_norm(dve, tail_run[sub], i, s, ATT)

        xt_run = {S_X0: 0, S_SIM: 1, S_REG: 2, S_LIN: 3, S_X1: 4, S_MLP: 5, S_X2: 6, S_MQA: 7,
                  S_LAT: 8, S_GATE: 9, S_MOE: 10}
        att_run = {S_X0: 0, S_REG: 1, S_LIN: 2, S_SELF2: 3, S_X2: 4, S_MQA: 5}
        qkv_run = {S_X0: 0, S_REG: 1, S_LIN: 2, S_X2: 3, S_MQA: 4}
        soft_run = {S_X0: 0, S_REG: 1, S_SELF2: 2, S_X2: 3, S_MQA: 4}
        
        mid_run = {S_LSTM: 0, S_LIN: 1, S_FF1: 2, S_FF2: 3, S_LAT: 4}
        tail_run = {S_LSTM: 0, S_X0: 1, S_REG: 2, S_LIN: 3, S_X1: 4, S_FF1: 5, S_SELF2: 6, S_X2: 7,
                    S_FF2: 8, S_MQA: 9, S_LAT: 10, S_MOE: 11}

        def name_cols(name, of=0, width=None):
            c = W_EARLY if name in W_EARLY.at else W_REST if name in W_REST.at else W_LATE
            return c(name, of, width)

        def reg_dve_q(dve, i, a):
            for s in range(2):
                dve.wait_ge(qT_sb, nth(a, i, s))
                qT = v_(s, ATT, "qkT", 0, 512).rearrange("p (t q) -> p t q", t=GROUPS)
                hm = cst("headmask").rearrange("p (t h) -> p t h", t=GROUPS)
                qb = v_(s, ATT, "regq").rearrange("p (t h r) -> p t h r", t=GROUPS, r=REG)
                for t in range(GROUPS):
                    mul = nc.vector.tensor_tensor(qb[:, t], qT[:, t, 0:REG].unsqueeze(1).broadcast_to([128, HEADS, REG]),
                                                  hm[:, t, :].unsqueeze(2).broadcast_to([128, HEADS, REG]), ALU.mult)
                mul.then_inc(reg_q, 1)

        def reg_pe(pe, i):
            for s in range(2):
                pe.wait_ge(reg_q, nth(0, i, s))
                kT = v_(s, ATT, "qkT", 512, 512).rearrange("p (t k) -> p t k", t=GROUPS)
                bank = ps[s][2][0:REG_ROWS, 0:128]
                for t in range(GROUPS):
                    nc.tensor.matmul(bank, v_(s, ATT, "regq", t * REG_ROWS, REG_ROWS), kT[:, t, :],
                                     start=t == 0, stop=False, skip_group_check=True)
                nc.tensor.matmul(bank, negrow_b[:, :],
                                 pos_rows[0:2, 1, bass.ds(i * 2 + s, 1), :].rearrange("p a k -> p (a k)"),
                                 start=False, stop=True, skip_group_check=True).then_inc(reg_ps, 1)
            for s in range(2):
                pe.wait_ge(reg_n, nth(0, i, s))
                nc.tensor.transpose(ps[s][3][:, 0:REG_ROWS], v_(s, ATT, "P", 0, 128)[0:REG_ROWS, :],
                                    ident[0:REG_ROWS, 0:REG_ROWS]).then_inc(reg_T, 1)
            for s in range(2):
                pe.wait_ge(reg_Tsb, nth(0, i, s))
                va = arena[s][:, VAUG].rearrange("p (h d) -> p h d", h=HEADS)
                nc.tensor.matmul(ps[s][2][0:REG_ROWS, 0:128], v_(s, ATT, "P", 128, REG_ROWS), va[:, :, 0:HD],
                                 start=True, stop=True, skip_group_check=True).then_inc(reg_o, 1)
            for s in range(2):
                pe.wait_ge(reg_om, nth(0, i, s))
                nc.tensor.matmul(ps[s][3][:, 0:128], cst("regsel")[0:REG_ROWS, :],
                                 v_(s, ATT, "P", 256, 128)[0:REG_ROWS, :],
                                 start=True, stop=True, skip_group_check=True).then_inc(reg_add, 1)

        def reg_act(act, i):
            for s in range(2):
                act.wait_ge(reg_m, nth(0, i, s))
                nc.scalar.activation(v_(s, ATT, "P", 0, 128)[0:REG_ROWS, :], ps[s][2][0:REG_ROWS, 0:128], ACT.Exp,
                                     bias=v_(s, ATT, "m2", 0, 1)[0:REG_ROWS, :], scale=SCALE,
                                     accum_out=v_(s, ATT, "m2", 1, 1)[0:REG_ROWS, :]).then_inc(reg_e, 1)
            for s in range(2):
                act.wait_ge(reg_T, nth(0, i, s))
                nc.scalar.copy(v_(s, ATT, "P", 128, REG_ROWS), ps[s][3][:, 0:REG_ROWS]).then_inc(reg_Tsb, 1)

        def reg_dve(dve, i):
            for s in range(2):
                dve.wait_ge(reg_ps, nth(0, i, s))
                nc.vector.tensor_reduce(v_(s, ATT, "m2", 2, 1)[0:REG_ROWS, :], ps[s][2][0:REG_ROWS, 0:128], AXX, ALU.max)
                dve.drain()
                nc.vector.tensor_scalar(v_(s, ATT, "m2", 0, 1)[0:REG_ROWS, :], v_(s, ATT, "m2", 2, 1)[0:REG_ROWS, :],
                                        -SCALE, None, ALU.mult).then_inc(reg_m, 1)
            for s in range(2):
                dve.wait_ge(reg_e, nth(0, i, s))
                nc.vector.reciprocal(v_(s, ATT, "m2", 3, 1)[0:REG_ROWS, :], v_(s, ATT, "m2", 1, 1)[0:REG_ROWS, :])
                dve.drain()
                p = v_(s, ATT, "P", 0, 128)[0:REG_ROWS, :]
                nc.vector.tensor_scalar(p, p, v_(s, ATT, "m2", 3, 1)[0:REG_ROWS, :], None, ALU.mult).then_inc(reg_n, 1)
            for s in range(2):
                dve.wait_ge(reg_o, nth(0, i, s))
                nc.vector.tensor_tensor(v_(s, ATT, "P", 256, 128)[0:REG_ROWS, :], ps[s][2][0:REG_ROWS, 0:128],
                                        cst("blockmask")[0:REG_ROWS, :], ALU.mult).then_inc(reg_om, 1)

        def loads(sp):
            sp.dma_start(WA[:, 0:164], w_early[:, 0:164]).then_inc(loaded, 16)
            sp.dma_start(C[:, :], const).then_inc(loaded, 16)
            sp.dma_start(arena[0][0:3, 0:BIAS.size], bias).then_inc(bias_in, 16)
            sp.dma_start(xT_all[:, :, :], x_T).then_inc(loaded, 16)
            sp.dma_start(R[:, :], rows).then_inc(loaded, 16)
            sp.dma_start(WA[:, W_EARLY("ff1_up", 0, 2 * FF)], w_early[:, W_EARLY("ff1_up", 0, 2 * FF)]).then_inc(loaded, 16)
            sp.dma_start(WB[:, :], w_rest).then_inc(loaded, 16)
            sp.dma_start(x_all[:, :, :], x_tok).then_inc(loaded, 16)
            sp.dma_start(arena[1][:, 0:2048].bitcast(I32), mask).then_inc(mask_in, 16)
            sp.dma_start(arena[1][0:1, 2048:4096].bitcast(I32), mask_row).then_inc(mask_in, 16)
            sp.dma_start(ctxT_all[:, :, :], ctx_T).then_inc(rest_in, 16)
            a, b = 164, W_EARLY.at["ff1_up"][0]
            sp.dma_start(WA[:, a:b], w_early[:, a:b]).then_inc(rest_in, 16)
            a = W_EARLY.at["mlp_up"][0]
            sp.dma_start(WA[:, a:W_EARLY.size], w_early[:, a:]).then_inc(rest_in, 16)

        loads_first, loads_rest = 7, 3
        TERN = (("ff1_up", 0), ("ff1_down", 1), ("ff2_up", 2), ("ff2_down", 3))

        def W_of(name, of=0, width=None):
            return (WA if name in W_EARLY.at or name in W_LATE.at else WB)[:, name_cols(name, of, width)]

        def start_act(act):
            act.wait_ge(loaded, 16 * loads_first)
            for name, k in TERN:
                nc.scalar.activation(abs_out[:, :], W_of(name), ACT.Abs, accum_out=small[:, k:k + 1])
                act.drain()
            act.sem_inc(w_sum, 1)

        def start_pe(pe):
            pe.wait_ge(w_sum, 1)
            pe.wait_ge(const_b, 1)
            nc.tensor.matmul(ps[0][0][:, 0:4], ones_f[:, :], small[:, 0:4], start=True, stop=True).then_inc(w_mean, 1)

        def start_dve(dve):
            nc.vector.memset(ones_f[:, :], 1.0)
            nc.vector.memset(ones_b[:, :], 1.0)
            for k in range(2):
                nc.vector.memset(hid[k][:, :], 0.0)
            nc.vector.memset(gates[:, :, :], 0.0)
            dve.wait_ge(loaded, 16 * loads_first)
            nc.vector.tensor_copy(ident_b[:, :], ident)
            nc.vector.tensor_copy(causal_b[:, :], cst("causal"))
            nc.vector.tensor_copy(negrow_b[:, :], cst("negrow")[0:2, :])
            ih, hh, ms = W_of("ih"), W_of("hh"), W_of("musig")
            nc.vector.tensor_scalar(ih[:, 0:60], ih[:, 0:60], 0.5, None, ALU.mult)
            nc.vector.tensor_scalar(hh[:, 0:60], hh[:, 0:60], 0.25, None, ALU.mult)
            nc.vector.tensor_scalar(hh[:, 60:80], hh[:, 60:80], 0.5, None, ALU.mult)
            nc.vector.tensor_scalar(ms, ms, 0.5, None, ALU.mult)
            dve.drain()
            dve.sem_inc(const_b, 1)
            dve.wait_ge(w_mean, 1)
            mean, inv, back = small[:, 4:8], small[:, 8:12], small[:, 12:16]
            nc.vector.tensor_scalar(mean, ps[0][0][:, 0:4], 1.0 / (DIM * FF), 1e-5, ALU.mult, ALU.max)
            dve.drain()
            nc.vector.reciprocal(inv, mean)
            dve.drain()
            nc.vector.reciprocal(back, inv)
            g = R[:, ROWS("g_query")]
            nc.vector.tensor_tensor(gsq[:, :], g, g, ALU.mult)
            dve.drain()
            nc.vector.tensor_reduce(small[:, 16:32], gsq[:, :].rearrange("p (h d) -> p h d", d=HD), AXX, ALU.add)
            dve.drain()
            dve.sem_inc(w_mean, 1)

        ones_f = sb("ones_f", [128, 128])
        gsq = arena[1][:, 8192:8320]
        abs_out = arena[1][:, 8320:8320 + FF]
        sim_all = arena[0][:, QKV_KEPT + 512:QKV_KEPT + 1024].rearrange("p (a b h) -> p a b h", a=2, b=BATCH)
        pos64 = sb("pos64", [128, 4, BATCH])
        pos64T = sb("pos64T", [64, TOK], BF16)

        def start_pool(pool):
            pool.wait_ge(bias_in, 16)
            pool.wait_ge(loaded, 16 * loads_first)
            t3 = cst("third")
            step = 1024
            hb, mb = arena[1][0:3, 4096:4608].bitcast(BF16), arena[1][0:3, 4608:5120].bitcast(BF16)
            rest, acc = arena[1][0:3, 5120:6144], arena[1][0:3, 6144:7168]
            edges = [0, 160] + list(range(160 + step, BIAS.size, step)) + [BIAS.size]
            for a, b in zip(edges, edges[1:]):
                n, src = b - a, arena[0][0:3, a:b]
                if a == 0:
                    for g in (0, 80):
                        nc.gpsimd.tensor_scalar(arena[0][0:3, g:g + 60], arena[0][0:3, g:g + 60], 0.5, None, ALU.mult)
                    pool.drain()
                nc.gpsimd.tensor_copy(hb[:, 0:n], src)
                pool.drain()
                nc.gpsimd.tensor_tensor(rest[:, 0:n], src, hb[:, 0:n], ALU.subtract)
                pool.drain()
                nc.gpsimd.tensor_copy(mb[:, 0:n], rest[:, 0:n])
                pool.drain()
                nc.gpsimd.tensor_tensor(rest[:, 0:n], rest[:, 0:n], mb[:, 0:n], ALU.subtract)
                nc.gpsimd.tensor_scalar(acc[:, 0:n], hb[:, 0:n], t3[0:3, 0:1], None, ALU.mult)
                nc.gpsimd.tensor_scalar(src, mb[:, 0:n], t3[0:3, 1:2], None, ALU.mult)
                pool.drain()
                nc.gpsimd.tensor_tensor(acc[:, 0:n], acc[:, 0:n], src, ALU.add)
                nc.gpsimd.tensor_scalar(rest[:, 0:n], rest[:, 0:n], t3[0:3, 2:3], None, ALU.mult)
                pool.drain()
                nc.gpsimd.tensor_tensor(bias3[:, a:b], acc[:, 0:n], rest[:, 0:n], ALU.add)
                pool.drain()
                pool.sem_inc(bias_cut, 1)
                if a == 0:
                    pool.wait_ge(w_mean, 2)
                    nc.gpsimd.tensor_tensor(small[:, 32:48], small[:, 16:32], cst("minushalf"), ALU.pow)
                    pool.drain()
                    pool.sem_inc(w_tern, 1)
            pool.wait_ge(mask_in, 32)
            m32 = arena[1][:, 0:2048].bitcast(I32)
            nc.gpsimd.tensor_scalar(maskadd[:, :, :].rearrange("p b k -> p (b k)"), m32, 0.0, NEG, ALU.is_equal, ALU.mult)
            nc.gpsimd.tensor_scalar(mrow[:, :, :].rearrange("p b k -> p (b k)"),
                                    arena[1][0:1, 2048:4096].bitcast(I32), 0.0, BIG, ALU.is_equal, ALU.mult)
            for name, k in TERN:
                w = W_of(name)
                nc.gpsimd.tensor_scalar(abs_out[:, :], w, small[:, 8 + k:9 + k], None, ALU.mult)
                pool.drain()
                nc.gpsimd.tensor_scalar(abs_out[:, :], abs_out[:, :], ROUND, None, ALU.add)
                pool.drain()
                nc.gpsimd.tensor_scalar(abs_out[:, :], abs_out[:, :], -ROUND, None, ALU.add)
                pool.drain()
                dst = {2: tern_up[:, :], 3: tern_down[:, :, :].rearrange("p a d -> p (a d)")}.get(k, abs_out[:, :])
                nc.gpsimd.tensor_scalar(dst, abs_out[:, :], 1.0, -1.0, ALU.min, ALU.max)
                pool.drain()
                if k < 2:
                    nc.gpsimd.tensor_scalar(abs_out[:, :], abs_out[:, :], small[:, 12 + k:13 + k], None, ALU.mult)
                    pool.drain()
                    nc.gpsimd.tensor_tensor(abs_out[:, :], abs_out[:, :], w, ALU.subtract)
                    pool.drain()
                    nc.gpsimd.tensor_tensor(w, w, abs_out[:, :], ALU.add)
                    pool.drain()
            for s in range(2):
                nc.gpsimd.memset(arena[s][:, QKP], 0.0)
                nc.gpsimd.memset(arena[s][:, VAUG], 0.0)
                pool.drain()
                nc.gpsimd.memset(arena[s][:, VAUG].rearrange("p (h d) -> p h d", h=HEADS)[:, :, HD:HD + 1], 1.0)
            pool.drain()
            pool.sem_inc(w_tern, 1)
            pool.sem_inc(seq_done, 2)

        STEPS, HALF = 16, 8
        gate_banks = [ps[0][1], ps[0][2]]
        ms_bank = ps[1][0]
        ms_all = arena[1][0:BATCH, 8832:9344].rearrange("p (t n) -> p t n", n=4)
        scan_t = arena[1][0:BATCH, 9344:10112].rearrange("p (n t) -> p n t", n=6)

        def lstm_pe(pe):
            pe.wait_ge(bias_cut, 1)
            pe.wait_ge(const_b, 1)
            with pe.Fori(0, TOK // STEPS) as it:
                for k in range(STEPS):
                    g = gate_banks[k // HALF][0:LSTM_H, :].rearrange("p (t g b) -> p t g b", t=HALF, g=4)
                    if k % HALF == 0:
                        xs = xT_all[:, :, bass.ds(it * STEPS + k, HALF)].rearrange("p b t -> p t b")
                        for gt in range(4):
                            w = slice(20 * gt, 20 * gt + 20)
                            nc.tensor.matmul(g[:, :, gt, :], W_of("ih")[:, w], xs, start=gt == 0, stop=False,
                                             skip_group_check=True)
                            for name in ("ih", "hh"):
                                nc.tensor.matmul(g[:, :, gt, :], bias3[:, BIAS(name, 20 * gt, 20)],
                                                 ones_b[0:3, :].rearrange("p (t b) -> p t b", t=HALF),
                                                 start=False, stop=False, skip_group_check=True)
                    pe.wait_ge(hid_new, it * STEPS + (k + 1))
                    h = hid[(k + 1) % 2][:, :]
                    for gt in range(4):
                        mm = nc.tensor.matmul(g[:, k % HALF, gt, :], W_of("hh")[:, 20 * gt:20 * gt + 20], h,
                                              start=False, stop=True, skip_group_check=True)
                    mm.then_inc(gates_sum, 1)
                    if k > 0:
                        nc.tensor.matmul(ms_bank[0:BATCH, 4 * (k - 1):4 * k], h, W_of("musig"),
                                         start=True, stop=True, skip_group_check=True)
                pe.wait_ge(hid_new, it * STEPS + (STEPS + 1))
                nc.tensor.matmul(ms_bank[0:BATCH, 4 * (STEPS - 1):4 * STEPS], hid[1][:, :], W_of("musig"),
                                 start=True, stop=True, skip_group_check=True).then_inc(musig_sum, 1)
                pe.wait_ge(musig_kept, it + 1)
            pe.wait_ge(scan_out, 2)
            nc.tensor.transpose(ps[0][1][:, 0:16], scan_t[:, 4, :], ident[0:16, 0:16])
            nc.tensor.transpose(ps[0][1][:, 16:32], scan_t[:, 5, :], ident[0:16, 0:16]).then_inc(scan_ps, 1)

        def lstm_act(act):
            with act.Fori(0, TOK // STEPS) as it:
                for k in range(STEPS):
                    g = gate_banks[k // HALF][0:LSTM_H, :].rearrange("p (t n) -> p t n", t=HALF)
                    act.wait_ge(gates_sum, it * STEPS + k + 1)
                    nc.scalar.activation(gates[:, 0:4, :].rearrange("p g b -> p (g b)"), g[:, k % HALF, :],
                                         ACT.Tanh).then_inc(gates_tanh, 1)
                    act.wait_ge(cell_new, it * STEPS + k + 1)
                    nc.scalar.activation(tanh_c[:, :], gates[:, 4, :], ACT.Tanh, scale=0.5).then_inc(cell_tanh, 1)
                act.wait_ge(musig_sum, it + 1)
                nc.scalar.copy(ms_all[:, bass.ds(it * STEPS, STEPS), :],
                               ms_bank[0:BATCH, 0:4 * STEPS].rearrange("p (t n) -> p t n", n=4)).then_inc(musig_kept, 1)
            act.wait_ge(scan_out, 1)
            nc.scalar.activation(scan_t[:, 3, :], scan_t[:, 3, :], ACT.Exp, scale=-1.0).then_inc(scan_exp, 1)

        def lstm_dve(dve):
            dve.sem_inc(hid_new, 1)
            with dve.Fori(0, TOK // STEPS) as it:
                for k in range(STEPS):
                    dve.wait_ge(gates_tanh, it * STEPS + k + 1)
                    nc.vector.scalar_tensor_tensor(prod[:, :, :], gates[:, 0:2, :], 1.0, gates[:, 3:5, :], ALU.add, ALU.mult)
                    dve.drain()
                    nc.vector.scalar_tensor_tensor(gates[:, 4, :], prod[:, 1, :], 0.5, prod[:, 0, :],
                                                   ALU.mult, ALU.add).then_inc(cell_new, 1)
                    dve.wait_ge(cell_tanh, it * STEPS + k + 1)
                    nc.vector.scalar_tensor_tensor(hid[k % 2][0:LSTM_H, :], gates[:, 2, :], 1.0, tanh_c[:, :],
                                                   ALU.add, ALU.mult).then_inc(hid_new, 1)
            dve.wait_ge(musig_kept, TOK // STEPS)
            z = ms_all[:, :, :]
            nc.vector.tensor_tensor(z, z, R[0:BATCH, ROWS("mu_b")].unsqueeze(1).broadcast_to([BATCH, TOK, 4]), ALU.add)
            dve.drain()
            zc = z.rearrange("p t n -> p n t")
            nc.vector.tensor_copy(scan_t[:, 3, :], zc[:, 3, :]).then_inc(scan_out, 1)
            nc.vector.tensor_scalar(scan_t[:, 0:3, :], zc[:, 0:3, :], 0.0, None, ALU.max)
            dve.drain()
            nc.vector.tensor_tensor(scan_t[:, 2, :], scan_t[:, 2, :], cst("step")[0:BATCH, :], ALU.mult)
            dve.drain()
            nc.vector.scalar_tensor_tensor(scan_t[:, 1, :], scan_t[:, 1, :], 1.0 / TOK, scan_t[:, 2, :], ALU.mult, ALU.add)
            dve.drain()
            nc.vector.tensor_tensor_scan(scan_t[:, 4, :], scan_t[:, 0, :], scan_t[:, 1, :], 0.0, ALU.mult, ALU.add)
            dve.drain()
            nc.vector.tensor_scalar(scan_t[:, 4, :], scan_t[:, 4, :], -1.0, None, ALU.mult)
            dve.wait_ge(scan_exp, 1)
            nc.vector.tensor_scalar(scan_t[:, 5, :], scan_t[:, 3, :], 1.0, None, ALU.add)
            dve.drain()
            dve.sem_inc(scan_out, 1)
            dve.wait_ge(scan_ps, 1)
            nc.vector.tensor_copy(mu_cols[:, 0:2, :], ps[0][1][:, 0:32].rearrange("p (a b) -> p a b", a=2))
            dve.drain()
            nc.vector.scalar_tensor_tensor(mu_cols[:, 1, :], mu_cols[:, 1, :], -0.5, mu_cols[:, 1, :], ALU.mult, ALU.mult)
            dve.drain()
            dve.sem_inc(scan_cols, 1)

        def pos_pool(pool):
            pool.wait_ge(scan_cols, 1)
            with pool.Fori(0, PAIRS) as i:
                stage_x(pool, S_LSTM, ATT, None, i)
                for s in range(2):
                    rstd(pool, mid_var, mid_rstd, mid_run[S_LSTM], i, s, ATT)
                for s in range(2):
                    rstd(pool, var_ok, rstd_ok, tail_run[S_LSTM], i, s, ATT)

        def pos_act(act):
            with act.Fori(0, PAIRS) as i:
                for s in range(2):
                    act.wait_ge(staged, nth(S_LSTM, i, s))
                    b = i * 2 + s
                    nc.scalar.activation(v_(s, ATT, "P", 0, 128), cst("rel"), ACT.Square,
                                         bias=mu_cols[:, 0, bass.ds(b, 1)])
                    act.drain()
                    nc.scalar.activation(v_(s, ATT, "P", 0, 128), v_(s, ATT, "P", 0, 128), ACT.Exp,
                                         scale=mu_cols[:, 1, bass.ds(b, 1)]).then_inc(pos_w, 1)
                for s in range(2):
                    act.wait_ge(pos_masked, nth(0, i, s))
                    nc.scalar.activation(v_(s, ATT, "P", 256, 128), v_(s, ATT, "P", 128, 128), ACT.Square,
                                         accum_out=v_(s, ATT, "m2", 0, 1)).then_inc(pos_sq, 1)
                for s in range(2):
                    act.wait_ge(pos_T, nth(0, i, s))
                    nc.scalar.copy(v_(s, ATT, "PT", 0, 128), ps[s][0][:, 0:128]).then_inc(pos_T_sb, 1)

        def pos_pe(pe):
            with pe.Fori(0, PAIRS) as i:
                for s in range(2):
                    pe.wait_ge(pos_masked, nth(0, i, s))
                    nc.tensor.transpose(ps[s][0][:, 0:128], v_(s, ATT, "P", 128, 128), ident).then_inc(pos_T, 1)
                for s in range(2):
                    pe.wait_ge(pos_T_sb, nth(0, i, s))
                    nc.tensor.matmul(ps[s][1][:, 0:128], v_(s, ATT, "PT", 0, 128), v_(s, ATT, "x"),
                                     start=True, stop=True).then_inc(y_ps, 1)

        def pos_dve(dve):
            with dve.Fori(0, PAIRS) as i:
                for s in range(2):
                    dve.wait_ge(pos_w, nth(0, i, s))
                    nc.vector.tensor_tensor(v_(s, ATT, "P", 128, 128), v_(s, ATT, "P", 0, 128), cst("tri"),
                                            ALU.mult).then_inc(pos_masked, 1)
                for s in range(2):
                    dve.wait_ge(pos_sq, nth(0, i, s))
                    nc.vector.tensor_scalar(v_(s, ATT, "mv", 1, 1), v_(s, ATT, "m2", 0, 1), 1e-24, None,
                                            ALU.max).then_inc(mid_var, 1)
                for s in range(2):
                    dve.wait_ge(mid_rstd, nth(mid_run[S_LSTM], i, s))
                    dve.wait_ge(y_ps, nth(tail_run[S_LSTM], i, s))
                    nc.vector.scalar_tensor_tensor(v_(s, ATT, "r"), ps[s][1][:, 0:128], v_(s, ATT, "rstd"),
                                                   v_(s, ATT, "x"), ALU.mult, ALU.add)
                    dve.drain()
                    stats(dve, s, ATT, v_(s, ATT, "r")).then_inc(var_ok, 1)
                for s in range(2):
                    tail_norm(dve, tail_run[S_LSTM], i, s, ATT)

        all_done = 2 + BATCH

        def sim_pool_(pool):
            nc.gpsimd.memset(xT_all[:, :, :], 0.0).then_inc(sim_pool, 1)
            with pool.Fori(0, PAIRS) as i:
                stage_x(pool, S_SIM, ATT, None, i)
            pool.wait_ge(seq_done, all_done + BATCH * S_SIM)
            n2 = sim_all[:, 0, :, :]
            nc.gpsimd.tensor_tensor(n2, n2, cst("minushalf").unsqueeze(1).broadcast_to([128, BATCH, HEADS]),
                                    ALU.pow).then_inc(sim_pool, 1)
            pool.wait_ge(rows_in, 64)

        def sim_sp(sp):
            sp.wait_ge(sim_mid, 5)
            sp.wait_ge(sim_pool, 1)
            for side in range(2):
                for r in range(2):
                    q = 32 * side + 16 * r
                    sp.dma_start(pos_rows[r:r + 1, side, :, :], pos64T[q:q + 16, :]).then_inc(rows_in, 16)

        def sim_pe(pe):
            with pe.Fori(0, PAIRS) as i:
                for s in range(2):
                    transpose_x(pe, S_SIM, i, s, ATT)
                for s in range(2):
                    pe.wait_ge(xT_sb, nth(xt_run[S_SIM], i, s))
                    nc.tensor.matmul(ps[s][1][:, 0:128], v_(s, ATT, "xcT", 0, 128), WA[:, W_EARLY("reg", 0, 128)],
                                     start=True, stop=True).then_inc(sim_q, 1)
            pe.wait_ge(sim_mid, 1)
            nc.tensor.transpose(ps[0][0][0:16, 0:128], small[:, 48:64], ident).then_inc(sim_rows, 1)
            pe.wait_ge(sim_mid, 2)
            nc.tensor.transpose(ps[0][1][0:2, 0:16], small[0:16, 64:66], ident[0:16, 0:16]).then_inc(sim_rows, 1)
            pe.wait_ge(sim_mid, 3)
            nc.tensor.matmul(ps[0][2][:, 0:2], ones_f[0:2, :], small[0:2, 68:70], start=True, stop=True).then_inc(sim_rows, 1)
            pe.wait_ge(sim_mid, 4)
            nc.tensor.transpose(ps[0][3][0:64, 0:128], pos64[:, :, :].rearrange("p a b -> p (a b)"), ident).then_inc(sim_rows, 1)
            pe.wait_ge(rows_in, 64)

        def sim_act(act):
            with act.Fori(0, PAIRS) as i:
                for s in range(2):
                    act.wait_ge(xT_ps, nth(xt_run[S_SIM], i, s))
                    nc.scalar.copy(v_(s, ATT, "xcT", 0, 128), ps[s][0][:, 0:128]).then_inc(xT_sb, 1)
                for s in range(2):
                    act.wait_ge(sim_q, nth(0, i, s))
                    nc.scalar.copy(v_(s, ATT, "qk", 0, 128), ps[s][1][:, 0:128])
                    nc.scalar.activation(v_(s, ATT, "qk", 128, 128), ps[s][1][:, 0:128], ACT.Square)
                    act.drain()
                    act.sem_inc(sim_sb, 1)

        def sim_dve(dve):
            dve.wait_ge(w_tern, 1)
            g3 = R[:, ROWS("g_query")].rearrange("p (h d) -> p h d", d=HD)
            nc.vector.tensor_tensor(g3, g3, small[:, 32:48].unsqueeze(2).broadcast_to([128, HEADS, HD]), ALU.mult)
            dve.drain()
            with dve.Fori(0, PAIRS) as i:
                for s in range(2):
                    dve.wait_ge(sim_sb, nth(0, i, s))
                    b = i * 2 + s
                    q, sq = v_(s, ATT, "qk", 0, 128), v_(s, ATT, "qk", 128, 128)
                    nc.vector.tensor_reduce(sim_all[:, 0, bass.ds(b, 1), :].rearrange("p a h -> p (a h)"),
                                            sq.rearrange("p (h d) -> p h d", d=HD), AXX, ALU.add)
                    nc.vector.tensor_tensor(v_(s, ATT, "r"), q, R[:, ROWS("g_query")], ALU.mult)
                    dve.drain()
                    nc.vector.tensor_reduce(sim_all[:, 1, bass.ds(b, 1), :].rearrange("p a h -> p (a h)"),
                                            v_(s, ATT, "r").rearrange("p (h d) -> p h d", d=HD), AXX,
                                            ALU.add).then_inc(seq_done, 1)
            dve.wait_ge(sim_pool, 2)
            n2, dot = sim_all[:, 0, :, :], sim_all[:, 1, :, :]
            sim = small[:, 48:64]
            nc.vector.tensor_tensor(dot, dot, n2, ALU.mult)
            dve.drain()
            nc.vector.tensor_reduce(sim, dot, AXX, ALU.add)
            dve.drain()
            nc.vector.tensor_scalar(sim, sim, 1.0 / HEADS, None, ALU.mult).then_inc(sim_mid, 1)
            dve.wait_ge(sim_rows, 1)
            nc.vector.tensor_reduce(small[0:16, 64:65], ps[0][0][0:16, REG:TOK], AXX, ALU.max)
            nc.vector.tensor_reduce(small[0:16, 65:66], ps[0][0][0:16, REG:TOK], AXX, ALU.min)
            dve.drain()
            nc.vector.tensor_scalar(small[0:16, 65:66], small[0:16, 65:66], -1.0, None, ALU.mult).then_inc(sim_mid, 1)
            dve.wait_ge(sim_rows, 2)
            nc.vector.tensor_reduce(small[0:2, 67:68], ps[0][1][0:2, 0:16], AXX, ALU.max)
            dve.drain()
            nc.vector.tensor_scalar(small[0:2, 68:70], ident[0:2, 0:2], small[0:2, 67:68], None, ALU.mult).then_inc(sim_mid, 1)
            dve.wait_ge(sim_rows, 3)
            nc.vector.tensor_copy(small[:, 70:72], ps[0][2][:, 0:2])
            dve.drain()
            nc.vector.tensor_tensor(small[:, 72:73], small[:, 70:71], small[:, 71:72], ALU.add)
            dve.drain()
            nc.vector.reciprocal(small[:, 73:74], small[:, 72:73])
            dve.drain()
            nc.vector.tensor_scalar(sim, sim, small[:, 71:72], small[:, 73:74], ALU.add, ALU.mult)
            dve.drain()
            pos = small[:, 80:96]
            nc.vector.tensor_scalar(pos, sim, 0.9, None, ALU.is_gt)
            dve.drain()
            notreg = cst("notreg")
            nc.vector.tensor_scalar(pos64[:, 3, :], pos, notreg, BIG, ALU.mult, ALU.mult)
            nc.vector.tensor_scalar(pos64[:, 2, :], pos, -1.0, 1.0, ALU.mult, ALU.add)
            nc.vector.tensor_scalar(pos64[:, 0, :], pos, -1.0, notreg, ALU.add, ALU.mult)
            dve.drain()
            nc.vector.tensor_scalar(pos64[:, 2, :], pos64[:, 2, :], notreg, BIG, ALU.mult, ALU.mult)
            nc.vector.tensor_scalar(pos64[:, 1, :], pos64[:, 0, :], -1.0, None, ALU.mult)
            nc.vector.tensor_scalar(small[:, 96:112], pos64[:, 0, :], 1.0, None, ALU.add)
            dve.drain()
            nc.vector.tensor_copy(pos64[:, 0, :], small[:, 96:112])
            dve.drain()
            dve.sem_inc(sim_mid, 1)
            dve.wait_ge(sim_rows, 4)
            nc.vector.tensor_copy(pos64T[:, :], ps[0][3][0:64, 0:128]).then_inc(sim_mid, 1)

        WSCALE = 1.0 / math.sqrt(DIM)

        def wide_pool(pool):
            with pool.Fori(0, PAIRS) as i:
                stage_x(pool, S_X1, ATT, ctxT_all, i)
                for s in range(2):
                    rstd(pool, var_ok, rstd_ok, tail_run[S_X1], i, s, ATT)

        def wide_pe(pe):
            ones3 = ones_b[0:3, :]
            with pe.Fori(0, PAIRS) as i:
                for s in range(2):
                    transpose_x(pe, S_X1, i, s, ATT)
                for s in range(2):
                    pe.wait_ge(xT_sb, nth(xt_run[S_X1], i, s))
                    xT, cT, bank = v_(s, ATT, "xcT"), v_(s, ATT, "c"), ps[s][1]
                    for k, src in ((0, xT), (1, cT)):
                        nc.tensor.matmul(bank[:, 128 * k:128 * k + 128], WA[:, W_EARLY("x1", 128 * k, 128)], src,
                                         start=True, stop=False, skip_group_check=True)
                        nc.tensor.matmul(bank[:, 128 * k:128 * k + 128], bias3[:, BIAS("x1", 128 * k, 128)], ones3,
                                         start=False, stop=True, skip_group_check=True)
                    nc.tensor.matmul(bank[:, 256:384], cT, WA[:, W_EARLY("x1", 256, 128)], start=True, stop=False,
                                     skip_group_check=True)
                    add_bias(bank[:, 256:384], "x1", 256, 128).then_inc(w_qk, 1)
                for s in range(2):
                    pe.wait_ge(w_qk_sb, nth(0, i, s))
                    bank = ps[s][2][:, 0:128]
                    nc.tensor.matmul(bank, v_(s, ATT, "qkT", 0, 128), v_(s, ATT, "qkT", 128, 128), start=True,
                                     stop=False, skip_group_check=True)
                    nc.tensor.matmul(bank, ones_b[0:1, :], mrow[:, bass.ds(i * 2 + s, 1), :].rearrange("p a k -> p (a k)"),
                                     start=False, stop=True, skip_group_check=True).then_inc(w_s, 1)
                for s in range(2):
                    pe.wait_ge(w_e, nth(0, i, s))
                    nc.tensor.transpose(ps[s][3][:, 0:128], v_(s, ATT, "P", 0, 128), ident).then_inc(w_T, 1)
                for s in range(2):
                    pe.wait_ge(w_Tsb, nth(0, i, s))
                    nc.tensor.matmul(ps[s][0][:, 0:128], v_(s, ATT, "PT", 0, 128), v_(s, ATT, "qkT", 256, 128),
                                     start=True, stop=True).then_inc(y_ps, 1)

        def wide_act(act):
            with act.Fori(0, PAIRS) as i:
                for s in range(2):
                    act.wait_ge(xT_ps, nth(xt_run[S_X1], i, s))
                    nc.scalar.copy(v_(s, ATT, "xcT", 0, 128), ps[s][0][:, 0:128]).then_inc(xT_sb, 1)
                for s in range(2):
                    act.wait_ge(w_qk, nth(0, i, s))
                    nc.scalar.copy(v_(s, ATT, "qkT", 0, 384), ps[s][1][:, 0:384]).then_inc(w_qk_sb, 1)
                for s in range(2):
                    act.wait_ge(w_m, nth(0, i, s))
                    nc.scalar.activation(v_(s, ATT, "P", 0, 128), ps[s][2][:, 0:128], ACT.Exp, scale=WSCALE,
                                         bias=v_(s, ATT, "m2", 0, 1), accum_out=v_(s, ATT, "m2", 1, 1)).then_inc(w_e, 1)
                for s in range(2):
                    act.wait_ge(w_T, nth(0, i, s))
                    nc.scalar.copy(v_(s, ATT, "PT", 0, 128), ps[s][3][:, 0:128]).then_inc(w_Tsb, 1)

        def wide_dve(dve):
            with dve.Fori(0, PAIRS) as i:
                for s in range(2):
                    dve.wait_ge(w_s, nth(0, i, s))
                    nc.vector.tensor_reduce(v_(s, ATT, "m2", 2, 1), ps[s][2][:, 0:128], AXX, ALU.max)
                    dve.drain()
                    nc.vector.tensor_scalar(v_(s, ATT, "m2", 0, 1), v_(s, ATT, "m2", 2, 1), -WSCALE, None,
                                            ALU.mult).then_inc(w_m, 1)
                for s in range(2):
                    dve.wait_ge(w_e, nth(0, i, s))
                    nc.vector.reciprocal(v_(s, ATT, "m2", 3, 1), v_(s, ATT, "m2", 1, 1))
                    dve.drain()
                    dve.wait_ge(y_ps, nth(tail_run[S_X1], i, s))
                    nc.vector.scalar_tensor_tensor(v_(s, ATT, "r"), ps[s][0][:, 0:128], v_(s, ATT, "m2", 3, 1),
                                                   v_(s, ATT, "x"), ALU.mult, ALU.add)
                    dve.drain()
                    stats(dve, s, ATT, v_(s, ATT, "r")).then_inc(var_ok, 1)
                for s in range(2):
                    tail_norm(dve, tail_run[S_X1], i, s, ATT)

        ff_run = {S_FF1: 0, S_FF2: 1}
        ff_v1, ff_r1 = sem("ff_v1"), sem("ff_r1")

        def ff_pool(pool, sub):
            with pool.Fori(0, PAIRS) as i:
                stage_x(pool, sub, FFN, None, i)
                for s in range(2):
                    rstd(pool, ff_v1, ff_r1, ff_run[sub], i, s, FFN)
                for s in range(2):
                    rstd(pool, mid_var, mid_rstd, mid_run[sub], i, s, FFN)
                for s in range(2):
                    rstd(pool, var_ok, rstd_ok, tail_run[sub], i, s, FFN)

        def ff_pe(pe, sub):
            quant, f = sub == S_FF2, ff_run[sub]
            with pe.Fori(0, PAIRS) as i:
                for s in range(2):
                    pe.wait_ge(h_sb, nth(f, i, s))
                    nc.tensor.transpose(ps[s][0][:, 0:128], v_(s, FFN, "h"), ident).then_inc(hT_ps, 1)
                for s in range(2):
                    pe.wait_ge(hT_sb, nth(f, i, s))
                    if quant:
                        nc.tensor.matmul(ps[s][1][:, :], v_(s, FFN, "hbT").bitcast(BF16), tern_up[:, :],
                                         start=True, stop=True).then_inc(up_ps, 1)
                    else:
                        nc.tensor.matmul(ps[s][1][:, :], v_(s, FFN, "hT"), WA[:, W_EARLY("ff1_up")],
                                         start=True, stop=False, skip_group_check=True)
                        add_bias(ps[s][1][:, :], "ff1_up").then_inc(up_ps, 1)
                for s in range(2):
                    pe.wait_ge(n_sb, nth(f, i, s))
                    for t in range(4):
                        mm = nc.tensor.transpose(ps[s][2][:, 128 * t:128 * t + 128], v_(s, FFN, "n", 128 * t, 128), ident)
                    mm.then_inc(nT_ps, 1)
                for s in range(2):
                    pe.wait_ge(nT_sb, nth(f, i, s))
                    y = ps[s][3][:, 0:128]
                    nbT = v_(s, FFN, "nbT").bitcast(BF16)
                    for t in range(4):
                        if quant:
                            mm = nc.tensor.matmul(y, nbT[:, 128 * t:128 * t + 128], tern_down[:, t, :],
                                                  start=t == 0, stop=t == 3, skip_group_check=True)
                        else:
                            nc.tensor.matmul(y, v_(s, FFN, "nT", 128 * t, 128), WA[:, W_EARLY("ff1_down", 128 * t, 128)],
                                             start=t == 0, stop=False, skip_group_check=True)
                    if not quant:
                        mm = add_bias(y, "ff1_down")
                    mm.then_inc(y_ps, 1)

        def ff_act(act, sub):
            quant, f = sub == S_FF2, ff_run[sub]
            with act.Fori(0, PAIRS) as i:
                for s in range(2):
                    act.wait_ge(hT_ps, nth(f, i, s))
                    dst = v_(s, FFN, "hbT").bitcast(BF16) if quant else v_(s, FFN, "hT")
                    nc.scalar.copy(dst, ps[s][0][:, 0:128]).then_inc(hT_sb, 1)
                for s in range(2):
                    if quant:
                        act.wait_ge(up_in, nth(0, i, s))
                        nc.scalar.activation(v_(s, FFN, "u"), v_(s, FFN, "u"), ACT.Gelu).then_inc(up_act, 1)
                    else:
                        act.wait_ge(up_ps, nth(f, i, s))
                        nc.scalar.activation(v_(s, FFN, "u"), ps[s][1][:, :], ACT.Gelu).then_inc(up_act, 1)
                for s in range(2):
                    act.wait_ge(nT_ps, nth(f, i, s))
                    dst = v_(s, FFN, "nbT").bitcast(BF16) if quant else v_(s, FFN, "nT")
                    nc.scalar.copy(dst, ps[s][2][:, :]).then_inc(nT_sb, 1)

        def affine(dve, dst, gamma, beta):
            nc.vector.tensor_tensor(dst, dst, R[:, ROWS(gamma)], ALU.mult)
            dve.drain()
            return nc.vector.tensor_tensor(dst, dst, R[:, ROWS(beta)], ALU.add)

        def quantize(dve, s, dst, at):
            top, scale, undo = (v_(s, FFN, "a", at + k, 1) for k in range(3))
            nc.vector.tensor_reduce(top, dst, AXX, ALU.max, apply_absolute_value=True)
            dve.drain()
            nc.vector.tensor_scalar(top, top, 1e-5, None, ALU.max)
            dve.drain()
            nc.vector.reciprocal(scale, top)
            dve.drain()
            nc.vector.tensor_scalar(scale, scale, 127.0, None, ALU.mult)
            dve.drain()
            nc.vector.reciprocal(undo, scale)
            nc.vector.tensor_scalar(dst, dst, scale, ROUND, ALU.mult, ALU.add)
            dve.drain()
            nc.vector.tensor_scalar(dst, dst, -ROUND, 127.0, ALU.add, ALU.min)
            dve.drain()
            return nc.vector.tensor_scalar(dst, dst, -128.0, None, ALU.max)

        def ff_dve(dve, sub):
            quant, f = sub == S_FF2, ff_run[sub]
            pre = "ff2_" if quant else "ff1_"
            with dve.Fori(0, PAIRS) as i:
                for s in range(2):
                    dve.wait_ge(staged, nth(sub, i, s))
                    stats(dve, s, FFN, v_(s, FFN, "x")).then_inc(ff_v1, 1)
                for s in range(2):
                    dve.wait_ge(ff_r1, nth(f, i, s))
                    h = v_(s, FFN, "h")
                    norm(dve, s, FFN, h, v_(s, FFN, "x"))
                    dve.drain()
                    ins = affine(dve, h, pre + "g1", pre + "b1")
                    if quant:
                        dve.drain()
                        ins = quantize(dve, s, h, 0)
                    ins.then_inc(h_sb, 1)
                if quant:
                    for s in range(2):
                        dve.wait_ge(up_ps, nth(f, i, s))
                        a = v_(s, FFN, "a", 6, 1)
                        nc.vector.tensor_tensor(a, v_(s, FFN, "a", 2, 1), small[:, 14:15], ALU.mult)
                        dve.drain()
                        nc.vector.scalar_tensor_tensor(v_(s, FFN, "u"), ps[s][1][:, :], a, R[:, ROWS("ff2_up")],
                                                       ALU.mult, ALU.add).then_inc(up_in, 1)
                for s in range(2):
                    dve.wait_ge(up_act, nth(f, i, s))
                    stats(dve, s, FFN, v_(s, FFN, "u")).then_inc(mid_var, 1)
                for s in range(2):
                    dve.wait_ge(mid_rstd, nth(mid_run[sub], i, s))
                    n = v_(s, FFN, "n")
                    norm(dve, s, FFN, n, v_(s, FFN, "u"))
                    dve.drain()
                    ins = affine(dve, n, pre + "g2", pre + "b2")
                    if quant:
                        dve.drain()
                        ins = quantize(dve, s, n, 3)
                    ins.then_inc(n_sb, 1)
                for s in range(2):
                    if quant:
                        dve.wait_ge(y_ps, nth(tail_run[sub], i, s))
                        a, r = v_(s, FFN, "a", 6, 1), v_(s, FFN, "r")
                        nc.vector.tensor_tensor(a, v_(s, FFN, "a", 5, 1), small[:, 15:16], ALU.mult)
                        dve.drain()
                        nc.vector.scalar_tensor_tensor(r, ps[s][3][:, 0:128], a, R[:, ROWS("ff2_down")], ALU.mult, ALU.add)
                        dve.drain()
                        nc.vector.tensor_tensor(r, r, v_(s, FFN, "x"), ALU.add)
                        dve.drain()
                        stats(dve, s, FFN, r).then_inc(var_ok, 1)
                    else:
                        tail_stats(dve, tail_run[sub], i, s, FFN, ps[s][3][:, 0:128])
                for s in range(2):
                    tail_norm(dve, tail_run[sub], i, s, FFN)

        def mlp_pool(pool):
            with pool.Fori(0, PAIRS) as i:
                stage_x(pool, S_MLP, MLP, None, i)

        def mlp_pe(pe):
            with pe.Fori(0, PAIRS) as i:
                for s in range(2):
                    transpose_x(pe, S_MLP, i, s, MLP)
                for s in range(2):
                    pe.wait_ge(xT_sb, nth(xt_run[S_MLP], i, s))
                    for m in range(3):
                        for t in range(4):
                            o = ps[s][1 + m][:, 128 * t:128 * t + 128]
                            nc.tensor.matmul(o, WA[:, W_EARLY("mlp_up", FF * m + 128 * t, 128)], v_(s, MLP, "xT"),
                                             start=True, stop=False, skip_group_check=True)
                            mm = nc.tensor.matmul(o, bias3[:, BIAS("mlp_up", FF * m + 128 * t, 128)], ones_b[0:3, :],
                                                  start=False, stop=True, skip_group_check=True)
                        mm.then_inc(mlp_ps, 1)
                for s in range(2):
                    for m in range(3):
                        pe.wait_ge(mlp_act, nth(0, i, s, 3, m + 1))
                        for t in range(4):
                            nc.tensor.matmul(ps[s][0][:, 128 * m:128 * m + 128], v_(s, MLP, "G", FF * m + 128 * t, 128),
                                             WA[:, W_EARLY("mlp_down", FF * m + 128 * t, 128)], start=t == 0, stop=False,
                                             skip_group_check=True)
                        mm = add_bias(ps[s][0][:, 128 * m:128 * m + 128], "mlp_down", 128 * m, 128)
                    mm.then_inc(mlp_out, 1)

        def mlp_act_(act):
            with act.Fori(0, PAIRS) as i:
                for s in range(2):
                    act.wait_ge(xT_ps, nth(xt_run[S_MLP], i, s))
                    nc.scalar.copy(v_(s, MLP, "xT"), ps[s][0][:, 0:128]).then_inc(xT_sb, 1)
                for s in range(2):
                    for m in range(3):
                        act.wait_ge(mlp_ps, nth(0, i, s, 3, m + 1))
                        nc.scalar.activation(v_(s, MLP, "G", FF * m, FF), ps[s][1 + m][:, :], ACT.Gelu).then_inc(mlp_act, 1)

        def mlp_dve(dve):
            with dve.Fori(0, PAIRS) as i:
                for s in range(2):
                    dve.wait_ge(mlp_out, nth(0, i, s))
                    nc.vector.tensor_copy(arena[s][:, bass.ds(i * 384 + QKV_KEPT, 384)], ps[s][0][:, 0:384]).then_inc(seq_done, 1)

        XSCALE = 1.0 / math.sqrt(XD)
        HALVES, HH = 2, XH // 2

        def lat_pool(pool):
            pool.wait_ge(seq_done, all_done + BATCH * S_MQA)
            pool.wait_ge(late_in, 32)
            with pool.Fori(0, PAIRS) as i:
                stage_x(pool, S_LAT, LAT, ctx_all, i)
                for s in range(2):
                    rstd(pool, mid_var, mid_rstd, mid_run[S_LAT], i, s, LAT, 2)
                for s in range(2):
                    rstd(pool, var_ok, rstd_ok, tail_run[S_LAT], i, s, LAT)

        def lat_pe(pe):
            pe.wait_ge(late_in, 32)
            with pe.Fori(0, PAIRS) as i:
                for s in range(2):
                    pe.wait_ge(h_sb, nth(2, i, s))
                    for k in range(2):
                        mm = nc.tensor.transpose(ps[s][0][:, 128 * k:128 * k + 128], v_(s, LAT, "n", 128 * k, 128), ident)
                    mm.then_inc(xT_ps, 1)
                for s in range(2):
                    pe.wait_ge(xT_sb, nth(xt_run[S_LAT], i, s))
                    nT = v_(s, LAT, "nT")
                    for t in range(8):
                        mm = nc.tensor.matmul(ps[s][t // 4][:, 128 * (t % 4):128 * (t % 4) + 128],
                                              WA[:, W_LATE("lat_q", 128 * t, 128)], nT[:, 128:256], start=True, stop=True,
                                              skip_group_check=True)
                    mm.then_inc(l_q, 1)
                    for t in range(8):
                        if t == 4:
                            pe.wait_ge(l_qsb, nth(0, i, s))
                        mm = nc.tensor.matmul(ps[s][(2 + t // 2) % 4][:, 256 * (t % 2):256 * (t % 2) + 256],
                                              WA[:, W_LATE("lat_k", 128 * t, 128)], nT, start=True, stop=True,
                                              skip_group_check=True)
                        if t % 4 == 3:
                            mm.then_inc(l_k, 1)
                for s in range(2):
                    nT = v_(s, LAT, "nT")
                    for k in range(2):
                        pe.wait_ge(l_ksb, nth(0, i, s, 2, k + 1))
                        for c in range(2):
                            mm = nc.tensor.matmul(ps[s][(2 + 2 * k + c) % 4][:, :], nT[:, 128 * k:128 * k + 128],
                                                  WA[:, W_LATE("lat_v", 512 * c, 512)], start=True, stop=True)
                        mm.then_inc(l_v, 1)
                for hf in range(HALVES):
                    for s in range(2):
                        if hf == 0:
                            pe.wait_ge(l_vsb, nth(0, i, s, 2, 2))
                        else:
                            pe.wait_ge(l_osb, i * 4 + (s + 1))
                        qT = v_(s, LAT, "qT").rearrange("p (t q) -> p t q", t=8)
                        kT = v_(s, LAT, "kT").rearrange("p (t k) -> p t k", t=8)
                        for n in range(HH):
                            p0, blk = XD * (n // 4), 4 * hf + n % 4
                            mm = nc.tensor.matmul(ps[s][n // 2][:, 256 * (n % 2):256 * (n % 2) + 256],
                                                  qT[p0:p0 + XD, blk, :], kT[p0:p0 + XD, blk, :], start=True,
                                                  stop=True, skip_group_check=True)
                            if n % 2 == 1:
                                mm.then_inc(l_s, 1)
                    for s in range(2):
                        P = v_(s, LAT, "P").rearrange("p (n k) -> p n k", k=128)
                        for t in range(4):
                            pe.wait_ge(l_sub, i * 16 + (8 * hf + 4 * s + t + 1))
                            for c in range(4):
                                mm = nc.tensor.transpose(ps[s][t][:, 128 * c:128 * c + 128], P[:, 4 * t + c, :], ident)
                            mm.then_inc(l_T, 1)
                    for s in range(2):
                        PT = v_(s, LAT, "PT").rearrange("p (h c q) -> p h c q", h=HH, c=2)
                        V = v_(s, LAT, "V").rearrange("p (c h d) -> p c h d", c=2, h=XH)
                        pe.wait_ge(l_Tsb, i * 16 + (8 * hf + 4 * s + 4))
                        for h in range(HH):
                            o = ps[s][0][XD * (h % 2):XD * (h % 2) + XD, 128 * (h // 2):128 * (h // 2) + 128]
                            for c in range(2):
                                mm = nc.tensor.matmul(o, V[:, c, HH * hf + h, 0:XD], PT[:, 4 * (h % 2) + h // 2, c, :],
                                                      start=c == 0, stop=c == 1, skip_group_check=True)
                        mm.then_inc(l_o, 1)
                for s in range(2):
                    pe.wait_ge(l_osb, i * 4 + (2 + s + 1))
                    OT = v_(s, LAT, "O")
                    for t in range(8):
                        mm = nc.tensor.matmul(ps[s][1][:, 0:128], OT[:, 128 * t:128 * t + 128],
                                              WA[:, W_LATE("lat_out", 128 * t, 128)], start=t == 0, stop=t == 7,
                                              skip_group_check=True)
                    mm.then_inc(y_ps, 1)

        def lat_act(act):
            with act.Fori(0, PAIRS) as i:
                for s in range(2):
                    act.wait_ge(xT_ps, nth(xt_run[S_LAT], i, s))
                    nc.scalar.copy(v_(s, LAT, "nT"), ps[s][0][:, 0:256]).then_inc(xT_sb, 1)
                for s in range(2):
                    act.wait_ge(l_q, nth(0, i, s))
                    for k in range(2):
                        nc.scalar.copy(v_(s, LAT, "qT", 512 * k, 512), ps[s][k][:, :])
                    act.drain()
                    act.sem_inc(l_qsb, 1)
                for s in range(2):
                    V = v_(s, LAT, "V").rearrange("p (c h d) -> p c h d", c=2, h=XH)
                    for k in range(2):
                        act.wait_ge(l_v, nth(0, i, s, 2, k + 1))
                        for c in range(2):
                            nc.scalar.copy(V[:, k, 8 * c:8 * c + 8, 0:XD],
                                           ps[s][(2 + 2 * k + c) % 4][:, :].rearrange("p (h d) -> p h d", d=XD))
                        act.drain()
                        act.sem_inc(l_vsb, 1)
                for hf in range(HALVES):
                    for s in range(2):
                        for t in range(4):
                            act.wait_ge(l_exp, i * 16 + (8 * hf + 4 * s + t + 1))
                            for j in range(2):
                                h = 2 * t + j
                                nc.scalar.activation(v_(s, LAT, "P", 256 * h, 256), ps[s][t][:, 256 * j:256 * j + 256],
                                                     ACT.Exp, scale=XSCALE, bias=v_(s, LAT, "m", h, 1),
                                                     accum_out=v_(s, LAT, "rec", h, 1))
                            act.drain()
                            act.sem_inc(l_osum, 1)
                    for s in range(2):
                        for t in range(4):
                            act.wait_ge(l_T, i * 16 + (8 * hf + 4 * s + t + 1))
                            nc.scalar.copy(v_(s, LAT, "PT", 512 * t, 512), ps[s][t][:, :]).then_inc(l_Tsb, 1)
                    for s in range(2):
                        act.wait_ge(l_o, i * 4 + (2 * hf + s + 1))
                        nc.scalar.copy(v_(s, LAT, "O", 512 * hf, 512), ps[s][0][:, :]).then_inc(l_osb, 1)

        def lat_dve(dve):
            with dve.Fori(0, PAIRS) as i:
                for s in range(2):
                    dve.wait_ge(staged, nth(S_LAT, i, s))
                    stats(dve, s, LAT, v_(s, LAT, "c"))
                    dve.drain()
                    stats(dve, s, LAT, v_(s, LAT, "x"), at=2).then_inc(mid_var, 1)
                for s in range(2):
                    dve.wait_ge(mid_rstd, nth(mid_run[S_LAT], i, s))
                    nk, nl = v_(s, LAT, "n", 0, 128), v_(s, LAT, "n", 128, 128)
                    norm(dve, s, LAT, nk, v_(s, LAT, "c"), 0)
                    norm(dve, s, LAT, nl, v_(s, LAT, "x"), 1)
                    dve.drain()
                    affine(dve, nk, "lat_mg", "lat_mb")
                    affine(dve, nl, "lat_lg", "lat_lb").then_inc(h_sb, 1)
                for s in range(2):
                    for k in range(2):
                        dve.wait_ge(l_k, nth(0, i, s, 2, k + 1))
                        for c in range(2):
                            nc.vector.tensor_copy(v_(s, LAT, "kT", 1024 * k + 512 * c, 512), ps[s][(2 + 2 * k + c) % 4][:, :])
                        dve.drain()
                        dve.sem_inc(l_ksb, 1)
                for hf in range(HALVES):
                    for s in range(2):
                        for t in range(4):
                            dve.wait_ge(l_s, i * 16 + (8 * hf + 4 * s + t + 1))
                            m = v_(s, LAT, "m", 2 * t, 2)
                            nc.vector.tensor_reduce(m, ps[s][t][:, :].rearrange("p (j k) -> p j k", j=2), AXX, ALU.max)
                            dve.drain()
                            nc.vector.tensor_scalar(m, m, -XSCALE, None, ALU.mult).then_inc(l_exp, 1)
                    for s in range(2):
                        for t in range(4):
                            dve.wait_ge(l_osum, i * 16 + (8 * hf + 4 * s + t + 1))
                            rec = v_(s, LAT, "rec", 2 * t, 2)
                            nc.vector.reciprocal(rec, rec)
                            dve.drain()
                            for j in range(2):
                                p = v_(s, LAT, "P", 512 * t + 256 * j, 256)
                                nc.vector.tensor_scalar(p, p, v_(s, LAT, "rec", 2 * t + j, 1), None, ALU.mult)
                            dve.drain()
                            dve.sem_inc(l_sub, 1)
                for s in range(2):
                    tail_stats(dve, tail_run[S_LAT], i, s, LAT, ps[s][1][:, 0:128])
                for s in range(2):
                    tail_norm(dve, tail_run[S_LAT], i, s, LAT)

        def gate_pool(pool):
            with pool.Fori(0, PAIRS) as i:
                stage_x(pool, S_GATE, MOE, None, i)

        def gate_pe(pe):
            with pe.Fori(0, PAIRS) as i:
                for s in range(2):
                    transpose_x(pe, S_GATE, i, s, MOE)
                for s in range(2):
                    pe.wait_ge(xT_sb, nth(xt_run[S_GATE], i, s))
                    nc.tensor.matmul(ps[s][1][:, 0:EXPERTS], v_(s, MOE, "xT"), WA[:, W_LATE("gate")],
                                     start=True, stop=True).then_inc(gate_ps, 1)

        def gate_act(act):
            with act.Fori(0, PAIRS) as i:
                for s in range(2):
                    act.wait_ge(xT_ps, nth(xt_run[S_GATE], i, s))
                    nc.scalar.copy(v_(s, MOE, "xT"), ps[s][0][:, 0:128]).then_inc(xT_sb, 1)
            act.wait_ge(gate_sub, 1)
            nc.scalar.activation(comb[:, :, :], comb[:, :, :], ACT.Exp).then_inc(gate_exp, 1)

        def gate_dve(dve):
            with dve.Fori(0, PAIRS) as i:
                for s in range(2):
                    dve.wait_ge(gate_ps, nth(0, i, s))
                    nc.vector.tensor_copy(comb[:, bass.ds(i * 2 + s, 1), :].rearrange("p a e -> p (a e)"),
                                          ps[s][1][:, 0:EXPERTS]).then_inc(seq_done, 1)
            wide = [128, BATCH, EXPERTS]
            cube = [128, BATCH * EXPERTS, EXPERTS]
            t = small[:, 96:112]
            dve.drain()
            nc.vector.tensor_reduce(t, comb[:, :, :], AXX, ALU.max)
            dve.drain()
            nc.vector.tensor_tensor(comb[:, :, :], comb[:, :, :], t.unsqueeze(2).broadcast_to(wide), ALU.subtract).then_inc(gate_sub, 1)
            dve.wait_ge(gate_exp, 1)
            nc.vector.tensor_reduce(t, comb[:, :, :], AXX, ALU.add)
            dve.drain()
            nc.vector.reciprocal(t, t)
            dve.drain()
            nc.vector.tensor_tensor(comb[:, :, :], comb[:, :, :], t.unsqueeze(2).broadcast_to(wide), ALU.mult)
            dve.drain()
            gt = arena[0][:, 4096:5120].rearrange("p (b e f) -> p b e f", b=BATCH, e=EXPERTS)
            eq = arena[0][:, 5120:6144].rearrange("p (b e f) -> p b e f", b=BATCH, e=EXPERTS)
            mine = comb[:, :, :].unsqueeze(3).broadcast_to([128, BATCH, EXPERTS, EXPERTS])
            other = comb[:, :, :].unsqueeze(2).broadcast_to([128, BATCH, EXPERTS, EXPERTS])
            early = cst("earlier").rearrange("p (e f) -> p e f", e=EXPERTS).unsqueeze(1).broadcast_to([128, BATCH, EXPERTS, EXPERTS])
            nc.vector.tensor_tensor(gt, other, mine, ALU.is_gt)
            nc.vector.tensor_tensor(eq, other, mine, ALU.is_equal)
            dve.drain()
            nc.vector.tensor_tensor(eq, eq, early, ALU.mult)
            dve.drain()
            nc.vector.tensor_tensor(gt, gt, eq, ALU.add)
            dve.drain()
            rank = arena[0][:, 6144:6272]
            nc.vector.tensor_reduce(rank, gt.rearrange("p b e f -> p (b e) f"), AXX, ALU.add)
            dve.drain()
            nc.vector.tensor_scalar(rank, rank, 1.5, None, ALU.is_lt)
            dve.drain()
            c2 = comb[:, :, :].rearrange("p b e -> p (b e)")
            nc.vector.tensor_tensor(c2, c2, rank, ALU.mult)
            dve.drain()
            nc.vector.tensor_reduce(t, comb[:, :, :], AXX, ALU.add)
            dve.drain()
            nc.vector.tensor_scalar(t, t, 1e-9, None, ALU.add)
            dve.drain()
            nc.vector.reciprocal(t, t)
            dve.drain()
            nc.vector.tensor_tensor(comb[:, :, :], comb[:, :, :], t.unsqueeze(2).broadcast_to(wide), ALU.mult)
            dve.drain()
            nc.vector.tensor_reduce(comb_sum[:, :], comb[:, :, :], AXX, ALU.add).then_inc(gate_sub, 1)

        def moe_pool(pool):
            pool.wait_ge(gate_sub, 2)
            with pool.Fori(0, PAIRS) as i:
                for s in range(2):
                    pool.wait_ge(seq_done, nth(S_MOE, i, s))
                    b = i * 2 + s
                    nc.gpsimd.tensor_copy(share[s][:, 0:EXPERTS], comb[:, bass.ds(b, 1), :].rearrange("p a e -> p (a e)"))
                    nc.gpsimd.tensor_copy(share[s][:, EXPERTS:EXPERTS + 1], comb_sum[:, bass.ds(b, 1)])
                stage_x(pool, S_MOE, MOE, None, i)
                for s in range(2):
                    rstd(pool, var_ok, rstd_ok, tail_run[S_MOE], i, s, MOE)

        share = [v_(s, MOE, "share") for s in range(2)]

        def moe_pe(pe):
            with pe.Fori(0, PAIRS) as i:
                for s in range(2):
                    transpose_x(pe, S_MOE, i, s, MOE)
                for s in range(2):
                    pe.wait_ge(xT_sb, nth(xt_run[S_MOE], i, s))
                for e in range(EXPERTS):
                    for s in range(2):
                        if e >= 3:
                            pe.wait_ge(e_acc, i * 16 + (2 * (e - 3) + s + 1))
                        o = ps[s][1 + e % 3][:, :]
                        nc.tensor.matmul(o, v_(s, MOE, "xT"), WA[:, W_LATE("experts", FF * e, FF)], start=True, stop=False,
                                         skip_group_check=True)
                        add_bias(o, "experts", FF * e, FF).then_inc(e_ps, 1)
                for s in range(2):
                    pe.wait_ge(e_acc, i * 16 + (2 * (EXPERTS - 1) + s + 1))
                    for k in range(2):
                        mm = nc.tensor.transpose(ps[s][0][:, 128 * k:128 * k + 128], v_(s, MOE, "acc", 128 * k, 128), ident)
                    mm.then_inc(acc_T, 1)
                for s in range(2):
                    pe.wait_ge(acc_Tsb, nth(0, i, s))
                    for k in range(2):
                        mm = nc.tensor.matmul(ps[s][1][:, 0:128], v_(s, MOE, "accT", 128 * k, 128),
                                              WA[:, W_LATE("moe_out", 128 * k, 128)], start=k == 0, stop=k == 1,
                                              skip_group_check=True)
                    mm.then_inc(y_ps, 1)

        def moe_act(act):
            with act.Fori(0, PAIRS) as i:
                for s in range(2):
                    act.wait_ge(xT_ps, nth(xt_run[S_MOE], i, s))
                    nc.scalar.copy(v_(s, MOE, "xT"), ps[s][0][:, 0:128]).then_inc(xT_sb, 1)
                for e in range(EXPERTS):
                    for s in range(2):
                        act.wait_ge(e_ps, i * 16 + (2 * e + s + 1))
                        if e >= 2:
                            act.wait_ge(e_acc, i * 16 + (2 * (e - 2) + s + 1))
                        nc.scalar.activation(v_(s, MOE, "sig", 256 * (e % 2), 256), ps[s][1 + e % 3][:, 256:512],
                                             ACT.Sigmoid).then_inc(e_sig, 1)
                for s in range(2):
                    act.wait_ge(acc_T, nth(0, i, s))
                    nc.scalar.copy(v_(s, MOE, "accT"), ps[s][0][:, 0:256]).then_inc(acc_Tsb, 1)

        def moe_dve(dve):
            with dve.Fori(0, PAIRS) as i:
                for e in range(EXPERTS):
                    for s in range(2):
                        dve.wait_ge(e_sig, i * 16 + (2 * e + s + 1))
                        t, acc = v_(s, MOE, "t", 256 * (e % 2), 256), v_(s, MOE, "acc")
                        nc.vector.tensor_tensor(t, ps[s][1 + e % 3][:, 0:256], v_(s, MOE, "sig", 256 * (e % 2), 256), ALU.mult)
                        dve.drain()
                        w = share[s][:, e:e + 1]
                        if e == 0:
                            nc.vector.tensor_scalar(acc, t, w, None, ALU.mult).then_inc(e_acc, 1)
                        else:
                            nc.vector.scalar_tensor_tensor(acc, t, w, acc, ALU.mult, ALU.add).then_inc(e_acc, 1)
                for s in range(2):
                    x = v_(s, MOE, "x")
                    nc.vector.scalar_tensor_tensor(x, R[:, ROWS("moe_bo")], share[s][:, EXPERTS:EXPERTS + 1], x,
                                                   ALU.mult, ALU.add)
                    dve.drain()
                    tail_stats(dve, tail_run[S_MOE], i, s, MOE, ps[s][1][:, 0:128])
                for s in range(2):
                    tail_norm(dve, tail_run[S_MOE], i, s, MOE)

        def on(sub):
            return sub <= last

        @block.sync
        def _(sp):
            loads(sp)
            if on(S_REG):
                sim_sp(sp)
            if on(S_LAT):
                sp.wait_ge(seq_done, all_done + BATCH * S_SELF2)
                sp.dma_start(WA[:, 0:W_LATE.size], w_late).then_inc(late_in, 16)
                sp.dma_start(ctx_all[:, :, :], ctx_tok).then_inc(late_in, 16)
            sp.wait_ge(rest_in, 16 * loads_rest)
            sp.wait_ge(seq_done, all_done + BATCH * last)
            sp.dma_start(out, x_all[:, :, :]).then_inc(stored, 16)
            sp.wait_ge(stored, 16)

        @block.gpsimd
        def _(pool):
            start_pool(pool)
            pos_pool(pool)
            if on(S_X0):
                pool.wait_ge(rest_in, 16 * loads_rest)
                att_pool(pool, S_X0, "cross")
            if on(S_SIM):
                sim_pool_(pool)
            if on(S_REG):
                att_pool(pool, S_REG, "self")
            if on(S_LIN):
                att_pool(pool, S_LIN, "linear")
            if on(S_X1):
                wide_pool(pool)
            if on(S_FF1):
                ff_pool(pool, S_FF1)
            if on(S_MLP):
                mlp_pool(pool)
            if on(S_SELF2):
                att_pool(pool, S_SELF2, "kept")
            if on(S_X2):
                att_pool(pool, S_X2, "cross")
            if on(S_FF2):
                ff_pool(pool, S_FF2)
            if on(S_MQA):
                att_pool(pool, S_MQA, "self")
            if on(S_LAT):
                lat_pool(pool)
            if on(S_GATE):
                gate_pool(pool)
            if on(S_MOE):
                moe_pool(pool)

        @block.tensor
        def _(pe):
            start_pe(pe)
            lstm_pe(pe)
            pos_pe(pe)
            pe.wait_ge(w_tern, 2)
            pe.wait_ge(rest_in, 16 * loads_rest)
            if on(S_X0):
                att_pe(pe, S_X0, "cross", WA, "x0", "x0", "full")
            if on(S_SIM):
                sim_pe(pe)
            if on(S_REG):
                att_pe(pe, S_REG, "self", WA, "reg", None, "pos")
            if on(S_LIN):
                att_pe(pe, S_LIN, "linear", WA, "lin", "lin", None)
            if on(S_X1):
                wide_pe(pe)
            if on(S_FF1):
                ff_pe(pe, S_FF1)
            if on(S_MLP):
                mlp_pe(pe)
            if on(S_SELF2):
                att_pe(pe, S_SELF2, "kept", WA, None, None, None, 0, "self2_out")
            if on(S_X2):
                att_pe(pe, S_X2, "cross", WB, "x2", "x2", None)
            if on(S_FF2):
                ff_pe(pe, S_FF2)
            if on(S_MQA):
                att_pe(pe, S_MQA, "self", WB, "mqa", "mqa", "causal")
            if on(S_LAT):
                lat_pe(pe)
            if on(S_GATE):
                gate_pe(pe)
            if on(S_MOE):
                moe_pe(pe)

        @block.scalar
        def _(act):
            start_act(act)
            lstm_act(act)
            pos_act(act)
            if on(S_X0):
                att_act(act, S_X0, "cross")
            if on(S_SIM):
                sim_act(act)
            if on(S_REG):
                att_act(act, S_REG, "self")
            if on(S_LIN):
                att_act(act, S_LIN, "linear")
            if on(S_X1):
                wide_act(act)
            if on(S_FF1):
                ff_act(act, S_FF1)
            if on(S_MLP):
                mlp_act_(act)
            if on(S_SELF2):
                att_act(act, S_SELF2, "kept")
            if on(S_X2):
                att_act(act, S_X2, "cross")
            if on(S_FF2):
                ff_act(act, S_FF2)
            if on(S_MQA):
                att_act(act, S_MQA, "self")
            if on(S_LAT):
                lat_act(act)
            if on(S_GATE):
                gate_act(act)
            if on(S_MOE):
                moe_act(act)

        @block.vector
        def _(dve):
            start_dve(dve)
            lstm_dve(dve)
            pos_dve(dve)
            if on(S_X0):
                att_dve(dve, S_X0, "cross")
            if on(S_SIM):
                sim_dve(dve)
            if on(S_REG):
                att_dve(dve, S_REG, "self")
            if on(S_LIN):
                att_dve(dve, S_LIN, "linear")
            if on(S_X1):
                wide_dve(dve)
            if on(S_FF1):
                ff_dve(dve, S_FF1)
            if on(S_MLP):
                mlp_dve(dve)
            if on(S_SELF2):
                att_dve(dve, S_SELF2, "kept")
            if on(S_X2):
                att_dve(dve, S_X2, "cross")
            if on(S_FF2):
                ff_dve(dve, S_FF2)
            if on(S_MQA):
                att_dve(dve, S_MQA, "self")
            if on(S_LAT):
                lat_dve(dve)
            if on(S_GATE):
                gate_dve(dve)
            if on(S_MOE):
                moe_dve(dve)


def constants():
    c = np.zeros((128, CONST.size), np.float32)

    def put(name, a):
        a = np.asarray(a, np.float32)
        c[:a.shape[0], CONST(name)] = a

    p = np.arange(128)
    row = p.astype(np.float32)
    put("ident", np.eye(128))
    put("rel", row[None, :] / (row[:, None] + np.float32(1)))
    put("tri", p[None, :] <= p[:, None])
    put("triT", p[None, :] >= p[:, None])
    put("causal", np.where(p[None, :] <= p[:, None], 0.0, BIG))
    half, turn = HD // 2, HD // 4
    theta = np.float32(10000.0) ** (-np.arange(half, dtype=np.float32) / np.float32(half))
    freqs = row[:, None] * theta[None, :]
    sin = np.sin(freqs)
    sin[:, :turn] *= -1
    put("cos", np.cos(freqs))
    put("sin", sin)
    hm = np.zeros((128, GROUPS, HEADS))
    for t in range(GROUPS):
        for j in range(4):
            hm[PAD * j:PAD * j + HD, t, 4 * t + j] = 1
    put("headmask", hm.reshape(128, -1))
    r = np.arange(REG_ROWS)
    put("blockmask", (r[:, None] // REG) == (p[None, :] // HD))
    put("regsel", 0.5 * ((r[:, None] % REG) == p[None, :]))
    put("notreg", p[:, None] >= REG)
    put("regscale", np.where(p[:, None] < REG, 0.5, 1.0))
    put("minushalf", np.full((128, 16), -0.5))
    put("third", np.eye(3))
    put("step", np.broadcast_to((row + 1) / np.float32(TOK), (128, 128)))
    e = np.arange(EXPERTS)
    put("earlier", np.broadcast_to((e[None, :] < e[:, None]).reshape(1, -1), (128, 64)))
    put("negrow", np.repeat([[0.0], [1.0]], REG_ROWS, 1))
    return c


def kernel(**inputs):
    import concourse.bacc as bacc
    from concourse.bass_utils import run_bass_kernel_spmd

    a = {k: np.asarray(v) for k, v in inputs.items()}

    def side(*parts):
        return np.concatenate(parts, axis=1)

    def blocks(w, n=4):
        return w.reshape(n, 128, -1).transpose(1, 0, 2).reshape(128, -1)

    def tall(w):
        return np.concatenate([w, np.zeros((128 - w.shape[0], w.shape[1]), w.dtype)], 0)

    def gates_order(w):
        h = LSTM_H
        return np.concatenate([w[:2 * h], w[3 * h:], w[2 * h:3 * h]], 0)

    def T(n):
        return a[n].T

    early = side(
        gates_order(a["L0_attn_W_ih"]).T, tall(gates_order(a["L0_attn_W_hh"]).T),
        tall(np.concatenate([a["L0_attn_W_mu"], a["L0_attn_W_sig"]], 0).T),
        T("L0_xattn_Wq"), T("L0_xattn_Wk"), T("L0_xattn_Wv"), T("L0_xattn_Wo"),
        a["L0_ffn_W_qkv"], a["L0_ffn_W_proj"], T("L1_attn_Wqkv"), T("L1_attn_Wout"),
        a["L1_xattn_Wq"], a["L1_xattn_Wk"], a["L1_xattn_Wv"], T("L1_ffn_w1"), blocks(T("L1_ffn_w2")),
        a["L2_attn_q_w1"], a["L2_attn_k_w1"], a["L2_attn_v_w1"],
        blocks(a["L2_attn_q_w2"]), blocks(a["L2_attn_k_w2"]), blocks(a["L2_attn_v_w2"]),
        a["L2_attn_proj_w"])
    late = side(
        a["L3_xattn_Wq"], a["L3_xattn_Wkv"], blocks(a["L3_xattn_Wout"], 8), T("L3_ffn_Wg"),
        a["L3_ffn_W1"].transpose(2, 0, 1).reshape(128, -1), blocks(T("L3_ffn_Wo"), 2))
    rest = side(
        T("L2_xattn_Wq"), T("L2_xattn_Wk"), T("L2_xattn_Wv"), T("L2_xattn_Wo"),
        a["L3_attn_Wq"], np.tile(a["L3_attn_Wk"], (1, HEADS)), np.tile(a["L3_attn_Wv"], (1, HEADS)),
        a["L3_attn_Wo"], T("L2_ffn_w1"), blocks(T("L2_ffn_w2")))
    bias = np.concatenate([
        gates_order(a["L0_attn_b_ih"][:, None])[:, 0], gates_order(a["L0_attn_b_hh"][:, None])[:, 0],
        a["L0_xattn_bq"], a["L0_xattn_bk"], a["L0_xattn_bv"], a["L0_xattn_bo"], a["L0_ffn_b_proj"],
        a["L1_attn_bqkv"], a["L1_attn_bout"], a["L1_xattn_bq"], a["L1_xattn_bk"], a["L1_xattn_bv"],
        a["L1_ffn_b1"], a["L1_ffn_b2"], a["L2_attn_q_b1"], a["L2_attn_k_b1"], a["L2_attn_v_b1"],
        a["L2_attn_q_b2"], a["L2_attn_k_b2"], a["L2_attn_v_b2"], a["L2_attn_proj_b"],
        a["L2_xattn_bq"], a["L2_xattn_bk"], a["L2_xattn_bv"], a["L2_xattn_bo"],
        a["L3_attn_bq"], np.tile(a["L3_attn_bk"], HEADS), np.tile(a["L3_attn_bv"], HEADS),
        a["L3_attn_bo"], a["L3_ffn_b1"].reshape(-1)])
    rows = np.concatenate([
        a["L0_ffn_g_info"][0, 0], a["L1_attn_gamma"], a["L1_attn_beta"], a["L1_ffn_ln1_g"],
        a["L1_ffn_ln1_b"], a["L1_ffn_ln2_g"], a["L1_ffn_ln2_b"], a["L2_ffn_ln1_g"], a["L2_ffn_ln1_b"],
        a["L2_ffn_ln2_g"], a["L2_ffn_ln2_b"], a["L2_ffn_b1"], a["L2_ffn_b2"], a["L3_xattn_ln_m_g"],
        a["L3_xattn_ln_m_b"], a["L3_xattn_ln_l_g"], a["L3_xattn_ln_l_b"], a["L3_ffn_bo"],
        a["L0_attn_b_mu"], a["L0_attn_b_sig"]])
    arrays = {
        "x_tok": a["x"].transpose(1, 0, 2), "x_T": a["x"].transpose(2, 0, 1),
        "ctx_tok": a["ctx_1024"].transpose(1, 0, 2), "ctx_T": a["ctx_1024"].transpose(2, 0, 1),
        "mask": a["mask_BxSxS2_ik1"].transpose(1, 0, 2).reshape(128, -1),
        "mask_row": a["mask_BxS2_if1"].reshape(1, -1),
        "w_early": early, "w_late": late, "w_rest": rest,
        "bias": np.repeat(bias[None], 3, 0), "rows": np.repeat(rows[None], 128, 0),
        "const": constants(),
    }
    nc = bacc.Bacc("TRN2", target_bir_lowering=False, num_devices=1)
    args = {}
    for name, v in arrays.items():
        arrays[name] = v = np.ascontiguousarray(v)
        args[name] = nc.dram_tensor(name, v.shape, mybir.dt.from_np(v.dtype), kind="ExternalInput").ap()
    out = nc.dram_tensor("out", (128, BATCH, DIM), F32, kind="ExternalOutput").ap()
    decoder(nc, **args, out=out)
    r = run_bass_kernel_spmd(nc, [arrays], core_ids=[0])
    return np.ascontiguousarray(r.results[0]["out"].transpose(1, 0, 2))
```

```python
import math
from contextlib import ExitStack

import numpy as np

import concourse.bass as bass
from concourse import mybir

F32 = mybir.dt.float32
BF16 = mybir.dt.bfloat16
I32 = mybir.dt.int32
ACT = mybir.ActivationFunctionType
ALU = mybir.AluOpType
AXX = mybir.AxisListType.X

BATCH, TOK, DIM, HEADS = 16, 128, 128, 16
HD = DIM // HEADS
PAD = 32
GROUPS = HEADS * PAD // 128
PAIRS = BATCH // 2
LSTM_H, REG = 20, 5
FF = 512
EXPERTS, XH, XD = 8, 16, 64
LN_EPS = 1e-5
NEG, BIG = -1.0e10, -2.0 ** 100
ROUND = 12582912.0
REG_ROWS = HEADS * REG
SCALE = 1.0 / math.sqrt(HD)

(S_LSTM, S_X0, S_SIM, S_REG, S_LIN, S_X1, S_FF1, S_MLP, S_SELF2, S_X2, S_FF2, S_MQA, S_LAT, S_GATE,
 S_MOE) = range(15)


def nth(run, i, s, each=1, part=None):
    part = each if part is None else part
    return i * (2 * each) + ((run * BATCH + s) * each + part)


class Columns:

    def __init__(self, *sizes):
        self.at, end = {}, 0
        for name, size in sizes:
            self.at[name] = (end, size)
            end += size
        self.size = end

    def __call__(self, name, of=0, width=None):
        a, n = self.at[name]
        return slice(a + of, a + (n if width is None else of + width))


W_EARLY = Columns(("ih", 4 * LSTM_H), ("hh", 4 * LSTM_H), ("musig", 4), ("x0", 512), ("reg", 512),
                  ("lin", 512), ("x1", 384), ("ff1_up", FF), ("ff1_down", FF),
                  ("mlp_up", 3 * FF), ("mlp_down", 3 * FF), ("self2_out", DIM))
W_LATE = Columns(("lat_q", 1024), ("lat_k", 1024), ("lat_v", 1024), ("lat_out", 1024),
                 ("gate", EXPERTS), ("experts", EXPERTS * FF), ("moe_out", 256))
W_REST = Columns(("x2", 512), ("mqa", 512), ("mqa_turned", 256), ("ff2_up", FF), ("ff2_down", FF))
BIAS = Columns(("ih", 80), ("hh", 80), ("x0", 512), ("reg_out", 128), ("lin", 512), ("x1", 384),
               ("ff1_up", FF), ("ff1_down", 128), ("mlp_up", 3 * FF), ("mlp_down", 384),
               ("self2_out", 128), ("x2", 512), ("mqa", 512), ("mqa_turned", 256), ("experts", EXPERTS * FF))
BIAS_COLS = -(-BIAS.size // 128)
ROWS = Columns(("g_query", 128), ("lin_g", 128), ("lin_b", 128), ("ff1_g1", 128), ("ff1_b1", 128),
               ("ff1_g2", FF), ("ff1_b2", FF), ("ff2_g1", 128), ("ff2_b1", 128), ("ff2_g2", FF),
               ("ff2_b2", FF), ("ff2_up", FF), ("ff2_down", 128), ("lat_mg", 128), ("lat_mb", 128),
               ("lat_lg", 128), ("lat_lb", 128), ("moe_bo", 128), ("mu_b", 4))
CONST = Columns(("ident", 128), ("rel", 128), ("tri", 128), ("triT", 128), ("causal", 128),
                ("cos", 128), ("sin", 128), ("headmask", HEADS), ("blockmask", 128),
                ("regsel", 128), ("notreg", 1), ("regscale", 1), ("minushalf", 16),
                ("step", 128), ("earlier", 64))

VAUG = slice(0, 512)
ARENA = 11200
ATT = Columns(("kept", 512), ("x", 128), ("c", 128), ("xcT", 128), ("qT", 128), ("kT", 128),
              ("wide", 2048), ("P", 2048), ("PT", 2048), ("O", 128), ("OnT", 128), ("r", 128),
              ("m", 16), ("rec", 16), ("stats", 8), ("mv", 4), ("rstd", 1), ("m2", 4),
              ("regq", REG_ROWS))
QKV_KEPT = ATT.size
assert QKV_KEPT + PAIRS * 384 <= ARENA
FFN = Columns(("kept", 512), ("x", 128), ("h", 128), ("hT", 128), ("u", FF), ("n", FF), ("nT", FF),
              ("hq", 128), ("hqb", 64), ("nb", FF // 2), ("nbT", FF // 2), ("hbT", 64), ("r", 128), ("stats", 8),
              ("mv", 4), ("rstd", 1), ("a", 8))
MLP = Columns(("kept", 512), ("x", 128), ("xT", 128), ("G", 3 * FF))
LAT = Columns(("x", 128), ("c", 128), ("n", 256), ("nT", 256), ("qT", 1024), ("kT", 2048),
              ("V", 2 * XH * XD), ("P", 2048), ("PT", 2048), ("O", 1024), ("r", 128),
              ("m", 16), ("rec", 16), ("stats", 16), ("mv", 4), ("rstd", 4))
MOE = Columns(("x", 128), ("xT", 128), ("sig", 512), ("t", 512), ("acc", 256), ("accT", 256),
              ("r", 128), ("stats", 8), ("mv", 4), ("rstd", 1), ("share", EXPERTS + 1))
for c in (ATT, FFN, MLP, LAT, MOE):
    assert c.size <= ARENA


def decoder(nc, x_tok, x_T, ctx_tok, ctx_T, mask, mask_row, w_early, w_late, w_rest, bias, rows,
            const, out, last=S_MOE):
    ctx = ExitStack()
    with ctx:
        def sb(name, shape, dt=F32):
            return ctx.enter_context(nc.sbuf_tensor(name, shape, dt))

        def sem(name):
            return ctx.enter_context(nc.semaphore(name))

        x_all = sb("x_all", [128, BATCH, DIM])
        xT_all = sb("xT_all", [128, BATCH, TOK])
        ctx_all = xT_all
        ctxT_all = sb("ctxT_all", [128, BATCH, TOK])
        maskadd = sb("maskadd", [128, BATCH, TOK], BF16)
        WA = sb("WA", [128, max(W_EARLY.size, W_LATE.size)])
        WB = sb("WB", [128, W_REST.size])
        bias3 = sb("bias3", [3, 128 * BIAS_COLS], BF16)
        half_b = sb("half_b", [3, 128], BF16)
        R = sb("R", [128, ROWS.size])
        C = sb("C", [128, CONST.size])
        arena = [sb(f"arena{s}", [128, ARENA]) for s in range(2)]
        ident_b = sb("ident_b", [128, 128], BF16)
        causal_b = sb("causal_b", [128, 128], BF16)
        ones_b = sb("ones_b", [128, 128], BF16)
        negrow_b = sb("negrow_b", [2, REG_ROWS], BF16)
        tern_up = sb("tern_up", [128, FF], BF16)
        tern_down = sb("tern_down", [128, 4, DIM], BF16)
        small = sb("small", [128, 112])
        gates = sb("gates", [LSTM_H, 5, BATCH])
        prod = sb("prod", [LSTM_H, 2, BATCH])
        tanh_c = sb("tanh_c", [LSTM_H, BATCH])
        hid = [sb(f"hid{k}", [128, BATCH]) for k in range(2)]
        mu_cols = sb("mu_cols", [128, 4, BATCH])
        pos_rows = xT_all[:, :, :].rearrange("p b t -> p (b t)").bitcast(BF16).rearrange(
            "p (a b t) -> p a b t", a=2, b=BATCH)
        pos_q = [arena[s][:, QKV_KEPT + 1024:QKV_KEPT + 1088].bitcast(BF16) for s in range(2)]
        comb = sb("comb", [128, BATCH, EXPERTS])
        comb_sum = sb("comb_sum", [128, BATCH])
        mrow = sb("mrow", [1, BATCH, TOK], BF16)
        ps = [[ctx.enter_context(nc.psum_tensor(f"ps{s}_{k}", [128, 512], F32)) for k in range(4)]
              for s in range(2)]

        ident = C[:, CONST("ident")]

        def cst(name):
            return C[:, CONST(name)]

        def heads(ap, h=4):
            return ap.rearrange("p (h k) -> p h k", h=h)

        first_in = sem("first_in")
        bias_rows = sem("bias_rows")
        loaded = sem("loaded")
        bias_in = sem("bias_in")
        mask_in = sem("mask_in")
        late_in = sem("late_in")
        rows_in = sem("rows_in")
        rest_in = sem("rest_in")
        stored = sem("stored")
        seq_done = sem("seq_done")
        const_b = sem("const_b")
        bias_cut = sem("bias_cut")
        w_sum = sem("w_sum")
        w_mean = sem("w_mean")
        w_tern = sem("w_tern")
        gates_sum = sem("gates_sum")
        gates_tanh = sem("gates_tanh")
        cell_new = sem("cell_new")
        cell_tanh = sem("cell_tanh")
        hid_new = sem("hid_new")
        musig_sum = sem("musig_sum")
        musig_kept = sem("musig_kept")
        scan_exp = sem("scan_exp")
        scan_out = sem("scan_out")
        scan_ps = sem("scan_ps")
        scan_cols = sem("scan_cols")
        pos_sq = sem("pos_sq")
        pos_w = sem("pos_w")
        pos_masked = sem("pos_masked")
        pos_T = sem("pos_T")
        pos_T_sb = sem("pos_T_sb")
        staged = sem("staged")
        xT_ps = sem("xT_ps")
        xT_sb = sem("xT_sb")
        y_ps = sem("y_ps")
        var_ok = sem("var_ok")
        rstd_ok = sem("rstd_ok")
        qkv_ps = sem("qkv_ps")
        qk_sb = sem("qk_sb")
        wide_pool_ok = sem("wide_pool_ok")
        wide_dve_ok = sem("wide_dve_ok")
        v_sb = sem("v_sb")
        s_ps = sem("s_ps")
        s_sub = sem("s_sub")
        p_exp = sem("p_exp")
        pT_ps = sem("pT_ps")
        pT_sb = sem("pT_sb")
        oT_ps = sem("oT_ps")
        oT_sb = sem("oT_sb")
        o_ps = sem("o_ps")
        o_sb = sem("o_sb")
        on_ps = sem("on_ps")
        on_sb = sem("on_sb")
        sim_q = sem("sim_q")
        sim_sb = sem("sim_sb")
        sim_mid = sem("sim_mid")
        sim_pool = sem("sim_pool")
        sim_rows = sem("sim_rows")
        reg_q = sem("reg_q")
        reg_ps = sem("reg_ps")
        reg_m = sem("reg_m")
        reg_e = sem("reg_e")
        reg_n = sem("reg_n")
        reg_T = sem("reg_T")
        reg_Tsb = sem("reg_Tsb")
        reg_o = sem("reg_o")
        reg_om = sem("reg_om")
        reg_add = sem("reg_add")
        lin_min = sem("lin_min")
        lin_exp = sem("lin_exp")
        h_sb = sem("h_sb")
        hT_ps = sem("hT_ps")
        hT_sb = sem("hT_sb")
        up_ps = sem("up_ps")
        up_in = sem("up_in")
        up_act = sem("up_act")
        n_sb = sem("n_sb")
        nT_ps = sem("nT_ps")
        nT_sb = sem("nT_sb")
        mid_var = sem("mid_var")
        mid_rstd = sem("mid_rstd")
        mlp_ps = sem("mlp_ps")
        mlp_act = sem("mlp_act")
        mlp_out = sem("mlp_out")
        w_qk = sem("w_qk")
        w_qk_sb = sem("w_qk_sb")
        w_s = sem("w_s")
        w_m = sem("w_m")
        w_e = sem("w_e")
        w_T = sem("w_T")
        w_Tsb = sem("w_Tsb")
        l_q = sem("l_q")
        l_qsb = sem("l_qsb")
        l_k = sem("l_k")
        l_ksb = sem("l_ksb")
        l_v = sem("l_v")
        l_vsb = sem("l_vsb")
        l_s = sem("l_s")
        l_sub = sem("l_sub")
        l_exp = sem("l_exp")
        l_T = sem("l_T")
        l_Tsb = sem("l_Tsb")
        l_o = sem("l_o")
        l_osb = sem("l_osb")
        l_osum = sem("l_osum")
        gate_ps = sem("gate_ps")
        gate_exp = sem("gate_exp")
        gate_sub = sem("gate_sub")
        e_ps = sem("e_ps")
        e_sig = sem("e_sig")
        e_acc = sem("e_acc")
        acc_T = sem("acc_T")
        acc_Tsb = sem("acc_Tsb")

        block = ctx.enter_context(nc.Block())

        def v_(s, cols, name, of=0, width=None):
            return arena[s][:, cols(name, of, width)]

        def add_bias(out_ap, name, of=0, width=None, stop=True):
            return nc.tensor.matmul(out_ap, ones_b[0:3, :], bias3[:, BIAS(name, of, width)],
                                    start=False, stop=stop, skip_group_check=True)

        def stage_x(pool, sub, cols, with_ctx=None, i=None):
            for s in range(2):
                pool.wait_ge(seq_done, nth(sub, i, s))
                b = i * 2 + s
                if with_ctx is not None:
                    nc.gpsimd.tensor_copy(v_(s, cols, "c"), with_ctx[:, bass.ds(b, 1), :].rearrange("p a d -> p (a d)"))
                nc.gpsimd.tensor_copy(v_(s, cols, "x"), x_all[:, bass.ds(b, 1), :].rearrange("p a d -> p (a d)"))
                pool.drain()
                pool.sem_inc(staged, 1)

        def rstd(pool, wait_sem, done_sem, run, i, s, cols, n=1, d=0):
            pool.wait_ge(wait_sem, nth(run, i, s + d))
            nc.gpsimd.tensor_tensor(v_(s, cols, "rstd", 0, n), v_(s, cols, "mv", 1, 2 * n - 1)[:, ::2] if n > 1
                                    else v_(s, cols, "mv", 1, 1),
                                    cst("minushalf")[:, 0:n], ALU.pow).then_inc(done_sem, 1)

        def stats(dve, s, cols, src, width=128, at=0):
            nc.vector.bn_stats(v_(s, cols, "stats", 0, 6), src)
            dve.drain()
            nc.vector.bn_aggr(v_(s, cols, "mv", at, 2), v_(s, cols, "stats", 0, 6))
            dve.drain()
            mv = v_(s, cols, "mv", at + 1, 1)
            return nc.vector.tensor_scalar(mv, mv, LN_EPS, None, ALU.add)

        def norm(dve, s, cols, dst, src, at=0):
            return nc.vector.tensor_scalar(dst, src, v_(s, cols, "mv", 2 * at, 1),
                                           v_(s, cols, "rstd", at, 1), ALU.subtract, ALU.mult)

        def x_of(i, s):
            return x_all[:, bass.ds(i * 2 + s, 1), :].rearrange("p a d -> p (a d)")

        def tail_stats(dve, run, i, s, cols, y, x=None):
            dve.wait_ge(y_ps, nth(run, i, s))
            nc.vector.tensor_tensor(v_(s, cols, "r"), y, v_(s, cols, "x") if x is None else x, ALU.add)
            dve.drain()
            stats(dve, s, cols, v_(s, cols, "r")).then_inc(var_ok, 1)

        def tail_norm(dve, run, i, s, cols):
            dve.wait_ge(rstd_ok, nth(run, i, s))
            norm(dve, s, cols, x_of(i, s), v_(s, cols, "r")).then_inc(seq_done, 1)

        def transpose_x(pe, sub, i, s, cols, src="x", bank=0):
            pe.wait_ge(staged, nth(sub, i, s))
            nc.tensor.transpose(ps[s][bank][:, 0:128], v_(s, cols, src), ident).then_inc(xT_ps, 1)

        WIDE_POOL, WIDE_DVE = (0, 3), (1, 2)

        BIASED = (1, 3)

        def pairs(eng, front, body):
            front(0, 0)
            with eng.Fori(0, PAIRS - 1) as i:
                body(i, True)
            body(PAIRS - 1, False)

        def x_at(src, i, n):
            return src[:, bass.ds(i * 2 + n, 1), :].rearrange("p a d -> p (a d)")

        def widen(eng, i, d, s, kind, t):
            if kind == "kept":
                src = arena[s][:, bass.ds(i * 384 + (QKV_KEPT + 128 + 192 * d), 128)]
            else:
                src = v_(s, ATT, "qT" if kind == "linear" else "kT")
            return eng.tensor_tensor(heads(v_(s, ATT, "wide", 512 * t, 512)),
                                     src.unsqueeze(1).broadcast_to([128, 4, 128]),
                                     cst("headmask")[:, 4 * t:4 * t + 4].unsqueeze(2).broadcast_to([128, 4, 128]),
                                     ALU.mult)

        def att_pool(pool, sub, kind):
            a = att_run[sub]

            def stage(i, d):
                for s in range(2):
                    if d == 0:
                        pool.wait_ge(seq_done, nth(sub, i, s))
                    else:
                        pool.wait_ge(s_ps, nth(a, i, s, GROUPS))
                    if kind == "cross":
                        nc.gpsimd.tensor_copy(v_(s, ATT, "c"), x_at(ctxT_all, i, s + d))
                    if sub == S_REG:
                        nc.gpsimd.tensor_copy(pos_q[s], pos_rows[:, 0, bass.ds(i * 2 + (s + d), 1), :]
                                              .rearrange("p a d -> p (a d)"))
                    if kind != "kept":
                        nc.gpsimd.tensor_copy(v_(s, ATT, "x"), x_at(x_all, i, s + d))
                        pool.drain()
                    pool.sem_inc(staged, 1)

            def wide(i, d, s):
                if kind != "kept":
                    pool.wait_ge(qk_sb, nth(a, i, s + d))
                elif d:
                    pool.wait_ge(o_ps, nth(a, i, s))
                for t in WIDE_POOL:
                    widen(nc.gpsimd, i, d, s, kind, t).then_inc(wide_pool_ok, 1)

            def body(i, ahead):
                if ahead:
                    stage(i, 2)
                if kind == "linear":
                    for s in range(2):
                        rstd(pool, mid_var, mid_rstd, mid_run[S_LIN], i, s, ATT)
                if ahead:
                    wide(i, 2, 0)
                for s in range(2):
                    rstd(pool, var_ok, rstd_ok, tail_run[sub], i, s, ATT)
                if ahead:
                    wide(i, 2, 1)

            def front(i, d):
                stage(i, d)
                for s in range(2):
                    wide(i, d, s)

            pairs(pool, front, body)

        def att_pe(pe, sub, kind, W, name, bias_name, mask_kind, out_w=384, out_name=None):
            out_name = out_name or name
            xt, a = xt_run.get(sub), att_run[sub]

            def front_x(i, d):
                if kind != "kept":
                    for s in range(2):
                        pe.wait_ge(staged, nth(sub, i, s + d))
                        nc.tensor.transpose(ps[s][2][:, 0:128], v_(s, ATT, "x"), ident).then_inc(xT_ps, 1)

            def front_qkv(i, d):
                if kind == "kept":
                    return
                for s in range(2):
                    pe.wait_ge(xT_sb, nth(xt, i, s + d))
                    xT = v_(s, ATT, "xcT")
                    cT = v_(s, ATT, "c") if kind == "cross" else xT
                    parts = [(name, bias_name, 0, xT), (name, bias_name, 128, cT)]
                    if sub == S_MQA:
                        parts += [("mqa_turned", "mqa_turned", 0, xT), ("mqa_turned", "mqa_turned", 128, xT)]
                    for n, (w, b, of, src) in enumerate(parts):
                        o = ps[s][3][:, 128 * n:128 * n + 128]
                        mm = nc.tensor.matmul(o, W[:, name_cols(w, of, 128)], src, start=True,
                                              stop=b is None, skip_group_check=True)
                        if b is not None:
                            mm = nc.tensor.matmul(o, bias3[:, BIAS(b, of, 128)], ones_b[0:3, :],
                                                  start=False, stop=True, skip_group_check=True)
                    mm.then_inc(qkv_ps, 1)
                    o = ps[s][2][:, 128:256]
                    mm = nc.tensor.matmul(o, cT, W[:, name_cols(name, 256, 128)], start=True,
                                          stop=bias_name is None, skip_group_check=True)
                    if bias_name is not None:
                        mm = add_bias(o, bias_name, 256, 128)
                    mm.then_inc(qkv_ps, 1)

            def scores(i):
                for s in range(2):
                    pe.wait_ge(qk_sb, nth(a, i, s))
                    pe.wait_ge(v_sb, nth(a, i, s))
                    for t in range(GROUPS):
                        if t in WIDE_POOL:
                            pe.wait_ge(wide_pool_ok, nth(a, i, s, len(WIDE_POOL), WIDE_POOL.index(t) + 1))
                        else:
                            pe.wait_ge(wide_dve_ok, nth(a, i, s, len(WIDE_DVE), WIDE_DVE.index(t) + 1))
                        bank = ps[s][t]
                        mm = nc.tensor.matmul(bank[:, :], v_(s, ATT, "kT" if kind == "linear" else "qT"),
                                              v_(s, ATT, "wide", 512 * t, 512), start=True,
                                              stop=mask_kind is None, skip_group_check=True)
                        if mask_kind is not None:
                            if mask_kind == "full":
                                l, r = ident_b[:, :], maskadd[:, bass.ds(i * 2 + s, 1), :].broadcast_to([128, 4, 128])
                            elif mask_kind == "causal":
                                l, r = ident_b[:, :], causal_b[:, :].unsqueeze(1).broadcast_to([128, 4, 128])
                            else:
                                l, r = pos_q[s], pos_rows[:, 1, bass.ds(i * 2 + s, 1), :].broadcast_to([128, 4, 128])
                            mm = nc.tensor.matmul(heads(bank[:, :]), l, r, start=False, stop=True,
                                                  skip_group_check=True)
                        mm.then_inc(s_ps, 1)

            def values(i, s):
                va = arena[s][:, VAUG].rearrange("p (h d) -> p h d", h=HEADS)
                for h in range(HEADS):
                    t, j = h // 4, h % 4
                    if j == 0:
                        pe.wait_ge(pT_sb, nth(a, i, s, GROUPS, t + 1))
                    mm = nc.tensor.matmul(ps[s][0][PAD * j:PAD * (j + 1), t * 128:(t + 1) * 128],
                                          va[:, h, :], v_(s, ATT, "PT", 128 * h, 128), start=True,
                                          stop=True, skip_group_check=True)
                mm.then_inc(oT_ps, 1)

            def body(i, ahead):
                scores(i)
                if kind != "linear":
                    for s in range(2):
                        for t in range(GROUPS):
                            pe.wait_ge(p_exp, nth(soft_run[sub], i, s, GROUPS, t + 1))
                            for j in range(4):
                                mm = nc.tensor.transpose(ps[s][t][:, j * 128:(j + 1) * 128],
                                                         v_(s, ATT, "P", 128 * (4 * t + j), 128), ident)
                            mm.then_inc(pT_ps, 1)
                        values(i, s)
                else:
                    for s in range(2):
                        values(i, s)
                if sub == S_REG:
                    reg_pe(pe, i)
                if ahead and sub != S_REG:
                    front_x(i, 2)
                for s in range(2):
                    pe.wait_ge(oT_sb, nth(a, i, s))
                    for t in range(GROUPS):
                        mm = nc.tensor.transpose(ps[s][1][:, t * 128:(t + 1) * 128],
                                                 v_(s, ATT, "wide", 128 * t, 128), ident)
                    mm.then_inc(o_ps, 1)
                if ahead and sub != S_REG:
                    front_qkv(i, 2)
                for s in range(2):
                    pe.wait_ge(o_sb, nth(a, i, s))
                    nc.tensor.transpose(ps[s][0][:, 0:128], v_(s, ATT, "O"), ident).then_inc(on_ps, 1)
                if ahead and sub == S_REG:
                    front_x(i, 2)
                for s in range(2):
                    pe.wait_ge(on_sb, nth(a, i, s))
                    yb = ps[s][1][:, 0:128]
                    nc.tensor.matmul(yb, v_(s, ATT, "OnT"), W[:, name_cols(out_name, out_w, 128)],
                                     start=True, stop=False, skip_group_check=True)
                    if bias_name in ("x0", "lin", "x2", "mqa"):
                        mm = add_bias(yb, bias_name, 384, 128)
                    else:
                        mm = add_bias(yb, "reg_out" if sub == S_REG else "self2_out")
                    mm.then_inc(y_ps, 1)
                if ahead and sub == S_REG:
                    front_qkv(i, 2)

            def front(i, d):
                front_x(i, d)
                front_qkv(i, d)

            pairs(pe, front, body)

        def att_act(act, sub, kind):
            xt, a = xt_run.get(sub), att_run[sub]

            def front_x(i, d):
                if kind != "kept":
                    for s in range(2):
                        act.wait_ge(xT_ps, nth(xt, i, s + d))
                        nc.scalar.copy(v_(s, ATT, "xcT", 0, 128), ps[s][2][:, 0:128]).then_inc(xT_sb, 1)

            def front_qkv(i, d):
                for s in range(2):
                    va = arena[s][:, VAUG].rearrange("p (h d) -> p h d", h=HEADS)
                    if kind == "kept":
                        act.wait_ge(staged, nth(sub, i, s + d))
                        kept = arena[s][:, bass.ds(i * 384 + (QKV_KEPT + 192 * d), 384)]
                        nc.scalar.copy(v_(s, ATT, "qT"), kept[:, 0:128]).then_inc(qk_sb, 1)
                        v = kept[:, 256:384]
                    else:
                        if kind != "linear" and sub != S_MQA:
                            act.wait_ge(qkv_ps, nth(qkv_run[sub], i, s + d, 2, 1))
                            nc.scalar.copy(qkT_of(s), ps[s][3][:, 0:256]).then_inc(qk_sb, 1)
                        act.wait_ge(qkv_ps, nth(qkv_run[sub], i, s + d, 2, 2))
                        v = ps[s][2][:, 128:256]
                    nc.scalar.copy(va[:, :, 0:HD], v.rearrange("p (h d) -> p h d", h=HEADS)).then_inc(v_sb, 1)
                if kind == "linear":
                    for s in range(2):
                        act.wait_ge(lin_min, nth(0, i, s + d))
                        e = v_(s, ATT, "P", 0, 256)
                        nc.scalar.activation(e, e, ACT.Exp).then_inc(lin_exp, 1)

            def body(i, ahead):
                if kind != "linear":
                    for s in range(2):
                        for t in range(GROUPS):
                            act.wait_ge(s_sub, nth(soft_run[sub], i, s, GROUPS, t + 1))
                            e = v_(s, ATT, "P", 512 * t, 512)
                            if t not in BIASED:
                                nc.scalar.activation(e, e, ACT.Exp, scale=SCALE).then_inc(p_exp, 1)
                                continue
                            for j in range(4):
                                ex = nc.scalar.activation(e[:, 128 * j:128 * j + 128], ps[s][t][:, 128 * j:128 * j + 128],
                                                          ACT.Exp, scale=SCALE, bias=v_(s, ATT, "m", 4 * t + j, 1))
                            ex.then_inc(p_exp, 1)
                        for t in range(GROUPS):
                            act.wait_ge(pT_ps, nth(soft_run[sub], i, s, GROUPS, t + 1))
                            nc.scalar.copy(v_(s, ATT, "PT", 512 * t, 512), ps[s][t][:, :]).then_inc(pT_sb, 1)
                if sub == S_REG:
                    reg_act(act, i)
                for s in range(2):
                    act.wait_ge(oT_ps, nth(a, i, s))
                    nc.scalar.copy(v_(s, ATT, "wide", 0, 512), ps[s][0][:, :]).then_inc(oT_sb, 1)
                if ahead and sub != S_REG:
                    front_x(i, 2)
                    front_qkv(i, 2)
                for s in range(2):
                    act.wait_ge(on_ps, nth(a, i, s))
                    nc.scalar.copy(v_(s, ATT, "OnT"), ps[s][0][:, 0:128]).then_inc(on_sb, 1)
                if ahead and sub == S_REG:
                    front_x(i, 2)
                    front_qkv(i, 2)

            def front(i, d):
                front_x(i, d)
                front_qkv(i, d)

            pairs(act, front, body)

        def qkT_of(s):
            a = ATT.at["qT"][0]
            return arena[s][:, a:a + 256]

        def att_dve(dve, sub, kind):
            a = att_run[sub]

            def front_q(i, d):
                for s in range(2):
                    if kind == "linear":
                        dve.wait_ge(qkv_ps, nth(qkv_run[sub], i, s + d, 2, 1))
                        nc.vector.tensor_scalar(v_(s, ATT, "P", 0, 256), ps[s][3][:, 0:256], 0.0, None,
                                                ALU.min).then_inc(lin_min, 1)
                    elif sub == S_MQA:
                        dve.wait_ge(qkv_ps, nth(qkv_run[sub], i, s + d, 2, 1))
                        qk, turn = qkT_of(s), v_(s, ATT, "P", 0, 256)
                        for dst, at, table in ((qk, 0, "cos"), (turn, 256, "sin")):
                            nc.vector.tensor_tensor(heads(dst, 2), heads(ps[s][3][:, at:at + 256], 2),
                                                    cst(table).unsqueeze(1).broadcast_to([128, 2, 128]), ALU.mult)
                        dve.drain()
                        nc.vector.tensor_tensor(qk, qk, turn, ALU.add).then_inc(qk_sb, 1)

            def front_wide(i, d):
                for s in range(2):
                    if kind == "linear":
                        dve.wait_ge(lin_exp, nth(0, i, s + d))
                        qk = qkT_of(s)
                        nc.vector.scalar_tensor_tensor(qk, ps[s][3][:, 0:256], 0.0, v_(s, ATT, "P", 0, 256),
                                                       ALU.max, ALU.add)
                        dve.drain()
                        nc.vector.tensor_scalar(qk[:, 0:128], qk[:, 0:128], 1e-4, SCALE, ALU.add, ALU.mult)
                        nc.vector.tensor_scalar(qk[:, 128:256], qk[:, 128:256], 1e-4, None, ALU.add)
                        dve.drain()
                        dve.sem_inc(qk_sb, 1)
                for s in range(2):
                    if kind == "kept":
                        dve.wait_ge(staged, nth(sub, i, s + d))
                    elif kind != "linear" and sub != S_MQA:
                        dve.wait_ge(qk_sb, nth(a, i, s + d))
                    elif s == 0:
                        dve.drain()
                    for t in WIDE_DVE:
                        widen(nc.vector, i, d, s, kind, t).then_inc(wide_dve_ok, 1)

            def body(i, ahead):
                if kind == "linear":
                    for s in range(2):
                        for t in range(GROUPS):
                            dve.wait_ge(s_ps, nth(a, i, s, GROUPS, t + 1))
                            nc.vector.tensor_tensor(heads(v_(s, ATT, "PT", 512 * t, 512)), heads(ps[s][t][:, :]),
                                                    cst("triT").unsqueeze(1).broadcast_to([128, 4, 128]),
                                                    ALU.mult).then_inc(pT_sb, 1)
                else:
                    if sub == S_REG:
                        reg_dve_q(dve, i, a)
                    for s in range(2):
                        m = v_(s, ATT, "m")
                        for t in range(GROUPS):
                            dve.wait_ge(s_ps, nth(a, i, s, GROUPS, t + 1))
                            nc.vector.tensor_reduce(m[:, 4 * t:4 * t + 4], heads(ps[s][t][:, :]), AXX, ALU.max)
                            dve.drain()
                            if t in BIASED:
                                nc.vector.tensor_scalar(m[:, 4 * t:4 * t + 4], m[:, 4 * t:4 * t + 4], -SCALE, None,
                                                        ALU.mult).then_inc(s_sub, 1)
                                continue
                            nc.vector.tensor_tensor(heads(v_(s, ATT, "P", 512 * t, 512)), heads(ps[s][t][:, :]),
                                                    m[:, 4 * t:4 * t + 4].unsqueeze(2).broadcast_to([128, 4, 128]),
                                                    ALU.subtract).then_inc(s_sub, 1)
                if sub == S_REG:
                    reg_dve(dve, i)
                for s in range(2):
                    dve.wait_ge(o_ps, nth(a, i, s))
                    o = ps[s][1][:, :].rearrange("p (h d) -> p h d", d=PAD)
                    rec = v_(s, ATT, "rec")
                    if kind == "linear":
                        nc.vector.tensor_scalar(rec, o[:, :, HD:HD + 1].rearrange("p h d -> p (h d)"), 1e-4, None, ALU.add)
                        dve.drain()
                        nc.vector.reciprocal(rec, rec)
                    else:
                        nc.vector.reciprocal(rec, o[:, :, HD:HD + 1].rearrange("p h d -> p (h d)"))
                    dve.drain()
                    if sub == S_REG:
                        nc.vector.tensor_scalar(rec, rec, cst("regscale"), None, ALU.mult)
                        dve.drain()
                    O = v_(s, ATT, "O").rearrange("p (h d) -> p h d", d=HD)
                    mul = nc.vector.tensor_tensor(O, o[:, :, 0:HD], rec.unsqueeze(2).broadcast_to([128, HEADS, HD]), ALU.mult)
                    if sub == S_REG:
                        dve.drain()
                        dve.wait_ge(reg_add, nth(0, i, s))
                        nc.vector.tensor_tensor(v_(s, ATT, "O"), v_(s, ATT, "O"), ps[s][3][:, 0:128],
                                                ALU.add).then_inc(o_sb, 1)
                    else:
                        mul.then_inc(o_sb, 1)
                if ahead:
                    front_q(i, 2)
                for s in range(2):
                    yb = ps[s][1][:, 0:128]
                    if kind == "linear":
                        dve.wait_ge(y_ps, nth(tail_run[sub], i, s))
                        nc.vector.tensor_copy(v_(s, ATT, "r"), yb)
                        dve.drain()
                        stats(dve, s, ATT, v_(s, ATT, "r")).then_inc(mid_var, 1)
                    else:
                        tail_stats(dve, tail_run[sub], i, s, ATT, yb, x_of(i, s))
                if ahead:
                    front_wide(i, 2)
                if kind == "linear":
                    for s in range(2):
                        dve.wait_ge(mid_rstd, nth(mid_run[S_LIN], i, s))
                        r = v_(s, ATT, "r")
                        norm(dve, s, ATT, r, r)
                        dve.drain()
                        nc.vector.tensor_tensor(r, r, R[:, ROWS("lin_g")], ALU.mult)
                        dve.drain()
                        nc.vector.tensor_tensor(r, r, R[:, ROWS("lin_b")], ALU.add)
                        dve.drain()
                        nc.vector.tensor_tensor(r, r, x_of(i, s), ALU.add)
                        dve.drain()
                        stats(dve, s, ATT, r).then_inc(var_ok, 1)
                for s in range(2):
                    tail_norm(dve, tail_run[sub], i, s, ATT)

            def front(i, d):
                front_q(i, d)
                front_wide(i, d)

            pairs(dve, front, body)

        xt_run = {S_X0: 0, S_SIM: 1, S_REG: 2, S_LIN: 3, S_X1: 4, S_MLP: 5, S_X2: 6, S_MQA: 7,
                  S_LAT: 8, S_GATE: 9, S_MOE: 10}
        att_run = {S_X0: 0, S_REG: 1, S_LIN: 2, S_SELF2: 3, S_X2: 4, S_MQA: 5}
        qkv_run = {S_X0: 0, S_REG: 1, S_LIN: 2, S_X2: 3, S_MQA: 4}
        soft_run = {S_X0: 0, S_REG: 1, S_SELF2: 2, S_X2: 3, S_MQA: 4}
        
        mid_run = {S_LSTM: 0, S_LIN: 1, S_FF1: 2, S_FF2: 3, S_LAT: 4}
        tail_run = {S_LSTM: 0, S_X0: 1, S_REG: 2, S_LIN: 3, S_X1: 4, S_FF1: 5, S_SELF2: 6, S_X2: 7,
                    S_FF2: 8, S_MQA: 9, S_LAT: 10, S_MOE: 11}

        def name_cols(name, of=0, width=None):
            c = W_EARLY if name in W_EARLY.at else W_REST if name in W_REST.at else W_LATE
            return c(name, of, width)

        def reg_dve_q(dve, i, a):
            for s in range(2):
                dve.wait_ge(qk_sb, nth(a, i, s))
                nc.vector.tensor_tensor(v_(s, ATT, "regq").rearrange("p (h r) -> p h r", r=REG),
                                        v_(s, ATT, "qT")[:, 0:REG].unsqueeze(1).broadcast_to([128, HEADS, REG]),
                                        cst("headmask").unsqueeze(2).broadcast_to([128, HEADS, REG]),
                                        ALU.mult).then_inc(reg_q, 1)

        def reg_pe(pe, i):
            for s in range(2):
                pe.wait_ge(reg_q, nth(0, i, s))
                bank = ps[s][2][0:REG_ROWS, 0:128]
                nc.tensor.matmul(bank, v_(s, ATT, "regq"), v_(s, ATT, "kT"), start=True, stop=False,
                                 skip_group_check=True)
                nc.tensor.matmul(bank, negrow_b[:, :],
                                 pos_rows[0:2, 1, bass.ds(i * 2 + s, 1), :].rearrange("p a k -> p (a k)"),
                                 start=False, stop=True, skip_group_check=True).then_inc(reg_ps, 1)
            for s in range(2):
                pe.wait_ge(reg_n, nth(0, i, s))
                nc.tensor.transpose(ps[s][3][:, 0:REG_ROWS], v_(s, ATT, "P", 0, 128)[0:REG_ROWS, :],
                                    ident[0:REG_ROWS, 0:REG_ROWS]).then_inc(reg_T, 1)
            for s in range(2):
                pe.wait_ge(reg_Tsb, nth(0, i, s))
                va = arena[s][:, VAUG].rearrange("p (h d) -> p h d", h=HEADS)
                nc.tensor.matmul(ps[s][2][0:REG_ROWS, 0:128], v_(s, ATT, "P", 128, REG_ROWS), va[:, :, 0:HD],
                                 start=True, stop=True, skip_group_check=True).then_inc(reg_o, 1)
            for s in range(2):
                pe.wait_ge(reg_om, nth(0, i, s))
                nc.tensor.matmul(ps[s][3][:, 0:128], cst("regsel")[0:REG_ROWS, :],
                                 v_(s, ATT, "P", 256, 128)[0:REG_ROWS, :],
                                 start=True, stop=True, skip_group_check=True).then_inc(reg_add, 1)

        def reg_act(act, i):
            for s in range(2):
                act.wait_ge(reg_m, nth(0, i, s))
                nc.scalar.activation(v_(s, ATT, "P", 0, 128)[0:REG_ROWS, :], ps[s][2][0:REG_ROWS, 0:128], ACT.Exp,
                                     bias=v_(s, ATT, "m2", 0, 1)[0:REG_ROWS, :], scale=SCALE,
                                     accum_out=v_(s, ATT, "m2", 1, 1)[0:REG_ROWS, :]).then_inc(reg_e, 1)
            for s in range(2):
                act.wait_ge(reg_T, nth(0, i, s))
                nc.scalar.copy(v_(s, ATT, "P", 128, REG_ROWS), ps[s][3][:, 0:REG_ROWS]).then_inc(reg_Tsb, 1)

        def reg_dve(dve, i):
            for s in range(2):
                dve.wait_ge(reg_ps, nth(0, i, s))
                nc.vector.tensor_reduce(v_(s, ATT, "m2", 2, 1)[0:REG_ROWS, :], ps[s][2][0:REG_ROWS, 0:128], AXX, ALU.max)
                dve.drain()
                nc.vector.tensor_scalar(v_(s, ATT, "m2", 0, 1)[0:REG_ROWS, :], v_(s, ATT, "m2", 2, 1)[0:REG_ROWS, :],
                                        -SCALE, None, ALU.mult).then_inc(reg_m, 1)
            for s in range(2):
                dve.wait_ge(reg_e, nth(0, i, s))
                nc.vector.reciprocal(v_(s, ATT, "m2", 3, 1)[0:REG_ROWS, :], v_(s, ATT, "m2", 1, 1)[0:REG_ROWS, :])
                dve.drain()
                p = v_(s, ATT, "P", 0, 128)[0:REG_ROWS, :]
                nc.vector.tensor_scalar(p, p, v_(s, ATT, "m2", 3, 1)[0:REG_ROWS, :], None, ALU.mult).then_inc(reg_n, 1)
            for s in range(2):
                dve.wait_ge(reg_o, nth(0, i, s))
                nc.vector.tensor_tensor(v_(s, ATT, "P", 256, 128)[0:REG_ROWS, :], ps[s][2][0:REG_ROWS, 0:128],
                                        cst("blockmask")[0:REG_ROWS, :], ALU.mult).then_inc(reg_om, 1)

        def loads(sp):
            sp.dma_start(bias_cols[:, :], bias).then_inc(bias_in, 16)
            sp.dma_start(WA[:, 0:164], w_early[:, 0:164]).then_inc(first_in, 16)
            sp.dma_start(C[:, :], const).then_inc(first_in, 16)
            sp.dma_start(xT_all[:, :, :], x_T).then_inc(first_in, 16)
            sp.dma_start(R[:, :], rows).then_inc(loaded, 16)
            sp.dma_start(WA[:, W_EARLY("ff1_up", 0, 2 * FF)], w_early[:, W_EARLY("ff1_up", 0, 2 * FF)]).then_inc(loaded, 16)
            sp.dma_start(WB[:, :], w_rest).then_inc(loaded, 16)
            sp.wait_ge(bias_cut, 1)
            for k in range(3):
                sp.dma_start(bias3[k:k + 1, :], bias_parts[:, k, :]).then_inc(bias_rows, 16)
            sp.dma_start(x_all[:, :, :], x_tok).then_inc(loaded, 16)
            sp.dma_start(arena[1][:, 0:2048].bitcast(I32), mask).then_inc(mask_in, 16)
            sp.dma_start(arena[1][0:1, 2048:4096].bitcast(I32), mask_row).then_inc(mask_in, 16)
            sp.dma_start(ctxT_all[:, :, :], ctx_T).then_inc(rest_in, 16)
            a, b = 164, W_EARLY.at["ff1_up"][0]
            sp.dma_start(WA[:, a:b], w_early[:, a:b]).then_inc(rest_in, 16)
            a = W_EARLY.at["mlp_up"][0]
            sp.dma_start(WA[:, a:W_EARLY.size], w_early[:, a:]).then_inc(rest_in, 16)

        loads_first, loads_early, loads_rest = 3, 4, 3
        TERN = (("ff1_up", 0), ("ff1_down", 1), ("ff2_up", 2), ("ff2_down", 3))

        def W_of(name, of=0, width=None):
            return (WA if name in W_EARLY.at or name in W_LATE.at else WB)[:, name_cols(name, of, width)]

        def start_act(act):
            act.wait_ge(loaded, 16 * loads_early)
            for name, k in TERN:
                nc.scalar.activation(abs_out[:, :], W_of(name), ACT.Abs, accum_out=small[:, k:k + 1])
                act.drain()
            act.sem_inc(w_sum, 1)

        def start_pe(pe):
            pe.wait_ge(w_sum, 1)
            nc.tensor.matmul(ps[0][0][:, 0:4], ones_f[:, :], small[:, 0:4], start=True, stop=True).then_inc(w_mean, 1)

        def start_dve(dve):
            nc.vector.memset(ones_f[:, :], 1.0)
            nc.vector.memset(ones_b[:, :], 1.0)
            for k in range(2):
                nc.vector.memset(hid[k][:, :], 0.0)
            nc.vector.memset(gates[:, :, :], 0.0)
            nc.vector.memset(half_b[:, :], 0.5)
            dve.wait_ge(bias_in, 16)
            hi, mid, lo = (bias_parts[:, k, :] for k in range(3))
            b = bias_cols[:, :]
            nc.vector.tensor_copy(hi, b)
            dve.drain()
            nc.vector.tensor_tensor(b, b, hi, ALU.subtract)
            dve.drain()
            nc.vector.tensor_copy(mid, b)
            dve.drain()
            nc.vector.tensor_tensor(lo, b, mid, ALU.subtract).then_inc(bias_cut, 1)
            dve.wait_ge(first_in, 16 * loads_first)
            nc.vector.tensor_copy(ident_b[:, :], ident)
            nc.vector.tensor_copy(causal_b[:, :], cst("causal"))
            nc.vector.tensor_copy(negrow_b[:, :], ident[0:2, 1:2].broadcast_to([2, REG_ROWS]))
            ih, hh, ms = W_of("ih"), W_of("hh"), W_of("musig")
            nc.vector.tensor_scalar(ih[:, 0:60], ih[:, 0:60], 0.5, None, ALU.mult)
            nc.vector.tensor_scalar(hh[:, 0:60], hh[:, 0:60], 0.25, None, ALU.mult)
            nc.vector.tensor_scalar(hh[:, 60:80], hh[:, 60:80], 0.5, None, ALU.mult)
            nc.vector.tensor_scalar(ms, ms, 0.5, None, ALU.mult)
            dve.drain()
            dve.sem_inc(const_b, 1)

        def mean_dve(dve):
            dve.wait_ge(w_mean, 1)
            mean, inv, back = small[:, 4:8], small[:, 8:12], small[:, 12:16]
            nc.vector.tensor_scalar(mean, ps[0][0][:, 0:4], 1.0 / (DIM * FF), 1e-5, ALU.mult, ALU.max)
            dve.drain()
            nc.vector.reciprocal(inv, mean)
            dve.drain()
            nc.vector.reciprocal(back, inv)
            g = R[:, ROWS("g_query")]
            nc.vector.tensor_tensor(gsq[:, :], g, g, ALU.mult)
            dve.drain()
            nc.vector.tensor_reduce(small[:, 16:32], gsq[:, :].rearrange("p (h d) -> p h d", d=HD), AXX, ALU.add)
            dve.drain()
            dve.sem_inc(w_mean, 1)

        ones_f = arena[0][:, QKV_KEPT + 1088:QKV_KEPT + 1216]
        bias_cols = arena[1][:, 4096:4096 + BIAS_COLS]
        bias_parts = arena[1][:, 4352:4352 + (3 * BIAS_COLS + 1) // 2].bitcast(BF16)[:, 0:3 * BIAS_COLS].rearrange(
            "p (k n) -> p k n", k=3)
        gsq = arena[1][:, 8192:8320]
        abs_out = arena[1][:, 8320:8320 + FF]
        sim_all = arena[0][:, QKV_KEPT + 512:QKV_KEPT + 1024].rearrange("p (a b h) -> p a b h", a=2, b=BATCH)
        pos64 = arena[0][:, QKV_KEPT + 1216:QKV_KEPT + 1280].rearrange("p (a b) -> p a b", a=4)
        pos64T = arena[0][0:64, QKV_KEPT + 1280:QKV_KEPT + 1344].bitcast(BF16)

        def start_pool(pool):
            pool.wait_ge(mask_in, 32)
            m32 = arena[1][:, 0:2048].bitcast(I32)
            nc.gpsimd.tensor_scalar(maskadd[:, :, :].rearrange("p b k -> p (b k)"), m32, 0.0, NEG, ALU.is_equal, ALU.mult)
            nc.gpsimd.tensor_scalar(mrow[:, :, :].rearrange("p b k -> p (b k)"),
                                    arena[1][0:1, 2048:4096].bitcast(I32), 0.0, BIG, ALU.is_equal, ALU.mult)
            pool.wait_ge(w_mean, 2)
            nc.gpsimd.tensor_tensor(small[:, 32:48], small[:, 16:32], cst("minushalf"), ALU.pow)
            for name, k in TERN:
                w = W_of(name)
                nc.gpsimd.tensor_scalar(abs_out[:, :], w, small[:, 8 + k:9 + k], None, ALU.mult)
                pool.drain()
                nc.gpsimd.tensor_scalar(abs_out[:, :], abs_out[:, :], ROUND, None, ALU.add)
                pool.drain()
                nc.gpsimd.tensor_scalar(abs_out[:, :], abs_out[:, :], -ROUND, None, ALU.add)
                pool.drain()
                dst = {2: tern_up[:, :], 3: tern_down[:, :, :].rearrange("p a d -> p (a d)")}.get(k, abs_out[:, :])
                nc.gpsimd.tensor_scalar(dst, abs_out[:, :], 1.0, -1.0, ALU.min, ALU.max)
                pool.drain()
                if k < 2:
                    nc.gpsimd.tensor_scalar(abs_out[:, :], abs_out[:, :], small[:, 12 + k:13 + k], None, ALU.mult)
                    pool.drain()
                    nc.gpsimd.tensor_tensor(abs_out[:, :], abs_out[:, :], w, ALU.subtract)
                    pool.drain()
                    nc.gpsimd.tensor_tensor(w, w, abs_out[:, :], ALU.add)
                    pool.drain()
            for s in range(2):
                nc.gpsimd.memset(arena[s][:, VAUG], 0.0)
                pool.drain()
                nc.gpsimd.memset(arena[s][:, VAUG].rearrange("p (h d) -> p h d", h=HEADS)[:, :, HD:HD + 1], 1.0)
            pool.drain()
            pool.sem_inc(w_tern, 2)
            pool.sem_inc(seq_done, 2)

        STEPS, HALF = 16, 8
        gate_banks = [ps[0][1], ps[0][2]]
        ms_bank = ps[1][0]
        ms_all = arena[1][0:BATCH, 8832:9344].rearrange("p (t n) -> p t n", n=4)
        scan_t = arena[1][0:BATCH, 9344:10112].rearrange("p (n t) -> p n t", n=6)

        def lstm_pe(pe):
            pe.wait_ge(bias_rows, 48)
            pe.wait_ge(const_b, 1)

            def turn(it):
                for k in range(STEPS):
                    g = gate_banks[k // HALF][0:LSTM_H, :].rearrange("p (t g b) -> p t g b", t=HALF, g=4)
                    if k % HALF == 0:
                        xs = xT_all[:, :, bass.ds(it * STEPS + k, HALF)].rearrange("p b t -> p t b")
                        for gt in range(4):
                            w = slice(20 * gt, 20 * gt + 20)
                            nc.tensor.matmul(g[:, :, gt, :], W_of("ih")[:, w], xs, start=gt == 0, stop=False,
                                             skip_group_check=True)
                            for name in ("ih", "hh"):
                                nc.tensor.matmul(g[:, :, gt, :], bias3[:, BIAS(name, 20 * gt, 20)],
                                                 (half_b if gt < 3 else ones_b)[0:3, :].rearrange("p (t b) -> p t b", t=HALF),
                                                 start=False, stop=False, skip_group_check=True)
                    pe.wait_ge(hid_new, it * STEPS + (k + 1))
                    h = hid[(k + 1) % 2][:, :]
                    for gt in range(4):
                        mm = nc.tensor.matmul(g[:, k % HALF, gt, :], W_of("hh")[:, 20 * gt:20 * gt + 20], h,
                                              start=False, stop=True, skip_group_check=True)
                    mm.then_inc(gates_sum, 1)
                    if k > 0:
                        nc.tensor.matmul(ms_bank[0:BATCH, 4 * (k - 1):4 * k], h, W_of("musig"),
                                         start=True, stop=True, skip_group_check=True)
                pe.wait_ge(hid_new, it * STEPS + (STEPS + 1))
                nc.tensor.matmul(ms_bank[0:BATCH, 4 * (STEPS - 1):4 * STEPS], hid[1][:, :], W_of("musig"),
                                 start=True, stop=True, skip_group_check=True).then_inc(musig_sum, 1)
                pe.wait_ge(musig_kept, it + 1)

            turn(0)
            start_pe(pe)
            with pe.Fori(1, TOK // STEPS) as it:
                turn(it)
            pe.wait_ge(scan_out, 2)
            nc.tensor.transpose(ps[0][1][:, 0:16], scan_t[:, 4, :], ident[0:16, 0:16])
            nc.tensor.transpose(ps[0][1][:, 16:32], scan_t[:, 5, :], ident[0:16, 0:16]).then_inc(scan_ps, 1)

        def lstm_act(act):
            def turn(it):
                for k in range(STEPS):
                    g = gate_banks[k // HALF][0:LSTM_H, :].rearrange("p (t n) -> p t n", t=HALF)
                    act.wait_ge(gates_sum, it * STEPS + k + 1)
                    nc.scalar.activation(gates[:, 0:4, :].rearrange("p g b -> p (g b)"), g[:, k % HALF, :],
                                         ACT.Tanh).then_inc(gates_tanh, 1)
                    act.wait_ge(cell_new, it * STEPS + k + 1)
                    nc.scalar.activation(tanh_c[:, :], gates[:, 4, :], ACT.Tanh, scale=0.5).then_inc(cell_tanh, 1)
                act.wait_ge(musig_sum, it + 1)
                nc.scalar.copy(ms_all[:, bass.ds(it * STEPS, STEPS), :],
                               ms_bank[0:BATCH, 0:4 * STEPS].rearrange("p (t n) -> p t n", n=4)).then_inc(musig_kept, 1)

            turn(0)
            start_act(act)
            with act.Fori(1, TOK // STEPS) as it:
                turn(it)
            act.wait_ge(scan_out, 1)
            nc.scalar.activation(scan_t[:, 3, :], scan_t[:, 3, :], ACT.Exp, scale=-1.0).then_inc(scan_exp, 1)

        def lstm_dve(dve):
            dve.sem_inc(hid_new, 1)

            def turn(it):
                for k in range(STEPS):
                    dve.wait_ge(gates_tanh, it * STEPS + k + 1)
                    nc.vector.scalar_tensor_tensor(prod[:, :, :], gates[:, 0:2, :], 1.0, gates[:, 3:5, :], ALU.add, ALU.mult)
                    dve.drain()
                    nc.vector.scalar_tensor_tensor(gates[:, 4, :], prod[:, 1, :], 0.5, prod[:, 0, :],
                                                   ALU.mult, ALU.add).then_inc(cell_new, 1)
                    dve.wait_ge(cell_tanh, it * STEPS + k + 1)
                    nc.vector.scalar_tensor_tensor(hid[k % 2][0:LSTM_H, :], gates[:, 2, :], 1.0, tanh_c[:, :],
                                                   ALU.add, ALU.mult).then_inc(hid_new, 1)

            turn(0)
            mean_dve(dve)
            with dve.Fori(1, TOK // STEPS) as it:
                turn(it)
            dve.wait_ge(musig_kept, TOK // STEPS)
            z = ms_all[:, :, :]
            nc.vector.tensor_tensor(z, z, R[0:BATCH, ROWS("mu_b")].unsqueeze(1).broadcast_to([BATCH, TOK, 4]), ALU.add)
            dve.drain()
            zc = z.rearrange("p t n -> p n t")
            nc.vector.tensor_copy(scan_t[:, 3, :], zc[:, 3, :]).then_inc(scan_out, 1)
            nc.vector.tensor_scalar(scan_t[:, 0:3, :], zc[:, 0:3, :], 0.0, None, ALU.max)
            dve.drain()
            nc.vector.tensor_tensor(scan_t[:, 2, :], scan_t[:, 2, :], cst("step")[0:BATCH, :], ALU.mult)
            dve.drain()
            nc.vector.scalar_tensor_tensor(scan_t[:, 1, :], scan_t[:, 1, :], 1.0 / TOK, scan_t[:, 2, :], ALU.mult, ALU.add)
            dve.drain()
            nc.vector.tensor_tensor_scan(scan_t[:, 4, :], scan_t[:, 0, :], scan_t[:, 1, :], 0.0, ALU.mult, ALU.add)
            dve.drain()
            nc.vector.tensor_scalar(scan_t[:, 4, :], scan_t[:, 4, :], -1.0, None, ALU.mult)
            dve.wait_ge(scan_exp, 1)
            nc.vector.tensor_scalar(scan_t[:, 5, :], scan_t[:, 3, :], 1.0, None, ALU.add)
            dve.drain()
            dve.sem_inc(scan_out, 1)
            dve.wait_ge(scan_ps, 1)
            nc.vector.tensor_copy(mu_cols[:, 0:2, :], ps[0][1][:, 0:32].rearrange("p (a b) -> p a b", a=2))
            dve.drain()
            nc.vector.scalar_tensor_tensor(mu_cols[:, 1, :], mu_cols[:, 1, :], -0.5, mu_cols[:, 1, :], ALU.mult, ALU.mult)
            dve.drain()
            dve.sem_inc(scan_cols, 1)

        def pos_pool(pool):
            pool.wait_ge(scan_cols, 1)
            with pool.Fori(0, PAIRS) as i:
                stage_x(pool, S_LSTM, ATT, None, i)
                for s in range(2):
                    rstd(pool, mid_var, mid_rstd, mid_run[S_LSTM], i, s, ATT)
                for s in range(2):
                    rstd(pool, var_ok, rstd_ok, tail_run[S_LSTM], i, s, ATT)

        def pos_act(act):
            with act.Fori(0, PAIRS) as i:
                for s in range(2):
                    act.wait_ge(staged, nth(S_LSTM, i, s))
                    b = i * 2 + s
                    nc.scalar.activation(v_(s, ATT, "P", 0, 128), cst("rel"), ACT.Square,
                                         bias=mu_cols[:, 0, bass.ds(b, 1)])
                    act.drain()
                    nc.scalar.activation(v_(s, ATT, "P", 0, 128), v_(s, ATT, "P", 0, 128), ACT.Exp,
                                         scale=mu_cols[:, 1, bass.ds(b, 1)]).then_inc(pos_w, 1)
                for s in range(2):
                    act.wait_ge(pos_masked, nth(0, i, s))
                    nc.scalar.activation(v_(s, ATT, "P", 256, 128), v_(s, ATT, "P", 128, 128), ACT.Square,
                                         accum_out=v_(s, ATT, "m2", 0, 1)).then_inc(pos_sq, 1)
                for s in range(2):
                    act.wait_ge(pos_T, nth(0, i, s))
                    nc.scalar.copy(v_(s, ATT, "PT", 0, 128), ps[s][0][:, 0:128]).then_inc(pos_T_sb, 1)

        def pos_pe(pe):
            with pe.Fori(0, PAIRS) as i:
                for s in range(2):
                    pe.wait_ge(pos_masked, nth(0, i, s))
                    nc.tensor.transpose(ps[s][0][:, 0:128], v_(s, ATT, "P", 128, 128), ident).then_inc(pos_T, 1)
                for s in range(2):
                    pe.wait_ge(pos_T_sb, nth(0, i, s))
                    nc.tensor.matmul(ps[s][1][:, 0:128], v_(s, ATT, "PT", 0, 128), v_(s, ATT, "x"),
                                     start=True, stop=True).then_inc(y_ps, 1)

        def pos_dve(dve):
            with dve.Fori(0, PAIRS) as i:
                for s in range(2):
                    dve.wait_ge(pos_w, nth(0, i, s))
                    nc.vector.tensor_tensor(v_(s, ATT, "P", 128, 128), v_(s, ATT, "P", 0, 128), cst("tri"),
                                            ALU.mult).then_inc(pos_masked, 1)
                for s in range(2):
                    dve.wait_ge(pos_sq, nth(0, i, s))
                    nc.vector.tensor_scalar(v_(s, ATT, "mv", 1, 1), v_(s, ATT, "m2", 0, 1), 1e-24, None,
                                            ALU.max).then_inc(mid_var, 1)
                for s in range(2):
                    dve.wait_ge(mid_rstd, nth(mid_run[S_LSTM], i, s))
                    dve.wait_ge(y_ps, nth(tail_run[S_LSTM], i, s))
                    nc.vector.scalar_tensor_tensor(v_(s, ATT, "r"), ps[s][1][:, 0:128], v_(s, ATT, "rstd"),
                                                   v_(s, ATT, "x"), ALU.mult, ALU.add)
                    dve.drain()
                    stats(dve, s, ATT, v_(s, ATT, "r")).then_inc(var_ok, 1)
                for s in range(2):
                    tail_norm(dve, tail_run[S_LSTM], i, s, ATT)

        all_done = 2 + BATCH

        def sim_pool_(pool):
            nc.gpsimd.memset(xT_all[:, :, :], 0.0).then_inc(sim_pool, 1)
            with pool.Fori(0, PAIRS) as i:
                stage_x(pool, S_SIM, ATT, None, i)
            pool.wait_ge(seq_done, all_done + BATCH * S_SIM)
            n2 = sim_all[:, 0, :, :]
            nc.gpsimd.tensor_tensor(n2, n2, cst("minushalf").unsqueeze(1).broadcast_to([128, BATCH, HEADS]),
                                    ALU.pow).then_inc(sim_pool, 1)
            pool.wait_ge(rows_in, 64)

        def sim_sp(sp):
            sp.wait_ge(sim_mid, 5)
            sp.wait_ge(sim_pool, 1)
            for side in range(2):
                for r in range(2):
                    q = 32 * side + 16 * r
                    sp.dma_start(pos_rows[r:r + 1, side, :, :], pos64T[q:q + 16, :]).then_inc(rows_in, 16)

        def sim_pe(pe):
            with pe.Fori(0, PAIRS) as i:
                for s in range(2):
                    transpose_x(pe, S_SIM, i, s, ATT)
                for s in range(2):
                    pe.wait_ge(xT_sb, nth(xt_run[S_SIM], i, s))
                    nc.tensor.matmul(ps[s][1][:, 0:128], v_(s, ATT, "xcT", 0, 128), WA[:, W_EARLY("reg", 0, 128)],
                                     start=True, stop=True).then_inc(sim_q, 1)
            pe.wait_ge(sim_mid, 1)
            nc.tensor.transpose(ps[0][0][0:16, 0:128], small[:, 48:64], ident).then_inc(sim_rows, 1)
            pe.wait_ge(sim_mid, 2)
            nc.tensor.transpose(ps[0][1][0:2, 0:16], small[0:16, 64:66], ident[0:16, 0:16]).then_inc(sim_rows, 1)
            pe.wait_ge(sim_mid, 3)
            nc.tensor.matmul(ps[0][2][:, 0:2], ones_f[0:2, :], small[0:2, 68:70], start=True, stop=True).then_inc(sim_rows, 1)
            pe.wait_ge(sim_mid, 4)
            nc.tensor.transpose(ps[0][3][0:64, 0:128], pos64[:, :, :].rearrange("p a b -> p (a b)"), ident).then_inc(sim_rows, 1)
            pe.wait_ge(rows_in, 64)

        def sim_act(act):
            with act.Fori(0, PAIRS) as i:
                for s in range(2):
                    act.wait_ge(xT_ps, nth(xt_run[S_SIM], i, s))
                    nc.scalar.copy(v_(s, ATT, "xcT", 0, 128), ps[s][0][:, 0:128]).then_inc(xT_sb, 1)
                for s in range(2):
                    act.wait_ge(sim_q, nth(0, i, s))
                    nc.scalar.copy(v_(s, ATT, "wide", 0, 128), ps[s][1][:, 0:128])
                    nc.scalar.activation(v_(s, ATT, "wide", 128, 128), ps[s][1][:, 0:128], ACT.Square)
                    act.drain()
                    act.sem_inc(sim_sb, 1)

        def sim_dve(dve):
            dve.wait_ge(w_tern, 1)
            g3 = R[:, ROWS("g_query")].rearrange("p (h d) -> p h d", d=HD)
            nc.vector.tensor_tensor(g3, g3, small[:, 32:48].unsqueeze(2).broadcast_to([128, HEADS, HD]), ALU.mult)
            dve.drain()
            with dve.Fori(0, PAIRS) as i:
                for s in range(2):
                    dve.wait_ge(sim_sb, nth(0, i, s))
                    b = i * 2 + s
                    q, sq = v_(s, ATT, "wide", 0, 128), v_(s, ATT, "wide", 128, 128)
                    nc.vector.tensor_reduce(sim_all[:, 0, bass.ds(b, 1), :].rearrange("p a h -> p (a h)"),
                                            sq.rearrange("p (h d) -> p h d", d=HD), AXX, ALU.add)
                    nc.vector.tensor_tensor(v_(s, ATT, "r"), q, R[:, ROWS("g_query")], ALU.mult)
                    dve.drain()
                    nc.vector.tensor_reduce(sim_all[:, 1, bass.ds(b, 1), :].rearrange("p a h -> p (a h)"),
                                            v_(s, ATT, "r").rearrange("p (h d) -> p h d", d=HD), AXX,
                                            ALU.add).then_inc(seq_done, 1)
            dve.wait_ge(sim_pool, 2)
            n2, dot = sim_all[:, 0, :, :], sim_all[:, 1, :, :]
            sim = small[:, 48:64]
            nc.vector.tensor_tensor(dot, dot, n2, ALU.mult)
            dve.drain()
            nc.vector.tensor_reduce(sim, dot, AXX, ALU.add)
            dve.drain()
            nc.vector.tensor_scalar(sim, sim, 1.0 / HEADS, None, ALU.mult).then_inc(sim_mid, 1)
            dve.wait_ge(sim_rows, 1)
            nc.vector.tensor_reduce(small[0:16, 64:65], ps[0][0][0:16, REG:TOK], AXX, ALU.max)
            nc.vector.tensor_reduce(small[0:16, 65:66], ps[0][0][0:16, REG:TOK], AXX, ALU.min)
            dve.drain()
            nc.vector.tensor_scalar(small[0:16, 65:66], small[0:16, 65:66], -1.0, None, ALU.mult).then_inc(sim_mid, 1)
            dve.wait_ge(sim_rows, 2)
            nc.vector.tensor_reduce(small[0:2, 67:68], ps[0][1][0:2, 0:16], AXX, ALU.max)
            dve.drain()
            nc.vector.tensor_scalar(small[0:2, 68:70], ident[0:2, 0:2], small[0:2, 67:68], None, ALU.mult).then_inc(sim_mid, 1)
            dve.wait_ge(sim_rows, 3)
            nc.vector.tensor_copy(small[:, 70:72], ps[0][2][:, 0:2])
            dve.drain()
            nc.vector.tensor_tensor(small[:, 72:73], small[:, 70:71], small[:, 71:72], ALU.add)
            dve.drain()
            nc.vector.reciprocal(small[:, 73:74], small[:, 72:73])
            dve.drain()
            nc.vector.tensor_scalar(sim, sim, small[:, 71:72], small[:, 73:74], ALU.add, ALU.mult)
            dve.drain()
            pos = small[:, 80:96]
            nc.vector.tensor_scalar(pos, sim, 0.9, None, ALU.is_gt)
            dve.drain()
            notreg = cst("notreg")
            nc.vector.tensor_scalar(pos64[:, 3, :], pos, notreg, BIG, ALU.mult, ALU.mult)
            nc.vector.tensor_scalar(pos64[:, 2, :], pos, -1.0, 1.0, ALU.mult, ALU.add)
            nc.vector.tensor_scalar(pos64[:, 0, :], pos, -1.0, notreg, ALU.add, ALU.mult)
            dve.drain()
            nc.vector.tensor_scalar(pos64[:, 2, :], pos64[:, 2, :], notreg, BIG, ALU.mult, ALU.mult)
            nc.vector.tensor_scalar(pos64[:, 1, :], pos64[:, 0, :], -1.0, None, ALU.mult)
            nc.vector.tensor_scalar(small[:, 96:112], pos64[:, 0, :], 1.0, None, ALU.add)
            dve.drain()
            nc.vector.tensor_copy(pos64[:, 0, :], small[:, 96:112])
            dve.drain()
            dve.sem_inc(sim_mid, 1)
            dve.wait_ge(sim_rows, 4)
            nc.vector.tensor_copy(pos64T[:, :], ps[0][3][0:64, 0:128]).then_inc(sim_mid, 1)

        WSCALE = 1.0 / math.sqrt(DIM)

        def wide_pool(pool):
            with pool.Fori(0, PAIRS) as i:
                stage_x(pool, S_X1, ATT, ctxT_all, i)
                for s in range(2):
                    rstd(pool, var_ok, rstd_ok, tail_run[S_X1], i, s, ATT)

        def wide_pe(pe):
            ones3 = ones_b[0:3, :]
            with pe.Fori(0, PAIRS) as i:
                for s in range(2):
                    transpose_x(pe, S_X1, i, s, ATT)
                for s in range(2):
                    pe.wait_ge(xT_sb, nth(xt_run[S_X1], i, s))
                    xT, cT, bank = v_(s, ATT, "xcT"), v_(s, ATT, "c"), ps[s][1]
                    for k, src in ((0, xT), (1, cT)):
                        nc.tensor.matmul(bank[:, 128 * k:128 * k + 128], WA[:, W_EARLY("x1", 128 * k, 128)], src,
                                         start=True, stop=False, skip_group_check=True)
                        nc.tensor.matmul(bank[:, 128 * k:128 * k + 128], bias3[:, BIAS("x1", 128 * k, 128)], ones3,
                                         start=False, stop=True, skip_group_check=True)
                    nc.tensor.matmul(bank[:, 256:384], cT, WA[:, W_EARLY("x1", 256, 128)], start=True, stop=False,
                                     skip_group_check=True)
                    add_bias(bank[:, 256:384], "x1", 256, 128).then_inc(w_qk, 1)
                for s in range(2):
                    pe.wait_ge(w_qk_sb, nth(0, i, s))
                    bank = ps[s][2][:, 0:128]
                    nc.tensor.matmul(bank, v_(s, ATT, "wide", 0, 128), v_(s, ATT, "wide", 128, 128), start=True,
                                     stop=False, skip_group_check=True)
                    nc.tensor.matmul(bank, ones_b[0:1, :], mrow[:, bass.ds(i * 2 + s, 1), :].rearrange("p a k -> p (a k)"),
                                     start=False, stop=True, skip_group_check=True).then_inc(w_s, 1)
                for s in range(2):
                    pe.wait_ge(w_e, nth(0, i, s))
                    nc.tensor.transpose(ps[s][3][:, 0:128], v_(s, ATT, "P", 0, 128), ident).then_inc(w_T, 1)
                for s in range(2):
                    pe.wait_ge(w_Tsb, nth(0, i, s))
                    nc.tensor.matmul(ps[s][0][:, 0:128], v_(s, ATT, "PT", 0, 128), v_(s, ATT, "wide", 256, 128),
                                     start=True, stop=True).then_inc(y_ps, 1)

        def wide_act(act):
            with act.Fori(0, PAIRS) as i:
                for s in range(2):
                    act.wait_ge(xT_ps, nth(xt_run[S_X1], i, s))
                    nc.scalar.copy(v_(s, ATT, "xcT", 0, 128), ps[s][0][:, 0:128]).then_inc(xT_sb, 1)
                for s in range(2):
                    act.wait_ge(w_qk, nth(0, i, s))
                    nc.scalar.copy(v_(s, ATT, "wide", 0, 384), ps[s][1][:, 0:384]).then_inc(w_qk_sb, 1)
                for s in range(2):
                    act.wait_ge(w_m, nth(0, i, s))
                    nc.scalar.activation(v_(s, ATT, "P", 0, 128), ps[s][2][:, 0:128], ACT.Exp, scale=WSCALE,
                                         bias=v_(s, ATT, "m2", 0, 1), accum_out=v_(s, ATT, "m2", 1, 1)).then_inc(w_e, 1)
                for s in range(2):
                    act.wait_ge(w_T, nth(0, i, s))
                    nc.scalar.copy(v_(s, ATT, "PT", 0, 128), ps[s][3][:, 0:128]).then_inc(w_Tsb, 1)

        def wide_dve(dve):
            with dve.Fori(0, PAIRS) as i:
                for s in range(2):
                    dve.wait_ge(w_s, nth(0, i, s))
                    nc.vector.tensor_reduce(v_(s, ATT, "m2", 2, 1), ps[s][2][:, 0:128], AXX, ALU.max)
                    dve.drain()
                    nc.vector.tensor_scalar(v_(s, ATT, "m2", 0, 1), v_(s, ATT, "m2", 2, 1), -WSCALE, None,
                                            ALU.mult).then_inc(w_m, 1)
                for s in range(2):
                    dve.wait_ge(w_e, nth(0, i, s))
                    nc.vector.reciprocal(v_(s, ATT, "m2", 3, 1), v_(s, ATT, "m2", 1, 1))
                    dve.drain()
                    dve.wait_ge(y_ps, nth(tail_run[S_X1], i, s))
                    nc.vector.scalar_tensor_tensor(v_(s, ATT, "r"), ps[s][0][:, 0:128], v_(s, ATT, "m2", 3, 1),
                                                   v_(s, ATT, "x"), ALU.mult, ALU.add)
                    dve.drain()
                    stats(dve, s, ATT, v_(s, ATT, "r")).then_inc(var_ok, 1)
                for s in range(2):
                    tail_norm(dve, tail_run[S_X1], i, s, ATT)

        ff_run = {S_FF1: 0, S_FF2: 1}
        ff_v1, ff_r1 = sem("ff_v1"), sem("ff_r1")

        def ff_pool(pool, sub):
            with pool.Fori(0, PAIRS) as i:
                stage_x(pool, sub, FFN, None, i)
                for s in range(2):
                    rstd(pool, ff_v1, ff_r1, ff_run[sub], i, s, FFN)
                for s in range(2):
                    rstd(pool, mid_var, mid_rstd, mid_run[sub], i, s, FFN)
                for s in range(2):
                    rstd(pool, var_ok, rstd_ok, tail_run[sub], i, s, FFN)

        def ff_pe(pe, sub):
            quant, f = sub == S_FF2, ff_run[sub]
            with pe.Fori(0, PAIRS) as i:
                for s in range(2):
                    pe.wait_ge(h_sb, nth(f, i, s))
                    nc.tensor.transpose(ps[s][0][:, 0:128], v_(s, FFN, "h"), ident).then_inc(hT_ps, 1)
                for s in range(2):
                    pe.wait_ge(hT_sb, nth(f, i, s))
                    if quant:
                        nc.tensor.matmul(ps[s][1][:, :], v_(s, FFN, "hbT").bitcast(BF16), tern_up[:, :],
                                         start=True, stop=True).then_inc(up_ps, 1)
                    else:
                        nc.tensor.matmul(ps[s][1][:, :], v_(s, FFN, "hT"), WA[:, W_EARLY("ff1_up")],
                                         start=True, stop=False, skip_group_check=True)
                        add_bias(ps[s][1][:, :], "ff1_up").then_inc(up_ps, 1)
                for s in range(2):
                    pe.wait_ge(n_sb, nth(f, i, s))
                    for t in range(4):
                        mm = nc.tensor.transpose(ps[s][2][:, 128 * t:128 * t + 128], v_(s, FFN, "n", 128 * t, 128), ident)
                    mm.then_inc(nT_ps, 1)
                for s in range(2):
                    pe.wait_ge(nT_sb, nth(f, i, s))
                    y = ps[s][3][:, 0:128]
                    nbT = v_(s, FFN, "nbT").bitcast(BF16)
                    for t in range(4):
                        if quant:
                            mm = nc.tensor.matmul(y, nbT[:, 128 * t:128 * t + 128], tern_down[:, t, :],
                                                  start=t == 0, stop=t == 3, skip_group_check=True)
                        else:
                            nc.tensor.matmul(y, v_(s, FFN, "nT", 128 * t, 128), WA[:, W_EARLY("ff1_down", 128 * t, 128)],
                                             start=t == 0, stop=False, skip_group_check=True)
                    if not quant:
                        mm = add_bias(y, "ff1_down")
                    mm.then_inc(y_ps, 1)

        def ff_act(act, sub):
            quant, f = sub == S_FF2, ff_run[sub]
            with act.Fori(0, PAIRS) as i:
                for s in range(2):
                    act.wait_ge(hT_ps, nth(f, i, s))
                    dst = v_(s, FFN, "hbT").bitcast(BF16) if quant else v_(s, FFN, "hT")
                    nc.scalar.copy(dst, ps[s][0][:, 0:128]).then_inc(hT_sb, 1)
                for s in range(2):
                    if quant:
                        act.wait_ge(up_in, nth(0, i, s))
                        nc.scalar.activation(v_(s, FFN, "u"), v_(s, FFN, "u"), ACT.Gelu).then_inc(up_act, 1)
                    else:
                        act.wait_ge(up_ps, nth(f, i, s))
                        nc.scalar.activation(v_(s, FFN, "u"), ps[s][1][:, :], ACT.Gelu).then_inc(up_act, 1)
                for s in range(2):
                    act.wait_ge(nT_ps, nth(f, i, s))
                    dst = v_(s, FFN, "nbT").bitcast(BF16) if quant else v_(s, FFN, "nT")
                    nc.scalar.copy(dst, ps[s][2][:, :]).then_inc(nT_sb, 1)

        def affine(dve, dst, gamma, beta):
            nc.vector.tensor_tensor(dst, dst, R[:, ROWS(gamma)], ALU.mult)
            dve.drain()
            return nc.vector.tensor_tensor(dst, dst, R[:, ROWS(beta)], ALU.add)

        def quantize(dve, s, dst, at):
            top, scale, undo = (v_(s, FFN, "a", at + k, 1) for k in range(3))
            nc.vector.tensor_reduce(top, dst, AXX, ALU.max, apply_absolute_value=True)
            dve.drain()
            nc.vector.tensor_scalar(top, top, 1e-5, None, ALU.max)
            dve.drain()
            nc.vector.reciprocal(scale, top)
            dve.drain()
            nc.vector.tensor_scalar(scale, scale, 127.0, None, ALU.mult)
            dve.drain()
            nc.vector.reciprocal(undo, scale)
            nc.vector.tensor_scalar(dst, dst, scale, ROUND, ALU.mult, ALU.add)
            dve.drain()
            nc.vector.tensor_scalar(dst, dst, -ROUND, 127.0, ALU.add, ALU.min)
            dve.drain()
            return nc.vector.tensor_scalar(dst, dst, -128.0, None, ALU.max)

        def ff_dve(dve, sub):
            quant, f = sub == S_FF2, ff_run[sub]
            pre = "ff2_" if quant else "ff1_"
            with dve.Fori(0, PAIRS) as i:
                for s in range(2):
                    dve.wait_ge(staged, nth(sub, i, s))
                    stats(dve, s, FFN, v_(s, FFN, "x")).then_inc(ff_v1, 1)
                for s in range(2):
                    dve.wait_ge(ff_r1, nth(f, i, s))
                    h = v_(s, FFN, "h")
                    norm(dve, s, FFN, h, v_(s, FFN, "x"))
                    dve.drain()
                    ins = affine(dve, h, pre + "g1", pre + "b1")
                    if quant:
                        dve.drain()
                        ins = quantize(dve, s, h, 0)
                    ins.then_inc(h_sb, 1)
                if quant:
                    for s in range(2):
                        dve.wait_ge(up_ps, nth(f, i, s))
                        a = v_(s, FFN, "a", 6, 1)
                        nc.vector.tensor_tensor(a, v_(s, FFN, "a", 2, 1), small[:, 14:15], ALU.mult)
                        dve.drain()
                        nc.vector.scalar_tensor_tensor(v_(s, FFN, "u"), ps[s][1][:, :], a, R[:, ROWS("ff2_up")],
                                                       ALU.mult, ALU.add).then_inc(up_in, 1)
                for s in range(2):
                    dve.wait_ge(up_act, nth(f, i, s))
                    stats(dve, s, FFN, v_(s, FFN, "u")).then_inc(mid_var, 1)
                for s in range(2):
                    dve.wait_ge(mid_rstd, nth(mid_run[sub], i, s))
                    n = v_(s, FFN, "n")
                    norm(dve, s, FFN, n, v_(s, FFN, "u"))
                    dve.drain()
                    ins = affine(dve, n, pre + "g2", pre + "b2")
                    if quant:
                        dve.drain()
                        ins = quantize(dve, s, n, 3)
                    ins.then_inc(n_sb, 1)
                for s in range(2):
                    if quant:
                        dve.wait_ge(y_ps, nth(tail_run[sub], i, s))
                        a, r = v_(s, FFN, "a", 6, 1), v_(s, FFN, "r")
                        nc.vector.tensor_tensor(a, v_(s, FFN, "a", 5, 1), small[:, 15:16], ALU.mult)
                        dve.drain()
                        nc.vector.scalar_tensor_tensor(r, ps[s][3][:, 0:128], a, R[:, ROWS("ff2_down")], ALU.mult, ALU.add)
                        dve.drain()
                        nc.vector.tensor_tensor(r, r, v_(s, FFN, "x"), ALU.add)
                        dve.drain()
                        stats(dve, s, FFN, r).then_inc(var_ok, 1)
                    else:
                        tail_stats(dve, tail_run[sub], i, s, FFN, ps[s][3][:, 0:128])
                for s in range(2):
                    tail_norm(dve, tail_run[sub], i, s, FFN)

        def mlp_pool(pool):
            with pool.Fori(0, PAIRS) as i:
                stage_x(pool, S_MLP, MLP, None, i)

        def mlp_pe(pe):
            with pe.Fori(0, PAIRS) as i:
                for s in range(2):
                    transpose_x(pe, S_MLP, i, s, MLP)
                for s in range(2):
                    pe.wait_ge(xT_sb, nth(xt_run[S_MLP], i, s))
                    for m in range(3):
                        for t in range(4):
                            o = ps[s][1 + m][:, 128 * t:128 * t + 128]
                            nc.tensor.matmul(o, WA[:, W_EARLY("mlp_up", FF * m + 128 * t, 128)], v_(s, MLP, "xT"),
                                             start=True, stop=False, skip_group_check=True)
                            mm = nc.tensor.matmul(o, bias3[:, BIAS("mlp_up", FF * m + 128 * t, 128)], ones_b[0:3, :],
                                                  start=False, stop=True, skip_group_check=True)
                        mm.then_inc(mlp_ps, 1)
                for s in range(2):
                    for m in range(3):
                        pe.wait_ge(mlp_act, nth(0, i, s, 3, m + 1))
                        o = ps[s][0][:, 128 * m:128 * m + 128]
                        for t in range(4):
                            g, w = v_(s, MLP, "G", FF * m + 128 * t, 128), WA[:, W_EARLY("mlp_down", FF * m + 128 * t, 128)]
                            l, r = (w, g) if m < 2 else (g, w)
                            nc.tensor.matmul(o, l, r, start=t == 0, stop=False, skip_group_check=True)
                        if m < 2:
                            mm = nc.tensor.matmul(o, bias3[:, BIAS("mlp_down", 128 * m, 128)], ones_b[0:3, :],
                                                  start=False, stop=True, skip_group_check=True)
                        else:
                            mm = add_bias(o, "mlp_down", 256, 128)
                    mm.then_inc(mlp_out, 1)

        def mlp_act_(act):
            with act.Fori(0, PAIRS) as i:
                for s in range(2):
                    act.wait_ge(xT_ps, nth(xt_run[S_MLP], i, s))
                    nc.scalar.copy(v_(s, MLP, "xT"), ps[s][0][:, 0:128]).then_inc(xT_sb, 1)
                for s in range(2):
                    for m in range(3):
                        act.wait_ge(mlp_ps, nth(0, i, s, 3, m + 1))
                        nc.scalar.activation(v_(s, MLP, "G", FF * m, FF), ps[s][1 + m][:, :], ACT.Gelu).then_inc(mlp_act, 1)

        def mlp_dve(dve):
            with dve.Fori(0, PAIRS) as i:
                for s in range(2):
                    dve.wait_ge(mlp_out, nth(0, i, s))
                    nc.vector.tensor_copy(arena[s][:, bass.ds(i * 384 + QKV_KEPT, 384)], ps[s][0][:, 0:384]).then_inc(seq_done, 1)

        XSCALE = 1.0 / math.sqrt(XD)
        HALVES, HH = 2, XH // 2

        def lat_pool(pool):
            pool.wait_ge(seq_done, all_done + BATCH * S_MQA)
            pool.wait_ge(late_in, 32)
            for s in range(2):
                nc.gpsimd.memset(v_(s, LAT, "qT"), 0.0)
            pool.drain()

            def stage(i, d):
                for s in range(2):
                    if d == 0:
                        pool.wait_ge(seq_done, nth(S_LAT, i, s))
                    else:
                        pool.wait_ge(h_sb, nth(2, i, s))
                    nc.gpsimd.tensor_copy(v_(s, LAT, "c"), x_at(ctx_all, i, s + d))
                    nc.gpsimd.tensor_copy(v_(s, LAT, "x"), x_at(x_all, i, s + d))
                    pool.drain()
                    pool.sem_inc(staged, 1)

            def norms(i, d):
                for s in range(2):
                    rstd(pool, mid_var, mid_rstd, mid_run[S_LAT], i, s, LAT, 2, d)

            def front(i, d):
                stage(i, d)
                norms(i, d)

            def body(i, ahead):
                if ahead:
                    stage(i, 2)
                if ahead:
                    norms(i, 2)
                for s in range(2):
                    rstd(pool, var_ok, rstd_ok, tail_run[S_LAT], i, s, LAT)

            pairs(pool, front, body)

        def lat_pe(pe):
            def project_q(s, hf):
                for t in range(4):
                    mm = nc.tensor.matmul(ps[s][hf][:, 128 * t:128 * t + 128],
                                          WA[:, W_LATE("lat_q", 512 * hf + 128 * t, 128)],
                                          v_(s, LAT, "nT", 128, 128), start=True, stop=True,
                                          skip_group_check=True)
                mm.then_inc(l_q, 1)

            pe.wait_ge(late_in, 32)

            def front(i, d):
                for s in range(2):
                    pe.wait_ge(h_sb, nth(2, i, s + d))
                    for k in range(2):
                        mm = nc.tensor.transpose(ps[s][3][:, 128 * k:128 * k + 128], v_(s, LAT, "n", 128 * k, 128), ident)
                    mm.then_inc(xT_ps, 1)

            def body(i, ahead):
                for s in range(2):
                    pe.wait_ge(xT_sb, nth(xt_run[S_LAT], i, s))
                    nT = v_(s, LAT, "nT")
                    project_q(s, 0)
                    for t in range(8):
                        if t == 4:
                            pe.wait_ge(l_qsb, i * 4 + (s + 1))
                            pe.wait_ge(var_ok, nth(tail_run[S_LAT], i, s - 2))
                        mm = nc.tensor.matmul(ps[s][(2 + t // 2) % 4][:, 256 * (t % 2):256 * (t % 2) + 256],
                                              WA[:, W_LATE("lat_k", 128 * t, 128)], nT, start=True, stop=True,
                                              skip_group_check=True)
                        if t % 4 == 3:
                            mm.then_inc(l_k, 1)
                for s in range(2):
                    nT = v_(s, LAT, "nT")
                    for k in range(2):
                        pe.wait_ge(l_ksb, nth(0, i, s, 2, k + 1))
                        for c in range(2):
                            mm = nc.tensor.matmul(ps[s][(2 + 2 * k + c) % 4][:, :], nT[:, 128 * k:128 * k + 128],
                                                  WA[:, W_LATE("lat_v", 512 * c, 512)], start=True, stop=True)
                        mm.then_inc(l_v, 1)

                def scores(hf, s):
                    if hf == 0:
                        pe.wait_ge(l_vsb, nth(0, i, s, 2, 2))
                    else:
                        pe.wait_ge(l_osb, i * 4 + (s + 1))
                        pe.wait_ge(l_qsb, i * 4 + (2 + s + 1))
                    kT = v_(s, LAT, "kT").rearrange("p (t k) -> p t k", t=8)
                    for h in range(HH):
                        mm = nc.tensor.matmul(ps[s][h // 2][:, 256 * (h % 2):256 * (h % 2) + 256],
                                              v_(s, LAT, "qT", 128 * h, 128), kT[:, 4 * hf + h // 2, :],
                                              start=True, stop=True, skip_group_check=True)
                        if h % 2 == 1:
                            mm.then_inc(l_s, 1)

                def values(hf, s):
                    P = v_(s, LAT, "P").rearrange("p (n k) -> p n k", k=128)
                    for t in range(4):
                        pe.wait_ge(l_sub, i * 16 + (8 * hf + 4 * s + t + 1))
                        for c in range(4):
                            mm = nc.tensor.transpose(ps[s][t][:, 128 * c:128 * c + 128], P[:, 4 * t + c, :], ident)
                        mm.then_inc(l_T, 1)
                    PT = v_(s, LAT, "PT").rearrange("p (h c q) -> p h c q", h=HH, c=2)
                    V = v_(s, LAT, "V").rearrange("p (c h d) -> p c h d", c=2, h=XH)
                    for h in range(HH):
                        if h % 2 == 0:
                            pe.wait_ge(l_Tsb, i * 16 + (8 * hf + 4 * s + h // 2 + 1))
                        if h == 2 and hf == 0:
                            project_q(s, 1)
                        o = ps[s][0][XD * (h % 2):XD * (h % 2) + XD, 128 * (h // 2):128 * (h // 2) + 128]
                        for c in range(2):
                            mm = nc.tensor.matmul(o, V[:, c, HH * hf + h, 0:XD], PT[:, h, c, :],
                                                  start=c == 0, stop=c == 1, skip_group_check=True)
                    mm.then_inc(l_o, 1)

                scores(0, 0)
                scores(0, 1)
                values(0, 0)
                scores(1, 0)
                values(0, 1)
                scores(1, 1)
                values(1, 0)
                values(1, 1)
                if ahead:
                    front(i, 2)
                for s in range(2):
                    pe.wait_ge(l_osb, i * 4 + (2 + s + 1))
                    OT = v_(s, LAT, "O")
                    for t in range(8):
                        mm = nc.tensor.matmul(ps[s][1][:, 0:128], OT[:, 128 * t:128 * t + 128],
                                              WA[:, W_LATE("lat_out", 128 * t, 128)], start=t == 0, stop=t == 7,
                                              skip_group_check=True)
                    mm.then_inc(y_ps, 1)

            pairs(pe, front, body)

        OUT_AT = 2

        def lat_act(act):
            def spread_q(i, s, hf):
                act.wait_ge(l_q, i * 4 + (2 * hf + s + 1))
                q = v_(s, LAT, "qT").rearrange("p (t j q) -> p t j q", t=4, j=2)
                for j in range(2):
                    rows = slice(XD * j, XD * j + XD)
                    nc.scalar.copy(q[rows, :, j, :], heads(ps[s][hf][rows, :]))
                act.drain()
                act.sem_inc(l_qsb, 1)

            def front(i, d):
                for s in range(2):
                    act.wait_ge(xT_ps, nth(xt_run[S_LAT], i, s + d))
                    nc.scalar.copy(v_(s, LAT, "nT"), ps[s][3][:, 0:256]).then_inc(xT_sb, 1)

            def body(i, ahead):
                for s in range(2):
                    spread_q(i, s, 0)
                for s in range(2):
                    V = v_(s, LAT, "V").rearrange("p (c h d) -> p c h d", c=2, h=XH)
                    for k in range(2):
                        act.wait_ge(l_v, nth(0, i, s, 2, k + 1))
                        for c in range(2):
                            nc.scalar.copy(V[:, k, 8 * c:8 * c + 8, 0:XD],
                                           ps[s][(2 + 2 * k + c) % 4][:, :].rearrange("p (h d) -> p h d", d=XD))
                        act.drain()
                        act.sem_inc(l_vsb, 1)

                def exps(hf, s, of, to):
                    for t in range(of, to):
                        act.wait_ge(l_exp, i * 16 + (8 * hf + 4 * s + t + 1))
                        for j in range(2):
                            h = 2 * t + j
                            nc.scalar.activation(v_(s, LAT, "P", 256 * h, 256), ps[s][t][:, 256 * j:256 * j + 256],
                                                 ACT.Exp, scale=XSCALE, bias=v_(s, LAT, "m", h, 1),
                                                 accum_out=v_(s, LAT, "rec", h, 1))
                        act.drain()
                        act.sem_inc(l_osum, 1)

                def weights(hf, s):
                    for t in range(4):
                        act.wait_ge(l_T, i * 16 + (8 * hf + 4 * s + t + 1))
                        nc.scalar.copy(v_(s, LAT, "PT", 512 * t, 512), ps[s][t][:, :]).then_inc(l_Tsb, 1)
                    if hf == 0:
                        spread_q(i, s, 1)

                def output(hf, s):
                    act.wait_ge(l_o, i * 4 + (2 * hf + s + 1))
                    nc.scalar.copy(v_(s, LAT, "O", 512 * hf, 512), ps[s][0][:, :]).then_inc(l_osb, 1)

                before = None
                for now in ((0, 0), (0, 1), (1, 0), (1, 1)):
                    exps(*now, 0, OUT_AT)
                    if before:
                        output(*before)
                    exps(*now, OUT_AT, 4)
                    weights(*now)
                    before = now
                output(*before)
                if ahead:
                    front(i, 2)

            pairs(act, front, body)

        def lat_dve(dve):
            def moments(i, d):
                for s in range(2):
                    dve.wait_ge(staged, nth(S_LAT, i, s + d))
                    stats(dve, s, LAT, v_(s, LAT, "c"))
                    dve.drain()
                    stats(dve, s, LAT, v_(s, LAT, "x"), at=2).then_inc(mid_var, 1)

            def norms(i, d):
                for s in range(2):
                    dve.wait_ge(mid_rstd, nth(mid_run[S_LAT], i, s + d))
                    nk, nl = v_(s, LAT, "n", 0, 128), v_(s, LAT, "n", 128, 128)
                    norm(dve, s, LAT, nk, v_(s, LAT, "c"), 0)
                    norm(dve, s, LAT, nl, v_(s, LAT, "x"), 1)
                    dve.drain()
                    affine(dve, nk, "lat_mg", "lat_mb")
                    affine(dve, nl, "lat_lg", "lat_lb").then_inc(h_sb, 1)

            def front(i, d):
                moments(i, d)
                norms(i, d)

            def body(i, ahead):
                for s in range(2):
                    for k in range(2):
                        dve.wait_ge(l_k, nth(0, i, s, 2, k + 1))
                        for c in range(2):
                            nc.vector.tensor_copy(v_(s, LAT, "kT", 1024 * k + 512 * c, 512), ps[s][(2 + 2 * k + c) % 4][:, :])
                        dve.drain()
                        dve.sem_inc(l_ksb, 1)

                def maxima(hf, s, t):
                    dve.wait_ge(l_s, i * 16 + (8 * hf + 4 * s + t + 1))
                    m = v_(s, LAT, "m", 2 * t, 2)
                    nc.vector.tensor_reduce(m, ps[s][t][:, :].rearrange("p (j k) -> p j k", j=2), AXX, ALU.max)
                    dve.drain()
                    nc.vector.tensor_scalar(m, m, -XSCALE, None, ALU.mult).then_inc(l_exp, 1)

                def shares(hf, s, t):
                    dve.wait_ge(l_osum, i * 16 + (8 * hf + 4 * s + t + 1))
                    rec = v_(s, LAT, "rec", 2 * t, 2)
                    nc.vector.reciprocal(rec, rec)
                    dve.drain()
                    p = v_(s, LAT, "P", 512 * t, 512).rearrange("p (j k) -> p j k", j=2)
                    nc.vector.tensor_tensor(p, p, rec.unsqueeze(2).broadcast_to([128, 2, 256]), ALU.mult).then_inc(l_sub, 1)

                for hf in range(HALVES):
                    for s in range(2):
                        if ahead and hf == 1:
                            (moments, norms)[s](i, 2)
                        for t in range(4):
                            maxima(hf, s, t)
                            if t > 0:
                                shares(hf, s, t - 1)
                        shares(hf, s, 3)
                for s in range(2):
                    tail_stats(dve, tail_run[S_LAT], i, s, LAT, ps[s][1][:, 0:128], x_of(i, s))
                for s in range(2):
                    tail_norm(dve, tail_run[S_LAT], i, s, LAT)

            pairs(dve, front, body)

        def gate_pool(pool):
            with pool.Fori(0, PAIRS) as i:
                stage_x(pool, S_GATE, MOE, None, i)

        def gate_pe(pe):
            with pe.Fori(0, PAIRS) as i:
                for s in range(2):
                    transpose_x(pe, S_GATE, i, s, MOE)
                for s in range(2):
                    pe.wait_ge(xT_sb, nth(xt_run[S_GATE], i, s))
                    nc.tensor.matmul(ps[s][1][:, 0:EXPERTS], v_(s, MOE, "xT"), WA[:, W_LATE("gate")],
                                     start=True, stop=True).then_inc(gate_ps, 1)

        def gate_act(act):
            with act.Fori(0, PAIRS) as i:
                for s in range(2):
                    act.wait_ge(xT_ps, nth(xt_run[S_GATE], i, s))
                    nc.scalar.copy(v_(s, MOE, "xT"), ps[s][0][:, 0:128]).then_inc(xT_sb, 1)
            act.wait_ge(gate_sub, 1)
            nc.scalar.activation(comb[:, :, :], comb[:, :, :], ACT.Exp).then_inc(gate_exp, 1)

        def gate_dve(dve):
            with dve.Fori(0, PAIRS) as i:
                for s in range(2):
                    dve.wait_ge(gate_ps, nth(0, i, s))
                    nc.vector.tensor_copy(comb[:, bass.ds(i * 2 + s, 1), :].rearrange("p a e -> p (a e)"),
                                          ps[s][1][:, 0:EXPERTS]).then_inc(seq_done, 1)
            wide = [128, BATCH, EXPERTS]
            cube = [128, BATCH * EXPERTS, EXPERTS]
            t = small[:, 96:112]
            dve.drain()
            nc.vector.tensor_reduce(t, comb[:, :, :], AXX, ALU.max)
            dve.drain()
            nc.vector.tensor_tensor(comb[:, :, :], comb[:, :, :], t.unsqueeze(2).broadcast_to(wide), ALU.subtract).then_inc(gate_sub, 1)
            dve.wait_ge(gate_exp, 1)
            nc.vector.tensor_reduce(t, comb[:, :, :], AXX, ALU.add)
            dve.drain()
            nc.vector.reciprocal(t, t)
            dve.drain()
            nc.vector.tensor_tensor(comb[:, :, :], comb[:, :, :], t.unsqueeze(2).broadcast_to(wide), ALU.mult)
            dve.drain()
            gt = arena[0][:, 4096:5120].rearrange("p (b e f) -> p b e f", b=BATCH, e=EXPERTS)
            eq = arena[0][:, 5120:6144].rearrange("p (b e f) -> p b e f", b=BATCH, e=EXPERTS)
            mine = comb[:, :, :].unsqueeze(3).broadcast_to([128, BATCH, EXPERTS, EXPERTS])
            other = comb[:, :, :].unsqueeze(2).broadcast_to([128, BATCH, EXPERTS, EXPERTS])
            early = cst("earlier").rearrange("p (e f) -> p e f", e=EXPERTS).unsqueeze(1).broadcast_to([128, BATCH, EXPERTS, EXPERTS])
            nc.vector.tensor_tensor(gt, other, mine, ALU.is_gt)
            nc.vector.tensor_tensor(eq, other, mine, ALU.is_equal)
            dve.drain()
            nc.vector.tensor_tensor(eq, eq, early, ALU.mult)
            dve.drain()
            nc.vector.tensor_tensor(gt, gt, eq, ALU.add)
            dve.drain()
            rank = arena[0][:, 6144:6272]
            nc.vector.tensor_reduce(rank, gt.rearrange("p b e f -> p (b e) f"), AXX, ALU.add)
            dve.drain()
            nc.vector.tensor_scalar(rank, rank, 1.5, None, ALU.is_lt)
            dve.drain()
            c2 = comb[:, :, :].rearrange("p b e -> p (b e)")
            nc.vector.tensor_tensor(c2, c2, rank, ALU.mult)
            dve.drain()
            nc.vector.tensor_reduce(t, comb[:, :, :], AXX, ALU.add)
            dve.drain()
            nc.vector.tensor_scalar(t, t, 1e-9, None, ALU.add)
            dve.drain()
            nc.vector.reciprocal(t, t)
            dve.drain()
            nc.vector.tensor_tensor(comb[:, :, :], comb[:, :, :], t.unsqueeze(2).broadcast_to(wide), ALU.mult)
            dve.drain()
            nc.vector.tensor_reduce(comb_sum[:, :], comb[:, :, :], AXX, ALU.add).then_inc(gate_sub, 1)

        def moe_pool(pool):
            pool.wait_ge(gate_sub, 2)
            with pool.Fori(0, PAIRS) as i:
                for s in range(2):
                    pool.wait_ge(seq_done, nth(S_MOE, i, s))
                    b = i * 2 + s
                    nc.gpsimd.tensor_copy(share[s][:, 0:EXPERTS], comb[:, bass.ds(b, 1), :].rearrange("p a e -> p (a e)"))
                    nc.gpsimd.tensor_copy(share[s][:, EXPERTS:EXPERTS + 1], comb_sum[:, bass.ds(b, 1)])
                stage_x(pool, S_MOE, MOE, None, i)
                for s in range(2):
                    rstd(pool, var_ok, rstd_ok, tail_run[S_MOE], i, s, MOE)

        share = [v_(s, MOE, "share") for s in range(2)]

        def moe_pe(pe):
            with pe.Fori(0, PAIRS) as i:
                for s in range(2):
                    transpose_x(pe, S_MOE, i, s, MOE)
                for s in range(2):
                    pe.wait_ge(xT_sb, nth(xt_run[S_MOE], i, s))
                for e in range(EXPERTS):
                    for s in range(2):
                        if e >= 3:
                            pe.wait_ge(e_acc, i * 16 + (2 * (e - 3) + s + 1))
                        o = ps[s][1 + e % 3][:, :]
                        nc.tensor.matmul(o, v_(s, MOE, "xT"), WA[:, W_LATE("experts", FF * e, FF)], start=True, stop=False,
                                         skip_group_check=True)
                        add_bias(o, "experts", FF * e, FF).then_inc(e_ps, 1)
                for s in range(2):
                    pe.wait_ge(e_acc, i * 16 + (2 * (EXPERTS - 1) + s + 1))
                    for k in range(2):
                        mm = nc.tensor.transpose(ps[s][0][:, 128 * k:128 * k + 128], v_(s, MOE, "acc", 128 * k, 128), ident)
                    mm.then_inc(acc_T, 1)
                for s in range(2):
                    pe.wait_ge(acc_Tsb, nth(0, i, s))
                    for k in range(2):
                        mm = nc.tensor.matmul(ps[s][1][:, 0:128], v_(s, MOE, "accT", 128 * k, 128),
                                              WA[:, W_LATE("moe_out", 128 * k, 128)], start=k == 0, stop=k == 1,
                                              skip_group_check=True)
                    mm.then_inc(y_ps, 1)

        def moe_act(act):
            with act.Fori(0, PAIRS) as i:
                for s in range(2):
                    act.wait_ge(xT_ps, nth(xt_run[S_MOE], i, s))
                    nc.scalar.copy(v_(s, MOE, "xT"), ps[s][0][:, 0:128]).then_inc(xT_sb, 1)
                for e in range(EXPERTS):
                    for s in range(2):
                        act.wait_ge(e_ps, i * 16 + (2 * e + s + 1))
                        if e >= 2:
                            act.wait_ge(e_acc, i * 16 + (2 * (e - 2) + s + 1))
                        nc.scalar.activation(v_(s, MOE, "sig", 256 * (e % 2), 256), ps[s][1 + e % 3][:, 256:512],
                                             ACT.Sigmoid).then_inc(e_sig, 1)
                for s in range(2):
                    act.wait_ge(acc_T, nth(0, i, s))
                    nc.scalar.copy(v_(s, MOE, "accT"), ps[s][0][:, 0:256]).then_inc(acc_Tsb, 1)

        def moe_dve(dve):
            with dve.Fori(0, PAIRS) as i:
                for e in range(EXPERTS):
                    for s in range(2):
                        dve.wait_ge(e_sig, i * 16 + (2 * e + s + 1))
                        t, acc = v_(s, MOE, "t", 256 * (e % 2), 256), v_(s, MOE, "acc")
                        nc.vector.tensor_tensor(t, ps[s][1 + e % 3][:, 0:256], v_(s, MOE, "sig", 256 * (e % 2), 256), ALU.mult)
                        dve.drain()
                        w = share[s][:, e:e + 1]
                        if e == 0:
                            nc.vector.tensor_scalar(acc, t, w, None, ALU.mult).then_inc(e_acc, 1)
                        else:
                            nc.vector.scalar_tensor_tensor(acc, t, w, acc, ALU.mult, ALU.add).then_inc(e_acc, 1)
                for s in range(2):
                    x = v_(s, MOE, "x")
                    nc.vector.scalar_tensor_tensor(x, R[:, ROWS("moe_bo")], share[s][:, EXPERTS:EXPERTS + 1], x,
                                                   ALU.mult, ALU.add)
                    dve.drain()
                    tail_stats(dve, tail_run[S_MOE], i, s, MOE, ps[s][1][:, 0:128])
                for s in range(2):
                    tail_norm(dve, tail_run[S_MOE], i, s, MOE)

        def on(sub):
            return sub <= last

        @block.sync
        def _(sp):
            loads(sp)
            if on(S_REG):
                sim_sp(sp)
            if on(S_LAT):
                sp.wait_ge(seq_done, all_done + BATCH * S_SELF2)
                sp.dma_start(WA[:, 0:W_LATE.size], w_late).then_inc(late_in, 16)
                sp.dma_start(ctx_all[:, :, :], ctx_tok).then_inc(late_in, 16)
            sp.wait_ge(rest_in, 16 * loads_rest)
            sp.wait_ge(seq_done, all_done + BATCH * last)
            sp.dma_start(out, x_all[:, :, :]).then_inc(stored, 16)
            sp.wait_ge(stored, 16)

        @block.gpsimd
        def _(pool):
            start_pool(pool)
            pos_pool(pool)
            if on(S_X0):
                pool.wait_ge(rest_in, 16 * loads_rest)
                att_pool(pool, S_X0, "cross")
            if on(S_SIM):
                sim_pool_(pool)
            if on(S_REG):
                att_pool(pool, S_REG, "self")
            if on(S_LIN):
                att_pool(pool, S_LIN, "linear")
            if on(S_X1):
                wide_pool(pool)
            if on(S_FF1):
                ff_pool(pool, S_FF1)
            if on(S_MLP):
                mlp_pool(pool)
            if on(S_SELF2):
                att_pool(pool, S_SELF2, "kept")
            if on(S_X2):
                att_pool(pool, S_X2, "cross")
            if on(S_FF2):
                ff_pool(pool, S_FF2)
            if on(S_MQA):
                att_pool(pool, S_MQA, "self")
            if on(S_LAT):
                lat_pool(pool)
            if on(S_GATE):
                gate_pool(pool)
            if on(S_MOE):
                moe_pool(pool)

        @block.tensor
        def _(pe):
            lstm_pe(pe)
            pos_pe(pe)
            pe.wait_ge(w_tern, 2)
            pe.wait_ge(rest_in, 16 * loads_rest)
            if on(S_X0):
                att_pe(pe, S_X0, "cross", WA, "x0", "x0", "full")
            if on(S_SIM):
                sim_pe(pe)
            if on(S_REG):
                att_pe(pe, S_REG, "self", WA, "reg", None, "pos")
            if on(S_LIN):
                att_pe(pe, S_LIN, "linear", WA, "lin", "lin", None)
            if on(S_X1):
                wide_pe(pe)
            if on(S_FF1):
                ff_pe(pe, S_FF1)
            if on(S_MLP):
                mlp_pe(pe)
            if on(S_SELF2):
                att_pe(pe, S_SELF2, "kept", WA, None, None, None, 0, "self2_out")
            if on(S_X2):
                att_pe(pe, S_X2, "cross", WB, "x2", "x2", None)
            if on(S_FF2):
                ff_pe(pe, S_FF2)
            if on(S_MQA):
                att_pe(pe, S_MQA, "self", WB, "mqa", "mqa", "causal")
            if on(S_LAT):
                lat_pe(pe)
            if on(S_GATE):
                gate_pe(pe)
            if on(S_MOE):
                moe_pe(pe)

        @block.scalar
        def _(act):
            lstm_act(act)
            pos_act(act)
            if on(S_X0):
                att_act(act, S_X0, "cross")
            if on(S_SIM):
                sim_act(act)
            if on(S_REG):
                att_act(act, S_REG, "self")
            if on(S_LIN):
                att_act(act, S_LIN, "linear")
            if on(S_X1):
                wide_act(act)
            if on(S_FF1):
                ff_act(act, S_FF1)
            if on(S_MLP):
                mlp_act_(act)
            if on(S_SELF2):
                att_act(act, S_SELF2, "kept")
            if on(S_X2):
                att_act(act, S_X2, "cross")
            if on(S_FF2):
                ff_act(act, S_FF2)
            if on(S_MQA):
                att_act(act, S_MQA, "self")
            if on(S_LAT):
                lat_act(act)
            if on(S_GATE):
                gate_act(act)
            if on(S_MOE):
                moe_act(act)

        @block.vector
        def _(dve):
            start_dve(dve)
            lstm_dve(dve)
            pos_dve(dve)
            if on(S_X0):
                att_dve(dve, S_X0, "cross")
            if on(S_SIM):
                sim_dve(dve)
            if on(S_REG):
                att_dve(dve, S_REG, "self")
            if on(S_LIN):
                att_dve(dve, S_LIN, "linear")
            if on(S_X1):
                wide_dve(dve)
            if on(S_FF1):
                ff_dve(dve, S_FF1)
            if on(S_MLP):
                mlp_dve(dve)
            if on(S_SELF2):
                att_dve(dve, S_SELF2, "kept")
            if on(S_X2):
                att_dve(dve, S_X2, "cross")
            if on(S_FF2):
                ff_dve(dve, S_FF2)
            if on(S_MQA):
                att_dve(dve, S_MQA, "self")
            if on(S_LAT):
                lat_dve(dve)
            if on(S_GATE):
                gate_dve(dve)
            if on(S_MOE):
                moe_dve(dve)


def constants():
    c = np.zeros((128, CONST.size), np.float32)

    def put(name, a):
        a = np.asarray(a, np.float32)
        c[:a.shape[0], CONST(name)] = a

    p = np.arange(128)
    row = p.astype(np.float32)
    put("ident", np.eye(128))
    put("rel", row[None, :] / (row[:, None] + np.float32(1)))
    put("tri", p[None, :] <= p[:, None])
    put("triT", p[None, :] >= p[:, None])
    put("causal", np.where(p[None, :] <= p[:, None], 0.0, BIG))
    half, turn = HD // 2, HD // 4
    theta = np.float32(10000.0) ** (-np.arange(half, dtype=np.float32) / np.float32(half))
    freqs = theta[:, None] * row[None, :]
    cos, sin = np.ones((HEADS, HD, TOK)), np.zeros((HEADS, HD, TOK))
    cos[:, :half], sin[:, :half] = np.cos(freqs), np.sin(freqs)
    sin[:, :turn] *= -1
    put("cos", cos.reshape(128, TOK))
    put("sin", sin.reshape(128, TOK))
    put("headmask", p[:, None] // HD == np.arange(HEADS)[None, :])
    r = np.arange(REG_ROWS)
    put("blockmask", (r[:, None] // REG) == (p[None, :] // HD))
    put("regsel", 0.5 * ((r[:, None] % REG) == p[None, :]))
    put("notreg", p[:, None] >= REG)
    put("regscale", np.where(p[:, None] < REG, 0.5, 1.0))
    put("minushalf", np.full((128, 16), -0.5))
    put("step", np.broadcast_to((row + 1) / np.float32(TOK), (128, 128)))
    e = np.arange(EXPERTS)
    put("earlier", np.broadcast_to((e[None, :] < e[:, None]).reshape(1, -1), (128, 64)))
    return c


def kernel(**inputs):
    import concourse.bacc as bacc
    from concourse.bass_utils import run_bass_kernel_spmd

    a = {k: np.asarray(v) for k, v in inputs.items()}

    def side(*parts):
        return np.concatenate(parts, axis=1)

    def blocks(w, n=4):
        return w.reshape(n, 128, -1).transpose(1, 0, 2).reshape(128, -1)

    def tall(w):
        return np.concatenate([w, np.zeros((128 - w.shape[0], w.shape[1]), w.dtype)], 0)

    def gates_order(w):
        h = LSTM_H
        return np.concatenate([w[:2 * h], w[3 * h:], w[2 * h:3 * h]], 0)

    def T(n):
        return a[n].T

    def turned(w):
        h = w.reshape(*w.shape[:-1], -1, HD)
        return np.concatenate([h[..., 2:4], h[..., 0:2], h[..., 4:]], -1).reshape(w.shape)

    wk16, bk16 = np.tile(a["L3_attn_Wk"], (1, HEADS)), np.tile(a["L3_attn_bk"], HEADS)

    early = side(
        gates_order(a["L0_attn_W_ih"]).T, tall(gates_order(a["L0_attn_W_hh"]).T),
        tall(np.concatenate([a["L0_attn_W_mu"], a["L0_attn_W_sig"]], 0).T),
        T("L0_xattn_Wq"), T("L0_xattn_Wk"), T("L0_xattn_Wv"), T("L0_xattn_Wo"),
        a["L0_ffn_W_qkv"], a["L0_ffn_W_proj"], T("L1_attn_Wqkv"), T("L1_attn_Wout"),
        a["L1_xattn_Wq"], a["L1_xattn_Wk"], a["L1_xattn_Wv"], T("L1_ffn_w1"), blocks(T("L1_ffn_w2")),
        a["L2_attn_q_w1"], a["L2_attn_k_w1"], a["L2_attn_v_w1"],
        blocks(a["L2_attn_q_w2"]), blocks(a["L2_attn_k_w2"]), blocks(a["L2_attn_v_w2"]),
        a["L2_attn_proj_w"])
    late = side(
        a["L3_xattn_Wq"], a["L3_xattn_Wkv"], blocks(a["L3_xattn_Wout"], 8), T("L3_ffn_Wg"),
        a["L3_ffn_W1"].transpose(2, 0, 1).reshape(128, -1), blocks(T("L3_ffn_Wo"), 2))
    rest = side(
        T("L2_xattn_Wq"), T("L2_xattn_Wk"), T("L2_xattn_Wv"), T("L2_xattn_Wo"),
        a["L3_attn_Wq"], wk16, np.tile(a["L3_attn_Wv"], (1, HEADS)), a["L3_attn_Wo"],
        turned(a["L3_attn_Wq"]), turned(wk16), T("L2_ffn_w1"), blocks(T("L2_ffn_w2")))
    bias = np.concatenate([
        gates_order(a["L0_attn_b_ih"][:, None])[:, 0], gates_order(a["L0_attn_b_hh"][:, None])[:, 0],
        a["L0_xattn_bq"], a["L0_xattn_bk"], a["L0_xattn_bv"], a["L0_xattn_bo"], a["L0_ffn_b_proj"],
        a["L1_attn_bqkv"], a["L1_attn_bout"], a["L1_xattn_bq"], a["L1_xattn_bk"], a["L1_xattn_bv"],
        a["L1_ffn_b1"], a["L1_ffn_b2"], a["L2_attn_q_b1"], a["L2_attn_k_b1"], a["L2_attn_v_b1"],
        a["L2_attn_q_b2"], a["L2_attn_k_b2"], a["L2_attn_v_b2"], a["L2_attn_proj_b"],
        a["L2_xattn_bq"], a["L2_xattn_bk"], a["L2_xattn_bv"], a["L2_xattn_bo"],
        a["L3_attn_bq"], bk16, np.tile(a["L3_attn_bv"], HEADS), a["L3_attn_bo"],
        turned(a["L3_attn_bq"]), turned(bk16), a["L3_ffn_b1"].reshape(-1)])
    bias = np.concatenate([bias, np.zeros(128 * BIAS_COLS - BIAS.size, bias.dtype)])
    rows = np.concatenate([
        a["L0_ffn_g_info"][0, 0], a["L1_attn_gamma"], a["L1_attn_beta"], a["L1_ffn_ln1_g"],
        a["L1_ffn_ln1_b"], a["L1_ffn_ln2_g"], a["L1_ffn_ln2_b"], a["L2_ffn_ln1_g"], a["L2_ffn_ln1_b"],
        a["L2_ffn_ln2_g"], a["L2_ffn_ln2_b"], a["L2_ffn_b1"], a["L2_ffn_b2"], a["L3_xattn_ln_m_g"],
        a["L3_xattn_ln_m_b"], a["L3_xattn_ln_l_g"], a["L3_xattn_ln_l_b"], a["L3_ffn_bo"],
        a["L0_attn_b_mu"], a["L0_attn_b_sig"]])
    arrays = {
        "x_tok": a["x"].transpose(1, 0, 2), "x_T": a["x"].transpose(2, 0, 1),
        "ctx_tok": a["ctx_1024"].transpose(1, 0, 2), "ctx_T": a["ctx_1024"].transpose(2, 0, 1),
        "mask": a["mask_BxSxS2_ik1"].transpose(1, 0, 2).reshape(128, -1),
        "mask_row": a["mask_BxS2_if1"].reshape(1, -1),
        "w_early": early, "w_late": late, "w_rest": rest,
        "bias": bias.reshape(128, BIAS_COLS), "rows": np.repeat(rows[None], 128, 0),
        "const": constants(),
    }
    nc = bacc.Bacc("TRN2", target_bir_lowering=False, num_devices=1)
    args = {}
    for name, v in arrays.items():
        arrays[name] = v = np.ascontiguousarray(v)
        args[name] = nc.dram_tensor(name, v.shape, mybir.dt.from_np(v.dtype), kind="ExternalInput").ap()
    out = nc.dram_tensor("out", (128, BATCH, DIM), F32, kind="ExternalOutput").ap()
    decoder(nc, **args, out=out)
    r = run_bass_kernel_spmd(nc, [arrays], core_ids=[0])
    return np.ascontiguousarray(r.results[0]["out"].transpose(1, 0, 2))
```

```python
import math
from contextlib import ExitStack

import numpy as np

import concourse.bass as bass
from concourse import mybir

F32 = mybir.dt.float32
BF16 = mybir.dt.bfloat16
I32 = mybir.dt.int32
ACT = mybir.ActivationFunctionType
ALU = mybir.AluOpType
AXX = mybir.AxisListType.X

BATCH, TOK, DIM, HEADS = 16, 128, 128, 16
HD = DIM // HEADS
PAD = 32
GROUPS = HEADS * PAD // 128
PAIRS = BATCH // 2
LSTM_H, REG = 20, 5
FF = 512
EXPERTS, XH, XD = 8, 16, 64
LN_EPS = 1e-5
NEG, BIG = -1.0e10, -2.0 ** 100
ROUND = 12582912.0
REG_ROWS = HEADS * REG
SCALE = 1.0 / math.sqrt(HD)

(S_LSTM, S_X0, S_SIM, S_REG, S_LIN, S_X1, S_FF1, S_MLP, S_SELF2, S_X2, S_FF2, S_MQA, S_LAT, S_GATE,
 S_MOE) = range(15)


def nth(run, i, s, each=1, part=None):
    part = each if part is None else part
    return i * (2 * each) + ((run * BATCH + s) * each + part)


class Columns:

    def __init__(self, *sizes):
        self.at, end = {}, 0
        for name, size in sizes:
            self.at[name] = (end, size)
            end += size
        self.size = end

    def __call__(self, name, of=0, width=None):
        a, n = self.at[name]
        return slice(a + of, a + (n if width is None else of + width))


W_EARLY = Columns(("ih", 4 * LSTM_H), ("hh", 4 * LSTM_H), ("musig", 4), ("x0", 512), ("reg", 512),
                  ("lin", 512), ("x1", 384), ("ff1_up", FF), ("ff1_down", FF),
                  ("mlp_up", 3 * FF), ("mlp_down", 3 * FF), ("self2_out", DIM))
W_LATE = Columns(("lat_q", 1024), ("lat_k", 1024), ("lat_v", 1024), ("lat_out", 1024),
                 ("gate", EXPERTS), ("experts", EXPERTS * FF), ("moe_out", 256))
W_REST = Columns(("x2", 512), ("mqa", 512), ("mqa_turned", 256), ("ff2_up", FF), ("ff2_down", FF))
BIAS = Columns(("ih", 80), ("hh", 80), ("x0", 512), ("reg_out", 128), ("lin", 512), ("x1", 384),
               ("ff1_up", FF), ("ff1_down", 128), ("mlp_up", 3 * FF), ("mlp_down", 384),
               ("self2_out", 128), ("x2", 512), ("mqa", 512), ("mqa_turned", 256), ("experts", EXPERTS * FF))
BIAS_COLS = -(-BIAS.size // 128)
ROWS = Columns(("g_query", 128), ("lin_g", 128), ("lin_b", 128), ("ff1_g1", 128), ("ff1_b1", 128),
               ("ff1_g2", FF), ("ff1_b2", FF), ("ff2_g1", 128), ("ff2_b1", 128), ("ff2_g2", FF),
               ("ff2_b2", FF), ("ff2_up", FF), ("ff2_down", 128), ("lat_mg", 128), ("lat_mb", 128),
               ("lat_lg", 128), ("lat_lb", 128), ("moe_bo", 128), ("mu_b", 4))
CONST = Columns(("ident", 128), ("rel", 128), ("tri", 128), ("triT", 128), ("causal", 128),
                ("cos", 128), ("sin", 128), ("headmask", HEADS), ("blockmask", 128),
                ("regsel", 128), ("notreg", 1), ("regscale", 1), ("minushalf", 16),
                ("step", 128), ("earlier", 64))

VAUG = slice(0, 512)
ARENA = 11200
ATT = Columns(("kept", 512), ("x", 128), ("c", 128), ("xcT", 128), ("qT", 128), ("kT", 128),
              ("wide", 2048), ("P", 2048), ("PT", 2048), ("O", 128), ("OnT", 128), ("r", 128),
              ("m", 16), ("rec", 16), ("stats", 8), ("mv", 4), ("rstd", 1), ("m2", 4),
              ("regq", REG_ROWS))
QKV_KEPT = ATT.size
assert QKV_KEPT + PAIRS * 384 <= ARENA
FFN = Columns(("kept", 512), ("x", 128), ("h", 128), ("hT", 128), ("u", FF), ("n", FF), ("nT", FF),
              ("nbT", FF // 2), ("hbT", 64), ("r", 128), ("stats", 8),
              ("mv", 4), ("rstd", 2), ("a", 8))
MLP = Columns(("kept", 512), ("x", 128), ("xT", 128), ("G", 3 * FF))
LAT = Columns(("x", 128), ("c", 128), ("n", 256), ("nT", 256), ("qT", 1024), ("kT", 2048),
              ("V", 2 * XH * XD), ("P", 2048), ("PT", 2048), ("O", 1024), ("r", 128),
              ("m", 16), ("rec", 16), ("stats", 16), ("mv", 4), ("rstd", 4))
MOE = Columns(("x", 128), ("xT", 128), ("sig", 512), ("t", 512), ("acc", 256), ("accT", 256),
              ("r", 128), ("stats", 8), ("mv", 4), ("rstd", 1), ("share", EXPERTS + 1))
for c in (ATT, FFN, MLP, LAT, MOE):
    assert c.size <= ARENA


def decoder(nc, x_tok, x_T, ctx_tok, ctx_T, mask, mask_row, w_early, w_late, w_rest, bias, rows,
            const, out, last=S_MOE):
    ctx = ExitStack()
    with ctx:
        def sb(name, shape, dt=F32):
            return ctx.enter_context(nc.sbuf_tensor(name, shape, dt))

        def sem(name):
            return ctx.enter_context(nc.semaphore(name))

        x_all = sb("x_all", [128, BATCH, DIM])
        xT_all = sb("xT_all", [128, BATCH, TOK])
        ctx_all = xT_all
        ctxT_all = sb("ctxT_all", [128, BATCH, TOK])
        maskadd = sb("maskadd", [128, BATCH, TOK], BF16)
        WA = sb("WA", [128, max(W_EARLY.size, W_LATE.size)])
        WB = sb("WB", [128, W_REST.size])
        bias3 = sb("bias3", [3, 128 * BIAS_COLS], BF16)
        minus_round = sb("minus_round", [128, 1])
        half_b = sb("half_b", [3, 128], BF16)
        R = sb("R", [128, ROWS.size])
        C = sb("C", [128, CONST.size])
        arena = [sb(f"arena{s}", [128, ARENA]) for s in range(2)]
        ident_b = sb("ident_b", [128, 128], BF16)
        causal_b = sb("causal_b", [128, 128], BF16)
        ones_b = sb("ones_b", [128, 128], BF16)
        negrow_b = sb("negrow_b", [2, REG_ROWS], BF16)
        tern_up = sb("tern_up", [128, FF], BF16)
        tern_down = sb("tern_down", [128, 4, DIM], BF16)
        small = sb("small", [128, 112])
        gates = sb("gates", [LSTM_H, 5, BATCH])
        prod = sb("prod", [LSTM_H, 2, BATCH])
        tanh_c = sb("tanh_c", [LSTM_H, BATCH])
        hid = [sb(f"hid{k}", [128, BATCH]) for k in range(2)]
        mu_cols = sb("mu_cols", [128, 4, BATCH])
        pos_rows = xT_all[:, :, :].rearrange("p b t -> p (b t)").bitcast(BF16).rearrange(
            "p (a b t) -> p a b t", a=2, b=BATCH)
        pos_q = [arena[s][:, QKV_KEPT + 1024:QKV_KEPT + 1088].bitcast(BF16) for s in range(2)]
        comb = sb("comb", [128, BATCH, EXPERTS])
        comb_sum = sb("comb_sum", [128, BATCH])
        mrow = sb("mrow", [1, BATCH, TOK], BF16)
        ps = [[ctx.enter_context(nc.psum_tensor(f"ps{s}_{k}", [128, 512], F32)) for k in range(4)]
              for s in range(2)]

        ident = C[:, CONST("ident")]

        def cst(name):
            return C[:, CONST(name)]

        def heads(ap, h=4):
            return ap.rearrange("p (h k) -> p h k", h=h)

        first_in = sem("first_in")
        bias_rows = sem("bias_rows")
        loaded = sem("loaded")
        bias_in = sem("bias_in")
        mask_in = sem("mask_in")
        late_in = sem("late_in")
        rows_in = sem("rows_in")
        rest_in = sem("rest_in")
        stored = sem("stored")
        seq_done = sem("seq_done")
        const_b = sem("const_b")
        bias_cut = sem("bias_cut")
        w_sum = sem("w_sum")
        w_mean = sem("w_mean")
        w_tern = sem("w_tern")
        gates_sum = sem("gates_sum")
        gates_tanh = sem("gates_tanh")
        cell_new = sem("cell_new")
        cell_tanh = sem("cell_tanh")
        hid_new = sem("hid_new")
        musig_sum = sem("musig_sum")
        musig_kept = sem("musig_kept")
        scan_exp = sem("scan_exp")
        scan_out = sem("scan_out")
        scan_ps = sem("scan_ps")
        scan_cols = sem("scan_cols")
        pos_sq = sem("pos_sq")
        pos_w = sem("pos_w")
        pos_masked = sem("pos_masked")
        pos_T = sem("pos_T")
        pos_T_sb = sem("pos_T_sb")
        staged = sem("staged")
        xT_ps = sem("xT_ps")
        xT_sb = sem("xT_sb")
        y_ps = sem("y_ps")
        var_ok = sem("var_ok")
        rstd_ok = sem("rstd_ok")
        qkv_ps = sem("qkv_ps")
        qk_sb = sem("qk_sb")
        wide_pool_ok = sem("wide_pool_ok")
        wide_dve_ok = sem("wide_dve_ok")
        v_sb = sem("v_sb")
        s_ps = sem("s_ps")
        s_sub = sem("s_sub")
        p_exp = sem("p_exp")
        pT_ps = sem("pT_ps")
        pT_sb = sem("pT_sb")
        oT_ps = sem("oT_ps")
        oT_sb = sem("oT_sb")
        o_ps = sem("o_ps")
        o_sb = sem("o_sb")
        on_ps = sem("on_ps")
        on_sb = sem("on_sb")
        sim_q = sem("sim_q")
        sim_sb = sem("sim_sb")
        sim_mid = sem("sim_mid")
        sim_pool = sem("sim_pool")
        sim_rows = sem("sim_rows")
        reg_q = sem("reg_q")
        reg_ps = sem("reg_ps")
        reg_m = sem("reg_m")
        reg_e = sem("reg_e")
        reg_n = sem("reg_n")
        reg_T = sem("reg_T")
        reg_Tsb = sem("reg_Tsb")
        reg_o = sem("reg_o")
        reg_om = sem("reg_om")
        reg_add = sem("reg_add")
        lin_min = sem("lin_min")
        lin_exp = sem("lin_exp")
        h_sb = sem("h_sb")
        hT_ps = sem("hT_ps")
        hT_sb = sem("hT_sb")
        up_ps = sem("up_ps")
        up_in = sem("up_in")
        up_act = sem("up_act")
        n_normed = sem("n_normed")
        n_sb = sem("n_sb")
        nT_ps = sem("nT_ps")
        nT_sb = sem("nT_sb")
        mid_var = sem("mid_var")
        mid_rstd = sem("mid_rstd")
        mlp_ps = sem("mlp_ps")
        mlp_act = sem("mlp_act")
        mlp_out = sem("mlp_out")
        w_qk = sem("w_qk")
        w_qk_sb = sem("w_qk_sb")
        w_s = sem("w_s")
        w_m = sem("w_m")
        w_e = sem("w_e")
        w_T = sem("w_T")
        w_Tsb = sem("w_Tsb")
        l_q = sem("l_q")
        l_qsb = sem("l_qsb")
        l_k = sem("l_k")
        l_ksb = sem("l_ksb")
        l_v = sem("l_v")
        l_vsb = sem("l_vsb")
        l_s = sem("l_s")
        l_sub = sem("l_sub")
        l_exp = sem("l_exp")
        l_T = sem("l_T")
        l_Tsb = sem("l_Tsb")
        l_o = sem("l_o")
        l_osb = sem("l_osb")
        l_osum = sem("l_osum")
        gate_ps = sem("gate_ps")
        gate_exp = sem("gate_exp")
        gate_sub = sem("gate_sub")
        share_in = sem("share_in")
        e_ps = sem("e_ps")
        e_sig = sem("e_sig")
        e_acc = sem("e_acc")
        acc_T = sem("acc_T")
        acc_Tsb = sem("acc_Tsb")

        block = ctx.enter_context(nc.Block())

        def v_(s, cols, name, of=0, width=None):
            return arena[s][:, cols(name, of, width)]

        def add_bias(out_ap, name, of=0, width=None, stop=True):
            return nc.tensor.matmul(out_ap, ones_b[0:3, :], bias3[:, BIAS(name, of, width)],
                                    start=False, stop=stop, skip_group_check=True)

        def stage_x(pool, sub, cols, with_ctx=None, i=None):
            for s in range(2):
                pool.wait_ge(seq_done, nth(sub, i, s))
                b = i * 2 + s
                if with_ctx is not None:
                    nc.gpsimd.tensor_copy(v_(s, cols, "c"), with_ctx[:, bass.ds(b, 1), :].rearrange("p a d -> p (a d)"))
                nc.gpsimd.tensor_copy(v_(s, cols, "x"), x_all[:, bass.ds(b, 1), :].rearrange("p a d -> p (a d)"))
                pool.drain()
                pool.sem_inc(staged, 1)

        def rstd(pool, wait_sem, done_sem, run, i, s, cols, n=1, d=0):
            pool.wait_ge(wait_sem, nth(run, i, s + d))
            nc.gpsimd.tensor_tensor(v_(s, cols, "rstd", 0, n), v_(s, cols, "mv", 1, 2 * n - 1)[:, ::2] if n > 1
                                    else v_(s, cols, "mv", 1, 1),
                                    cst("minushalf")[:, 0:n], ALU.pow).then_inc(done_sem, 1)

        def stats(dve, s, cols, src, width=128, at=0):
            nc.vector.bn_stats(v_(s, cols, "stats", 0, 6), src)
            dve.drain()
            nc.vector.bn_aggr(v_(s, cols, "mv", at, 2), v_(s, cols, "stats", 0, 6))
            dve.drain()
            mv = v_(s, cols, "mv", at + 1, 1)
            return nc.vector.tensor_scalar(mv, mv, LN_EPS, None, ALU.add)

        def norm(dve, s, cols, dst, src, at=0):
            return nc.vector.tensor_scalar(dst, src, v_(s, cols, "mv", 2 * at, 1),
                                           v_(s, cols, "rstd", at, 1), ALU.subtract, ALU.mult)

        def norm_affine(dve, s, cols, dst, src, gamma, beta, at=0):
            nc.vector.scalar_tensor_tensor(dst, src, v_(s, cols, "mv", 2 * at, 1), R[:, ROWS(gamma)],
                                           ALU.subtract, ALU.mult)
            dve.drain()
            return nc.vector.scalar_tensor_tensor(dst, dst, v_(s, cols, "rstd", at, 1), R[:, ROWS(beta)],
                                                  ALU.mult, ALU.add)

        def stage_ahead(pool, sub, cols):
            def stage(i, d):
                for s in range(2):
                    if d == 0:
                        pool.wait_ge(seq_done, nth(sub, i, s))
                    else:
                        pool.wait_ge(xT_ps, nth(xt_run[sub], i, s))
                    nc.gpsimd.tensor_copy(v_(s, cols, "x"), x_at(x_all, i, s + d))
                    pool.drain()
                    pool.sem_inc(staged, 1)

            stage(0, 0)
            with pool.Fori(0, PAIRS - 1) as i:
                stage(i, 2)

        def x_of(i, s):
            return x_all[:, bass.ds(i * 2 + s, 1), :].rearrange("p a d -> p (a d)")

        def tail_stats(dve, run, i, s, cols, y, x=None):
            dve.wait_ge(y_ps, nth(run, i, s))
            nc.vector.tensor_tensor(v_(s, cols, "r"), y, v_(s, cols, "x") if x is None else x, ALU.add)
            dve.drain()
            stats(dve, s, cols, v_(s, cols, "r")).then_inc(var_ok, 1)

        def tail_norm(dve, run, i, s, cols):
            dve.wait_ge(rstd_ok, nth(run, i, s))
            norm(dve, s, cols, x_of(i, s), v_(s, cols, "r")).then_inc(seq_done, 1)

        def transpose_x(pe, sub, i, s, cols, src="x", bank=0):
            pe.wait_ge(staged, nth(sub, i, s))
            nc.tensor.transpose(ps[s][bank][:, 0:128], v_(s, cols, src), ident).then_inc(xT_ps, 1)

        ORDER = (1, 2, 3, 0)
        WIDE_POOL, WIDE_DVE = (1, 2, 3), (0,)

        BIASED = (1, 3)

        def pairs(eng, front, body):
            front(0, 0)
            with eng.Fori(0, PAIRS - 1) as i:
                body(i, True)
            body(PAIRS - 1, False)

        def x_at(src, i, n):
            return src[:, bass.ds(i * 2 + n, 1), :].rearrange("p a d -> p (a d)")

        def widen(eng, i, d, s, kind, t):
            if kind == "kept":
                src = arena[s][:, bass.ds(i * 384 + (QKV_KEPT + 128 + 192 * d), 128)]
            else:
                src = v_(s, ATT, "qT" if kind == "linear" else "kT")
            return eng.tensor_tensor(heads(v_(s, ATT, "wide", 512 * t, 512)),
                                     src.unsqueeze(1).broadcast_to([128, 4, 128]),
                                     cst("headmask")[:, 4 * t:4 * t + 4].unsqueeze(2).broadcast_to([128, 4, 128]),
                                     ALU.mult)

        def att_pool(pool, sub, kind):
            a = att_run[sub]

            def stage(i, d):
                for s in range(2):
                    if d == 0:
                        pool.wait_ge(seq_done, nth(sub, i, s))
                    else:
                        pool.wait_ge(s_ps, nth(a, i, s, GROUPS))
                    if kind == "cross":
                        nc.gpsimd.tensor_copy(v_(s, ATT, "c"), x_at(ctxT_all, i, s + d))
                    if sub == S_REG:
                        nc.gpsimd.tensor_copy(pos_q[s], pos_rows[:, 0, bass.ds(i * 2 + (s + d), 1), :]
                                              .rearrange("p a d -> p (a d)"))
                    if kind != "kept":
                        nc.gpsimd.tensor_copy(v_(s, ATT, "x"), x_at(x_all, i, s + d))
                        pool.drain()
                    pool.sem_inc(staged, 1)

            def wide(i, d, s):
                if kind != "kept":
                    pool.wait_ge(qk_sb, nth(a, i, s + d))
                elif d:
                    pool.wait_ge(o_ps, nth(a, i, s))
                for t in WIDE_POOL:
                    widen(nc.gpsimd, i, d, s, kind, t).then_inc(wide_pool_ok, 1)

            def body(i, ahead):
                if ahead:
                    stage(i, 2)
                if kind == "linear":
                    for s in range(2):
                        rstd(pool, mid_var, mid_rstd, mid_run[S_LIN], i, s, ATT)
                if ahead:
                    wide(i, 2, 0)
                for s in range(2):
                    rstd(pool, var_ok, rstd_ok, tail_run[sub], i, s, ATT)
                if ahead:
                    wide(i, 2, 1)

            def front(i, d):
                stage(i, d)
                for s in range(2):
                    wide(i, d, s)

            pairs(pool, front, body)

        def att_pe(pe, sub, kind, W, name, bias_name, mask_kind, out_w=384, out_name=None):
            out_name = out_name or name
            xt, a = xt_run.get(sub), att_run[sub]

            def front_x(i, d):
                if kind != "kept":
                    for s in range(2):
                        pe.wait_ge(staged, nth(sub, i, s + d))
                        nc.tensor.transpose(ps[s][2][:, 0:128], v_(s, ATT, "x"), ident).then_inc(xT_ps, 1)

            def front_qkv(i, d):
                if kind == "kept":
                    return
                for s in range(2):
                    pe.wait_ge(xT_sb, nth(xt, i, s + d))
                    xT = v_(s, ATT, "xcT")
                    cT = v_(s, ATT, "c") if kind == "cross" else xT
                    parts = [(name, bias_name, 0, xT), (name, bias_name, 128, cT)]
                    if sub == S_MQA:
                        parts += [("mqa_turned", "mqa_turned", 0, xT), ("mqa_turned", "mqa_turned", 128, xT)]
                    for n, (w, b, of, src) in enumerate(parts):
                        o = ps[s][3][:, 128 * n:128 * n + 128]
                        mm = nc.tensor.matmul(o, W[:, name_cols(w, of, 128)], src, start=True,
                                              stop=b is None, skip_group_check=True)
                        if b is not None:
                            mm = nc.tensor.matmul(o, bias3[:, BIAS(b, of, 128)], ones_b[0:3, :],
                                                  start=False, stop=True, skip_group_check=True)
                    mm.then_inc(qkv_ps, 1)
                    o = ps[s][2][:, 128:256]
                    mm = nc.tensor.matmul(o, cT, W[:, name_cols(name, 256, 128)], start=True,
                                          stop=bias_name is None, skip_group_check=True)
                    if bias_name is not None:
                        mm = add_bias(o, bias_name, 256, 128)
                    mm.then_inc(qkv_ps, 1)

            def scores(i):
                for s in range(2):
                    pe.wait_ge(qk_sb, nth(a, i, s))
                    pe.wait_ge(v_sb, nth(a, i, s))
                    for t in ORDER:
                        if t in WIDE_POOL:
                            pe.wait_ge(wide_pool_ok, nth(a, i, s, len(WIDE_POOL), WIDE_POOL.index(t) + 1))
                        else:
                            pe.wait_ge(wide_dve_ok, nth(a, i, s, len(WIDE_DVE), WIDE_DVE.index(t) + 1))
                        bank = ps[s][t]
                        mm = nc.tensor.matmul(bank[:, :], v_(s, ATT, "kT" if kind == "linear" else "qT"),
                                              v_(s, ATT, "wide", 512 * t, 512), start=True,
                                              stop=mask_kind is None, skip_group_check=True)
                        if mask_kind is not None:
                            if mask_kind == "full":
                                l, r = ident_b[:, :], maskadd[:, bass.ds(i * 2 + s, 1), :].broadcast_to([128, 4, 128])
                            elif mask_kind == "causal":
                                l, r = ident_b[:, :], causal_b[:, :].unsqueeze(1).broadcast_to([128, 4, 128])
                            else:
                                l, r = pos_q[s], pos_rows[:, 1, bass.ds(i * 2 + s, 1), :].broadcast_to([128, 4, 128])
                            mm = nc.tensor.matmul(heads(bank[:, :]), l, r, start=False, stop=True,
                                                  skip_group_check=True)
                        mm.then_inc(s_ps, 1)

            def values(i, s):
                va = arena[s][:, VAUG].rearrange("p (h d) -> p h d", h=HEADS)
                for n, t in enumerate(ORDER):
                    pe.wait_ge(pT_sb, nth(a, i, s, GROUPS, n + 1))
                    for j in range(4):
                        mm = nc.tensor.matmul(ps[s][1][PAD * j:PAD * (j + 1), t * 128:(t + 1) * 128],
                                              va[:, 4 * t + j, :], v_(s, ATT, "PT", 128 * (4 * t + j), 128),
                                              start=True, stop=True, skip_group_check=True)
                    if sub == S_REG and n == 1:
                        reg_scores(pe, i, s)
                mm.then_inc(oT_ps, 1)

            def body(i, ahead):
                scores(i)
                if kind != "linear":
                    for s in range(2):
                        for n, t in enumerate(ORDER):
                            pe.wait_ge(p_exp, nth(soft_run[sub], i, s, GROUPS, n + 1))
                            for j in range(4):
                                mm = nc.tensor.transpose(ps[s][t][:, j * 128:(j + 1) * 128],
                                                         v_(s, ATT, "P", 128 * (4 * t + j), 128), ident)
                            mm.then_inc(pT_ps, 1)
                        values(i, s)
                else:
                    for s in range(2):
                        values(i, s)
                if sub == S_REG:
                    reg_turn(pe, i)
                if ahead and sub != S_REG:
                    front_x(i, 2)
                for s in range(2):
                    pe.wait_ge(oT_sb, nth(a, i, s))
                    for t in range(GROUPS):
                        mm = nc.tensor.transpose(ps[s][0][:, t * 128:(t + 1) * 128],
                                                 v_(s, ATT, "wide", 128 * t, 128), ident)
                    mm.then_inc(o_ps, 1)
                if sub == S_REG:
                    reg_output(pe, i)
                elif ahead:
                    front_qkv(i, 2)
                for s in range(2):
                    pe.wait_ge(o_sb, nth(a, i, s))
                    nc.tensor.transpose(ps[s][1][:, 0:128], v_(s, ATT, "O"), ident).then_inc(on_ps, 1)
                if ahead and sub == S_REG:
                    front_x(i, 2)
                for s in range(2):
                    pe.wait_ge(on_sb, nth(a, i, s))
                    yb = ps[s][0][:, 0:128]
                    nc.tensor.matmul(yb, v_(s, ATT, "OnT"), W[:, name_cols(out_name, out_w, 128)],
                                     start=True, stop=False, skip_group_check=True)
                    if bias_name in ("x0", "lin", "x2", "mqa"):
                        mm = add_bias(yb, bias_name, 384, 128)
                    else:
                        mm = add_bias(yb, "reg_out" if sub == S_REG else "self2_out")
                    mm.then_inc(y_ps, 1)
                if ahead and sub == S_REG:
                    front_qkv(i, 2)

            def front(i, d):
                front_x(i, d)
                front_qkv(i, d)

            pairs(pe, front, body)

        def att_act(act, sub, kind):
            xt, a = xt_run.get(sub), att_run[sub]

            def front_x(i, d):
                if kind != "kept":
                    for s in range(2):
                        act.wait_ge(xT_ps, nth(xt, i, s + d))
                        nc.scalar.copy(v_(s, ATT, "xcT", 0, 128), ps[s][2][:, 0:128]).then_inc(xT_sb, 1)

            def front_qkv(i, d):
                for s in range(2):
                    va = arena[s][:, VAUG].rearrange("p (h d) -> p h d", h=HEADS)
                    if kind == "kept":
                        act.wait_ge(staged, nth(sub, i, s + d))
                        kept = arena[s][:, bass.ds(i * 384 + (QKV_KEPT + 192 * d), 384)]
                        nc.scalar.copy(v_(s, ATT, "qT"), kept[:, 0:128]).then_inc(qk_sb, 1)
                        v = kept[:, 256:384]
                    else:
                        if kind != "linear" and sub != S_MQA:
                            act.wait_ge(qkv_ps, nth(qkv_run[sub], i, s + d, 2, 1))
                            nc.scalar.copy(qkT_of(s), ps[s][3][:, 0:256]).then_inc(qk_sb, 1)
                        act.wait_ge(qkv_ps, nth(qkv_run[sub], i, s + d, 2, 2))
                        v = ps[s][2][:, 128:256]
                    nc.scalar.copy(va[:, :, 0:HD], v.rearrange("p (h d) -> p h d", h=HEADS)).then_inc(v_sb, 1)
                if kind == "linear":
                    for s in range(2):
                        act.wait_ge(lin_min, nth(0, i, s + d))
                        e = v_(s, ATT, "P", 0, 256)
                        nc.scalar.activation(e, e, ACT.Exp).then_inc(lin_exp, 1)

            def body(i, ahead):
                if kind != "linear":
                    for s in range(2):
                        for n, t in enumerate(ORDER):
                            act.wait_ge(s_sub, nth(soft_run[sub], i, s, GROUPS, n + 1))
                            e = v_(s, ATT, "P", 512 * t, 512)
                            if t not in BIASED:
                                nc.scalar.activation(e, e, ACT.Exp, scale=SCALE).then_inc(p_exp, 1)
                                continue
                            for j in range(4):
                                ex = nc.scalar.activation(e[:, 128 * j:128 * j + 128], ps[s][t][:, 128 * j:128 * j + 128],
                                                          ACT.Exp, scale=SCALE, bias=v_(s, ATT, "m", 4 * t + j, 1))
                            ex.then_inc(p_exp, 1)
                        for n, t in enumerate(ORDER):
                            act.wait_ge(pT_ps, nth(soft_run[sub], i, s, GROUPS, n + 1))
                            nc.scalar.copy(v_(s, ATT, "PT", 512 * t, 512), ps[s][t][:, :]).then_inc(pT_sb, 1)
                if sub == S_REG:
                    reg_exp(act, i)
                for s in range(2):
                    act.wait_ge(oT_ps, nth(a, i, s))
                    nc.scalar.copy(v_(s, ATT, "wide", 0, 512), ps[s][1][:, :]).then_inc(oT_sb, 1)
                if sub == S_REG:
                    reg_copy(act, i)
                if ahead and sub != S_REG:
                    front_x(i, 2)
                    front_qkv(i, 2)
                for s in range(2):
                    act.wait_ge(on_ps, nth(a, i, s))
                    nc.scalar.copy(v_(s, ATT, "OnT"), ps[s][1][:, 0:128]).then_inc(on_sb, 1)
                if ahead and sub == S_REG:
                    front_x(i, 2)
                    front_qkv(i, 2)

            def front(i, d):
                front_x(i, d)
                front_qkv(i, d)

            pairs(act, front, body)

        def qkT_of(s):
            a = ATT.at["qT"][0]
            return arena[s][:, a:a + 256]

        def att_dve(dve, sub, kind):
            a = att_run[sub]

            def front_q(i, d):
                for s in range(2):
                    if kind == "linear":
                        dve.wait_ge(qkv_ps, nth(qkv_run[sub], i, s + d, 2, 1))
                        nc.vector.tensor_scalar(v_(s, ATT, "P", 0, 256), ps[s][3][:, 0:256], 0.0, None,
                                                ALU.min).then_inc(lin_min, 1)
                    elif sub == S_MQA:
                        dve.wait_ge(qkv_ps, nth(qkv_run[sub], i, s + d, 2, 1))
                        qk, turn = qkT_of(s), v_(s, ATT, "P", 0, 256)
                        for dst, at, table in ((qk, 0, "cos"), (turn, 256, "sin")):
                            nc.vector.tensor_tensor(heads(dst, 2), heads(ps[s][3][:, at:at + 256], 2),
                                                    cst(table).unsqueeze(1).broadcast_to([128, 2, 128]), ALU.mult)
                        dve.drain()
                        nc.vector.tensor_tensor(qk, qk, turn, ALU.add).then_inc(qk_sb, 1)

            def front_wide(i, d):
                for s in range(2):
                    if kind == "linear":
                        dve.wait_ge(lin_exp, nth(0, i, s + d))
                        qk = qkT_of(s)
                        nc.vector.scalar_tensor_tensor(qk, ps[s][3][:, 0:256], 0.0, v_(s, ATT, "P", 0, 256),
                                                       ALU.max, ALU.add)
                        dve.drain()
                        nc.vector.tensor_scalar(qk[:, 0:128], qk[:, 0:128], 1e-4, SCALE, ALU.add, ALU.mult)
                        nc.vector.tensor_scalar(qk[:, 128:256], qk[:, 128:256], 1e-4, None, ALU.add)
                        dve.drain()
                        dve.sem_inc(qk_sb, 1)
                for s in range(2):
                    if kind == "kept":
                        dve.wait_ge(staged, nth(sub, i, s + d))
                    elif kind != "linear" and sub != S_MQA:
                        dve.wait_ge(qk_sb, nth(a, i, s + d))
                    elif s == 0:
                        dve.drain()
                    for t in WIDE_DVE:
                        widen(nc.vector, i, d, s, kind, t).then_inc(wide_dve_ok, 1)

            def body(i, ahead):
                if kind == "linear":
                    for s in range(2):
                        for n, t in enumerate(ORDER):
                            dve.wait_ge(s_ps, nth(a, i, s, GROUPS, n + 1))
                            nc.vector.tensor_tensor(heads(v_(s, ATT, "PT", 512 * t, 512)), heads(ps[s][t][:, :]),
                                                    cst("triT").unsqueeze(1).broadcast_to([128, 4, 128]),
                                                    ALU.mult).then_inc(pT_sb, 1)
                else:
                    if sub == S_REG:
                        reg_dve_q(dve, i, a)
                    for s in range(2):
                        m = v_(s, ATT, "m")
                        for n, t in enumerate(ORDER):
                            dve.wait_ge(s_ps, nth(a, i, s, GROUPS, n + 1))
                            nc.vector.tensor_reduce(m[:, 4 * t:4 * t + 4], heads(ps[s][t][:, :]), AXX, ALU.max)
                            dve.drain()
                            if t in BIASED:
                                nc.vector.tensor_scalar(m[:, 4 * t:4 * t + 4], m[:, 4 * t:4 * t + 4], -SCALE, None,
                                                        ALU.mult).then_inc(s_sub, 1)
                                continue
                            nc.vector.tensor_tensor(heads(v_(s, ATT, "P", 512 * t, 512)), heads(ps[s][t][:, :]),
                                                    m[:, 4 * t:4 * t + 4].unsqueeze(2).broadcast_to([128, 4, 128]),
                                                    ALU.subtract).then_inc(s_sub, 1)
                if sub == S_REG:
                    reg_dve(dve, i)
                for s in range(2):
                    dve.wait_ge(o_ps, nth(a, i, s))
                    o = ps[s][0][:, :].rearrange("p (h d) -> p h d", d=PAD)
                    rec = v_(s, ATT, "rec")
                    if kind == "linear":
                        nc.vector.tensor_scalar(rec, o[:, :, HD:HD + 1].rearrange("p h d -> p (h d)"), 1e-4, None, ALU.add)
                        dve.drain()
                        nc.vector.reciprocal(rec, rec)
                    else:
                        nc.vector.reciprocal(rec, o[:, :, HD:HD + 1].rearrange("p h d -> p (h d)"))
                    dve.drain()
                    if sub == S_REG:
                        nc.vector.tensor_scalar(rec, rec, cst("regscale"), None, ALU.mult)
                        dve.drain()
                    O = v_(s, ATT, "O").rearrange("p (h d) -> p h d", d=HD)
                    mul = nc.vector.tensor_tensor(O, o[:, :, 0:HD], rec.unsqueeze(2).broadcast_to([128, HEADS, HD]), ALU.mult)
                    if sub == S_REG:
                        dve.drain()
                        dve.wait_ge(reg_add, nth(0, i, s))
                        nc.vector.tensor_tensor(v_(s, ATT, "O"), v_(s, ATT, "O"), ps[s][3][:, 0:128],
                                                ALU.add).then_inc(o_sb, 1)
                    else:
                        mul.then_inc(o_sb, 1)
                if ahead:
                    front_q(i, 2)
                for s in range(2):
                    yb = ps[s][0][:, 0:128]
                    if kind == "linear":
                        dve.wait_ge(y_ps, nth(tail_run[sub], i, s))
                        nc.vector.tensor_copy(v_(s, ATT, "r"), yb)
                        dve.drain()
                        stats(dve, s, ATT, v_(s, ATT, "r")).then_inc(mid_var, 1)
                    else:
                        tail_stats(dve, tail_run[sub], i, s, ATT, yb, x_of(i, s))
                if ahead:
                    front_wide(i, 2)
                if kind == "linear":
                    for s in range(2):
                        dve.wait_ge(mid_rstd, nth(mid_run[S_LIN], i, s))
                        r = v_(s, ATT, "r")
                        norm_affine(dve, s, ATT, r, r, "lin_g", "lin_b")
                        dve.drain()
                        nc.vector.tensor_tensor(r, r, x_of(i, s), ALU.add)
                        dve.drain()
                        stats(dve, s, ATT, r).then_inc(var_ok, 1)
                for s in range(2):
                    tail_norm(dve, tail_run[sub], i, s, ATT)

            def front(i, d):
                front_q(i, d)
                front_wide(i, d)

            pairs(dve, front, body)

        xt_run = {S_X0: 0, S_SIM: 1, S_REG: 2, S_LIN: 3, S_X1: 4, S_MLP: 5, S_X2: 6, S_MQA: 7,
                  S_LAT: 8, S_GATE: 9, S_MOE: 10}
        att_run = {S_X0: 0, S_REG: 1, S_LIN: 2, S_SELF2: 3, S_X2: 4, S_MQA: 5}
        qkv_run = {S_X0: 0, S_REG: 1, S_LIN: 2, S_X2: 3, S_MQA: 4}
        soft_run = {S_X0: 0, S_REG: 1, S_SELF2: 2, S_X2: 3, S_MQA: 4}

        mid_run = {S_LSTM: 0, S_LIN: 1, S_FF1: 2, S_FF2: 3, S_LAT: 4}
        tail_run = {S_LSTM: 0, S_X0: 1, S_REG: 2, S_LIN: 3, S_X1: 4, S_FF1: 5, S_SELF2: 6, S_X2: 7,
                    S_FF2: 8, S_MQA: 9, S_LAT: 10, S_MOE: 11}

        def name_cols(name, of=0, width=None):
            c = W_EARLY if name in W_EARLY.at else W_REST if name in W_REST.at else W_LATE
            return c(name, of, width)

        def reg_dve_q(dve, i, a):
            for s in range(2):
                dve.wait_ge(qk_sb, nth(a, i, s))
                nc.vector.tensor_tensor(v_(s, ATT, "regq").rearrange("p (h r) -> p h r", r=REG),
                                        v_(s, ATT, "qT")[:, 0:REG].unsqueeze(1).broadcast_to([128, HEADS, REG]),
                                        cst("headmask").unsqueeze(2).broadcast_to([128, HEADS, REG]),
                                        ALU.mult).then_inc(reg_q, 1)

        def reg_scores(pe, i, s):
            pe.wait_ge(reg_q, nth(0, i, s))
            bank = ps[s][2][0:REG_ROWS, 0:128]
            nc.tensor.matmul(bank, v_(s, ATT, "regq"), v_(s, ATT, "kT"), start=True, stop=False,
                             skip_group_check=True)
            nc.tensor.matmul(bank, negrow_b[:, :],
                             pos_rows[0:2, 1, bass.ds(i * 2 + s, 1), :].rearrange("p a k -> p (a k)"),
                             start=False, stop=True, skip_group_check=True).then_inc(reg_ps, 1)

        def reg_turn(pe, i):
            for s in range(2):
                pe.wait_ge(reg_n, nth(0, i, s))
                nc.tensor.transpose(ps[s][3][:, 0:REG_ROWS], v_(s, ATT, "P", 0, 128)[0:REG_ROWS, :],
                                    ident[0:REG_ROWS, 0:REG_ROWS]).then_inc(reg_T, 1)

        def reg_output(pe, i):
            for s in range(2):
                pe.wait_ge(reg_Tsb, nth(0, i, s))
                va = arena[s][:, VAUG].rearrange("p (h d) -> p h d", h=HEADS)
                nc.tensor.matmul(ps[s][2][0:REG_ROWS, 0:128], v_(s, ATT, "P", 128, REG_ROWS), va[:, :, 0:HD],
                                 start=True, stop=True, skip_group_check=True).then_inc(reg_o, 1)
            for s in range(2):
                pe.wait_ge(reg_om, nth(0, i, s))
                nc.tensor.matmul(ps[s][3][:, 0:128], cst("regsel")[0:REG_ROWS, :],
                                 v_(s, ATT, "P", 256, 128)[0:REG_ROWS, :],
                                 start=True, stop=True, skip_group_check=True).then_inc(reg_add, 1)

        def reg_exp(act, i):
            for s in range(2):
                act.wait_ge(reg_m, nth(0, i, s))
                nc.scalar.activation(v_(s, ATT, "P", 0, 128)[0:REG_ROWS, :], ps[s][2][0:REG_ROWS, 0:128], ACT.Exp,
                                     bias=v_(s, ATT, "m2", 0, 1)[0:REG_ROWS, :], scale=SCALE,
                                     accum_out=v_(s, ATT, "m2", 1, 1)[0:REG_ROWS, :]).then_inc(reg_e, 1)

        def reg_copy(act, i):
            for s in range(2):
                act.wait_ge(reg_T, nth(0, i, s))
                nc.scalar.copy(v_(s, ATT, "P", 128, REG_ROWS), ps[s][3][:, 0:REG_ROWS]).then_inc(reg_Tsb, 1)

        def reg_dve(dve, i):
            for s in range(2):
                dve.wait_ge(reg_ps, nth(0, i, s))
                nc.vector.tensor_reduce(v_(s, ATT, "m2", 2, 1)[0:REG_ROWS, :], ps[s][2][0:REG_ROWS, 0:128], AXX, ALU.max)
                dve.drain()
                nc.vector.tensor_scalar(v_(s, ATT, "m2", 0, 1)[0:REG_ROWS, :], v_(s, ATT, "m2", 2, 1)[0:REG_ROWS, :],
                                        -SCALE, None, ALU.mult).then_inc(reg_m, 1)
            for s in range(2):
                dve.wait_ge(reg_e, nth(0, i, s))
                nc.vector.reciprocal(v_(s, ATT, "m2", 3, 1)[0:REG_ROWS, :], v_(s, ATT, "m2", 1, 1)[0:REG_ROWS, :])
                dve.drain()
                p = v_(s, ATT, "P", 0, 128)[0:REG_ROWS, :]
                nc.vector.tensor_scalar(p, p, v_(s, ATT, "m2", 3, 1)[0:REG_ROWS, :], None, ALU.mult).then_inc(reg_n, 1)
            for s in range(2):
                dve.wait_ge(reg_o, nth(0, i, s))
                nc.vector.tensor_tensor(v_(s, ATT, "P", 256, 128)[0:REG_ROWS, :], ps[s][2][0:REG_ROWS, 0:128],
                                        cst("blockmask")[0:REG_ROWS, :], ALU.mult).then_inc(reg_om, 1)

        def loads(sp):
            sp.dma_start(bias_cols[:, :], bias).then_inc(bias_in, 16)
            sp.dma_start(WA[:, 0:164], w_early[:, 0:164]).then_inc(first_in, 16)
            sp.dma_start(C[:, :], const).then_inc(first_in, 16)
            sp.dma_start(xT_all[:, :, :], x_T).then_inc(first_in, 16)
            sp.dma_start(R[:, :], rows).then_inc(loaded, 16)
            sp.dma_start(WA[:, W_EARLY("ff1_up", 0, 2 * FF)], w_early[:, W_EARLY("ff1_up", 0, 2 * FF)]).then_inc(loaded, 16)
            sp.dma_start(WB[:, :], w_rest).then_inc(loaded, 16)
            sp.wait_ge(bias_cut, 1)
            for k in range(3):
                sp.dma_start(bias3[k:k + 1, :], bias_parts[:, k, :]).then_inc(bias_rows, 16)
            sp.dma_start(x_all[:, :, :], x_tok).then_inc(loaded, 16)
            sp.dma_start(arena[1][:, 0:2048].bitcast(I32), mask).then_inc(mask_in, 16)
            sp.dma_start(arena[1][0:1, 2048:4096].bitcast(I32), mask_row).then_inc(mask_in, 16)
            sp.dma_start(ctxT_all[:, :, :], ctx_T).then_inc(rest_in, 16)
            a, b = 164, W_EARLY.at["ff1_up"][0]
            sp.dma_start(WA[:, a:b], w_early[:, a:b]).then_inc(rest_in, 16)
            a = W_EARLY.at["mlp_up"][0]
            sp.dma_start(WA[:, a:W_EARLY.size], w_early[:, a:]).then_inc(rest_in, 16)

        loads_first, loads_early, loads_rest = 3, 4, 3
        TERN = (("ff1_up", 0), ("ff1_down", 1), ("ff2_up", 2), ("ff2_down", 3))

        def W_of(name, of=0, width=None):
            return (WA if name in W_EARLY.at or name in W_LATE.at else WB)[:, name_cols(name, of, width)]

        def start_act(act):
            act.wait_ge(loaded, 16 * loads_early)
            for name, k in TERN:
                nc.scalar.activation(abs_out[:, :], W_of(name), ACT.Abs, accum_out=small[:, k:k + 1])
                act.drain()
            act.sem_inc(w_sum, 1)

        def start_pe(pe):
            pe.wait_ge(w_sum, 1)
            nc.tensor.matmul(ps[0][0][:, 0:4], ones_f[:, :], small[:, 0:4], start=True, stop=True).then_inc(w_mean, 1)

        def start_dve(dve):
            nc.vector.memset(ones_f[:, :], 1.0)
            nc.vector.memset(ones_b[:, :], 1.0)
            for k in range(2):
                nc.vector.memset(hid[k][:, :], 0.0)
            nc.vector.memset(gates[:, :, :], 0.0)
            nc.vector.memset(half_b[:, :], 0.5)
            nc.vector.memset(minus_round[:, :], -ROUND)
            dve.wait_ge(bias_in, 16)
            hi, mid, lo = (bias_parts[:, k, :] for k in range(3))
            b = bias_cols[:, :]
            nc.vector.tensor_copy(hi, b)
            dve.drain()
            nc.vector.tensor_tensor(b, b, hi, ALU.subtract)
            dve.drain()
            nc.vector.tensor_copy(mid, b)
            dve.drain()
            nc.vector.tensor_tensor(lo, b, mid, ALU.subtract).then_inc(bias_cut, 1)
            dve.wait_ge(first_in, 16 * loads_first)
            nc.vector.tensor_copy(ident_b[:, :], ident)
            nc.vector.tensor_copy(causal_b[:, :], cst("causal"))
            nc.vector.tensor_copy(negrow_b[:, :], ident[0:2, 1:2].broadcast_to([2, REG_ROWS]))
            ih, hh, ms = W_of("ih"), W_of("hh"), W_of("musig")
            nc.vector.tensor_scalar(ih[:, 0:60], ih[:, 0:60], 0.5, None, ALU.mult)
            nc.vector.tensor_scalar(hh[:, 0:60], hh[:, 0:60], 0.25, None, ALU.mult)
            nc.vector.tensor_scalar(hh[:, 60:80], hh[:, 60:80], 0.5, None, ALU.mult)
            nc.vector.tensor_scalar(ms, ms, 0.5, None, ALU.mult)
            dve.drain()
            dve.sem_inc(const_b, 1)

        def mean_dve(dve):
            dve.wait_ge(w_mean, 1)
            mean, inv, back = small[:, 4:8], small[:, 8:12], small[:, 12:16]
            nc.vector.tensor_scalar(mean, ps[0][0][:, 0:4], 1.0 / (DIM * FF), 1e-5, ALU.mult, ALU.max)
            dve.drain()
            nc.vector.reciprocal(inv, mean)
            dve.drain()
            nc.vector.reciprocal(back, inv)
            g = R[:, ROWS("g_query")]
            nc.vector.tensor_tensor(gsq[:, :], g, g, ALU.mult)
            dve.drain()
            nc.vector.tensor_reduce(small[:, 16:32], gsq[:, :].rearrange("p (h d) -> p h d", d=HD), AXX, ALU.add)
            dve.drain()
            dve.sem_inc(w_mean, 1)

        ones_f = arena[0][:, QKV_KEPT + 1088:QKV_KEPT + 1216]
        bias_cols = arena[1][:, 4096:4096 + BIAS_COLS]
        bias_parts = arena[1][:, 4352:4352 + (3 * BIAS_COLS + 1) // 2].bitcast(BF16)[:, 0:3 * BIAS_COLS].rearrange(
            "p (k n) -> p k n", k=3)
        gsq = arena[1][:, 8192:8320]
        abs_out = arena[1][:, 8320:8320 + FF]
        sim_all = arena[0][:, QKV_KEPT + 512:QKV_KEPT + 1024].rearrange("p (a b h) -> p a b h", a=2, b=BATCH)
        pos64 = arena[0][:, QKV_KEPT + 1216:QKV_KEPT + 1280].rearrange("p (a b) -> p a b", a=4)
        pos64T = arena[0][0:64, QKV_KEPT + 1280:QKV_KEPT + 1344].bitcast(BF16)

        def start_pool(pool):
            pool.wait_ge(mask_in, 32)
            m32 = arena[1][:, 0:2048].bitcast(I32)
            nc.gpsimd.tensor_scalar(maskadd[:, :, :].rearrange("p b k -> p (b k)"), m32, 0.0, NEG, ALU.is_equal, ALU.mult)
            nc.gpsimd.tensor_scalar(mrow[:, :, :].rearrange("p b k -> p (b k)"),
                                    arena[1][0:1, 2048:4096].bitcast(I32), 0.0, BIG, ALU.is_equal, ALU.mult)
            pool.wait_ge(w_mean, 2)
            nc.gpsimd.tensor_tensor(small[:, 32:48], small[:, 16:32], cst("minushalf"), ALU.pow)
            for name, k in TERN:
                w = W_of(name)
                nc.gpsimd.tensor_scalar(abs_out[:, :], w, small[:, 8 + k:9 + k], None, ALU.mult)
                pool.drain()
                nc.gpsimd.tensor_scalar(abs_out[:, :], abs_out[:, :], ROUND, None, ALU.add)
                pool.drain()
                nc.gpsimd.tensor_scalar(abs_out[:, :], abs_out[:, :], -ROUND, None, ALU.add)
                pool.drain()
                dst = {2: tern_up[:, :], 3: tern_down[:, :, :].rearrange("p a d -> p (a d)")}.get(k, abs_out[:, :])
                nc.gpsimd.tensor_scalar(dst, abs_out[:, :], 1.0, -1.0, ALU.min, ALU.max)
                pool.drain()
                if k < 2:
                    nc.gpsimd.tensor_scalar(abs_out[:, :], abs_out[:, :], small[:, 12 + k:13 + k], None, ALU.mult)
                    pool.drain()
                    nc.gpsimd.tensor_tensor(abs_out[:, :], abs_out[:, :], w, ALU.subtract)
                    pool.drain()
                    nc.gpsimd.tensor_tensor(w, w, abs_out[:, :], ALU.add)
                    pool.drain()
            for s in range(2):
                nc.gpsimd.memset(arena[s][:, VAUG], 0.0)
                pool.drain()
                nc.gpsimd.memset(arena[s][:, VAUG].rearrange("p (h d) -> p h d", h=HEADS)[:, :, HD:HD + 1], 1.0)
            pool.drain()
            pool.sem_inc(w_tern, 2)
            pool.sem_inc(seq_done, 2)

        STEPS, HALF = 16, 8
        gate_banks = [ps[0][1], ps[0][2]]
        ms_bank = ps[1][0]
        ms_all = arena[1][0:BATCH, 8832:9344].rearrange("p (t n) -> p t n", n=4)
        scan_t = arena[1][0:BATCH, 9344:10112].rearrange("p (n t) -> p n t", n=6)

        def lstm_pe(pe):
            pe.wait_ge(bias_rows, 48)
            pe.wait_ge(const_b, 1)

            def bank(half):
                return gate_banks[half][0:LSTM_H, :].rearrange("p (t g b) -> p t g b", t=HALF, g=4)

            def inputs(it, half, gt):
                xs = xT_all[:, :, bass.ds(it * STEPS + half * HALF, HALF)].rearrange("p b t -> p t b")
                o = bank(half % 2)[:, :, gt, :]
                nc.tensor.matmul(o, W_of("ih")[:, 20 * gt:20 * gt + 20], xs, start=gt == 0, stop=False,
                                 skip_group_check=True)
                for name in ("ih", "hh"):
                    nc.tensor.matmul(o, bias3[:, BIAS(name, 20 * gt, 20)],
                                     (half_b if gt < 3 else ones_b)[0:3, :].rearrange("p (t b) -> p t b", t=HALF),
                                     start=False, stop=False, skip_group_check=True)

            def turn(it, ahead=True):
                for k in range(STEPS):
                    g = bank(k // HALF)
                    pe.wait_ge(hid_new, it * STEPS + (k + 1))
                    h = hid[(k + 1) % 2][:, :]
                    for gt in range(4):
                        mm = nc.tensor.matmul(g[:, k % HALF, gt, :], W_of("hh")[:, 20 * gt:20 * gt + 20], h,
                                              start=False, stop=True, skip_group_check=True)
                    mm.then_inc(gates_sum, 1)
                    if k > 0:
                        nc.tensor.matmul(ms_bank[0:BATCH, 4 * (k - 1):4 * k], h, W_of("musig"),
                                         start=True, stop=True, skip_group_check=True)
                    if k < 4:
                        inputs(it, 1, k)
                    elif HALF <= k < HALF + 4 and ahead:
                        inputs(it, 2, k - HALF)
                pe.wait_ge(hid_new, it * STEPS + (STEPS + 1))
                nc.tensor.matmul(ms_bank[0:BATCH, 4 * (STEPS - 1):4 * STEPS], hid[1][:, :], W_of("musig"),
                                 start=True, stop=True, skip_group_check=True).then_inc(musig_sum, 1)
                pe.wait_ge(musig_kept, it + 1)

            for gt in range(4):
                inputs(0, 0, gt)
            turn(0)
            start_pe(pe)
            with pe.Fori(1, TOK // STEPS - 1) as it:
                turn(it)
            turn(TOK // STEPS - 1, False)
            pe.wait_ge(scan_out, 2)
            nc.tensor.transpose(ps[0][1][:, 0:16], scan_t[:, 4, :], ident[0:16, 0:16])
            nc.tensor.transpose(ps[0][1][:, 16:32], scan_t[:, 5, :], ident[0:16, 0:16]).then_inc(scan_ps, 1)

        def lstm_act(act):
            def turn(it):
                for k in range(STEPS):
                    g = gate_banks[k // HALF][0:LSTM_H, :].rearrange("p (t n) -> p t n", t=HALF)
                    act.wait_ge(gates_sum, it * STEPS + k + 1)
                    nc.scalar.activation(gates[:, 0:4, :].rearrange("p g b -> p (g b)"), g[:, k % HALF, :],
                                         ACT.Tanh).then_inc(gates_tanh, 1)
                    act.wait_ge(cell_new, it * STEPS + k + 1)
                    nc.scalar.activation(tanh_c[:, :], gates[:, 4, :], ACT.Tanh, scale=0.5).then_inc(cell_tanh, 1)
                act.wait_ge(musig_sum, it + 1)
                nc.scalar.copy(ms_all[:, bass.ds(it * STEPS, STEPS), :],
                               ms_bank[0:BATCH, 0:4 * STEPS].rearrange("p (t n) -> p t n", n=4)).then_inc(musig_kept, 1)

            turn(0)
            start_act(act)
            with act.Fori(1, TOK // STEPS) as it:
                turn(it)
            act.wait_ge(scan_out, 1)
            nc.scalar.activation(scan_t[:, 3, :], scan_t[:, 3, :], ACT.Exp, scale=-1.0).then_inc(scan_exp, 1)

        def lstm_dve(dve):
            dve.sem_inc(hid_new, 1)

            def turn(it):
                for k in range(STEPS):
                    dve.wait_ge(gates_tanh, it * STEPS + k + 1)
                    nc.vector.scalar_tensor_tensor(prod[:, :, :], gates[:, 0:2, :], 1.0, gates[:, 3:5, :], ALU.add, ALU.mult)
                    dve.drain()
                    nc.vector.scalar_tensor_tensor(gates[:, 4, :], prod[:, 1, :], 0.5, prod[:, 0, :],
                                                   ALU.mult, ALU.add).then_inc(cell_new, 1)
                    dve.wait_ge(cell_tanh, it * STEPS + k + 1)
                    nc.vector.scalar_tensor_tensor(hid[k % 2][0:LSTM_H, :], gates[:, 2, :], 1.0, tanh_c[:, :],
                                                   ALU.add, ALU.mult).then_inc(hid_new, 1)

            turn(0)
            mean_dve(dve)
            with dve.Fori(1, TOK // STEPS) as it:
                turn(it)
            dve.wait_ge(musig_kept, TOK // STEPS)
            z = ms_all[:, :, :]
            nc.vector.tensor_tensor(z, z, R[0:BATCH, ROWS("mu_b")].unsqueeze(1).broadcast_to([BATCH, TOK, 4]), ALU.add)
            dve.drain()
            zc = z.rearrange("p t n -> p n t")
            nc.vector.tensor_copy(scan_t[:, 3, :], zc[:, 3, :]).then_inc(scan_out, 1)
            nc.vector.tensor_scalar(scan_t[:, 0:3, :], zc[:, 0:3, :], 0.0, None, ALU.max)
            dve.drain()
            nc.vector.tensor_tensor(scan_t[:, 2, :], scan_t[:, 2, :], cst("step")[0:BATCH, :], ALU.mult)
            dve.drain()
            nc.vector.scalar_tensor_tensor(scan_t[:, 1, :], scan_t[:, 1, :], 1.0 / TOK, scan_t[:, 2, :], ALU.mult, ALU.add)
            dve.drain()
            nc.vector.tensor_tensor_scan(scan_t[:, 4, :], scan_t[:, 0, :], scan_t[:, 1, :], 0.0, ALU.mult, ALU.add)
            dve.drain()
            nc.vector.tensor_scalar(scan_t[:, 4, :], scan_t[:, 4, :], -1.0, None, ALU.mult)
            dve.wait_ge(scan_exp, 1)
            nc.vector.tensor_scalar(scan_t[:, 5, :], scan_t[:, 3, :], 1.0, None, ALU.add)
            dve.drain()
            dve.sem_inc(scan_out, 1)
            dve.wait_ge(scan_ps, 1)
            nc.vector.tensor_copy(mu_cols[:, 0:2, :], ps[0][1][:, 0:32].rearrange("p (a b) -> p a b", a=2))
            dve.drain()
            nc.vector.scalar_tensor_tensor(mu_cols[:, 1, :], mu_cols[:, 1, :], -0.5, mu_cols[:, 1, :], ALU.mult, ALU.mult)
            dve.drain()
            dve.sem_inc(scan_cols, 1)

        def pos_pool(pool):
            pool.wait_ge(scan_cols, 1)
            def stage(i, d):
                for s in range(2):
                    if d == 0:
                        pool.wait_ge(seq_done, nth(S_LSTM, i, s))
                    else:
                        pool.wait_ge(y_ps, nth(tail_run[S_LSTM], i, s))
                    nc.gpsimd.tensor_copy(v_(s, ATT, "x"), x_at(x_all, i, s + d))
                    pool.drain()
                    pool.sem_inc(staged, 1)

            def body(i, ahead):
                for s in range(2):
                    rstd(pool, mid_var, mid_rstd, mid_run[S_LSTM], i, s, ATT)
                for s in range(2):
                    rstd(pool, var_ok, rstd_ok, tail_run[S_LSTM], i, s, ATT)
                if ahead:
                    stage(i, 2)

            pairs(pool, stage, body)

        def pos_act(act):
            def front(i, d):
                for s in range(2):
                    if d == 0:
                        act.wait_ge(staged, nth(S_LSTM, i, s))
                    b = i * 2 + (s + d)
                    nc.scalar.activation(v_(s, ATT, "P", 0, 128), cst("rel"), ACT.Square,
                                         bias=mu_cols[:, 0, bass.ds(b, 1)])
                    act.drain()
                    nc.scalar.activation(v_(s, ATT, "P", 0, 128), v_(s, ATT, "P", 0, 128), ACT.Exp,
                                         scale=mu_cols[:, 1, bass.ds(b, 1)]).then_inc(pos_w, 1)

            def body(i, ahead):
                for s in range(2):
                    act.wait_ge(pos_masked, nth(0, i, s))
                    nc.scalar.activation(v_(s, ATT, "P", 256, 128), v_(s, ATT, "P", 128, 128), ACT.Square,
                                         accum_out=v_(s, ATT, "m2", 0, 1)).then_inc(pos_sq, 1)
                for s in range(2):
                    act.wait_ge(pos_T, nth(0, i, s))
                    nc.scalar.copy(v_(s, ATT, "PT", 0, 128), ps[s][0][:, 0:128]).then_inc(pos_T_sb, 1)
                if ahead:
                    front(i, 2)

            pairs(act, front, body)

        def pos_pe(pe):
            with pe.Fori(0, PAIRS) as i:
                for s in range(2):
                    pe.wait_ge(pos_masked, nth(0, i, s))
                    nc.tensor.transpose(ps[s][0][:, 0:128], v_(s, ATT, "P", 128, 128), ident).then_inc(pos_T, 1)
                for s in range(2):
                    pe.wait_ge(staged, nth(S_LSTM, i, s))
                    pe.wait_ge(pos_T_sb, nth(0, i, s))
                    nc.tensor.matmul(ps[s][1][:, 0:128], v_(s, ATT, "PT", 0, 128), v_(s, ATT, "x"),
                                     start=True, stop=True).then_inc(y_ps, 1)

        def pos_dve(dve):
            def front(i, d):
                for s in range(2):
                    dve.wait_ge(pos_w, nth(0, i, s + d))
                    nc.vector.tensor_tensor(v_(s, ATT, "P", 128, 128), v_(s, ATT, "P", 0, 128), cst("tri"),
                                            ALU.mult).then_inc(pos_masked, 1)

            def body(i, ahead):
                for s in range(2):
                    dve.wait_ge(pos_sq, nth(0, i, s))
                    nc.vector.tensor_scalar(v_(s, ATT, "mv", 1, 1), v_(s, ATT, "m2", 0, 1), 1e-24, None,
                                            ALU.max).then_inc(mid_var, 1)
                for s in range(2):
                    dve.wait_ge(mid_rstd, nth(mid_run[S_LSTM], i, s))
                    dve.wait_ge(y_ps, nth(tail_run[S_LSTM], i, s))
                    nc.vector.scalar_tensor_tensor(v_(s, ATT, "r"), ps[s][1][:, 0:128], v_(s, ATT, "rstd"),
                                                   x_of(i, s), ALU.mult, ALU.add)
                    dve.drain()
                    stats(dve, s, ATT, v_(s, ATT, "r")).then_inc(var_ok, 1)
                if ahead:
                    front(i, 2)
                for s in range(2):
                    tail_norm(dve, tail_run[S_LSTM], i, s, ATT)

            pairs(dve, front, body)

        all_done = 2 + BATCH

        def sim_pool_(pool):
            nc.gpsimd.memset(xT_all[:, :, :], 0.0).then_inc(sim_pool, 1)
            stage_ahead(pool, S_SIM, ATT)
            pool.wait_ge(rows_in, 64)

        def sim_sp(sp):
            sp.wait_ge(sim_mid, 5)
            sp.wait_ge(sim_pool, 1)
            for side in range(2):
                for r in range(2):
                    q = 32 * side + 16 * r
                    sp.dma_start(pos_rows[r:r + 1, side, :, :], pos64T[q:q + 16, :]).then_inc(rows_in, 16)

        def sim_pe(pe):
            with pe.Fori(0, PAIRS) as i:
                for s in range(2):
                    transpose_x(pe, S_SIM, i, s, ATT)
                for s in range(2):
                    pe.wait_ge(xT_sb, nth(xt_run[S_SIM], i, s))
                    pe.wait_ge(seq_done, nth(S_SIM, i, s))
                    nc.tensor.matmul(ps[s][1][:, 0:128], v_(s, ATT, "xcT", 0, 128), WA[:, W_EARLY("reg", 0, 128)],
                                     start=True, stop=True).then_inc(sim_q, 1)
            pe.wait_ge(sim_mid, 1)
            nc.tensor.transpose(ps[0][0][0:16, 0:128], small[:, 48:64], ident).then_inc(sim_rows, 1)
            pe.wait_ge(sim_mid, 2)
            nc.tensor.transpose(ps[0][1][0:2, 0:16], small[0:16, 64:66], ident[0:16, 0:16]).then_inc(sim_rows, 1)
            pe.wait_ge(sim_mid, 3)
            nc.tensor.matmul(ps[0][2][:, 0:2], ones_f[0:2, :], small[0:2, 68:70], start=True, stop=True).then_inc(sim_rows, 1)
            pe.wait_ge(sim_mid, 4)
            nc.tensor.transpose(ps[0][3][0:64, 0:128], pos64[:, :, :].rearrange("p a b -> p (a b)"), ident).then_inc(sim_rows, 1)
            pe.wait_ge(rows_in, 64)

        def sim_act(act):
            with act.Fori(0, PAIRS) as i:
                for s in range(2):
                    act.wait_ge(xT_ps, nth(xt_run[S_SIM], i, s))
                    nc.scalar.copy(v_(s, ATT, "xcT", 0, 128), ps[s][0][:, 0:128]).then_inc(xT_sb, 1)
                for s in range(2):
                    act.wait_ge(seq_done, nth(S_SIM, i, s))
                    act.wait_ge(sim_q, nth(0, i, s))
                    nc.scalar.copy(v_(s, ATT, "wide", 0, 128), ps[s][1][:, 0:128])
                    nc.scalar.activation(v_(s, ATT, "wide", 128, 128), ps[s][1][:, 0:128], ACT.Square)
                    act.drain()
                    act.sem_inc(sim_sb, 1)
            act.wait_ge(seq_done, all_done + BATCH * S_SIM)
            nc.scalar.activation(sim_root, sim_all[:, 0, :, :].rearrange("p b h -> p (b h)"), ACT.Sqrt).then_inc(sim_sb, 1)

        sim_root = v_(0, ATT, "P", 768, 256)

        def sim_dve(dve):
            dve.wait_ge(w_tern, 1)
            g3 = R[:, ROWS("g_query")].rearrange("p (h d) -> p h d", d=HD)
            nc.vector.tensor_tensor(g3, g3, small[:, 32:48].unsqueeze(2).broadcast_to([128, HEADS, HD]), ALU.mult)
            dve.drain()
            with dve.Fori(0, PAIRS) as i:
                for s in range(2):
                    dve.wait_ge(sim_sb, nth(0, i, s))
                    b = i * 2 + s
                    q, sq = v_(s, ATT, "wide", 0, 128), v_(s, ATT, "wide", 128, 128)
                    nc.vector.tensor_reduce(sim_all[:, 0, bass.ds(b, 1), :].rearrange("p a h -> p (a h)"),
                                            sq.rearrange("p (h d) -> p h d", d=HD), AXX, ALU.add)
                    nc.vector.tensor_tensor(v_(s, ATT, "r"), q, R[:, ROWS("g_query")], ALU.mult)
                    dve.drain()
                    nc.vector.tensor_reduce(sim_all[:, 1, bass.ds(b, 1), :].rearrange("p a h -> p (a h)"),
                                            v_(s, ATT, "r").rearrange("p (h d) -> p h d", d=HD), AXX,
                                            ALU.add).then_inc(seq_done, 1)
            n2, dot = (sim_all[:, k, :, :].rearrange("p b h -> p (b h)") for k in range(2))
            dve.wait_ge(sim_sb, BATCH + 1)
            y, z = sim_root, v_(0, ATT, "P", 512, 256)
            nc.vector.reciprocal(y, y)
            dve.drain()
            nc.vector.tensor_tensor(z, y, y, ALU.mult)
            dve.drain()
            nc.vector.scalar_tensor_tensor(z, z, -0.5, n2, ALU.mult, ALU.mult)
            dve.drain()
            nc.vector.scalar_tensor_tensor(n2, z, 1.5, y, ALU.add, ALU.mult)
            dve.drain()
            sim = small[:, 48:64]
            nc.vector.tensor_tensor(dot, dot, n2, ALU.mult)
            dve.drain()
            nc.vector.tensor_reduce(sim, sim_all[:, 1, :, :], AXX, ALU.add)
            dve.drain()
            nc.vector.tensor_scalar(sim, sim, 1.0 / HEADS, None, ALU.mult).then_inc(sim_mid, 1)
            dve.wait_ge(sim_rows, 1)
            nc.vector.tensor_reduce(small[0:16, 64:65], ps[0][0][0:16, REG:TOK], AXX, ALU.max)
            nc.vector.tensor_reduce(small[0:16, 65:66], ps[0][0][0:16, REG:TOK], AXX, ALU.min)
            dve.drain()
            nc.vector.tensor_scalar(small[0:16, 65:66], small[0:16, 65:66], -1.0, None, ALU.mult).then_inc(sim_mid, 1)
            dve.wait_ge(sim_rows, 2)
            nc.vector.tensor_reduce(small[0:2, 67:68], ps[0][1][0:2, 0:16], AXX, ALU.max)
            dve.drain()
            nc.vector.tensor_scalar(small[0:2, 68:70], ident[0:2, 0:2], small[0:2, 67:68], None, ALU.mult).then_inc(sim_mid, 1)
            dve.wait_ge(sim_rows, 3)
            nc.vector.tensor_copy(small[:, 70:72], ps[0][2][:, 0:2])
            dve.drain()
            nc.vector.tensor_tensor(small[:, 72:73], small[:, 70:71], small[:, 71:72], ALU.add)
            dve.drain()
            nc.vector.reciprocal(small[:, 73:74], small[:, 72:73])
            dve.drain()
            nc.vector.tensor_scalar(sim, sim, small[:, 71:72], small[:, 73:74], ALU.add, ALU.mult)
            dve.drain()
            pos = small[:, 80:96]
            nc.vector.tensor_scalar(pos, sim, 0.9, None, ALU.is_gt)
            dve.drain()
            notreg = cst("notreg")
            nc.vector.tensor_scalar(pos64[:, 3, :], pos, notreg, BIG, ALU.mult, ALU.mult)
            nc.vector.tensor_scalar(pos64[:, 2, :], pos, -1.0, 1.0, ALU.mult, ALU.add)
            nc.vector.tensor_scalar(pos64[:, 0, :], pos, -1.0, notreg, ALU.add, ALU.mult)
            dve.drain()
            nc.vector.tensor_scalar(pos64[:, 2, :], pos64[:, 2, :], notreg, BIG, ALU.mult, ALU.mult)
            nc.vector.tensor_scalar(pos64[:, 1, :], pos64[:, 0, :], -1.0, None, ALU.mult)
            nc.vector.tensor_scalar(small[:, 96:112], pos64[:, 0, :], 1.0, None, ALU.add)
            dve.drain()
            nc.vector.tensor_copy(pos64[:, 0, :], small[:, 96:112])
            dve.drain()
            dve.sem_inc(sim_mid, 1)
            dve.wait_ge(sim_rows, 4)
            nc.vector.tensor_copy(pos64T[:, :], ps[0][3][0:64, 0:128]).then_inc(sim_mid, 1)

        WSCALE = 1.0 / math.sqrt(DIM)

        def wide_pool(pool):
            def stage(i, d):
                for s in range(2):
                    if d == 0:
                        pool.wait_ge(seq_done, nth(S_X1, i, s))
                    else:
                        pool.wait_ge(w_s, nth(0, i, s))
                    nc.gpsimd.tensor_copy(v_(s, ATT, "c"), x_at(ctxT_all, i, s + d))
                    nc.gpsimd.tensor_copy(v_(s, ATT, "x"), x_at(x_all, i, s + d))
                    pool.drain()
                    pool.sem_inc(staged, 1)

            def body(i, ahead):
                if ahead:
                    stage(i, 2)
                for s in range(2):
                    rstd(pool, var_ok, rstd_ok, tail_run[S_X1], i, s, ATT)

            pairs(pool, stage, body)

        def wide_pe(pe):
            ones3 = ones_b[0:3, :]

            def front_x(i, d):
                for s in range(2):
                    pe.wait_ge(staged, nth(S_X1, i, s + d))
                    nc.tensor.transpose(ps[s][2][:, 0:128], v_(s, ATT, "x"), ident).then_inc(xT_ps, 1)

            def front_qkv(i, d):
                for s in range(2):
                    pe.wait_ge(xT_sb, nth(xt_run[S_X1], i, s + d))
                    xT, cT, bank = v_(s, ATT, "xcT"), v_(s, ATT, "c"), ps[s][1]
                    for k, src in ((0, xT), (1, cT)):
                        nc.tensor.matmul(bank[:, 128 * k:128 * k + 128], WA[:, W_EARLY("x1", 128 * k, 128)], src,
                                         start=True, stop=False, skip_group_check=True)
                        nc.tensor.matmul(bank[:, 128 * k:128 * k + 128], bias3[:, BIAS("x1", 128 * k, 128)], ones3,
                                         start=False, stop=True, skip_group_check=True)
                    nc.tensor.matmul(bank[:, 256:384], cT, WA[:, W_EARLY("x1", 256, 128)], start=True, stop=False,
                                     skip_group_check=True)
                    add_bias(bank[:, 256:384], "x1", 256, 128).then_inc(w_qk, 1)

            def body(i, ahead):
                for s in range(2):
                    pe.wait_ge(w_qk_sb, nth(0, i, s))
                    bank = ps[s][2][:, 0:128]
                    nc.tensor.matmul(bank, v_(s, ATT, "wide", 0, 128), v_(s, ATT, "wide", 128, 128), start=True,
                                     stop=False, skip_group_check=True)
                    nc.tensor.matmul(bank, ones_b[0:1, :], x_at(mrow, i, s),
                                     start=False, stop=True, skip_group_check=True).then_inc(w_s, 1)
                for s in range(2):
                    pe.wait_ge(w_e, nth(0, i, s))
                    nc.tensor.transpose(ps[s][3][:, 0:128], v_(s, ATT, "P", 0, 128), ident).then_inc(w_T, 1)
                if ahead:
                    front_x(i, 2)
                for s in range(2):
                    pe.wait_ge(w_Tsb, nth(0, i, s))
                    nc.tensor.matmul(ps[s][0][:, 0:128], v_(s, ATT, "PT", 0, 128), v_(s, ATT, "wide", 256, 128),
                                     start=True, stop=True).then_inc(y_ps, 1)
                if ahead:
                    front_qkv(i, 2)

            def front(i, d):
                front_x(i, d)
                front_qkv(i, d)

            pairs(pe, front, body)

        def wide_act(act):
            def front_x(i, d):
                for s in range(2):
                    act.wait_ge(xT_ps, nth(xt_run[S_X1], i, s + d))
                    nc.scalar.copy(v_(s, ATT, "xcT", 0, 128), ps[s][2][:, 0:128]).then_inc(xT_sb, 1)

            def front_qkv(i, d):
                for s in range(2):
                    act.wait_ge(w_qk, nth(0, i, s + d))
                    nc.scalar.copy(v_(s, ATT, "wide", 0, 384), ps[s][1][:, 0:384]).then_inc(w_qk_sb, 1)

            def body(i, ahead):
                for s in range(2):
                    act.wait_ge(w_m, nth(0, i, s))
                    nc.scalar.activation(v_(s, ATT, "P", 0, 128), ps[s][2][:, 0:128], ACT.Exp, scale=WSCALE,
                                         bias=v_(s, ATT, "m2", 0, 1), accum_out=v_(s, ATT, "m2", 1, 1)).then_inc(w_e, 1)
                for s in range(2):
                    act.wait_ge(w_T, nth(0, i, s))
                    nc.scalar.copy(v_(s, ATT, "PT", 0, 128), ps[s][3][:, 0:128]).then_inc(w_Tsb, 1)
                if ahead:
                    front_x(i, 2)
                    front_qkv(i, 2)

            def front(i, d):
                front_x(i, d)
                front_qkv(i, d)

            pairs(act, front, body)

        def wide_dve(dve):
            with dve.Fori(0, PAIRS) as i:
                for s in range(2):
                    dve.wait_ge(w_s, nth(0, i, s))
                    nc.vector.tensor_reduce(v_(s, ATT, "m2", 2, 1), ps[s][2][:, 0:128], AXX, ALU.max)
                    dve.drain()
                    nc.vector.tensor_scalar(v_(s, ATT, "m2", 0, 1), v_(s, ATT, "m2", 2, 1), -WSCALE, None,
                                            ALU.mult).then_inc(w_m, 1)
                for s in range(2):
                    dve.wait_ge(w_e, nth(0, i, s))
                    nc.vector.reciprocal(v_(s, ATT, "m2", 3, 1), v_(s, ATT, "m2", 1, 1))
                    dve.drain()
                    dve.wait_ge(y_ps, nth(tail_run[S_X1], i, s))
                    nc.vector.scalar_tensor_tensor(v_(s, ATT, "r"), ps[s][0][:, 0:128], v_(s, ATT, "m2", 3, 1),
                                                   x_of(i, s), ALU.mult, ALU.add)
                    dve.drain()
                    stats(dve, s, ATT, v_(s, ATT, "r")).then_inc(var_ok, 1)
                for s in range(2):
                    tail_norm(dve, tail_run[S_X1], i, s, ATT)

        ff_run = {S_FF1: 0, S_FF2: 1}
        ff_v1, ff_r1 = sem("ff_v1"), sem("ff_r1")

        def ff_pool(pool, sub):
            f, pre = ff_run[sub], "ff2_" if sub == S_FF2 else "ff1_"

            def front(i, d):
                for s in range(2):
                    if d == 0:
                        pool.wait_ge(seq_done, nth(sub, i, s))
                    else:
                        pool.wait_ge(h_sb, nth(f, i, s))
                    nc.gpsimd.tensor_copy(v_(s, FFN, "x"), x_at(x_all, i, s + d))
                    pool.drain()
                    pool.sem_inc(staged, 1)
                for s in range(2):
                    pool.wait_ge(ff_v1, nth(f, i, s + d))
                    nc.gpsimd.tensor_tensor(v_(s, FFN, "rstd", 1, 1), v_(s, FFN, "mv", 3, 1),
                                            cst("minushalf")[:, 0:1], ALU.pow).then_inc(ff_r1, 1)

            def body(i, ahead):
                if ahead:
                    front(i, 2)
                for s in range(2):
                    rstd(pool, mid_var, mid_rstd, mid_run[sub], i, s, FFN)
                    if sub == S_FF1 or s == 0:
                        continue
                    pool.drain()
                    n = v_(s, FFN, "n")
                    nc.gpsimd.tensor_scalar(n, v_(s, FFN, "u"), v_(s, FFN, "mv", 0, 1), v_(s, FFN, "rstd", 0, 1),
                                            ALU.subtract, ALU.mult)
                    pool.drain()
                    nc.gpsimd.tensor_tensor(n, n, R[:, ROWS(pre + "g2")], ALU.mult)
                    pool.drain()
                    nc.gpsimd.tensor_tensor(n, n, R[:, ROWS(pre + "b2")],
                                            ALU.add).then_inc(n_normed, 1)
                for s in range(2):
                    rstd(pool, var_ok, rstd_ok, tail_run[sub], i, s, FFN)

            pairs(pool, front, body)

        def ff_pe(pe, sub):
            quant, f = sub == S_FF2, ff_run[sub]

            def front(i, d):
                for s in range(2):
                    pe.wait_ge(h_sb, nth(f, i, s + d))
                    nc.tensor.transpose(ps[s][0][:, 0:128], v_(s, FFN, "h"), ident).then_inc(hT_ps, 1)

            def body(i, ahead):
                for s in range(2):
                    pe.wait_ge(hT_sb, nth(f, i, s))
                    if quant:
                        nc.tensor.matmul(ps[s][1][:, :], v_(s, FFN, "hbT").bitcast(BF16), tern_up[:, :],
                                         start=True, stop=True).then_inc(up_ps, 1)
                    else:
                        nc.tensor.matmul(ps[s][1][:, :], v_(s, FFN, "hT"), WA[:, W_EARLY("ff1_up")],
                                         start=True, stop=False, skip_group_check=True)
                        add_bias(ps[s][1][:, :], "ff1_up").then_inc(up_ps, 1)
                if ahead:
                    front(i, 2)
                for s in range(2):
                    pe.wait_ge(n_sb, nth(f, i, s))
                    for t in range(4):
                        mm = nc.tensor.transpose(ps[s][2][:, 128 * t:128 * t + 128], v_(s, FFN, "n", 128 * t, 128), ident)
                    mm.then_inc(nT_ps, 1)
                for s in range(2):
                    pe.wait_ge(nT_sb, nth(f, i, s))
                    y = ps[s][3][:, 0:128]
                    nbT = v_(s, FFN, "nbT").bitcast(BF16)
                    for t in range(4):
                        if quant:
                            mm = nc.tensor.matmul(y, nbT[:, 128 * t:128 * t + 128], tern_down[:, t, :],
                                                  start=t == 0, stop=t == 3, skip_group_check=True)
                        else:
                            nc.tensor.matmul(y, v_(s, FFN, "nT", 128 * t, 128), WA[:, W_EARLY("ff1_down", 128 * t, 128)],
                                             start=t == 0, stop=False, skip_group_check=True)
                    if not quant:
                        mm = add_bias(y, "ff1_down")
                    mm.then_inc(y_ps, 1)

            pairs(pe, front, body)

        def ff_act(act, sub):
            quant, f = sub == S_FF2, ff_run[sub]

            def out_of(dst, dst_b, src):
                if quant:
                    return nc.scalar.activation(dst_b.bitcast(BF16), src, ACT.Identity, bias=minus_round[:, 0:1])
                return nc.scalar.copy(dst, src)

            def front(i, d):
                for s in range(2):
                    act.wait_ge(hT_ps, nth(f, i, s + d))
                    out_of(v_(s, FFN, "hT"), v_(s, FFN, "hbT"), ps[s][0][:, 0:128]).then_inc(hT_sb, 1)

            def body(i, ahead):
                for s in range(2):
                    if quant:
                        act.wait_ge(up_in, nth(0, i, s))
                        nc.scalar.activation(v_(s, FFN, "u"), v_(s, FFN, "u"), ACT.Gelu).then_inc(up_act, 1)
                    else:
                        act.wait_ge(up_ps, nth(f, i, s))
                        nc.scalar.activation(v_(s, FFN, "u"), ps[s][1][:, :], ACT.Gelu).then_inc(up_act, 1)
                if ahead:
                    front(i, 2)
                for s in range(2):
                    act.wait_ge(nT_ps, nth(f, i, s))
                    out_of(v_(s, FFN, "nT"), v_(s, FFN, "nbT"), ps[s][2][:, :]).then_inc(nT_sb, 1)

            pairs(act, front, body)

        def quantize(dve, name, at, second_ready=None):
            def a(s, k):
                return v_(s, FFN, "a", at + k, 1)

            def each(f):
                dve.drain()
                for s in range(2):
                    done = f(s, v_(s, FFN, name))
                return done

            dve.drain()
            for s in range(2):
                if s == 1 and second_ready:
                    second_ready()
                nc.vector.tensor_reduce(a(s, 0), v_(s, FFN, name), AXX, ALU.max, apply_absolute_value=True)
            each(lambda s, t: nc.vector.tensor_scalar(a(s, 0), a(s, 0), 1e-5, None, ALU.max))
            each(lambda s, t: nc.vector.reciprocal(a(s, 1), a(s, 0)))
            each(lambda s, t: nc.vector.tensor_scalar(a(s, 1), a(s, 1), 127.0, None, ALU.mult))
            each(lambda s, t: nc.vector.reciprocal(a(s, 2), a(s, 1)))
            for s in range(2):
                t = v_(s, FFN, name)
                nc.vector.tensor_scalar(t, t, a(s, 1), ROUND, ALU.mult, ALU.add)
            dve.drain()
            for s in range(2):
                t = v_(s, FFN, name)
                nc.vector.tensor_scalar(t, t, ROUND + 127.0, ROUND - 128.0, ALU.min,
                                        ALU.max).then_inc(h_sb if name == "h" else n_sb, 1)

        def ff_dve(dve, sub):
            quant, f = sub == S_FF2, ff_run[sub]
            pre = "ff2_" if quant else "ff1_"

            def moments(i, d):
                for s in range(2):
                    dve.wait_ge(staged, nth(sub, i, s + d))
                    stats(dve, s, FFN, v_(s, FFN, "x"), at=2).then_inc(ff_v1, 1)

            def normed(i, d):
                for s in range(2):
                    dve.wait_ge(ff_r1, nth(f, i, s + d))
                    h = v_(s, FFN, "h")
                    done = norm_affine(dve, s, FFN, h, v_(s, FFN, "x"), pre + "g1", pre + "b1", 1)
                    if not quant:
                        done.then_inc(h_sb, 1)
                if quant:
                    quantize(dve, "h", 0)

            def front(i, d):
                moments(i, d)
                normed(i, d)

            def body(i, ahead):
                if quant:
                    for s in range(2):
                        dve.wait_ge(up_ps, nth(f, i, s))
                        a = v_(s, FFN, "a", 6, 1)
                        nc.vector.tensor_tensor(a, v_(s, FFN, "a", 2, 1), small[:, 14:15], ALU.mult)
                        dve.drain()
                        nc.vector.scalar_tensor_tensor(v_(s, FFN, "u"), ps[s][1][:, :], a, R[:, ROWS("ff2_up")],
                                                       ALU.mult, ALU.add).then_inc(up_in, 1)
                if ahead:
                    moments(i, 2)
                for s in range(2):
                    dve.wait_ge(up_act, nth(f, i, s))
                    stats(dve, s, FFN, v_(s, FFN, "u")).then_inc(mid_var, 1)
                if ahead:
                    normed(i, 2)
                for s in range(2):
                    n = v_(s, FFN, "n")
                    if quant and s == 1:
                        continue
                    dve.wait_ge(mid_rstd, nth(mid_run[sub], i, s))
                    done = norm_affine(dve, s, FFN, n, v_(s, FFN, "u"), pre + "g2", pre + "b2")
                    if not quant:
                        done.then_inc(n_sb, 1)
                if quant:
                    quantize(dve, "n", 3, lambda: dve.wait_ge(n_normed, i + 1))
                for s in range(2):
                    if quant:
                        dve.wait_ge(y_ps, nth(tail_run[sub], i, s))
                        a, r = v_(s, FFN, "a", 6, 1), v_(s, FFN, "r")
                        nc.vector.tensor_tensor(a, v_(s, FFN, "a", 5, 1), small[:, 15:16], ALU.mult)
                        dve.drain()
                        nc.vector.scalar_tensor_tensor(r, ps[s][3][:, 0:128], a, R[:, ROWS("ff2_down")], ALU.mult, ALU.add)
                        dve.drain()
                        nc.vector.tensor_tensor(r, r, x_of(i, s), ALU.add)
                        dve.drain()
                        stats(dve, s, FFN, r).then_inc(var_ok, 1)
                    else:
                        dve.wait_ge(mid_rstd, nth(mid_run[sub], i, s))
                        tail_stats(dve, tail_run[sub], i, s, FFN, ps[s][3][:, 0:128], x_of(i, s))
                for s in range(2):
                    tail_norm(dve, tail_run[sub], i, s, FFN)

            pairs(dve, front, body)

        def mlp_pool(pool):
            with pool.Fori(0, PAIRS) as i:
                stage_x(pool, S_MLP, MLP, None, i)

        def mlp_pe(pe):
            with pe.Fori(0, PAIRS) as i:
                for s in range(2):
                    transpose_x(pe, S_MLP, i, s, MLP)
                for s in range(2):
                    pe.wait_ge(xT_sb, nth(xt_run[S_MLP], i, s))
                    for m in range(3):
                        for t in range(4):
                            o = ps[s][1 + m][:, 128 * t:128 * t + 128]
                            nc.tensor.matmul(o, WA[:, W_EARLY("mlp_up", FF * m + 128 * t, 128)], v_(s, MLP, "xT"),
                                             start=True, stop=False, skip_group_check=True)
                            mm = nc.tensor.matmul(o, bias3[:, BIAS("mlp_up", FF * m + 128 * t, 128)], ones_b[0:3, :],
                                                  start=False, stop=True, skip_group_check=True)
                        mm.then_inc(mlp_ps, 1)
                for s in range(2):
                    for m in range(3):
                        pe.wait_ge(mlp_act, nth(0, i, s, 3, m + 1))
                        o = ps[s][0][:, 128 * m:128 * m + 128]
                        for t in range(4):
                            g, w = v_(s, MLP, "G", FF * m + 128 * t, 128), WA[:, W_EARLY("mlp_down", FF * m + 128 * t, 128)]
                            l, r = (w, g) if m < 2 else (g, w)
                            nc.tensor.matmul(o, l, r, start=t == 0, stop=False, skip_group_check=True)
                        if m < 2:
                            mm = nc.tensor.matmul(o, bias3[:, BIAS("mlp_down", 128 * m, 128)], ones_b[0:3, :],
                                                  start=False, stop=True, skip_group_check=True)
                        else:
                            mm = add_bias(o, "mlp_down", 256, 128)
                    mm.then_inc(mlp_out, 1)

        def mlp_act_(act):
            with act.Fori(0, PAIRS) as i:
                for s in range(2):
                    act.wait_ge(xT_ps, nth(xt_run[S_MLP], i, s))
                    nc.scalar.copy(v_(s, MLP, "xT"), ps[s][0][:, 0:128]).then_inc(xT_sb, 1)
                for s in range(2):
                    for m in range(3):
                        act.wait_ge(mlp_ps, nth(0, i, s, 3, m + 1))
                        nc.scalar.activation(v_(s, MLP, "G", FF * m, FF), ps[s][1 + m][:, :], ACT.Gelu).then_inc(mlp_act, 1)

        def mlp_dve(dve):
            with dve.Fori(0, PAIRS) as i:
                for s in range(2):
                    dve.wait_ge(mlp_out, nth(0, i, s))
                    nc.vector.tensor_copy(arena[s][:, bass.ds(i * 384 + QKV_KEPT, 384)], ps[s][0][:, 0:384]).then_inc(seq_done, 1)

        XSCALE = 1.0 / math.sqrt(XD)
        HALVES, HH = 2, XH // 2

        def lat_pool(pool):
            pool.wait_ge(seq_done, all_done + BATCH * S_MQA)
            pool.wait_ge(late_in, 32)
            for s in range(2):
                nc.gpsimd.memset(v_(s, LAT, "qT"), 0.0)
            pool.drain()

            def stage(i, d):
                for s in range(2):
                    if d == 0:
                        pool.wait_ge(seq_done, nth(S_LAT, i, s))
                    else:
                        pool.wait_ge(h_sb, nth(2, i, s))
                    nc.gpsimd.tensor_copy(v_(s, LAT, "c"), x_at(ctx_all, i, s + d))
                    nc.gpsimd.tensor_copy(v_(s, LAT, "x"), x_at(x_all, i, s + d))
                    pool.drain()
                    pool.sem_inc(staged, 1)

            def norms(i, d):
                for s in range(2):
                    rstd(pool, mid_var, mid_rstd, mid_run[S_LAT], i, s, LAT, 2, d)

            def front(i, d):
                stage(i, d)
                norms(i, d)

            def body(i, ahead):
                if ahead:
                    stage(i, 2)
                if ahead:
                    norms(i, 2)
                for s in range(2):
                    rstd(pool, var_ok, rstd_ok, tail_run[S_LAT], i, s, LAT)

            pairs(pool, front, body)

        LORDER = ((0, 1, 2, 3), (1, 2, 3, 0))

        def lat_pe(pe):
            def project_q(s, hf):
                for t in range(4):
                    mm = nc.tensor.matmul(ps[s][hf][:, 128 * t:128 * t + 128],
                                          WA[:, W_LATE("lat_q", 512 * hf + 128 * t, 128)],
                                          v_(s, LAT, "nT", 128, 128), start=True, stop=True,
                                          skip_group_check=True)
                mm.then_inc(l_q, 1)

            pe.wait_ge(late_in, 32)

            def front(i, d):
                for s in range(2):
                    pe.wait_ge(h_sb, nth(2, i, s + d))
                    for k in range(2):
                        mm = nc.tensor.transpose(ps[s][3][:, 128 * k:128 * k + 128], v_(s, LAT, "n", 128 * k, 128), ident)
                    mm.then_inc(xT_ps, 1)

            def body(i, ahead):
                for s in range(2):
                    pe.wait_ge(xT_sb, nth(xt_run[S_LAT], i, s))
                    nT = v_(s, LAT, "nT")
                    project_q(s, 0)
                    for t in range(8):
                        if t == 4:
                            pe.wait_ge(l_qsb, i * 4 + (s + 1))
                            pe.wait_ge(var_ok, nth(tail_run[S_LAT], i, s - 2))
                        mm = nc.tensor.matmul(ps[s][(2 + t // 2) % 4][:, 256 * (t % 2):256 * (t % 2) + 256],
                                              WA[:, W_LATE("lat_k", 128 * t, 128)], nT, start=True, stop=True,
                                              skip_group_check=True)
                        if t % 4 == 3:
                            mm.then_inc(l_k, 1)
                for s in range(2):
                    nT = v_(s, LAT, "nT")
                    for k in range(2):
                        pe.wait_ge(l_ksb, nth(0, i, s, 2, k + 1))
                        for c in range(2):
                            mm = nc.tensor.matmul(ps[s][(2 + 2 * k + c) % 4][:, :], nT[:, 128 * k:128 * k + 128],
                                                  WA[:, W_LATE("lat_v", 512 * c, 512)], start=True, stop=True)
                        mm.then_inc(l_v, 1)

                def scores(hf, s):
                    if hf == 0:
                        pe.wait_ge(l_vsb, nth(0, i, s, 2, 2))
                    else:
                        pe.wait_ge(l_qsb, i * 4 + (2 + s + 1))
                    kT = v_(s, LAT, "kT").rearrange("p (t k) -> p t k", t=8)
                    for t in LORDER[hf]:
                        if hf == 1 and t == 0:
                            pe.wait_ge(l_osb, i * 4 + (s + 1))
                        for h in (2 * t, 2 * t + 1):
                            mm = nc.tensor.matmul(ps[s][t][:, 256 * (h % 2):256 * (h % 2) + 256],
                                                  v_(s, LAT, "qT", 128 * h, 128), kT[:, 4 * hf + t, :],
                                                  start=True, stop=True, skip_group_check=True)
                        mm.then_inc(l_s, 1)

                def values(hf, s):
                    P = v_(s, LAT, "P").rearrange("p (n k) -> p n k", k=128)
                    for n, t in enumerate(LORDER[hf]):
                        pe.wait_ge(l_sub, i * 16 + (8 * hf + 4 * s + n + 1))
                        for c in range(4):
                            mm = nc.tensor.transpose(ps[s][t][:, 128 * c:128 * c + 128], P[:, 4 * t + c, :], ident)
                        mm.then_inc(l_T, 1)
                    PT = v_(s, LAT, "PT").rearrange("p (h c q) -> p h c q", h=HH, c=2)
                    V = v_(s, LAT, "V").rearrange("p (c h d) -> p c h d", c=2, h=XH)
                    for n, t in enumerate(LORDER[hf]):
                        pe.wait_ge(l_Tsb, i * 16 + (8 * hf + 4 * s + n + 1))
                        if n == 1 and hf == 0:
                            project_q(s, 1)
                        for h in (2 * t, 2 * t + 1):
                            o = ps[s][hf][XD * (h % 2):XD * (h % 2) + XD, 128 * t:128 * t + 128]
                            for c in range(2):
                                mm = nc.tensor.matmul(o, V[:, c, HH * hf + h, 0:XD], PT[:, h, c, :],
                                                      start=c == 0, stop=c == 1, skip_group_check=True)
                    mm.then_inc(l_o, 1)

                scores(0, 0)
                scores(0, 1)
                values(0, 0)
                scores(1, 0)
                values(0, 1)
                scores(1, 1)
                values(1, 0)
                values(1, 1)
                if ahead:
                    front(i, 2)
                for s in range(2):
                    pe.wait_ge(l_osb, i * 4 + (2 + s + 1))
                    OT = v_(s, LAT, "O")
                    for t in range(8):
                        mm = nc.tensor.matmul(ps[s][1][:, 0:128], OT[:, 128 * t:128 * t + 128],
                                              WA[:, W_LATE("lat_out", 128 * t, 128)], start=t == 0, stop=t == 7,
                                              skip_group_check=True)
                    mm.then_inc(y_ps, 1)

            pairs(pe, front, body)

        OUT_AT = 2

        def lat_act(act):
            def spread_q(i, s, hf):
                act.wait_ge(l_q, i * 4 + (2 * hf + s + 1))
                q = v_(s, LAT, "qT").rearrange("p (t j q) -> p t j q", t=4, j=2)
                for j in range(2):
                    rows = slice(XD * j, XD * j + XD)
                    nc.scalar.copy(q[rows, :, j, :], heads(ps[s][hf][rows, :]))
                act.drain()
                act.sem_inc(l_qsb, 1)

            def front(i, d):
                for s in range(2):
                    act.wait_ge(xT_ps, nth(xt_run[S_LAT], i, s + d))
                    nc.scalar.copy(v_(s, LAT, "nT"), ps[s][3][:, 0:256]).then_inc(xT_sb, 1)

            def body(i, ahead):
                for s in range(2):
                    spread_q(i, s, 0)
                for s in range(2):
                    V = v_(s, LAT, "V").rearrange("p (c h d) -> p c h d", c=2, h=XH)
                    for k in range(2):
                        act.wait_ge(l_v, nth(0, i, s, 2, k + 1))
                        for c in range(2):
                            nc.scalar.copy(V[:, k, 8 * c:8 * c + 8, 0:XD],
                                           ps[s][(2 + 2 * k + c) % 4][:, :].rearrange("p (h d) -> p h d", d=XD))
                        act.drain()
                        act.sem_inc(l_vsb, 1)

                def exps(hf, s, of, to):
                    for n in range(of, to):
                        t = LORDER[hf][n]
                        act.wait_ge(l_exp, i * 16 + (8 * hf + 4 * s + n + 1))
                        for j in range(2):
                            h = 2 * t + j
                            nc.scalar.activation(v_(s, LAT, "P", 256 * h, 256), ps[s][t][:, 256 * j:256 * j + 256],
                                                 ACT.Exp, scale=XSCALE, bias=v_(s, LAT, "m", h, 1),
                                                 accum_out=v_(s, LAT, "rec", h, 1))
                        act.drain()
                        act.sem_inc(l_osum, 1)

                def weights(hf, s):
                    for n, t in enumerate(LORDER[hf]):
                        act.wait_ge(l_T, i * 16 + (8 * hf + 4 * s + n + 1))
                        nc.scalar.copy(v_(s, LAT, "PT", 512 * t, 512), ps[s][t][:, :]).then_inc(l_Tsb, 1)
                    if hf == 0:
                        spread_q(i, s, 1)

                def output(hf, s):
                    act.wait_ge(l_o, i * 4 + (2 * hf + s + 1))
                    nc.scalar.copy(v_(s, LAT, "O", 512 * hf, 512), ps[s][hf][:, :]).then_inc(l_osb, 1)

                before = None
                for now in ((0, 0), (0, 1), (1, 0), (1, 1)):
                    exps(*now, 0, OUT_AT)
                    if before:
                        output(*before)
                    exps(*now, OUT_AT, 4)
                    weights(*now)
                    before = now
                output(*before)
                if ahead:
                    front(i, 2)

            pairs(act, front, body)

        def lat_dve(dve):
            def moments(i, d):
                for s in range(2):
                    dve.wait_ge(staged, nth(S_LAT, i, s + d))
                    stats(dve, s, LAT, v_(s, LAT, "c"))
                    dve.drain()
                    stats(dve, s, LAT, v_(s, LAT, "x"), at=2).then_inc(mid_var, 1)

            def norms(i, d):
                for s in range(2):
                    dve.wait_ge(mid_rstd, nth(mid_run[S_LAT], i, s + d))
                    nk, nl = v_(s, LAT, "n", 0, 128), v_(s, LAT, "n", 128, 128)
                    norm_affine(dve, s, LAT, nk, v_(s, LAT, "c"), "lat_mg", "lat_mb", 0)
                    norm_affine(dve, s, LAT, nl, v_(s, LAT, "x"), "lat_lg", "lat_lb", 1).then_inc(h_sb, 1)

            def front(i, d):
                moments(i, d)
                norms(i, d)

            def body(i, ahead):
                for s in range(2):
                    for k in range(2):
                        dve.wait_ge(l_k, nth(0, i, s, 2, k + 1))
                        for c in range(2):
                            nc.vector.tensor_copy(v_(s, LAT, "kT", 1024 * k + 512 * c, 512), ps[s][(2 + 2 * k + c) % 4][:, :])
                        dve.drain()
                        dve.sem_inc(l_ksb, 1)

                def maxima(hf, s, n):
                    t = LORDER[hf][n]
                    dve.wait_ge(l_s, i * 16 + (8 * hf + 4 * s + n + 1))
                    m = v_(s, LAT, "m", 2 * t, 2)
                    nc.vector.tensor_reduce(m, ps[s][t][:, :].rearrange("p (j k) -> p j k", j=2), AXX, ALU.max)
                    dve.drain()
                    nc.vector.tensor_scalar(m, m, -XSCALE, None, ALU.mult).then_inc(l_exp, 1)

                def shares(hf, s, n):
                    t = LORDER[hf][n]
                    dve.wait_ge(l_osum, i * 16 + (8 * hf + 4 * s + n + 1))
                    rec = v_(s, LAT, "rec", 2 * t, 2)
                    nc.vector.reciprocal(rec, rec)
                    dve.drain()
                    p = v_(s, LAT, "P", 512 * t, 512).rearrange("p (j k) -> p j k", j=2)
                    nc.vector.tensor_tensor(p, p, rec.unsqueeze(2).broadcast_to([128, 2, 256]), ALU.mult).then_inc(l_sub, 1)

                for hf in range(HALVES):
                    for s in range(2):
                        if ahead and hf == 1:
                            (moments, norms)[s](i, 2)
                        for n in range(4):
                            maxima(hf, s, n)
                            if n > 0:
                                shares(hf, s, n - 1)
                        shares(hf, s, 3)
                for s in range(2):
                    tail_stats(dve, tail_run[S_LAT], i, s, LAT, ps[s][1][:, 0:128], x_of(i, s))
                for s in range(2):
                    tail_norm(dve, tail_run[S_LAT], i, s, LAT)

            pairs(dve, front, body)

        def gate_pool(pool):
            stage_ahead(pool, S_GATE, MOE)

        def gate_pe(pe):
            with pe.Fori(0, PAIRS) as i:
                for s in range(2):
                    transpose_x(pe, S_GATE, i, s, MOE)
                for s in range(2):
                    pe.wait_ge(xT_sb, nth(xt_run[S_GATE], i, s))
                    pe.wait_ge(seq_done, nth(S_GATE, i, s))
                    nc.tensor.matmul(ps[s][1][:, 0:EXPERTS], v_(s, MOE, "xT"), WA[:, W_LATE("gate")],
                                     start=True, stop=True).then_inc(gate_ps, 1)

        def gate_act(act):
            with act.Fori(0, PAIRS) as i:
                for s in range(2):
                    act.wait_ge(xT_ps, nth(xt_run[S_GATE], i, s))
                    nc.scalar.copy(v_(s, MOE, "xT"), ps[s][0][:, 0:128]).then_inc(xT_sb, 1)
            act.wait_ge(gate_sub, 1)
            nc.scalar.activation(comb[:, :, :], comb[:, :, :], ACT.Exp).then_inc(gate_exp, 1)

        def gate_dve(dve):
            with dve.Fori(0, PAIRS) as i:
                for s in range(2):
                    dve.wait_ge(gate_ps, nth(0, i, s))
                    nc.vector.tensor_copy(comb[:, bass.ds(i * 2 + s, 1), :].rearrange("p a e -> p (a e)"),
                                          ps[s][1][:, 0:EXPERTS]).then_inc(seq_done, 1)
            wide = [128, BATCH, EXPERTS]
            cube = [128, BATCH * EXPERTS, EXPERTS]
            t = small[:, 96:112]
            dve.drain()
            nc.vector.tensor_reduce(t, comb[:, :, :], AXX, ALU.max)
            dve.drain()
            nc.vector.tensor_tensor(comb[:, :, :], comb[:, :, :], t.unsqueeze(2).broadcast_to(wide), ALU.subtract).then_inc(gate_sub, 1)
            dve.wait_ge(gate_exp, 1)
            nc.vector.tensor_reduce(t, comb[:, :, :], AXX, ALU.add)
            dve.drain()
            nc.vector.reciprocal(t, t)
            dve.drain()
            nc.vector.tensor_tensor(comb[:, :, :], comb[:, :, :], t.unsqueeze(2).broadcast_to(wide), ALU.mult)
            dve.drain()
            gt = arena[0][:, 4096:5120].rearrange("p (b e f) -> p b e f", b=BATCH, e=EXPERTS)
            eq = arena[0][:, 5120:6144].rearrange("p (b e f) -> p b e f", b=BATCH, e=EXPERTS)
            mine = comb[:, :, :].unsqueeze(3).broadcast_to([128, BATCH, EXPERTS, EXPERTS])
            other = comb[:, :, :].unsqueeze(2).broadcast_to([128, BATCH, EXPERTS, EXPERTS])
            early = cst("earlier").rearrange("p (e f) -> p e f", e=EXPERTS).unsqueeze(1).broadcast_to([128, BATCH, EXPERTS, EXPERTS])
            nc.vector.tensor_tensor(gt, other, mine, ALU.is_gt)
            nc.vector.tensor_tensor(eq, other, mine, ALU.is_equal)
            dve.drain()
            nc.vector.tensor_tensor(eq, eq, early, ALU.mult)
            dve.drain()
            nc.vector.tensor_tensor(gt, gt, eq, ALU.add)
            dve.drain()
            rank = arena[0][:, 6144:6272]
            nc.vector.tensor_reduce(rank, gt.rearrange("p b e f -> p (b e) f"), AXX, ALU.add)
            dve.drain()
            nc.vector.tensor_scalar(rank, rank, 1.5, None, ALU.is_lt)
            dve.drain()
            c2 = comb[:, :, :].rearrange("p b e -> p (b e)")
            nc.vector.tensor_tensor(c2, c2, rank, ALU.mult)
            dve.drain()
            nc.vector.tensor_reduce(t, comb[:, :, :], AXX, ALU.add)
            dve.drain()
            nc.vector.tensor_scalar(t, t, 1e-9, None, ALU.add)
            dve.drain()
            nc.vector.reciprocal(t, t)
            dve.drain()
            nc.vector.tensor_tensor(comb[:, :, :], comb[:, :, :], t.unsqueeze(2).broadcast_to(wide), ALU.mult)
            dve.drain()
            nc.vector.tensor_reduce(comb_sum[:, :], comb[:, :, :], AXX, ALU.add).then_inc(gate_sub, 1)

        def moe_pool(pool):
            pool.wait_ge(gate_sub, 2)

            def stage(i, d):
                for s in range(2):
                    if d == 0:
                        pool.wait_ge(seq_done, nth(S_MOE, i, s))
                    else:
                        pool.wait_ge(xT_ps, nth(xt_run[S_MOE], i, s))
                    nc.gpsimd.tensor_copy(v_(s, MOE, "x"), x_at(x_all, i, s + d))
                    pool.drain()
                    pool.sem_inc(staged, 1)

            def shares(i, d):
                for s in range(2):
                    nc.gpsimd.tensor_copy(share[s][:, 0:EXPERTS], x_at(comb, i, s + d))
                    nc.gpsimd.tensor_copy(share[s][:, EXPERTS:EXPERTS + 1], comb_sum[:, bass.ds(i * 2 + (s + d), 1)])
                    pool.drain()
                    pool.sem_inc(share_in, 1)

            def front(i, d):
                stage(i, d)
                shares(i, d)

            def body(i, ahead):
                if ahead:
                    stage(i, 2)
                for s in range(2):
                    rstd(pool, var_ok, rstd_ok, tail_run[S_MOE], i, s, MOE)
                if ahead:
                    shares(i, 2)

            pairs(pool, front, body)

        share = [v_(s, MOE, "share") for s in range(2)]

        def moe_pe(pe):
            def front(i, d):
                for s in range(2):
                    pe.wait_ge(staged, nth(S_MOE, i, s + d))
                    if d:
                        pe.wait_ge(e_acc, i * 16 + (2 * 5 + s + 1))
                    nc.tensor.transpose(ps[s][3][:, 0:128], v_(s, MOE, "x"), ident).then_inc(xT_ps, 1)

            def body(i, ahead):
                for s in range(2):
                    pe.wait_ge(xT_sb, nth(xt_run[S_MOE], i, s))
                for e in range(EXPERTS):
                    for s in range(2):
                        if e >= 3:
                            pe.wait_ge(e_acc, i * 16 + (2 * (e - 3) + s + 1))
                        o = ps[s][1 + e % 3][:, :]
                        nc.tensor.matmul(o, v_(s, MOE, "xT"), WA[:, W_LATE("experts", FF * e, FF)], start=True, stop=False,
                                         skip_group_check=True)
                        add_bias(o, "experts", FF * e, FF).then_inc(e_ps, 1)
                if ahead:
                    front(i, 2)
                for s in range(2):
                    pe.wait_ge(e_acc, i * 16 + (2 * (EXPERTS - 1) + s + 1))
                    for k in range(2):
                        mm = nc.tensor.transpose(ps[s][0][:, 128 * k:128 * k + 128], v_(s, MOE, "acc", 128 * k, 128), ident)
                    mm.then_inc(acc_T, 1)
                for s in range(2):
                    pe.wait_ge(acc_Tsb, nth(0, i, s))
                    for k in range(2):
                        mm = nc.tensor.matmul(ps[s][0][:, 256:384], v_(s, MOE, "accT", 128 * k, 128),
                                              WA[:, W_LATE("moe_out", 128 * k, 128)], start=k == 0, stop=k == 1,
                                              skip_group_check=True)
                    mm.then_inc(y_ps, 1)

            pairs(pe, front, body)

        def moe_act(act):
            def front(i, d):
                for s in range(2):
                    act.wait_ge(xT_ps, nth(xt_run[S_MOE], i, s + d))
                    nc.scalar.copy(v_(s, MOE, "xT"), ps[s][3][:, 0:128]).then_inc(xT_sb, 1)

            def body(i, ahead):
                for e in range(EXPERTS):
                    for s in range(2):
                        act.wait_ge(e_ps, i * 16 + (2 * e + s + 1))
                        if e >= 2:
                            act.wait_ge(e_acc, i * 16 + (2 * (e - 2) + s + 1))
                        nc.scalar.activation(v_(s, MOE, "sig", 256 * (e % 2), 256), ps[s][1 + e % 3][:, 256:512],
                                             ACT.Sigmoid).then_inc(e_sig, 1)
                if ahead:
                    front(i, 2)
                for s in range(2):
                    act.wait_ge(acc_T, nth(0, i, s))
                    nc.scalar.copy(v_(s, MOE, "accT"), ps[s][0][:, 0:256]).then_inc(acc_Tsb, 1)

            pairs(act, front, body)

        def moe_dve(dve):
            with dve.Fori(0, PAIRS) as i:
                for s in range(2):
                    dve.wait_ge(share_in, nth(0, i, s))
                for e in range(EXPERTS):
                    for s in range(2):
                        dve.wait_ge(e_sig, i * 16 + (2 * e + s + 1))
                        t = v_(s, MOE, "t", 256 * (e % 2), 256)
                        nc.vector.tensor_tensor(t, ps[s][1 + e % 3][:, 0:256], v_(s, MOE, "sig", 256 * (e % 2), 256), ALU.mult)
                    dve.drain()
                    for s in range(2):
                        t, acc, w = v_(s, MOE, "t", 256 * (e % 2), 256), v_(s, MOE, "acc"), share[s][:, e:e + 1]
                        if e == 0:
                            nc.vector.tensor_scalar(acc, t, w, None, ALU.mult).then_inc(e_acc, 1)
                        else:
                            nc.vector.scalar_tensor_tensor(acc, t, w, acc, ALU.mult, ALU.add).then_inc(e_acc, 1)
                for s in range(2):
                    nc.vector.scalar_tensor_tensor(v_(s, MOE, "t", 0, 128), R[:, ROWS("moe_bo")],
                                                   share[s][:, EXPERTS:EXPERTS + 1], x_of(i, s), ALU.mult, ALU.add)
                dve.drain()
                for s in range(2):
                    tail_stats(dve, tail_run[S_MOE], i, s, MOE, ps[s][0][:, 256:384], v_(s, MOE, "t", 0, 128))
                for s in range(2):
                    tail_norm(dve, tail_run[S_MOE], i, s, MOE)

        def on(sub):
            return sub <= last

        @block.sync
        def _(sp):
            loads(sp)
            if on(S_REG):
                sim_sp(sp)
            if on(S_LAT):
                sp.wait_ge(seq_done, all_done + BATCH * S_SELF2)
                sp.dma_start(WA[:, 0:W_LATE.size], w_late).then_inc(late_in, 16)
                sp.dma_start(ctx_all[:, :, :], ctx_tok).then_inc(late_in, 16)
            sp.wait_ge(rest_in, 16 * loads_rest)
            sp.wait_ge(seq_done, all_done + BATCH * last)
            sp.dma_start(out, x_all[:, :, :]).then_inc(stored, 16)
            sp.wait_ge(stored, 16)

        @block.gpsimd
        def _(pool):
            start_pool(pool)
            pos_pool(pool)
            if on(S_X0):
                pool.wait_ge(rest_in, 16 * loads_rest)
                att_pool(pool, S_X0, "cross")
            if on(S_SIM):
                sim_pool_(pool)
            if on(S_REG):
                att_pool(pool, S_REG, "self")
            if on(S_LIN):
                att_pool(pool, S_LIN, "linear")
            if on(S_X1):
                wide_pool(pool)
            if on(S_FF1):
                ff_pool(pool, S_FF1)
            if on(S_MLP):
                mlp_pool(pool)
            if on(S_SELF2):
                att_pool(pool, S_SELF2, "kept")
            if on(S_X2):
                att_pool(pool, S_X2, "cross")
            if on(S_FF2):
                ff_pool(pool, S_FF2)
            if on(S_MQA):
                att_pool(pool, S_MQA, "self")
            if on(S_LAT):
                lat_pool(pool)
            if on(S_GATE):
                gate_pool(pool)
            if on(S_MOE):
                moe_pool(pool)

        @block.tensor
        def _(pe):
            lstm_pe(pe)
            pos_pe(pe)
            pe.wait_ge(w_tern, 2)
            pe.wait_ge(rest_in, 16 * loads_rest)
            if on(S_X0):
                att_pe(pe, S_X0, "cross", WA, "x0", "x0", "full")
            if on(S_SIM):
                sim_pe(pe)
            if on(S_REG):
                att_pe(pe, S_REG, "self", WA, "reg", None, "pos")
            if on(S_LIN):
                att_pe(pe, S_LIN, "linear", WA, "lin", "lin", None)
            if on(S_X1):
                wide_pe(pe)
            if on(S_FF1):
                ff_pe(pe, S_FF1)
            if on(S_MLP):
                mlp_pe(pe)
            if on(S_SELF2):
                att_pe(pe, S_SELF2, "kept", WA, None, None, None, 0, "self2_out")
            if on(S_X2):
                att_pe(pe, S_X2, "cross", WB, "x2", "x2", None)
            if on(S_FF2):
                ff_pe(pe, S_FF2)
            if on(S_MQA):
                att_pe(pe, S_MQA, "self", WB, "mqa", "mqa", "causal")
            if on(S_LAT):
                lat_pe(pe)
            if on(S_GATE):
                gate_pe(pe)
            if on(S_MOE):
                moe_pe(pe)

        @block.scalar
        def _(act):
            lstm_act(act)
            pos_act(act)
            if on(S_X0):
                att_act(act, S_X0, "cross")
            if on(S_SIM):
                sim_act(act)
            if on(S_REG):
                att_act(act, S_REG, "self")
            if on(S_LIN):
                att_act(act, S_LIN, "linear")
            if on(S_X1):
                wide_act(act)
            if on(S_FF1):
                ff_act(act, S_FF1)
            if on(S_MLP):
                mlp_act_(act)
            if on(S_SELF2):
                att_act(act, S_SELF2, "kept")
            if on(S_X2):
                att_act(act, S_X2, "cross")
            if on(S_FF2):
                ff_act(act, S_FF2)
            if on(S_MQA):
                att_act(act, S_MQA, "self")
            if on(S_LAT):
                lat_act(act)
            if on(S_GATE):
                gate_act(act)
            if on(S_MOE):
                moe_act(act)

        @block.vector
        def _(dve):
            start_dve(dve)
            lstm_dve(dve)
            pos_dve(dve)
            if on(S_X0):
                att_dve(dve, S_X0, "cross")
            if on(S_SIM):
                sim_dve(dve)
            if on(S_REG):
                att_dve(dve, S_REG, "self")
            if on(S_LIN):
                att_dve(dve, S_LIN, "linear")
            if on(S_X1):
                wide_dve(dve)
            if on(S_FF1):
                ff_dve(dve, S_FF1)
            if on(S_MLP):
                mlp_dve(dve)
            if on(S_SELF2):
                att_dve(dve, S_SELF2, "kept")
            if on(S_X2):
                att_dve(dve, S_X2, "cross")
            if on(S_FF2):
                ff_dve(dve, S_FF2)
            if on(S_MQA):
                att_dve(dve, S_MQA, "self")
            if on(S_LAT):
                lat_dve(dve)
            if on(S_GATE):
                gate_dve(dve)
            if on(S_MOE):
                moe_dve(dve)


def constants():
    c = np.zeros((128, CONST.size), np.float32)

    def put(name, a):
        a = np.asarray(a, np.float32)
        c[:a.shape[0], CONST(name)] = a

    p = np.arange(128)
    row = p.astype(np.float32)
    put("ident", np.eye(128))
    put("rel", row[None, :] / (row[:, None] + np.float32(1)))
    put("tri", p[None, :] <= p[:, None])
    put("triT", p[None, :] >= p[:, None])
    put("causal", np.where(p[None, :] <= p[:, None], 0.0, BIG))
    half, turn = HD // 2, HD // 4
    theta = np.float32(10000.0) ** (-np.arange(half, dtype=np.float32) / np.float32(half))
    freqs = theta[:, None] * row[None, :]
    cos, sin = np.ones((HEADS, HD, TOK)), np.zeros((HEADS, HD, TOK))
    cos[:, :half], sin[:, :half] = np.cos(freqs), np.sin(freqs)
    sin[:, :turn] *= -1
    put("cos", cos.reshape(128, TOK))
    put("sin", sin.reshape(128, TOK))
    put("headmask", p[:, None] // HD == np.arange(HEADS)[None, :])
    r = np.arange(REG_ROWS)
    put("blockmask", (r[:, None] // REG) == (p[None, :] // HD))
    put("regsel", 0.5 * ((r[:, None] % REG) == p[None, :]))
    put("notreg", p[:, None] >= REG)
    put("regscale", np.where(p[:, None] < REG, 0.5, 1.0))
    put("minushalf", np.full((128, 16), -0.5))
    put("step", np.broadcast_to((row + 1) / np.float32(TOK), (128, 128)))
    e = np.arange(EXPERTS)
    put("earlier", np.broadcast_to((e[None, :] < e[:, None]).reshape(1, -1), (128, 64)))
    return c


def kernel(**inputs):
    import concourse.bacc as bacc
    from concourse.bass_utils import run_bass_kernel_spmd

    a = {k: np.asarray(v) for k, v in inputs.items()}

    def side(*parts):
        return np.concatenate(parts, axis=1)

    def blocks(w, n=4):
        return w.reshape(n, 128, -1).transpose(1, 0, 2).reshape(128, -1)

    def tall(w):
        return np.concatenate([w, np.zeros((128 - w.shape[0], w.shape[1]), w.dtype)], 0)

    def gates_order(w):
        h = LSTM_H
        return np.concatenate([w[:2 * h], w[3 * h:], w[2 * h:3 * h]], 0)

    def T(n):
        return a[n].T

    def turned(w):
        h = w.reshape(*w.shape[:-1], -1, HD)
        return np.concatenate([h[..., 2:4], h[..., 0:2], h[..., 4:]], -1).reshape(w.shape)

    wk16, bk16 = np.tile(a["L3_attn_Wk"], (1, HEADS)), np.tile(a["L3_attn_bk"], HEADS)

    early = side(
        gates_order(a["L0_attn_W_ih"]).T, tall(gates_order(a["L0_attn_W_hh"]).T),
        tall(np.concatenate([a["L0_attn_W_mu"], a["L0_attn_W_sig"]], 0).T),
        T("L0_xattn_Wq"), T("L0_xattn_Wk"), T("L0_xattn_Wv"), T("L0_xattn_Wo"),
        a["L0_ffn_W_qkv"], a["L0_ffn_W_proj"], T("L1_attn_Wqkv"), T("L1_attn_Wout"),
        a["L1_xattn_Wq"], a["L1_xattn_Wk"], a["L1_xattn_Wv"], T("L1_ffn_w1"), blocks(T("L1_ffn_w2")),
        a["L2_attn_q_w1"], a["L2_attn_k_w1"], a["L2_attn_v_w1"],
        blocks(a["L2_attn_q_w2"]), blocks(a["L2_attn_k_w2"]), blocks(a["L2_attn_v_w2"]),
        a["L2_attn_proj_w"])
    late = side(
        a["L3_xattn_Wq"], a["L3_xattn_Wkv"], blocks(a["L3_xattn_Wout"], 8), T("L3_ffn_Wg"),
        a["L3_ffn_W1"].transpose(2, 0, 1).reshape(128, -1), blocks(T("L3_ffn_Wo"), 2))
    rest = side(
        T("L2_xattn_Wq"), T("L2_xattn_Wk"), T("L2_xattn_Wv"), T("L2_xattn_Wo"),
        a["L3_attn_Wq"], wk16, np.tile(a["L3_attn_Wv"], (1, HEADS)), a["L3_attn_Wo"],
        turned(a["L3_attn_Wq"]), turned(wk16), T("L2_ffn_w1"), blocks(T("L2_ffn_w2")))
    bias = np.concatenate([
        gates_order(a["L0_attn_b_ih"][:, None])[:, 0], gates_order(a["L0_attn_b_hh"][:, None])[:, 0],
        a["L0_xattn_bq"], a["L0_xattn_bk"], a["L0_xattn_bv"], a["L0_xattn_bo"], a["L0_ffn_b_proj"],
        a["L1_attn_bqkv"], a["L1_attn_bout"], a["L1_xattn_bq"], a["L1_xattn_bk"], a["L1_xattn_bv"],
        a["L1_ffn_b1"], a["L1_ffn_b2"], a["L2_attn_q_b1"], a["L2_attn_k_b1"], a["L2_attn_v_b1"],
        a["L2_attn_q_b2"], a["L2_attn_k_b2"], a["L2_attn_v_b2"], a["L2_attn_proj_b"],
        a["L2_xattn_bq"], a["L2_xattn_bk"], a["L2_xattn_bv"], a["L2_xattn_bo"],
        a["L3_attn_bq"], bk16, np.tile(a["L3_attn_bv"], HEADS), a["L3_attn_bo"],
        turned(a["L3_attn_bq"]), turned(bk16), a["L3_ffn_b1"].reshape(-1)])
    bias = np.concatenate([bias, np.zeros(128 * BIAS_COLS - BIAS.size, bias.dtype)])
    rows = np.concatenate([
        a["L0_ffn_g_info"][0, 0], a["L1_attn_gamma"], a["L1_attn_beta"], a["L1_ffn_ln1_g"],
        a["L1_ffn_ln1_b"], a["L1_ffn_ln2_g"], a["L1_ffn_ln2_b"], a["L2_ffn_ln1_g"], a["L2_ffn_ln1_b"],
        a["L2_ffn_ln2_g"], a["L2_ffn_ln2_b"], a["L2_ffn_b1"], a["L2_ffn_b2"], a["L3_xattn_ln_m_g"],
        a["L3_xattn_ln_m_b"], a["L3_xattn_ln_l_g"], a["L3_xattn_ln_l_b"], a["L3_ffn_bo"],
        a["L0_attn_b_mu"], a["L0_attn_b_sig"]])
    arrays = {
        "x_tok": a["x"].transpose(1, 0, 2), "x_T": a["x"].transpose(2, 0, 1),
        "ctx_tok": a["ctx_1024"].transpose(1, 0, 2), "ctx_T": a["ctx_1024"].transpose(2, 0, 1),
        "mask": a["mask_BxSxS2_ik1"].transpose(1, 0, 2).reshape(128, -1),
        "mask_row": a["mask_BxS2_if1"].reshape(1, -1),
        "w_early": early, "w_late": late, "w_rest": rest,
        "bias": bias.reshape(128, BIAS_COLS), "rows": np.repeat(rows[None], 128, 0),
        "const": constants(),
    }
    nc = bacc.Bacc("TRN2", target_bir_lowering=False, num_devices=1)
    args = {}
    for name, v in arrays.items():
        arrays[name] = v = np.ascontiguousarray(v)
        args[name] = nc.dram_tensor(name, v.shape, mybir.dt.from_np(v.dtype), kind="ExternalInput").ap()
    out = nc.dram_tensor("out", (128, BATCH, DIM), F32, kind="ExternalOutput").ap()
    decoder(nc, **args, out=out)
    r = run_bass_kernel_spmd(nc, [arrays], core_ids=[0])
    return np.ascontiguousarray(r.results[0]["out"].transpose(1, 0, 2))
```
